# Optimizing a Trainium2 kernel written in Bass

```python
import numpy as np
import jax
import jax.numpy as jnp

def _softmax(x, axis=-1):
    return jax.nn.softmax(x, axis=axis)

def _gelu(x):
    return jax.nn.gelu(x, approximate=True)

def _silu(x):
    return jax.nn.silu(x)

def _sigmoid(x):
    return jax.nn.sigmoid(x)

def _layernorm(x, axis=-1, eps=1e-05):
    m = jnp.mean(x, axis=axis, keepdims=True)
    v = jnp.var(x, axis=axis, keepdims=True)
    return (x - m) / jnp.sqrt(v + eps)

def _scatter_add(tgt, idx, src, axis=0):
    return tgt.at[idx].add(src)

def _segment_sum(src, seg, n):
    return jax.ops.segment_sum(src, seg, n)
kernel_name = 'mk_decoder_preln_d4_seqx_r8_c445e1'

def setup_inputs(seed: int=0):
    np.random.seed(seed)
    _w = jnp.asarray

    def _rec_inputs():
        import jax
        import jax.numpy as jnp
        _rk = jax.random.key(seed)
        x = 0.0002279 + 0.9999 * jax.random.normal(jax.random.fold_in(_rk, 1), (32, 56, 128), jnp.float32)
        _lenS = 56 - jax.random.randint(jax.random.fold_in(_rk, 7), (32,), 0, max(1, 56 // 4) + 1, jnp.int32)
        _lenS2 = 1500 - jax.random.randint(jax.random.fold_in(_rk, 8), (32,), 0, max(1, 1500 // 4) + 1, jnp.int32)
        _ctx_1024P = jax.random.normal(jax.random.fold_in(_rk, 11), (32, 16, 128), jnp.float32)
        _ctx_1024c = jax.random.dirichlet(jax.random.fold_in(_rk, 511), 0.3 * jnp.ones((16,), jnp.float32), (32, 1500))
        _ctx_1024t = jnp.einsum('bsk,bkd->bsd', _ctx_1024c, _ctx_1024P)
        _ctx_1024t = _ctx_1024t * jax.lax.rsqrt(jnp.mean(jnp.square(_ctx_1024t)) + 1e-12) * 0.953939
        ctx_1024 = -0.000125008 + 0.999885 * (_ctx_1024t + 0.3 * jax.random.normal(jax.random.fold_in(_rk, 611), (32, 1500, 128), jnp.float32))
        _validS = jnp.arange(56)[None, :] < _lenS[:, None]
        _validS2 = jnp.arange(1500)[None, :] < _lenS2[:, None]
        _causal = jnp.tril(jnp.ones((56, 56), dtype=bool))
        mask_Bx1x1xS2_ff0 = jnp.where(jnp.ones((32, 1, 1, 1500), dtype=bool), 0.0, -1000000000.0).astype(jnp.float32)
        return (x, ctx_1024, mask_Bx1x1xS2_ff0)
    x, ctx_1024, mask_Bx1x1xS2_ff0 = _rec_inputs()

    def _L0_attn_setup():
        import jax, jax.numpy as jnp
        import numpy as np
        EMBED_DIM = 128
        NUM_HEADS = 16
        HEAD_DIM = EMBED_DIM // NUM_HEADS
        BATCH = 2
        SEQ = 256
        NEG_INF = float('-inf')
        key = jax.random.key(seed)
        k1, k2, k3, k4, k5 = jax.random.split(key, 5)
        return {'query': jax.random.normal(k1, (BATCH, SEQ, EMBED_DIM), dtype=jnp.float32), 'key': jax.random.normal(k2, (BATCH, SEQ, EMBED_DIM), dtype=jnp.float32), 'value': jax.random.normal(k3, (BATCH, SEQ, EMBED_DIM), dtype=jnp.float32), 'in_proj_weight': jax.random.normal(k4, (3 * EMBED_DIM, EMBED_DIM), dtype=jnp.float32) * (1.0 / np.sqrt(EMBED_DIM)), 'out_proj_weight': jax.random.normal(k5, (EMBED_DIM, EMBED_DIM), dtype=jnp.float32) * (1.0 / np.sqrt(EMBED_DIM))}
    _L0_attn_all = _L0_attn_setup()
    _L0_attn_in = {k: v for k, v in _L0_attn_all.items() if k in ('key', 'value', 'in_proj_weight', 'out_proj_weight')}
    del _L0_attn_all

    def _L0_xattn_setup():
        import jax, jax.numpy as jnp
        import numpy as np
        DIM = 128
        HEADS = 8
        DIM_HEAD = 64
        INNER = HEADS * DIM_HEAD
        EPS = 1e-05

        def layernorm(x, w, b):
            mu = jnp.mean(x, axis=-1, keepdims=True)
            var = jnp.var(x, axis=-1, keepdims=True)
            return (x - mu) * jax.lax.rsqrt(var + EPS) * w + b
        key = jax.random.key(seed)
        ks = jax.random.split(key, 7)
        b, n_media, n_lat = (16, 256, 64)
        x = jax.random.normal(ks[0], (b, n_media, DIM), dtype=jnp.float32)
        latents = jax.random.normal(ks[1], (b, n_lat, DIM), dtype=jnp.float32)
        ln_m_w = jnp.ones((DIM,), jnp.float32)
        ln_m_b = jnp.zeros((DIM,), jnp.float32)
        ln_l_w = jnp.ones((DIM,), jnp.float32)
        ln_l_b = jnp.zeros((DIM,), jnp.float32)
        Wq = jax.random.normal(ks[2], (DIM, INNER), dtype=jnp.float32) * DIM ** (-0.5)
        Wkv = jax.random.normal(ks[3], (DIM, 2 * INNER), dtype=jnp.float32) * DIM ** (-0.5)
        Wout = jax.random.normal(ks[4], (INNER, DIM), dtype=jnp.float32) * INNER ** (-0.5)
        return {'x': x, 'latents': latents, 'ln_m_w': ln_m_w, 'ln_m_b': ln_m_b, 'ln_l_w': ln_l_w, 'ln_l_b': ln_l_b, 'Wq': Wq, 'Wkv': Wkv, 'Wout': Wout}
    _L0_xattn_all = _L0_xattn_setup()
    _L0_xattn_in = {k: v for k, v in _L0_xattn_all.items() if k in ('ln_m_w', 'ln_m_b', 'ln_l_w', 'ln_l_b', 'Wq', 'Wkv', 'Wout')}
    del _L0_xattn_all

    def _L0_ffn_setup():
        import jax, jax.numpy as jnp
        import numpy as np
        LN_EPS = 1e-12
        key = jax.random.key(seed)
        ks = jax.random.split(key, 8)
        B, S, H, I, E = (4, 256, 128, 512, 8)
        sH = 1.0 / np.sqrt(H)
        sI = 1.0 / np.sqrt(I)
        return {'hidden_states': jax.random.normal(ks[0], (B, S, H), dtype=jnp.float32), 'Wr': jax.random.uniform(ks[1], (E, H), jnp.float32, -sH, sH), 'W1': jax.random.uniform(ks[2], (E, H, I), jnp.float32, -sH, sH), 'b1': jax.random.uniform(ks[3], (E, I), jnp.float32, -sH, sH), 'Wo': jax.random.uniform(ks[4], (I, H), jnp.float32, -sI, sI), 'bo': jax.random.uniform(ks[5], (H,), jnp.float32, -sI, sI), 'gamma': jnp.ones((H,), jnp.float32), 'beta': jnp.zeros((H,), jnp.float32)}
    _L0_ffn_all = _L0_ffn_setup()
    _L0_ffn_in = {k: v for k, v in _L0_ffn_all.items() if k in ('Wr', 'W1', 'b1', 'Wo', 'bo', 'gamma', 'beta')}
    del _L0_ffn_all

    def _L1_attn_setup():
        import jax, jax.numpy as jnp
        import numpy as np
        B, T, C = (4, 128, 128)
        HEAD_SIZE = 64
        H = C // HEAD_SIZE
        N_LAYER, LAYER_ID = (24, 12)
        D_MIX_LORA, D_DECAY_LORA = (32, 64)
        HEAD_SIZE_DIVISOR = 8
        LN_EPS = 1e-05 * HEAD_SIZE_DIVISOR ** 2

        def _wkv6(r, k, v, w, u):

            def step(S, inp):
                r_t, k_t, v_t, w_t = inp
                y = jnp.einsum('bhj,bhji->bhi', r_t, S) + jnp.sum(r_t * u * k_t, axis=-1, keepdims=True) * v_t
                decay = jnp.exp(-jnp.exp(w_t))
                S = decay[..., None] * S + k_t[..., None] * v_t[..., None, :]
                return (S, y)
            to_t = lambda a: jnp.transpose(a, (1, 0, 2, 3))
            S0 = jnp.zeros(r.shape[:1] + (r.shape[2], r.shape[3], r.shape[3]), r.dtype)
            _, ys = jax.lax.scan(step, S0, (to_t(r), to_t(k), to_t(v), to_t(w)))
            return jnp.transpose(ys, (1, 0, 2, 3))
        key = jax.random.key(seed)
        ks = jax.random.split(key, 16)
        x = jax.random.normal(ks[0], (B, T, C), jnp.float32)
        r01 = LAYER_ID / (N_LAYER - 1)
        r10 = 1.0 - LAYER_ID / N_LAYER
        ddd = np.arange(C, dtype=np.float64) / C
        time_maa_x = jnp.asarray((1.0 - ddd ** r10).astype(np.float32))
        time_maa_w = jnp.asarray((1.0 - ddd ** r10).astype(np.float32))
        time_maa_k = jnp.asarray((1.0 - ddd ** r10).astype(np.float32))
        time_maa_v = jnp.asarray((1.0 - (ddd ** r10 + 0.3 * r01)).astype(np.float32))
        time_maa_r = jnp.asarray((1.0 - ddd ** (0.5 * r10)).astype(np.float32))
        time_maa_g = jnp.asarray((1.0 - ddd ** (0.5 * r10)).astype(np.float32))
        n = np.arange(C, dtype=np.float64)
        time_decay = jnp.asarray((-6.0 + 5.0 * (n / (C - 1)) ** (0.7 + 1.3 * r01)).astype(np.float32))
        zigzag = ((n + 1) % 3 - 1) * 0.1
        time_faaaa = jnp.asarray((r01 * (1.0 - n / (C - 1)) + zigzag).astype(np.float32)).reshape(H, HEAD_SIZE)
        u = lambda k, shp: jax.random.uniform(k, shp, jnp.float32, -0.01, 0.01)
        time_maa_w1 = u(ks[1], (C, D_MIX_LORA * 5))
        time_maa_w2 = u(ks[2], (5, D_MIX_LORA, C))
        time_decay_w1 = u(ks[3], (C, D_DECAY_LORA))
        time_decay_w2 = u(ks[4], (D_DECAY_LORA, C))
        s = 1.0 / np.sqrt(C)
        Wr = jax.random.normal(ks[5], (C, C), jnp.float32) * s
        Wk = jax.random.normal(ks[6], (C, C), jnp.float32) * s
        Wv = jax.random.normal(ks[7], (C, C), jnp.float32) * s
        Wg = jax.random.normal(ks[8], (C, C), jnp.float32) * s
        Wo = jax.random.normal(ks[9], (C, C), jnp.float32) * s
        ln_w = jnp.ones((C,), jnp.float32)
        ln_b = jnp.zeros((C,), jnp.float32)
        return dict(x=x, time_maa_x=time_maa_x, time_maa_w=time_maa_w, time_maa_k=time_maa_k, time_maa_v=time_maa_v, time_maa_r=time_maa_r, time_maa_g=time_maa_g, time_maa_w1=time_maa_w1, time_maa_w2=time_maa_w2, time_decay=time_decay, time_decay_w1=time_decay_w1, time_decay_w2=time_decay_w2, time_faaaa=time_faaaa, Wr=Wr, Wk=Wk, Wv=Wv, Wg=Wg, Wo=Wo, ln_w=ln_w, ln_b=ln_b)
    _L1_attn_all = _L1_attn_setup()
    _L1_attn_in = {k: v for k, v in _L1_attn_all.items() if k in ('time_maa_x', 'time_maa_w', 'time_maa_k', 'time_maa_v', 'time_maa_r', 'time_maa_g', 'time_maa_w1', 'time_maa_w2', 'time_decay', 'time_decay_w1', 'time_decay_w2', 'time_faaaa', 'Wr', 'Wk', 'Wv', 'Wg', 'Wo', 'ln_w', 'ln_b')}
    del _L1_attn_all

    def _L1_xattn_setup():
        import jax, jax.numpy as jnp
        import numpy as np
        N_HEAD = 16

        def _split_heads(t):
            B, S, D = t.shape
            return t.reshape(B, S, N_HEAD, D // N_HEAD).transpose(0, 2, 1, 3)
        key = jax.random.key(seed)
        ks = jax.random.split(key, 8)
        B, Sq, Sk, D = (4, 128, 256, 128)
        s = 0.02
        return {'x': jax.random.normal(ks[0], (B, Sq, D), jnp.float32), 'ctx': jax.random.normal(ks[1], (B, Sk, D), jnp.float32), 'attention_mask': jnp.zeros((B, 1, 1, Sk), jnp.float32), 'Wq': jax.random.normal(ks[2], (D, D), jnp.float32) * s, 'bq': jnp.zeros((D,), jnp.float32), 'Wkv': jax.random.normal(ks[3], (D, 2 * D), jnp.float32) * s, 'bkv': jnp.zeros((2 * D,), jnp.float32), 'Wp': jax.random.normal(ks[4], (D, D), jnp.float32) * s, 'bp': jnp.zeros((D,), jnp.float32)}
    _L1_xattn_all = _L1_xattn_setup()
    _L1_xattn_in = {k: v for k, v in _L1_xattn_all.items() if k in ('Wq', 'bq', 'Wkv', 'bkv', 'Wp', 'bp')}
    del _L1_xattn_all

    def _L1_ffn_setup():
        import jax, jax.numpy as jnp
        import numpy as np
        B, S, D, F, E = (8, 128, 128, 512, 8)
        EPS = 1e-05
        key = jax.random.key(seed)
        ks = jax.random.split(key, 4)
        s = 0.02
        return {'input_features': jax.random.normal(ks[0], (B, S, D), jnp.float32), 'centroids': jax.random.normal(ks[1], (E, D), jnp.float32) * 0.1, 'ln_g': jnp.ones((E, D), jnp.float32), 'ln_b': jnp.zeros((E, D), jnp.float32), 'w1': jax.random.normal(ks[2], (E, D, F), jnp.float32) * s, 'b1': jnp.zeros((E, F), jnp.float32), 'w2': jax.random.normal(ks[3], (E, F, D), jnp.float32) * s, 'b2': jnp.zeros((E, D), jnp.float32)}
    _L1_ffn_all = _L1_ffn_setup()
    _L1_ffn_in = {k: v for k, v in _L1_ffn_all.items() if k in ('centroids', 'ln_g', 'ln_b', 'w1', 'b1', 'w2', 'b2')}
    del _L1_ffn_all

    def _L2_attn_setup():
        import jax, jax.numpy as jnp
        import numpy as np
        from jax import lax
        D_MODEL = 128
        D_STATE = 16
        key = jax.random.key(seed)
        ks = jax.random.split(key, 7)
        B, L = (4, 256)
        x = jax.random.normal(ks[0], (B, L, D_MODEL), dtype=jnp.float32)
        s = 1.0 / np.sqrt(D_MODEL)
        W_dt = jax.random.uniform(ks[1], (D_MODEL, D_MODEL), jnp.float32, -s, s)
        b_dt = jax.random.uniform(ks[2], (D_MODEL,), jnp.float32, -s, s)
        W_B = jax.random.uniform(ks[3], (D_STATE, D_MODEL), jnp.float32, -s, s)
        W_C = jax.random.uniform(ks[4], (D_STATE, D_MODEL), jnp.float32, -s, s)
        A = jax.random.normal(ks[5], (D_MODEL, D_STATE), dtype=jnp.float32)
        A_log = jnp.log(jnp.abs(A) + 0.0001)
        D = jnp.ones((D_MODEL,), dtype=jnp.float32)
        return {'x': x, 'W_dt': W_dt, 'b_dt': b_dt, 'W_B': W_B, 'W_C': W_C, 'A_log': A_log, 'D': D}
    _L2_attn_all = _L2_attn_setup()
    _L2_attn_in = {k: v for k, v in _L2_attn_all.items() if k in ('W_dt', 'b_dt', 'W_B', 'W_C', 'A_log', 'D')}
    del _L2_attn_all

    def _L2_xattn_setup():
        import jax, jax.numpy as jnp
        import numpy as np
        B, C_LEN, Q_LEN, D = (8, 256, 64, 128)
        key = jax.random.key(seed)
        ks = jax.random.split(key, 10)
        scale = 1.0 / np.sqrt(D)
        return {'c': jax.random.normal(ks[0], (B, C_LEN, D), dtype=jnp.float32), 'q': jax.random.normal(ks[1], (B, Q_LEN, D), dtype=jnp.float32), 'w_cq': jax.random.normal(ks[2], (D,), dtype=jnp.float32) * scale, 'b_cq': jax.random.normal(ks[3], (), dtype=jnp.float32) * scale, 'w_c': jax.random.normal(ks[4], (D,), dtype=jnp.float32) * scale, 'b_c': jax.random.normal(ks[5], (), dtype=jnp.float32) * scale, 'w_q': jax.random.normal(ks[6], (D,), dtype=jnp.float32) * scale, 'b_q': jax.random.normal(ks[7], (), dtype=jnp.float32) * scale, 'W_l': jax.random.normal(ks[8], (D, 4 * D), dtype=jnp.float32) * (1.0 / np.sqrt(4 * D)), 'b_l': jax.random.normal(ks[9], (D,), dtype=jnp.float32) * (1.0 / np.sqrt(4 * D))}
    _L2_xattn_all = _L2_xattn_setup()
    _L2_xattn_in = {k: v for k, v in _L2_xattn_all.items() if k in ('w_cq', 'b_cq', 'w_c', 'b_c', 'w_q', 'b_q', 'W_l', 'b_l')}
    del _L2_xattn_all

    def _L2_ffn_setup():
        import jax, jax.numpy as jnp
        import numpy as np
        EPS = 1e-05
        NUM_HEADS = 16
        NUM_KV_HEADS = 4
        NUM_EXPERTS = 8
        TOP_K = 2

        def _layernorm(x, w, b):
            mu = jnp.mean(x, axis=-1, keepdims=True)
            var = jnp.mean((x - mu) ** 2, axis=-1, keepdims=True)
            return (x - mu) * jax.lax.rsqrt(var + EPS) * w + b
        key = jax.random.key(seed)
        ks = jax.random.split(key, 8)
        S, B, H = (128, 4, 128)
        F = 256
        hd = H // NUM_HEADS
        qkv_out = (NUM_HEADS + 2 * NUM_KV_HEADS) * hd
        w_scale = 0.02
        return {'hidden_states': jax.random.normal(ks[0], (S, B, H), jnp.float32), 'ln1_weight': jnp.ones((H,), jnp.float32), 'ln1_bias': jnp.zeros((H,), jnp.float32), 'ln2_weight': jnp.ones((H,), jnp.float32), 'ln2_bias': jnp.zeros((H,), jnp.float32), 'qkv_weight': jax.random.normal(ks[1], (qkv_out, H), jnp.float32) * w_scale, 'proj_weight': jax.random.normal(ks[2], (H, H), jnp.float32) * w_scale, 'router_weight': jax.random.normal(ks[3], (NUM_EXPERTS, H), jnp.float32) * w_scale, 'moe_w1': jax.random.normal(ks[4], (NUM_EXPERTS, H, F), jnp.float32) * w_scale, 'moe_w2': jax.random.normal(ks[5], (NUM_EXPERTS, F, H), jnp.float32) * w_scale}
    _L2_ffn_all = _L2_ffn_setup()
    _L2_ffn_in = {k: v for k, v in _L2_ffn_all.items() if k in ('ln1_weight', 'ln1_bias', 'ln2_weight', 'ln2_bias', 'qkv_weight', 'proj_weight', 'router_weight', 'moe_w1', 'moe_w2')}
    del _L2_ffn_all

    def _L3_attn_setup():
        import jax, jax.numpy as jnp
        import numpy as np
        EPS = 1e-06

        def _rmsnorm(x, scale):
            var = jnp.mean(jnp.square(x), axis=-1, keepdims=True)
            return x * jax.lax.rsqrt(var + EPS) * scale
        key = jax.random.key(seed)
        ks = jax.random.split(key, 6)
        B, S, D, H, Dh = (2, 256, 128, 16, 64)
        x = jax.random.normal(ks[0], (B, S, D), dtype=jnp.float32)
        norm_scale = jnp.ones((D,), dtype=jnp.float32)
        wq = jax.random.normal(ks[1], (D, H, Dh), dtype=jnp.float32) / np.sqrt(D)
        wk = jax.random.normal(ks[2], (D, H, Dh), dtype=jnp.float32) / np.sqrt(D)
        wv = jax.random.normal(ks[3], (D, H, Dh), dtype=jnp.float32) / np.sqrt(D)
        w_out = jax.random.normal(ks[4], (H, Dh, D), dtype=jnp.float32) / np.sqrt(H * Dh)
        b_out = jnp.zeros((D,), dtype=jnp.float32)
        return {'x': x, 'norm_scale': norm_scale, 'wq': wq, 'wk': wk, 'wv': wv, 'w_out': w_out, 'b_out': b_out}
    _L3_attn_all = _L3_attn_setup()
    _L3_attn_in = {k: v for k, v in _L3_attn_all.items() if k in ('norm_scale', 'wq', 'wk', 'wv', 'w_out', 'b_out')}
    del _L3_attn_all

    def _L3_xattn_setup():
        import jax, jax.numpy as jnp
        import numpy as np
        D1, D2, D3 = (128, 128, 128)
        key = jax.random.key(seed)
        k1, k2, kw, kb = jax.random.split(key, 4)
        x1 = jax.random.normal(k1, (8, 256, D1), dtype=jnp.float32)
        x2 = jax.random.normal(k2, (8, 256, D2), dtype=jnp.float32)
        bound = 1.0 / np.sqrt(D1 + D2)
        W = jax.random.uniform(kw, (D3, D1 + D2), minval=-bound, maxval=bound, dtype=jnp.float32)
        b = jax.random.uniform(kb, (D3,), minval=-bound, maxval=bound, dtype=jnp.float32)
        return {'x1': x1, 'x2': x2, 'W': W, 'b': b}
    _L3_xattn_all = _L3_xattn_setup()
    _L3_xattn_in = {k: v for k, v in _L3_xattn_all.items() if k in ('W', 'b')}
    del _L3_xattn_all

    def _L3_ffn_setup():
        import jax, jax.numpy as jnp
        import numpy as np
        B, S, D, O, H, E, K = (4, 128, 128, 128, 256, 16, 4)
        key = jax.random.key(seed)
        ks = jax.random.split(key, 8)
        x = jax.random.normal(ks[0], (B, S, D), dtype=jnp.float32)
        w_gate = jax.random.normal(ks[1], (D, E), dtype=jnp.float32) * 0.01
        w_noise = jnp.zeros((D, E), dtype=jnp.float32)
        W1 = jax.random.normal(ks[2], (E, D, H), dtype=jnp.float32) * (1.0 / np.sqrt(D))
        b1 = jnp.zeros((E, H), dtype=jnp.float32)
        W2 = jax.random.normal(ks[3], (E, H, O), dtype=jnp.float32) * (1.0 / np.sqrt(H))
        b2 = jnp.zeros((E, O), dtype=jnp.float32)
        return {'x': x, 'w_gate': w_gate, 'w_noise': w_noise, 'W1': W1, 'b1': b1, 'W2': W2, 'b2': b2}
    _L3_ffn_all = _L3_ffn_setup()
    _L3_ffn_in = {k: v for k, v in _L3_ffn_all.items() if k in ('w_gate', 'w_noise', 'W1', 'b1', 'W2', 'b2')}
    del _L3_ffn_all
    return {'x': x, 'ctx_1024': ctx_1024, 'mask_Bx1x1xS2_ff0': mask_Bx1x1xS2_ff0, 'L0_attn_key': _L0_attn_in['key'], 'L0_attn_value': _L0_attn_in['value'], 'L0_attn_in_proj_weight': _L0_attn_in['in_proj_weight'], 'L0_attn_out_proj_weight': _L0_attn_in['out_proj_weight'], 'L0_xattn_ln_m_w': _L0_xattn_in['ln_m_w'], 'L0_xattn_ln_m_b': _L0_xattn_in['ln_m_b'], 'L0_xattn_ln_l_w': _L0_xattn_in['ln_l_w'], 'L0_xattn_ln_l_b': _L0_xattn_in['ln_l_b'], 'L0_xattn_Wq': _L0_xattn_in['Wq'], 'L0_xattn_Wkv': _L0_xattn_in['Wkv'], 'L0_xattn_Wout': _L0_xattn_in['Wout'], 'L0_ffn_Wr': _L0_ffn_in['Wr'], 'L0_ffn_W1': _L0_ffn_in['W1'], 'L0_ffn_b1': _L0_ffn_in['b1'], 'L0_ffn_Wo': _L0_ffn_in['Wo'], 'L0_ffn_bo': _L0_ffn_in['bo'], 'L0_ffn_gamma': _L0_ffn_in['gamma'], 'L0_ffn_beta': _L0_ffn_in['beta'], 'L1_attn_time_maa_x': _L1_attn_in['time_maa_x'], 'L1_attn_time_maa_w': _L1_attn_in['time_maa_w'], 'L1_attn_time_maa_k': _L1_attn_in['time_maa_k'], 'L1_attn_time_maa_v': _L1_attn_in['time_maa_v'], 'L1_attn_time_maa_r': _L1_attn_in['time_maa_r'], 'L1_attn_time_maa_g': _L1_attn_in['time_maa_g'], 'L1_attn_time_maa_w1': _L1_attn_in['time_maa_w1'], 'L1_attn_time_maa_w2': _L1_attn_in['time_maa_w2'], 'L1_attn_time_decay': _L1_attn_in['time_decay'], 'L1_attn_time_decay_w1': _L1_attn_in['time_decay_w1'], 'L1_attn_time_decay_w2': _L1_attn_in['time_decay_w2'], 'L1_attn_time_faaaa': _L1_attn_in['time_faaaa'], 'L1_attn_Wr': _L1_attn_in['Wr'], 'L1_attn_Wk': _L1_attn_in['Wk'], 'L1_attn_Wv': _L1_attn_in['Wv'], 'L1_attn_Wg': _L1_attn_in['Wg'], 'L1_attn_Wo': _L1_attn_in['Wo'], 'L1_attn_ln_w': _L1_attn_in['ln_w'], 'L1_attn_ln_b': _L1_attn_in['ln_b'], 'L1_xattn_Wq': _L1_xattn_in['Wq'], 'L1_xattn_bq': _L1_xattn_in['bq'], 'L1_xattn_Wkv': _L1_xattn_in['Wkv'], 'L1_xattn_bkv': _L1_xattn_in['bkv'], 'L1_xattn_Wp': _L1_xattn_in['Wp'], 'L1_xattn_bp': _L1_xattn_in['bp'], 'L1_ffn_centroids': _L1_ffn_in['centroids'], 'L1_ffn_ln_g': _L1_ffn_in['ln_g'], 'L1_ffn_ln_b': _L1_ffn_in['ln_b'], 'L1_ffn_w1': _L1_ffn_in['w1'], 'L1_ffn_b1': _L1_ffn_in['b1'], 'L1_ffn_w2': _L1_ffn_in['w2'], 'L1_ffn_b2': _L1_ffn_in['b2'], 'L2_attn_W_dt': _L2_attn_in['W_dt'], 'L2_attn_b_dt': _L2_attn_in['b_dt'], 'L2_attn_W_B': _L2_attn_in['W_B'], 'L2_attn_W_C': _L2_attn_in['W_C'], 'L2_attn_A_log': _L2_attn_in['A_log'], 'L2_attn_D': _L2_attn_in['D'], 'L2_xattn_w_cq': _L2_xattn_in['w_cq'], 'L2_xattn_b_cq': _L2_xattn_in['b_cq'], 'L2_xattn_w_c': _L2_xattn_in['w_c'], 'L2_xattn_b_c': _L2_xattn_in['b_c'], 'L2_xattn_w_q': _L2_xattn_in['w_q'], 'L2_xattn_b_q': _L2_xattn_in['b_q'], 'L2_xattn_W_l': _L2_xattn_in['W_l'], 'L2_xattn_b_l': _L2_xattn_in['b_l'], 'L2_ffn_ln1_weight': _L2_ffn_in['ln1_weight'], 'L2_ffn_ln1_bias': _L2_ffn_in['ln1_bias'], 'L2_ffn_ln2_weight': _L2_ffn_in['ln2_weight'], 'L2_ffn_ln2_bias': _L2_ffn_in['ln2_bias'], 'L2_ffn_qkv_weight': _L2_ffn_in['qkv_weight'], 'L2_ffn_proj_weight': _L2_ffn_in['proj_weight'], 'L2_ffn_router_weight': _L2_ffn_in['router_weight'], 'L2_ffn_moe_w1': _L2_ffn_in['moe_w1'], 'L2_ffn_moe_w2': _L2_ffn_in['moe_w2'], 'L3_attn_norm_scale': _L3_attn_in['norm_scale'], 'L3_attn_wq': _L3_attn_in['wq'], 'L3_attn_wk': _L3_attn_in['wk'], 'L3_attn_wv': _L3_attn_in['wv'], 'L3_attn_w_out': _L3_attn_in['w_out'], 'L3_attn_b_out': _L3_attn_in['b_out'], 'L3_xattn_W': _L3_xattn_in['W'], 'L3_xattn_b': _L3_xattn_in['b'], 'L3_ffn_w_gate': _L3_ffn_in['w_gate'], 'L3_ffn_w_noise': _L3_ffn_in['w_noise'], 'L3_ffn_W1': _L3_ffn_in['W1'], 'L3_ffn_b1': _L3_ffn_in['b1'], 'L3_ffn_W2': _L3_ffn_in['W2'], 'L3_ffn_b2': _L3_ffn_in['b2']}

def reference(x, ctx_1024, mask_Bx1x1xS2_ff0, L0_attn_key, L0_attn_value, L0_attn_in_proj_weight, L0_attn_out_proj_weight, L0_xattn_ln_m_w, L0_xattn_ln_m_b, L0_xattn_ln_l_w, L0_xattn_ln_l_b, L0_xattn_Wq, L0_xattn_Wkv, L0_xattn_Wout, L0_ffn_Wr, L0_ffn_W1, L0_ffn_b1, L0_ffn_Wo, L0_ffn_bo, L0_ffn_gamma, L0_ffn_beta, L1_attn_time_maa_x, L1_attn_time_maa_w, L1_attn_time_maa_k, L1_attn_time_maa_v, L1_attn_time_maa_r, L1_attn_time_maa_g, L1_attn_time_maa_w1, L1_attn_time_maa_w2, L1_attn_time_decay, L1_attn_time_decay_w1, L1_attn_time_decay_w2, L1_attn_time_faaaa, L1_attn_Wr, L1_attn_Wk, L1_attn_Wv, L1_attn_Wg, L1_attn_Wo, L1_attn_ln_w, L1_attn_ln_b, L1_xattn_Wq, L1_xattn_bq, L1_xattn_Wkv, L1_xattn_bkv, L1_xattn_Wp, L1_xattn_bp, L1_ffn_centroids, L1_ffn_ln_g, L1_ffn_ln_b, L1_ffn_w1, L1_ffn_b1, L1_ffn_w2, L1_ffn_b2, L2_attn_W_dt, L2_attn_b_dt, L2_attn_W_B, L2_attn_W_C, L2_attn_A_log, L2_attn_D, L2_xattn_w_cq, L2_xattn_b_cq, L2_xattn_w_c, L2_xattn_b_c, L2_xattn_w_q, L2_xattn_b_q, L2_xattn_W_l, L2_xattn_b_l, L2_ffn_ln1_weight, L2_ffn_ln1_bias, L2_ffn_ln2_weight, L2_ffn_ln2_bias, L2_ffn_qkv_weight, L2_ffn_proj_weight, L2_ffn_router_weight, L2_ffn_moe_w1, L2_ffn_moe_w2, L3_attn_norm_scale, L3_attn_wq, L3_attn_wk, L3_attn_wv, L3_attn_w_out, L3_attn_b_out, L3_xattn_W, L3_xattn_b, L3_ffn_w_gate, L3_ffn_w_noise, L3_ffn_W1, L3_ffn_b1, L3_ffn_W2, L3_ffn_b2):
    import jax
    import jax.numpy as jnp

    def _L0_attn_ref(query, key, value, in_proj_weight, out_proj_weight):
        import jax, jax.numpy as jnp
        import numpy as np
        EMBED_DIM = 128
        NUM_HEADS = 16
        HEAD_DIM = EMBED_DIM // NUM_HEADS
        BATCH = 2
        SEQ = 256
        NEG_INF = float('-inf')
        B, T, E = query.shape
        H, D = (NUM_HEADS, HEAD_DIM)
        projected = jnp.einsum('bte,fe->btf', query, in_proj_weight)
        packed = projected.reshape(B, T, 3, H, D).transpose(0, 3, 2, 1, 4)
        q, k, v = (packed[:, :, 0], packed[:, :, 1], packed[:, :, 2])
        q = q / jnp.sqrt(jnp.asarray(D, dtype=q.dtype))
        attention = jnp.einsum('bhtd,bhkd->bhtk', q, k)
        qpos = jnp.arange(T)[:, None]
        kpos = jnp.arange(T)[None, :]
        mask = jnp.where(qpos - kpos >= 0, 0.0, NEG_INF).astype(attention.dtype)
        attention = attention + mask[None, None]
        activation = jax.nn.softmax(attention, axis=-1)
        x = jnp.einsum('bhtk,bhkd->bhtd', activation, v)
        x = x.transpose(0, 2, 1, 3).reshape(B, T, E)
        out = jnp.einsum('bte,fe->btf', x, out_proj_weight)
        return out

    def _L0_xattn_ref(x, latents, ln_m_w, ln_m_b, ln_l_w, ln_l_b, Wq, Wkv, Wout):
        import jax, jax.numpy as jnp
        import numpy as np
        DIM = 128
        HEADS = 8
        DIM_HEAD = 64
        INNER = HEADS * DIM_HEAD
        EPS = 1e-05

        def layernorm(x, w, b):
            mu = jnp.mean(x, axis=-1, keepdims=True)
            var = jnp.var(x, axis=-1, keepdims=True)
            return (x - mu) * jax.lax.rsqrt(var + EPS) * w + b
        scale = DIM_HEAD ** (-0.5)
        xn = layernorm(x, ln_m_w, ln_m_b)
        ln = layernorm(latents, ln_l_w, ln_l_b)
        b = xn.shape[0]
        q = ln @ Wq
        kv_input = jnp.concatenate([xn, ln], axis=-2)
        kv = kv_input @ Wkv
        k, v = jnp.split(kv, 2, axis=-1)

        def to_heads(t):
            return t.reshape(b, t.shape[1], HEADS, DIM_HEAD).transpose(0, 2, 1, 3)
        q, k, v = (to_heads(q) * scale, to_heads(k), to_heads(v))
        sim = jnp.einsum('bhid,bhjd->bhij', q, k)
        attn = jax.nn.softmax(sim, axis=-1)
        out = jnp.einsum('bhij,bhjd->bhid', attn, v)
        out = out.transpose(0, 2, 1, 3).reshape(b, out.shape[2], INNER)
        return out @ Wout

    def _L0_ffn_ref(hidden_states, Wr, W1, b1, Wo, bo, gamma, beta):
        import jax, jax.numpy as jnp
        import numpy as np
        LN_EPS = 1e-12
        B, S, H = hidden_states.shape
        E = Wr.shape[0]
        x = hidden_states.reshape(-1, H)
        router_logits = x @ Wr.T
        expert_idx = jnp.argmax(jax.nn.softmax(router_logits, axis=-1), axis=-1)
        inter = jnp.zeros((x.shape[0], W1.shape[2]), dtype=x.dtype)
        for e in range(E):
            mask = (expert_idx == e)[:, None].astype(x.dtype)
            inter = inter + mask * jax.nn.gelu(x @ W1[e] + b1[e], approximate=False)
        y = inter @ Wo + bo + x
        mu = jnp.mean(y, axis=-1, keepdims=True)
        var = jnp.mean(jnp.square(y - mu), axis=-1, keepdims=True)
        out = (y - mu) * jax.lax.rsqrt(var + LN_EPS) * gamma + beta
        return out.reshape(B, S, H)

    def _L1_attn_ref(x, time_maa_x, time_maa_w, time_maa_k, time_maa_v, time_maa_r, time_maa_g, time_maa_w1, time_maa_w2, time_decay, time_decay_w1, time_decay_w2, time_faaaa, Wr, Wk, Wv, Wg, Wo, ln_w, ln_b):
        import jax, jax.numpy as jnp
        import numpy as np
        B, T, C = (4, 128, 128)
        HEAD_SIZE = 64
        H = C // HEAD_SIZE
        N_LAYER, LAYER_ID = (24, 12)
        D_MIX_LORA, D_DECAY_LORA = (32, 64)
        HEAD_SIZE_DIVISOR = 8
        LN_EPS = 1e-05 * HEAD_SIZE_DIVISOR ** 2

        def _wkv6(r, k, v, w, u):

            def step(S, inp):
                r_t, k_t, v_t, w_t = inp
                y = jnp.einsum('bhj,bhji->bhi', r_t, S) + jnp.sum(r_t * u * k_t, axis=-1, keepdims=True) * v_t
                decay = jnp.exp(-jnp.exp(w_t))
                S = decay[..., None] * S + k_t[..., None] * v_t[..., None, :]
                return (S, y)
            to_t = lambda a: jnp.transpose(a, (1, 0, 2, 3))
            S0 = jnp.zeros(r.shape[:1] + (r.shape[2], r.shape[3], r.shape[3]), r.dtype)
            _, ys = jax.lax.scan(step, S0, (to_t(r), to_t(k), to_t(v), to_t(w)))
            return jnp.transpose(ys, (1, 0, 2, 3))
        b, t, c = x.shape
        h, n = (H, HEAD_SIZE)
        xx = jnp.concatenate([jnp.zeros_like(x[:, :1]), x[:, :-1]], axis=1) - x
        xxx = x + xx * time_maa_x
        mix = jnp.tanh(xxx @ time_maa_w1).reshape(b, t, 5, D_MIX_LORA)
        m = jnp.einsum('btsd,sdc->sbtc', mix, time_maa_w2)
        xw = x + xx * (time_maa_w + m[0])
        xk = x + xx * (time_maa_k + m[1])
        xv = x + xx * (time_maa_v + m[2])
        xr = x + xx * (time_maa_r + m[3])
        xg = x + xx * (time_maa_g + m[4])
        r = xr @ Wr
        k = xk @ Wk
        v = xv @ Wv
        g = jax.nn.silu(xg @ Wg)
        w = time_decay + jnp.tanh(xw @ time_decay_w1) @ time_decay_w2
        y = _wkv6(r.reshape(b, t, h, n), k.reshape(b, t, h, n), v.reshape(b, t, h, n), w.reshape(b, t, h, n), time_faaaa)
        mu = y.mean(-1, keepdims=True)
        var = y.var(-1, keepdims=True)
        yn = ((y - mu) / jnp.sqrt(var + LN_EPS)).reshape(b, t, c) * ln_w + ln_b
        return yn * g @ Wo

    def _L1_xattn_ref(x, ctx, attention_mask, Wq, bq, Wkv, bkv, Wp, bp):
        import jax, jax.numpy as jnp
        import numpy as np
        N_HEAD = 16

        def _split_heads(t):
            B, S, D = t.shape
            return t.reshape(B, S, N_HEAD, D // N_HEAD).transpose(0, 2, 1, 3)
        B, Sq, D = x.shape
        dh = D // N_HEAD
        q = _split_heads(x @ Wq + bq)
        kv = ctx @ Wkv + bkv
        k = _split_heads(kv[..., :D])
        v = _split_heads(kv[..., D:])
        w = jnp.einsum('bhqd,bhkd->bhqk', q, k) / jnp.sqrt(jnp.float32(dh))
        w = w + attention_mask
        w = jax.nn.softmax(w, axis=-1)
        a = jnp.einsum('bhqk,bhkd->bhqd', w, v)
        a = a.transpose(0, 2, 1, 3).reshape(B, Sq, D)
        return a @ Wp + bp

    def _L1_ffn_ref(input_features, centroids, ln_g, ln_b, w1, b1, w2, b2):
        import jax, jax.numpy as jnp
        import numpy as np
        B, S, D, F, E = (8, 128, 128, 512, 8)
        EPS = 1e-05
        x = input_features.reshape(-1, D)
        aff = jax.lax.stop_gradient(x @ centroids.T)
        eid = jnp.argmax(aff, axis=-1)
        alpha = jax.nn.sigmoid(jnp.sum(x * centroids[eid], axis=-1, keepdims=True))
        mu = jnp.mean(x, axis=-1, keepdims=True)
        var = jnp.mean((x - mu) ** 2, axis=-1, keepdims=True)
        xn = (x - mu) * jax.lax.rsqrt(var + EPS)
        xln = xn * ln_g[eid] + ln_b[eid]
        onehot = jax.nn.one_hot(eid, E, dtype=x.dtype)
        ffn = jnp.zeros_like(x)
        for e in range(E):
            h = jax.nn.relu(xln @ w1[e] + b1[e])
            ffn = ffn + onehot[:, e:e + 1] * (h @ w2[e] + b2[e])
        out = x + alpha * ffn
        return out.reshape(input_features.shape)

    def _L2_attn_ref(x, W_dt, b_dt, W_B, W_C, A_log, D):
        import jax, jax.numpy as jnp
        import numpy as np
        from jax import lax
        D_MODEL = 128
        D_STATE = 16
        B, L, Dm = x.shape
        N = A_log.shape[1]
        dt = jax.nn.softplus(jnp.einsum('bld,ed->ble', x, W_dt) + b_dt)
        Bp = jnp.einsum('bld,nd->bln', x, W_B)
        Cp = jnp.einsum('bld,nd->bln', x, W_C)
        A = -jnp.exp(A_log)
        dA = jnp.exp(dt[..., None] * A)
        dBx = dt[..., None] * Bp[:, :, None, :] * x[..., None]

        def step(h, inp):
            dA_t, dBx_t, C_t, x_t = inp
            h = dA_t * h + dBx_t
            y = jnp.einsum('bdn,bn->bd', h, C_t) + D * x_t
            return (h, y)
        h0 = jnp.zeros((B, Dm, N), dtype=x.dtype)
        xs = (jnp.swapaxes(dA, 0, 1), jnp.swapaxes(dBx, 0, 1), jnp.swapaxes(Cp, 0, 1), jnp.swapaxes(x, 0, 1))
        _, ys = lax.scan(step, h0, xs)
        return jnp.swapaxes(ys, 0, 1)

    def _L2_xattn_ref(c, q, w_cq, b_cq, w_c, b_c, w_q, b_q, W_l, b_l):
        import jax, jax.numpy as jnp
        import numpy as np
        B, C_LEN, Q_LEN, D = (8, 256, 64, 128)
        cq = jnp.einsum('bcd,bqd,d->bcq', c, q, w_cq) + b_cq
        s = (c @ w_c + b_c)[:, :, None] + (q @ w_q + b_q)[:, None, :] + cq
        a = jax.nn.softmax(s, axis=2)
        c2q_att = jnp.einsum('bcq,bqd->bcd', a, q)
        b_att = jax.nn.softmax(jnp.max(s, axis=2), axis=1)
        q2c_att = jnp.einsum('bc,bcd->bd', b_att, c)[:, None, :]
        x = jnp.concatenate([c, c2q_att, c * c2q_att, c * q2c_att], axis=-1)
        z = x @ W_l.T + b_l
        return z

    def _L2_ffn_ref(hidden_states, ln1_weight, ln1_bias, ln2_weight, ln2_bias, qkv_weight, proj_weight, router_weight, moe_w1, moe_w2):
        import jax, jax.numpy as jnp
        import numpy as np
        EPS = 1e-05
        NUM_HEADS = 16
        NUM_KV_HEADS = 4
        NUM_EXPERTS = 8
        TOP_K = 2

        def _layernorm(x, w, b):
            mu = jnp.mean(x, axis=-1, keepdims=True)
            var = jnp.mean((x - mu) ** 2, axis=-1, keepdims=True)
            return (x - mu) * jax.lax.rsqrt(var + EPS) * w + b
        S, B, H = hidden_states.shape
        hd = H // NUM_HEADS
        rep = NUM_HEADS // NUM_KV_HEADS
        scale = 1.0 / hd ** 0.5
        ln1_out = _layernorm(hidden_states, ln1_weight, ln1_bias)
        qkv = jnp.einsum('sbh,oh->sbo', ln1_out, qkv_weight)
        q = qkv[..., :NUM_HEADS * hd].reshape(S, B, NUM_HEADS, hd)
        k = qkv[..., NUM_HEADS * hd:(NUM_HEADS + NUM_KV_HEADS) * hd].reshape(S, B, NUM_KV_HEADS, hd)
        v = qkv[..., (NUM_HEADS + NUM_KV_HEADS) * hd:].reshape(S, B, NUM_KV_HEADS, hd)
        k = jnp.repeat(k, rep, axis=2)
        v = jnp.repeat(v, rep, axis=2)
        scores = jnp.einsum('sbhd,tbhd->bhst', q, k) * scale
        causal = jnp.tril(jnp.ones((S, S), bool))
        scores = jnp.where(causal, scores, jnp.finfo(scores.dtype).min)
        probs = jax.nn.softmax(scores, axis=-1)
        attn = jnp.einsum('bhst,tbhd->sbhd', probs, v).reshape(S, B, H)
        proj_out = jnp.einsum('sbh,oh->sbo', attn, proj_weight)
        hidden_after_attn = hidden_states + proj_out
        ln2_out = _layernorm(hidden_after_attn, ln2_weight, ln2_bias)
        x = ln2_out.reshape(-1, H)
        logits = jnp.einsum('th,eh->te', x, router_weight)
        gate = jax.nn.softmax(logits, axis=-1)
        top_probs, top_idx = jax.lax.top_k(gate, TOP_K)
        h_mid = jax.nn.gelu(jnp.einsum('th,ehf->etf', x, moe_w1))
        expert_out = jnp.einsum('etf,efh->eth', h_mid, moe_w2)
        e_ids = jnp.arange(NUM_EXPERTS)[:, None, None]
        weights = jnp.sum(jnp.where(top_idx[None] == e_ids, top_probs[None], 0.0), axis=-1)
        moe_out = jnp.einsum('eth,et->th', expert_out, weights).reshape(S, B, H)
        return hidden_after_attn + moe_out

    def _L3_attn_ref(x, norm_scale, wq, wk, wv, w_out, b_out):
        import jax, jax.numpy as jnp
        import numpy as np
        EPS = 1e-06

        def _rmsnorm(x, scale):
            var = jnp.mean(jnp.square(x), axis=-1, keepdims=True)
            return x * jax.lax.rsqrt(var + EPS) * scale
        dtype = x.dtype
        softmax_dtype = jnp.float32
        h = _rmsnorm(x, norm_scale)
        q = jnp.einsum('bsd,dhe->bshe', h, wq)
        k = jnp.einsum('bsd,dhe->bshe', h, wk)
        v = jnp.einsum('bsd,dhe->bshe', h, wv)
        head_dim = q.shape[-1]
        scale = head_dim ** (-0.5)
        q = (q * scale).astype(softmax_dtype)
        kf = k.astype(softmax_dtype)
        weights = jnp.einsum('bqhd,bkhd->bhqk', q, kf)
        weights = jax.nn.softmax(weights, axis=-1).astype(dtype)
        new_vals = jnp.einsum('bhqk,bkhd->bqhd', weights, v).astype(dtype)
        out = jnp.einsum('bqhe,hed->bqd', new_vals, w_out) + b_out
        return out

    def _L3_xattn_ref(x1, x2, W, b):
        import jax, jax.numpy as jnp
        import numpy as np
        D1, D2, D3 = (128, 128, 128)
        d1 = x1.shape[-1]
        W1 = W[:, :d1]
        W2 = W[:, d1:]
        part1 = jnp.einsum('bld,ed->ble', x1, W1)
        part2 = jnp.einsum('bld,ed->be', x2, W2) / x2.shape[1]
        return part1 + part2[:, None, :] + b

    def _L3_ffn_ref(x, w_gate, w_noise, W1, b1, W2, b2):
        import jax, jax.numpy as jnp
        import numpy as np
        B, S, D, O, H, E, K = (4, 128, 128, 128, 256, 16, 4)
        logits = jnp.zeros((x.shape[0], x.shape[1], E), dtype=x.dtype).at[..., 1].set(100.0)
        top_vals, top_idx = jax.lax.top_k(logits, K)
        gates_k = jax.nn.softmax(top_vals, axis=-1)
        gates = jnp.einsum('bske,bsk->bse', jax.nn.one_hot(top_idx, E, dtype=x.dtype), gates_k)
        h = jax.nn.relu(jnp.einsum('bsd,edh->ebsh', x, W1) + b1[:, None, None, :])
        y = jnp.einsum('ebsh,eho->ebso', h, W2) + b2[:, None, None, :]
        out = jnp.einsum('ebso,bse->bso', y, gates)
        return out
    x = x + _L0_attn_ref(_layernorm(x, axis=-1), L0_attn_key, L0_attn_value, L0_attn_in_proj_weight, L0_attn_out_proj_weight)
    x = x + _L0_xattn_ref(ctx_1024, _layernorm(x, axis=-1), L0_xattn_ln_m_w, L0_xattn_ln_m_b, L0_xattn_ln_l_w, L0_xattn_ln_l_b, L0_xattn_Wq, L0_xattn_Wkv, L0_xattn_Wout)
    x = x + _L0_ffn_ref(_layernorm(x, axis=-1), L0_ffn_Wr, L0_ffn_W1, L0_ffn_b1, L0_ffn_Wo, L0_ffn_bo, L0_ffn_gamma, L0_ffn_beta)
    x = x + _L1_attn_ref(_layernorm(x, axis=-1), L1_attn_time_maa_x, L1_attn_time_maa_w, L1_attn_time_maa_k, L1_attn_time_maa_v, L1_attn_time_maa_r, L1_attn_time_maa_g, L1_attn_time_maa_w1, L1_attn_time_maa_w2, L1_attn_time_decay, L1_attn_time_decay_w1, L1_attn_time_decay_w2, L1_attn_time_faaaa, L1_attn_Wr, L1_attn_Wk, L1_attn_Wv, L1_attn_Wg, L1_attn_Wo, L1_attn_ln_w, L1_attn_ln_b)
    x = x + _L1_xattn_ref(_layernorm(x, axis=-1), ctx_1024, mask_Bx1x1xS2_ff0, L1_xattn_Wq, L1_xattn_bq, L1_xattn_Wkv, L1_xattn_bkv, L1_xattn_Wp, L1_xattn_bp)
    x = x + _L1_ffn_ref(_layernorm(x, axis=-1), L1_ffn_centroids, L1_ffn_ln_g, L1_ffn_ln_b, L1_ffn_w1, L1_ffn_b1, L1_ffn_w2, L1_ffn_b2)
    x = x + _L2_attn_ref(_layernorm(x, axis=-1), L2_attn_W_dt, L2_attn_b_dt, L2_attn_W_B, L2_attn_W_C, L2_attn_A_log, L2_attn_D)
    x = x + _L2_xattn_ref(_layernorm(x, axis=-1), ctx_1024, L2_xattn_w_cq, L2_xattn_b_cq, L2_xattn_w_c, L2_xattn_b_c, L2_xattn_w_q, L2_xattn_b_q, L2_xattn_W_l, L2_xattn_b_l)
    x = x + _L2_ffn_ref(_layernorm(x, axis=-1), L2_ffn_ln1_weight, L2_ffn_ln1_bias, L2_ffn_ln2_weight, L2_ffn_ln2_bias, L2_ffn_qkv_weight, L2_ffn_proj_weight, L2_ffn_router_weight, L2_ffn_moe_w1, L2_ffn_moe_w2)
    x = x + _L3_attn_ref(_layernorm(x, axis=-1), L3_attn_norm_scale, L3_attn_wq, L3_attn_wk, L3_attn_wv, L3_attn_w_out, L3_attn_b_out)
    x = x + _L3_xattn_ref(_layernorm(x, axis=-1), ctx_1024, L3_xattn_W, L3_xattn_b)
    x = x + _L3_ffn_ref(_layernorm(x, axis=-1), L3_ffn_w_gate, L3_ffn_w_noise, L3_ffn_W1, L3_ffn_b1, L3_ffn_W2, L3_ffn_b2)
    return x

_drawn_inputs = setup_inputs


def setup_inputs(seed=0):
    import zlib

    import numpy as np

    out = dict(_drawn_inputs(seed))
    spreads = {'L0_xattn_ln_m_w': (1.0, 0.2),
     'L0_xattn_ln_m_b': (0.0, 0.1),
     'L0_xattn_ln_l_w': (1.0, 0.2),
     'L0_xattn_ln_l_b': (0.0, 0.1),
     'L0_ffn_gamma': (1.0, 0.2),
     'L0_ffn_beta': (0.0, 0.1),
     'L1_attn_ln_w': (1.0, 0.2),
     'L1_attn_ln_b': (0.0, 0.315),
     'L1_xattn_bq': (0.0, 0.8),
     'L1_xattn_bkv': (0.0, 0.501),
     'L1_xattn_bp': (0.0, 0.1),
     'L1_ffn_ln_g': (1.0, 0.6),
     'L1_ffn_ln_b': (0.0, 0.8),
     'L1_ffn_b1': (0.0, 0.8),
     'L1_ffn_b2': (0.0, 0.1),
     'L2_attn_D': (1.0, 0.2),
     'L2_ffn_ln1_weight': (1.0, 0.6),
     'L2_ffn_ln1_bias': (0.0, 0.8),
     'L2_ffn_ln2_weight': (1.0, 0.6),
     'L2_ffn_ln2_bias': (0.0, 0.8),
     'L3_attn_norm_scale': (1.0, 0.6),
     'L3_attn_b_out': (0.0, 0.495),
     'L3_ffn_w_noise': (0.0, 0.1),
     'L3_ffn_b1': (0.0, 0.682),
     'L3_ffn_b2': (0.0, 0.442)}
    factors = {'L0_ffn_b1': 4.834,
     'L1_attn_time_maa_x': 8.0,
     'L1_attn_time_maa_w': 8.0,
     'L1_attn_time_maa_w1': 8.0,
     'L1_attn_time_maa_w2': 8.0,
     'L1_attn_time_decay_w1': 8.0,
     'L1_attn_time_decay_w2': 8.0,
     'L1_xattn_Wq': 8.0,
     'L1_xattn_Wkv': 3.368,
     'L1_ffn_w1': 3.102,
     'L2_attn_b_dt': 4.593,
     'L2_xattn_w_c': 2.677,
     'L2_xattn_b_l': 5.454,
     'L2_ffn_qkv_weight': 8.0,
     'L2_ffn_proj_weight': 8.0,
     'L2_ffn_router_weight': 8.0,
     'L2_ffn_moe_w1': 8.0,
     'L2_ffn_moe_w2': 8.0,
     'L3_xattn_b': 8.0}
    for name, (base, spread) in spreads.items():
        noise = np.random.default_rng([zlib.crc32(name.encode()), seed]).standard_normal(out[name].shape)
        drawn = base * np.exp(spread * noise) if base else spread * noise
        out[name] = jnp.asarray(drawn.astype(out[name].dtype))
    for name, factor in factors.items():
        out[name] = (out[name] * factor).astype(out[name].dtype)
    return out
```

```python
from contextlib import ExitStack, contextmanager

import numpy as np

import concourse.bass as bass
from concourse import mybir

F32 = mybir.dt.float32
ALU = mybir.AluOpType
ACT = mybir.ActivationFunctionType
AX = mybir.AxisListType

BATCH, SEQ, D = 32, 56, 128
PAIRS = BATCH // 2
PT = 2 * SEQ
TOK = BATCH * SEQ
GROUP = 4
GT = GROUP * PT
CTX, TILES = 1500, 12
TP = CTX // TILES
BANKC = 4 * TP
NEG = -1.0e30
EXPERTS = 8


@contextmanager
def stage(nc, name, sems):
    with ExitStack() as es:
        handles = [nc.alloc_semaphore(f"{name}_{s}") for s in sems.split()]
        s = dict(zip(sems.split(), handles))

        def sb(label, shape):
            return es.enter_context(nc.sbuf_tensor(f"{name}_{label}", shape, F32))

        def ps(label, shape):
            return es.enter_context(nc.psum_tensor(f"{name}_{label}", shape, F32))

        yield s, sb, ps
        nc.clear_and_free_semaphores(handles)
        nc.all_engine_barrier()


def bc(ap, shape):
    return ap.to_broadcast(shape)


def wait(eng, s, n, *names):
    for name in names:
        eng.wait_ge(s[name], n)


def apart(eng):
    eng.nop(nofuse=True)



def normalise(nc, g, name, rounds, gain=None, shift=None):
    x, h_n, h_t, sq, ident, half = g["x"], g["h_n"], g["h_t"], g["sq"], g["ident"], g["half"]
    full = [PT, PAIRS, D]
    with stage(nc, name, "loaded summed mean centred squared sumsq var rstd normed turned copied") as (s, sb, ps):
        sums, mean, ssq, var, rstd = (sb(f"s{k}", [PT, PAIRS]) for k in range(5))
        aff = sb("affine", [D, 2])
        turn = ps("turn", [D, 4, 512])
        with nc.Block() as block:
            @block.sync
            def _(sp):
                if gain is not None:
                    sp.dma_start(aff[:, 0:1], gain).then_inc(s["loaded"], 16)
                if shift is not None:
                    sp.dma_start(aff[:, 1:2], shift).then_inc(s["loaded"], 16)

            @block.vector
            def _(v):
                for k, (kind, eps) in enumerate(rounds):
                    src = x if k == 0 else h_n
                    n = k + 1
                    if k:
                        v.wait_ge(s["normed"], k)
                    if kind == "layer":
                        v.tensor_reduce(sums[:], src[:], AX.X, ALU.add).then_inc(s["summed"], 1)
                        v.wait_ge(s["summed"], n)
                        v.tensor_scalar(mean[:], sums[:], 1.0 / D, None, ALU.mult).then_inc(s["mean"], 1)
                        v.wait_ge(s["mean"], n)
                        v.tensor_tensor(h_n[:], src[:], bc(mean[:, :, None], full), ALU.subtract).then_inc(s["centred"], 1)
                        src = h_n
                    v.wait_ge(s["squared"], n)
                    v.tensor_reduce(ssq[:], sq[:], AX.X, ALU.add).then_inc(s["sumsq"], 1)
                    v.wait_ge(s["sumsq"], n)
                    v.tensor_scalar(var[:], ssq[:], 1.0 / D, eps, ALU.mult, ALU.add).then_inc(s["var"], 1)
                    v.wait_ge(s["rstd"], n)
                    v.tensor_tensor(h_n[:], src[:], bc(rstd[:, :, None], full), ALU.mult).then_inc(s["normed"], 1)

            @block.gpsimd
            def _(pool):
                for k in range(len(rounds)):
                    pool.wait_ge(s["var"], k + 1)
                    pool.tensor_tensor(rstd[:], var[:], half[0:PT, 0:PAIRS], ALU.pow).then_inc(s["rstd"], 1)

            @block.scalar
            def _(act):
                centred = 0
                for k, (kind, eps) in enumerate(rounds):
                    if kind == "layer":
                        centred += 1
                        act.wait_ge(s["centred"], centred)
                        src = h_n
                    else:
                        if k:
                            act.wait_ge(s["normed"], k)
                        src = x if k == 0 else h_n
                    act.activation(sq[:], src[:], ACT.Square).then_inc(s["squared"], 1)
                loads = (gain is not None) + (shift is not None)
                if loads:
                    act.wait_ge(s["loaded"], 16 * loads)
                for b in range(4):
                    act.wait_ge(s["turned"], b + 1)
                    act.activation(h_t[:, b * GT:(b + 1) * GT], turn[:, b, 0:GT], ACT.Identity,
                                   scale=aff[:, 0:1] if gain is not None else 1.0,
                                   bias=aff[:, 1:2] if shift is not None else 0.0).then_inc(s["copied"], 1)

            @block.tensor
            def _(pe):
                pe.wait_ge(s["normed"], len(rounds))
                for t in range(PAIRS):
                    mm = pe.transpose(turn[:, t // 4, (t % 4) * PT:(t % 4 + 1) * PT], h_n[:, t, :], ident[0:PT, 0:PT])
                    if t % 4 == 3:
                        mm.then_inc(s["turned"], 1)



HEADS = 16


class PairTokens:
    fixed = staticmethod(lambda buf: buf[:])
    part = staticmethod(lambda buf, i: buf[:, bass.ts(i, PT)])
    heads = staticmethod(lambda buf: buf[:])
    all_heads = staticmethod(lambda buf, i: bc(buf[:, bass.ts(i, PT)][:, None, :], [D, HEADS, PT]))
    mask = staticmethod(lambda hm: bc(hm[:, :, None], [D, HEADS, PT]))


class SequenceTokens:
    fixed = staticmethod(lambda buf: buf.rearrange("d (b t) -> d b t", t=BATCH))
    part = staticmethod(lambda buf, i: buf.rearrange("d (t b) -> d b t", t=BATCH)[:, bass.ts(i, 4), :])
    heads = staticmethod(lambda buf: buf.rearrange("d h (b t) -> d h b t", t=BATCH))
    all_heads = staticmethod(lambda buf, i: bc(SequenceTokens.part(buf, i)[:, None, :, :], [D, HEADS, 4, BATCH]))
    mask = staticmethod(lambda hm: bc(hm[:, :, None, None], [D, HEADS, 4, BATCH]))


def softmax_vector(v, s, n, R, scores, mask, pr, mx, ls, rl):
    full, four = [R, HEADS, R], [R, 4, 4, R]
    v.wait_ge(s["scores"], n)
    v.tensor_tensor(pr.rearrange("q (a b) k -> q a b k", a=4), scores[0:R, :, 0:4 * R].rearrange("q a (b k) -> q a b k", b=4),
                    bc(mask[:, None, None, :], four), ALU.add).then_inc(s["masked"], 1)
    v.wait_ge(s["masked"], n)
    v.tensor_reduce(mx, pr, AX.X, ALU.max).then_inc(s["rowmax"], 1)
    v.wait_ge(s["rowmax"], n)
    v.tensor_tensor(pr, pr, bc(mx[:, :, None], full), ALU.subtract).then_inc(s["shifted"], 1)
    v.wait_ge(s["probs"], n)
    v.tensor_reduce(ls, pr, AX.X, ALU.add).then_inc(s["rowsum"], 1)
    v.wait_ge(s["rowsum"], n)
    v.reciprocal(rl, ls).then_inc(s["inverse"], 1)


def turn_probs(pe, s, n, R, scores, pr, ident):
    pe.wait_ge(s["probs"], n)
    for h in range(HEADS):
        mm = pe.transpose(scores[0:R, h // 4, (h % 4) * R:(h % 4 + 1) * R], pr[:, h, :], ident[0:R, 0:R])
    mm.then_inc(s["turned"], 1)


def narrow_attention(nc, g, name, R, count, src, mask, scale, wqkv, wo_add, order=None):
    ident, h_t, x = g["ident"], g["h_t"], g["x"]
    last = "o_copied" if order else "done"
    names = ("loaded projected evacuated staged_q staged_k staged_h v_ready v_copied scores masked rowmax shifted "
             "probs rowsum inverse turned pt_act pt_vec pv o_ready o_turned o_copied out_ready done out2 added")
    with stage(nc, name, names) as (s, sb, ps):
        w = sb("w", [D, 3 * D]); wo = sb("wo", [D, D]); mk = sb("mask", [R, R]); hm = sb("hm", [D, HEADS])
        q_t = sb("q_t", [D, TOK]); k_t = sb("k_t", [D, TOK])
        qs = sb("qs", [D, R]); kb = sb("kb", [D, HEADS, R]); hs = sb("hs", [D, R]); vs = sb("vs", [R, D])
        pr = sb("pr", [R, HEADS, R]); pt = sb("pt", [R, HEADS, R]); on = sb("on", [R, D]); ot = sb("ot", [D, R])
        mx = sb("mx", [R, HEADS]); ls = sb("ls", [R, HEADS]); rl = sb("rl", [R, HEADS])
        o_t = sb("o_t", [D, TOK]) if order else None
        scores = ps("scores", [D, 4, 512]); pv = ps("pv", [D, 512]); mi = ps("mi", [D, 3, 512])
        with nc.Block() as block:
            @block.sync
            def _(sp):
                for dst, drm in ((w[:], wqkv), (wo[:], wo_add), (mk[:], mask), (hm[:], g["headmask"])):
                    sp.dma_start(dst, drm).then_inc(s["loaded"], 16)

            @block.tensor
            def _(pe):
                pe.wait_ge(s["loaded"], 64)
                for m in range(2):
                    for b in range(4):
                        if m:
                            pe.wait_ge(s["evacuated"], b + 1)
                        pe.matmul(scores[:, b, 0:GT], w[:, m * D:(m + 1) * D], h_t[:, b * GT:(b + 1) * GT],
                                  start=True, stop=True).then_inc(s["projected"], 1)
                pe.wait_ge(s["evacuated"], 8)
                with pe.Fori(0, count) as i:
                    n = i + 1
                    wait(pe, s, n, "staged_h")
                    pe.matmul(mi[0:R, 0, 0:D], hs[:], w[:, 2 * D:3 * D], start=True, stop=True).then_inc(s["v_ready"], 1)
                    wait(pe, s, n, "staged_q", "staged_k")
                    for b in range(4):
                        mm = pe.matmul(scores[0:R, b, 0:4 * R], qs[:], kb[:, 4 * b:4 * b + 4, :], start=True, stop=True)
                    mm.then_inc(s["scores"], 1)
                    turn_probs(pe, s, n, R, scores, pr, ident)
                    wait(pe, s, n, "pt_act", "pt_vec", "v_copied")
                    for h in range(HEADS):
                        mm = pe.matmul(pv[0:R, 8 * h:8 * h + 8], pt[:, h, :], vs[:, 8 * h:8 * h + 8], start=True, stop=True)
                    mm.then_inc(s["pv"], 1)
                    wait(pe, s, n, "o_ready")
                    pe.transpose(mi[:, 1, 0:R], on[:], ident[0:R, 0:R]).then_inc(s["o_turned"], 1)
                    if not order:
                        wait(pe, s, n, "o_copied")
                        pe.matmul(mi[0:R, 2, 0:D], ot[:], wo[:], start=True, stop=True).then_inc(s["out_ready"], 1)
                if order:
                    pe.wait_ge(s["o_copied"], count)
                    for t in range(PAIRS):
                        mm = pe.matmul(scores[0:PT, t // 4, (t % 4) * D:(t % 4 + 1) * D], o_t[:, t * PT:(t + 1) * PT],
                                       wo[:], start=True, stop=True)
                    mm.then_inc(s["out2"], 1)

            @block.scalar
            def _(act):
                for b in range(8):
                    act.wait_ge(s["projected"], b + 1)
                    dst = (q_t if b < 4 else k_t)[:, (b % 4) * GT:(b % 4 + 1) * GT]
                    act.activation(dst, scores[:, b % 4, 0:GT], ACT.Copy, scale=scale if b < 4 else 1.0)\
                        .then_inc(s["evacuated"], 1)
                act.wait_ge(s["evacuated"], 8)
                act.wait_ge(s["loaded"], 64)
                with act.Fori(0, count) as i:
                    n = i + 1
                    act.wait_ge(s[last], i)
                    act.activation(src.fixed(hs), src.part(h_t, i), ACT.Copy).then_inc(s["staged_h"], 1)
                    act.activation(src.fixed(qs), src.part(q_t, i), ACT.Copy).then_inc(s["staged_q"], 1)
                    wait(act, s, n, "v_ready")
                    act.activation(vs[:], mi[0:R, 0, 0:D], ACT.Copy).then_inc(s["v_copied"], 1)
                    wait(act, s, n, "shifted")
                    act.activation(pr[:], pr[:], ACT.Exp).then_inc(s["probs"], 1)
                    wait(act, s, n, "turned")
                    act.activation(pt[:, 0:8, :].rearrange("k (a b) q -> k a (b q)", a=2), scores[0:R, 0:2, 0:4 * R], ACT.Copy)\
                        .then_inc(s["pt_act"], 1)
                    wait(act, s, n, "o_turned")
                    if order:
                        act.activation(order(o_t, i), mi[:, 1, 0:R].rearrange("d (b t) -> d b t", t=BATCH), ACT.Copy)\
                            .then_inc(s["o_copied"], 1)
                    else:
                        act.activation(ot[:], mi[:, 1, 0:R], ACT.Copy).then_inc(s["o_copied"], 1)

            @block.vector
            def _(v):
                v.wait_ge(s["evacuated"], 8)
                v.wait_ge(s["loaded"], 64)
                with v.Fori(0, count) as i:
                    n = i + 1
                    v.wait_ge(s[last], i)
                    v.tensor_tensor(src.heads(kb), src.all_heads(k_t, i), src.mask(hm), ALU.mult).then_inc(s["staged_k"], 1)
                    softmax_vector(v, s, n, R, scores, mk, pr[:], mx[:], ls[:], rl[:])
                    wait(v, s, n, "turned")
                    v.tensor_copy(pt[:, 8:16, :].rearrange("k (a b) q -> k a (b q)", a=2), scores[0:R, 2:4, 0:4 * R])\
                        .then_inc(s["pt_vec"], 1)
                    wait(v, s, n, "pv", "inverse")
                    v.tensor_tensor(on.rearrange("q (h e) -> q h e", h=HEADS), pv[0:R, 0:D].rearrange("q (h e) -> q h e", h=HEADS),
                                    bc(rl[:, :, None], [R, HEADS, 8]), ALU.mult).then_inc(s["o_ready"], 1)
                    if not order:
                        wait(v, s, n, "out_ready")
                        v.tensor_tensor(x[:, i, :], mi[0:R, 2, 0:D], x[:, i, :], ALU.add).then_inc(s["done"], 1)
                if order:
                    v.wait_ge(s["out2"], 1)
                    v.tensor_tensor(x.rearrange("t (a b) d -> t a (b d)", a=4), scores[0:PT, :, :],
                                    x.rearrange("t (a b) d -> t a (b d)", a=4), ALU.add).then_inc(s["added"], 1)


def l0_attention(nc, g, a):
    normalise(nc, g, "n0", [("layer", 1e-5)])
    narrow_attention(nc, g, "a0", PT, PAIRS, PairTokens, g["consts"]["causal_mask"], 8 ** -0.5,
                     a["L0_attn_in_proj_weight"], a["L0_attn_out_proj_weight"])



def rounds(eng, body):
    body(0)
    with eng.Fori(1, PAIRS - 1) as i:
        body(i)
    body(PAIRS - 1)


def l0_cross(nc, g, a):
    normalise(nc, g, "n1", [("layer", 1e-5), ("layer", 1e-5)], a["L0_xattn_ln_l_w"], a["L0_xattn_ln_l_b"])
    ident, ones, x, h_t, half = g["ident"], g["ones"], g["x"], g["h_t"], g["half"]
    QH, C, S = 8, 4, SEQ
    names = ("loaded negb heads heads_copied q_made q_act q_vec ctx0 ctx1 stats mv var rstd centred z_ready "
             "lat_ready q_ready turned freed0 freed1 scores max_ctx max_lat negmax probs sums inverse diag pl pv ol_copied mixed "
             "o_norm o_ready out_ready done")
    with stage(nc, "x0", names) as (s, sb, ps):
        wqt = sb("wq_t", [64, QH, D]); wkt = sb("wk_t", [64, QH, D]); wv = sb("wv", [D, 512]); wout = sb("wout", [D, C, D])
        ab = sb("gain_shift", [D, 3]); mh = sb("heads", [D, QH, D]); q = sb("q", [D, QH, TOK])
        cx = [sb(f"ctx{j}", [TP, TILES, D]) for j in range(2)]; z = [sb(f"z{j}", [TP, TILES, D]) for j in range(2)]
        bst = sb("bst", [TP, TILES, 6]); mv = [sb(f"mv{j}", [TP, TILES, 2]) for j in range(2)]; rstd = sb("rstd", [TP, TILES, 1])
        zt = sb("z_t", [D, CTX]); lt = [sb(f"lat_t{j}", [D, S]) for j in range(2)]; ln = [sb(f"lat{j}", [S, D]) for j in range(2)]
        ql = [sb(f"q_lat{j}", [D, QH, S]) for j in range(2)]; qz = [sb(f"q_ctx{j}", [D, QH, S]) for j in range(2)]
        pr = [sb(f"pr{k}", [PT, CTX + S]) for k in range(C)]; sl = [sb(f"lat_scores{j}", [PT, C, S]) for j in range(2)]; pt = sb("pt", [TP, TILES, C * PT]); ptl = sb("ptl", [S, C * PT])
        mx = sb("mx", [PT, 2]); nm = sb("nm", [PT, 2]); l = [sb(f"l{j}", [PT, C, 2]) for j in range(2)]; ls = sb("ls", [PT, C]); rl = sb("rl", [PT, C])
        dg = sb("dg", [PT, C, PT]); ols = sb("ols", [D, C * PT]); o1 = sb("o1", [D, C * PT]); ut = sb("ut", [D, C, PT])
        sc = ps("sc", [D, 6, 512]); turn = ps("turn", [D, 2, 512])
        oz, ol, spread = (sc[:, b, :] for b in (3, 4, 5))
        FRONT = 4
        TURNS = 4 * C + FRONT + 2
        SHIFT = FRONT - 2
        OUT = C * S + D

        def cnt(i, j, per, k):
            return i * (2 * per) + (j * per + k)

        def is_first(i, j):
            return isinstance(i, int) and i == 0 and j == 0

        def is_last(i, j):
            return isinstance(i, int) and i == PAIRS - 1 and j == 1

        def chunk_group(i, j, c, b):
            if c == 0:
                return (i, j, 2 + b if is_first(i, j) or b >= 2 else b)
            return (i, j, 2 + 4 * c + b + (0 if c < 2 or is_last(i, j) else 2 if c == 2 else 4))

        def front_group(i, j, b):
            if is_first(i, j):
                return (i, j, b - SHIFT)
            return (*((i, 0) if j else (i - 1, 1)), (10, 11, 16, 17)[b])

        def project_group(i, j, r):
            return (i, j, 2 + 4 * C + r) if is_last(i, j) else (*after_of(i, j), 2 + r)

        def after_of(i, j):
            return (i, 1) if j == 0 else (i + 1, 0)

        def emitted(i, j, k):
            return i * (2 * TURNS) + (SHIFT + TURNS * j + k + 1)

        def half_of(i, j, k):
            n = SHIFT + TURNS * j + k + 1
            return i * TURNS + (n + 1) // 2, i * TURNS + n // 2

        def lat_scored(eng, i, j):
            eng.wait_ge(s["freed1"], half_of(*front_group(i, j, 3))[1])

        with nc.Block() as block:
            @block.sync
            def _(sp):
                for dst, drm in ((wqt[:], a["L0_xattn_wq_t"]), (wkt[:], a["L0_xattn_wk_t"]), (wv[:], a["L0_xattn_wv"]), (wout[:], a["L0_xattn_wout"]),
                                 (ab[:, 0:1], a["L0_xattn_ln_m_w"]), (ab[:, 1:2], a["L0_xattn_ln_m_b"])):
                    sp.dma_start(dst, drm).then_inc(s["loaded"], 16)

                def body(i):
                    for j in range(2):
                        if not (isinstance(i, int) and i == 0):
                            sp.wait_ge(s["centred"], cnt(i, j, 1, -1))
                        sp.dma_start(cx[j][:], a["ctx"][bass.ds(i * 2 + j, 1), :, :, :].rearrange("o p t d -> (o p) t d")).then_inc(s[f"ctx{j}"], 16)
                rounds(sp, body)

            @block.tensor
            def _(pe):
                pe.wait_ge(s["loaded"], 96)
                for h in range(QH):
                    mm = pe.matmul(sc[:, h // 4, (h % 4) * D:(h % 4 + 1) * D], wqt[:, h, :], wkt[:, h, :], start=True, stop=True)
                mm.then_inc(s["heads"], 1)
                pe.wait_ge(s["heads_copied"], 1)
                for k in range(4 * QH):
                    if k >= 2:
                        pe.wait_ge(s["q_act" if k % 2 == 0 else "q_vec"], k // 2)
                    pe.matmul(sc[:, k % 2, 0:GT], mh[:, k // 4, :], h_t[:, (k % 4) * GT:(k % 4 + 1) * GT], start=True, stop=True)\
                        .then_inc(s["q_made"], 1)
                pe.wait_ge(s["q_act"], 2 * QH)
                pe.wait_ge(s["q_vec"], 2 * QH)

                def group(i, j, k, emit):
                    bank = (SHIFT + k) % 2
                    if not (is_first(i, j) and SHIFT + k < 2):
                        pe.wait_ge(s[f"freed{bank}"], half_of(i, j, k - 2)[bank])
                    apart(pe)
                    emit(turn[:, bank, :]).then_inc(s["turned"], 1)

                def copied(i, j, k):
                    bank = (SHIFT + k) % 2
                    pe.wait_ge(s[f"freed{bank}"], half_of(i, j, k)[bank])

                def project(i, j, r):
                    def half_heads(bank):
                        for c in range(2 * r, 2 * r + 2):
                            mm = pe.matmul(bank[:, (c % 2) * PT:(c % 2 + 1) * PT], wv[:, c * D:(c + 1) * D], o1[:, c * PT:(c + 1) * PT], start=True, stop=True)
                        return mm
                    pe.wait_ge(s["o_ready"], cnt(i, j, 1, 1))
                    group(*project_group(i, j, r), half_heads)

                def pair_out(i, bank):
                    for c in range(C):
                        mm = pe.matmul(bank[0:PT, OUT:OUT + D], ut[:, c, :], wout[:, c, :], start=(c == 0), stop=(c == C - 1))
                    return mm

                def front(i, j, b):
                    def turn_context(bank):
                        for t in range(4):
                            mm = pe.transpose(bank[:, t * TP:(t + 1) * TP], z[j][:, 4 * b + t, :], ident[0:TP, 0:TP])
                        return mm

                    def latents(bank):
                        pe.transpose(bank[0:S, C * S:C * S + D], lt[j][:], ident[:])
                        for c in range(C):
                            mm = pe.matmul(bank[0:PT, c * S:(c + 1) * S], ql[j][:, 2 * c:2 * c + 2, :], lt[j][:], start=True, stop=True)
                        if j == 1 and not (isinstance(i, int) and i == 0):
                            mm = pair_out(i - 1, bank)
                        return mm

                    if b == 0:
                        pe.wait_ge(s["z_ready"], cnt(i, j, 1, 1))
                    if b < 3:
                        group(*front_group(i, j, b), turn_context)
                    else:
                        pe.wait_ge(s["lat_ready"], cnt(i, j, 1, 1))
                        pe.wait_ge(s["q_ready"], cnt(i, j, 1, 1))
                        group(*front_group(i, j, 3), latents)

                def score(i, j, c, turned=None):
                    if c >= 2:
                        pe.wait_ge(s["probs"], cnt(i, j, C, c - 1))
                    elif not (isinstance(i, int) and i == 0 and j == 0):
                        if c == 0:
                            pe.wait_ge(s["probs"], cnt(i, j, C, -1))
                        else:
                            pe.wait_ge(s["o_norm"], cnt(i, j, 1, 0))
                    if c == 0:
                        for b in (1, 2):
                            copied(*front_group(i, j, b))
                    for b in range(3):
                        mm = pe.matmul(sc[0:PT, 3 * (c % 2) + b, 0:BANKC], qz[j][:, 2 * c:2 * c + 2, :], zt[:, b * BANKC:(b + 1) * BANKC],
                                       start=True, stop=True)
                        if turned is not None and b < 2:
                            turned(b)
                    mm.then_inc(s["scores"], 1)

                def body(i):
                    for j in range(2):
                        first = isinstance(i, int) and i == 0 and j == 0
                        last = isinstance(i, int) and i == PAIRS - 1 and j == 1
                        before = (i, 0) if j else (i - 1, 1)
                        after = after_of(i, j)

                        def turn_group(c, b):
                            def tiles(bank):
                                if b == 3:
                                    return pe.transpose(bank[0:S, 0:PT], pr[c][:, CTX:CTX + S], ident[0:PT, 0:PT])
                                for t in range(4):
                                    mm = pe.transpose(bank[0:TP, t * PT:(t + 1) * PT], pr[c][:, (4 * b + t) * TP:(4 * b + t + 1) * TP], ident[0:PT, 0:PT])
                                return mm
                            if b == 0:
                                pe.wait_ge(s["probs"], cnt(i, j, C, c + 1))
                            group(*chunk_group(i, j, c, b), tiles)

                        def sums(b, tiles):
                            if tiles[0] % 4 == 0:
                                copied(*chunk_group(i, j, C - 1, b))
                            for t in tiles:
                                mm = pe.matmul(oz[:, 0:C * PT], z[j][:, t, :], pt[:, t, :], start=(t == 0), stop=(t == TILES - 1))
                            return mm

                        def later(b):
                            if not last:
                                front(*after, b)

                        if not first:
                            turn_group(0, 0)
                            turn_group(0, 1)
                        score(i, j, 1, None if first else lambda b: project(*before, b))
                        if first:
                            turn_group(0, 0)
                            turn_group(0, 1)
                        score(i, j, 2, lambda b: turn_group(0, 2 + b))
                        turn_group(1, 0)
                        turn_group(1, 1)
                        score(i, j, 3, lambda b: turn_group(1, 2 + b))
                        later(0)
                        later(1)
                        for b in range(4):
                            turn_group(2, b)
                        later(2)
                        later(3)
                        if not last:
                            score(*after, 0)
                        turn_group(3, 0)
                        turn_group(3, 1)
                        sums(0, (0, 1))
                        turn_group(3, 2)
                        sums(0, (2, 3))
                        turn_group(3, 3)
                        sums(1, (4, 5, 6, 7))
                        copied(*chunk_group(i, j, C - 1, 3))
                        pe.matmul(ol[:, 0:C * PT], ln[j][:], ptl[:], start=True, stop=True).then_inc(s["pl"], 1)
                        pe.wait_ge(s["diag"], cnt(i, j, 1, 1))
                        pe.matmul(spread[:, 0:C * PT], ones[0:PT, :], dg[:], start=True, stop=True)
                        mm = sums(2, (8, 9, 10, 11))
                        mm.then_inc(s["pv"], 1)

                for b in range(FRONT):
                    front(0, 0, b)
                score(0, 0, 0)
                rounds(pe, body)
                for r in range(2):
                    project(PAIRS - 1, 1, r)
                for r in range(2):
                    copied(*project_group(PAIRS - 1, 1, r))
                pair_out(PAIRS - 1, turn[:, 0, :]).then_inc(s["out_ready"], 1)

            @block.scalar
            def _(act):
                act.wait_ge(s["heads"], 1)
                act.activation(mh.rearrange("k (a b) d -> k a (b d)", a=2), sc[:, 0:2, :], ACT.Copy, scale=64 ** -0.5).then_inc(s["heads_copied"], 1)
                for k in range(0, 4 * QH, 2):
                    act.wait_ge(s["q_made"], k + 1)
                    act.activation(q[:, k // 4, (k % 4) * GT:(k % 4 + 1) * GT], sc[:, 0, 0:GT], ACT.Copy).then_inc(s["q_act"], 1)
                act.wait_ge(s["q_act"], 2 * QH)
                act.wait_ge(s["q_vec"], 2 * QH)
                act.wait_ge(s["negb"], 1)

                def stage_queries(i, j):
                    cols = bass.ds((i * 2 + j) * S, S)
                    act.activation(lt[j][:], h_t[:, cols], ACT.Identity, bias=ab[:, 2:3]).then_inc(s["lat_ready"], 1)
                    act.activation(ql[j][:], q[:, :, cols], ACT.Copy)
                    act.activation(qz[j][:], q[:, :, cols], ACT.Identity, scale=ab[:, 0:1]).then_inc(s["q_ready"], 1)

                def shift_sums(i, j):
                    act.wait_ge(s["o_norm"], cnt(i, j, 1, 1))
                    act.activation(o1[:], o1[:], ACT.Identity, bias=ab[:, 1:2]).then_inc(s["o_ready"], 1)

                def exps(i, j, c):
                    act.wait_ge(s["negmax"], cnt(i, j, C, c + 1))
                    if c == 0:
                        lat_scored(act, i, j)
                    act.activation(pr[c][:, CTX:CTX + S], sl[j][:, c, :], ACT.Exp, bias=nm[:, c % 2:c % 2 + 1], accum_out=l[j][:, c, 1:2])
                    act.activation(pr[c][:, 0:CTX].rearrange("q (a b) -> q a b", a=3), sc[0:PT, 3 * (c % 2):3 * (c % 2) + 3, 0:BANKC], ACT.Exp,
                                   bias=nm[:, c % 2:c % 2 + 1], accum_out=l[j][:, c, 0:1]).then_inc(s["probs"], 1)

                def group_ready(i, j, k):
                    act.wait_ge(s["turned"], emitted(i, j, k))

                def front_copies(i, j, b):
                    group_ready(*front_group(i, j, b))
                    act.activation(zt[:, b * BANKC:(b + 1) * BANKC], turn[:, 0, 0:BANKC], ACT.Copy).then_inc(s["freed0"], 1)

                def copy_heads(i, j):
                    group_ready(*project_group(i, j, 0))
                    for e in range(2):
                        ins = act.activation(ut[64 * e:64 * e + 64, 0:2, j * S:(j + 1) * S],
                                             turn[64 * e:64 * e + 64, 0, 0:2 * PT].rearrange("d (c t) -> d c t", c=2)[:, :, e * S:(e + 1) * S], ACT.Copy)
                    ins.then_inc(s["freed0"], 1)

                stage_queries(0, 0)
                front_copies(0, 0, 0)
                front_copies(0, 0, 2)
                exps(0, 0, 0)

                def body(i):
                    for j in range(2):
                        first = isinstance(i, int) and i == 0 and j == 0
                        last = isinstance(i, int) and i == PAIRS - 1 and j == 1
                        before = (i, 0) if j else (i - 1, 1)
                        after = after_of(i, j)

                        def copy(c, b):
                            group_ready(*chunk_group(i, j, c, b))
                            act.activation(pt[:, 4 * b:4 * b + 4, c * PT:(c + 1) * PT], turn[0:TP, 0, 0:4 * PT].rearrange("p (t q) -> p t q", t=4),
                                           ACT.Copy).then_inc(s["freed0"], 1)

                        copy(0, 0)
                        if not first:
                            copy_heads(*before)
                        exps(i, j, 1)
                        copy(0, 2)
                        copy(1, 0)
                        exps(i, j, 2)
                        copy(1, 2)
                        if not last:
                            stage_queries(*after)
                            front_copies(*after, 0)
                        copy(2, 0)
                        exps(i, j, 3)
                        copy(2, 2)
                        if not last:
                            front_copies(*after, 2)
                        copy(3, 0)
                        if not last:
                            exps(*after, 0)
                        copy(3, 2)
                        act.wait_ge(s["pl"], cnt(i, j, 1, 1))
                        act.activation(ols[:], ol[:, 0:C * PT], ACT.Copy).then_inc(s["ol_copied"], 1)
                        shift_sums(i, j)

                rounds(act, body)
                copy_heads(PAIRS - 1, 1)

            @block.gpsimd
            def _(pool):
                shape = [TP, TILES, D]

                def body(i):
                    for j in range(2):
                        pool.wait_ge(s["mv"], cnt(i, j, 1, 1))
                        if not is_first(i, j):
                            pool.wait_ge(s["z_ready"], cnt(i, j, 1, 0))
                        apart(pool)
                        pool.tensor_scalar(rstd[:], mv[j][:, :, 1:2], 1e-5, None, ALU.add).then_inc(s["var"], 1)
                        pool.wait_ge(s["var"], cnt(i, j, 1, 1))
                        pool.tensor_tensor(rstd[:], rstd[:], half[0:TP, 0:TILES].rearrange("p (t o) -> p t o", o=1), ALU.pow).then_inc(s["rstd"], 1)
                        if not (isinstance(i, int) and i == 0):
                            pool.wait_ge(s["pv"], cnt(i, j, 1, -1))
                        pool.tensor_tensor(z[j][:], cx[j][:], bc(mv[j][:, :, 0:1], shape), ALU.subtract).then_inc(s["centred"], 1)
                        pool.wait_ge(s["centred"], cnt(i, j, 1, 1))
                        pool.wait_ge(s["rstd"], cnt(i, j, 1, 1))
                        pool.tensor_tensor(z[j][:], z[j][:], bc(rstd[:], shape), ALU.mult).then_inc(s["z_ready"], 1)
                rounds(pool, body)

            @block.vector
            def _(v):
                v.wait_ge(s["loaded"], 96)
                v.tensor_scalar(ab[:, 2:3], ab[:, 1:2], -1.0, None, ALU.mult).then_inc(s["negb"], 1)
                for k in range(1, 4 * QH, 2):
                    v.wait_ge(s["q_made"], k + 1)
                    v.tensor_copy(q[:, k // 4, (k % 4) * GT:(k % 4 + 1) * GT], sc[:, 1, 0:GT]).then_inc(s["q_vec"], 1)

                def statistics(i, j):
                    v.wait_ge(s[f"ctx{j}"], i * 16 + 16)
                    if not is_first(i, j):
                        v.wait_ge(s["mv"], cnt(i, j, 1, 0))
                    if not (isinstance(i, int) and i == 0):
                        v.wait_ge(s["z_ready"], cnt(i, j, 1, -1))
                    for t in range(TILES):
                        v.bn_stats(bst[:, t, :], cx[j][:, t, :]).then_inc(s["stats"], 1)
                    v.wait_ge(s["stats"], cnt(i, j, TILES, TILES))
                    apart(v)
                    for t in range(TILES):
                        ins = v.bn_aggr(mv[j][:, t, :], bst[:, t, :])
                    ins.then_inc(s["mv"], 1)

                def group_ready(i, j, k):
                    v.wait_ge(s["turned"], emitted(i, j, k))

                def add_out(i, bank):
                    v.tensor_tensor(x[:, i, :], turn[0:PT, bank, OUT:OUT + D], x[:, i, :], ALU.add).then_inc(s["done"], 1)

                def front_context(i, j):
                    group_ready(*front_group(i, j, 1))
                    v.tensor_copy(zt[:, BANKC:2 * BANKC], turn[:, 1, 0:BANKC]).then_inc(s["freed1"], 1)

                def front_latents(i, j):
                    group_ready(*front_group(i, j, 3))
                    if j == 1 and not (isinstance(i, int) and i == 0):
                        add_out(i - 1, 1)
                    v.tensor_copy(ln[j][:], turn[0:S, 1, C * S:C * S + D])
                    v.tensor_copy(sl[j][:], turn[0:PT, 1, 0:C * S].rearrange("q (c t) -> q c t", c=C)).then_inc(s["freed1"], 1)

                def copy_heads(i, j):
                    group_ready(*project_group(i, j, 1))
                    for e in range(2):
                        ins = v.tensor_copy(ut[64 * e:64 * e + 64, 2:4, j * S:(j + 1) * S],
                                            turn[64 * e:64 * e + 64, 1, 0:2 * PT].rearrange("d (c t) -> d c t", c=2)[:, :, e * S:(e + 1) * S])
                    ins.then_inc(s["freed1"], 1)

                def maxima(i, j, c):
                    first = isinstance(i, int) and i == 0 and j == 0
                    v.wait_ge(s["scores"], cnt(i, j, C, c + 1))
                    if not (first and c < 2):
                        v.wait_ge(s["probs"], cnt(i, j, C, c - 1))
                    if not (first and c == 0):
                        v.wait_ge(s["negmax"], cnt(i, j, C, c))
                    v.tensor_reduce(mx[:, 0:1], sc[0:PT, 3 * (c % 2):3 * (c % 2) + 3, 0:BANKC], AX.XY, ALU.max).then_inc(s["max_ctx"], 1)
                    if c == 0:
                        lat_scored(v, i, j)
                    v.tensor_reduce(mx[:, 1:2], sl[j][:, c, :], AX.X, ALU.max).then_inc(s["max_lat"], 1)
                    v.wait_ge(s["max_ctx"], cnt(i, j, C, c + 1))
                    v.wait_ge(s["max_lat"], cnt(i, j, C, c + 1))
                    v.tensor_reduce(nm[:, c % 2:c % 2 + 1], mx[:], AX.X, ALU.max, negate=True).then_inc(s["negmax"], 1)

                statistics(0, 0)
                statistics(0, 1)
                front_context(0, 0)
                front_latents(0, 0)
                maxima(0, 0, 0)

                def body(i):
                    for j in range(2):
                        first = isinstance(i, int) and i == 0 and j == 0
                        last = isinstance(i, int) and i == PAIRS - 1 and j == 1
                        before = (i, 0) if j else (i - 1, 1)
                        after = after_of(i, j)

                        def copy_context(c):
                            group_ready(*chunk_group(i, j, c, 1))
                            v.tensor_copy(pt[:, 4:8, c * PT:(c + 1) * PT], turn[0:TP, 1, 0:4 * PT].rearrange("p (t q) -> p t q", t=4)).then_inc(s["freed1"], 1)

                        def copy_latents(c):
                            group_ready(*chunk_group(i, j, c, 3))
                            v.tensor_copy(ptl[:, c * PT:(c + 1) * PT], turn[0:S, 1, 0:PT]).then_inc(s["freed1"], 1)

                        copy_context(0)
                        if not first:
                            copy_heads(*before)
                        maxima(i, j, 1)
                        copy_latents(0)
                        maxima(i, j, 2)
                        copy_context(1)
                        copy_latents(1)
                        maxima(i, j, 3)
                        if not last:
                            front_context(*after)
                        copy_context(2)
                        copy_latents(2)
                        if not last:
                            front_latents(*after)
                            maxima(*after, 0)
                        copy_context(3)
                        copy_latents(3)
                        v.wait_ge(s["probs"], cnt(i, j, C, C))
                        v.tensor_reduce(ls[:], l[j][:], AX.X, ALU.add).then_inc(s["sums"], 1)
                        v.wait_ge(s["sums"], cnt(i, j, 1, 1))
                        v.reciprocal(rl[:], ls[:]).then_inc(s["inverse"], 1)
                        v.wait_ge(s["inverse"], cnt(i, j, 1, 1))
                        v.tensor_tensor(dg[:], bc(ident[0:PT, None, 0:PT], [PT, C, PT]), bc(rl[:, :, None], [PT, C, PT]), ALU.mult).then_inc(s["diag"], 1)
                        if not last and not is_last(*after):
                            statistics(*after_of(*after))
                        v.wait_ge(s["ol_copied"], cnt(i, j, 1, 1))
                        v.wait_ge(s["pv"], cnt(i, j, 1, 1))
                        v.scalar_tensor_tensor(o1[:], oz[:, 0:C * PT], ab[:, 0:1], ols[:], ALU.mult, ALU.add).then_inc(s["mixed"], 1)
                        v.wait_ge(s["mixed"], cnt(i, j, 1, 1))
                        v.tensor_tensor(o1[:], o1[:], spread[:, 0:C * PT], ALU.mult).then_inc(s["o_norm"], 1)

                rounds(v, body)
                copy_heads(PAIRS - 1, 1)
                v.wait_ge(s["out_ready"], 1)
                add_out(PAIRS - 1, 0)



NORM_STEPS = "n_sum n_mean n_centred n_squared n_sumsq n_var n_rstd n_normed "
ROUTE_STEPS = "r_logits r_max r_best r_order r_first r_picked "


def norm_vector(v, s, n, y, sq, st, size, eps):
    shape = list(y.shape)
    v.tensor_reduce(st[0], y, AX.X, ALU.add).then_inc(s["n_sum"], 1)
    wait(v, s, n, "n_sum")
    v.tensor_scalar(st[1], st[0], 1.0 / size, None, ALU.mult).then_inc(s["n_mean"], 1)
    wait(v, s, n, "n_mean")
    v.tensor_tensor(y, y, bc(st[1][:, :, None], shape), ALU.subtract).then_inc(s["n_centred"], 1)
    wait(v, s, n, "n_centred")
    v.tensor_tensor(sq, y, y, ALU.mult).then_inc(s["n_squared"], 1)
    wait(v, s, n, "n_squared")
    v.tensor_reduce(st[2], sq, AX.X, ALU.add).then_inc(s["n_sumsq"], 1)
    wait(v, s, n, "n_sumsq")
    v.tensor_scalar(st[3], st[2], 1.0 / size, eps, ALU.mult, ALU.add).then_inc(s["n_var"], 1)
    wait(v, s, n, "n_rstd")
    v.tensor_tensor(y, y, bc(st[4][:, :, None], shape), ALU.mult).then_inc(s["n_normed"], 1)


def norm_pool(pool, s, n, st, half):
    wait(pool, s, n, "n_var")
    pool.tensor_tensor(st[4], st[3], half, ALU.pow).then_inc(s["n_rstd"], 1)


def argmax_vector(v, s, n, p, value, top, rank, earlier, picked):
    shape = list(value.shape)
    v.tensor_reduce(top, value, AX.X, ALU.max).then_inc(s[p + "_max"], 1)
    wait(v, s, n, p + "_max")
    v.tensor_tensor(rank, value, bc(top[:, :, None], shape), ALU.is_equal).then_inc(s[p + "_best"], 1)
    wait(v, s, n, p + "_best")
    v.tensor_tensor(rank, rank, bc(earlier[0:shape[0], None, :], shape), ALU.mult).then_inc(s[p + "_order"], 1)
    wait(v, s, n, p + "_order")
    v.tensor_reduce(top, rank, AX.X, ALU.max).then_inc(s[p + "_first"], 1)
    wait(v, s, n, p + "_first")
    v.tensor_tensor(picked, rank, bc(top[:, :, None], shape), ALU.is_equal).then_inc(s[p + "_picked"], 1)



def l0_ffn(nc, g, a):
    normalise(nc, g, "n2", [("layer", 1e-5)])
    ident, x, h_n, h_t, C = g["ident"], g["x"], g["h_n"], g["h_t"], g["consts"]
    names = ("loaded staged picked_t mask_t spread masked inner gelu outer sum1 sum2 gained shifted done "
             + NORM_STEPS + ROUTE_STEPS)
    with stage(nc, "f0", names) as (s, sb, ps):
        wr = sb("router", [D, EXPERTS]); w1 = sb("w1", [D, EXPERTS, 512]); b1 = sb("b1", [EXPERTS, 512])
        wo = sb("wo", [D, 4, D]); rows = sb("rows", [PT, 3, D]); pick = sb("pick", [EXPERTS, EXPERTS, D])
        early = sb("earlier", [D, EXPERTS])
        hs = sb("hs", [D, GT]); xm = sb("xm", [D, EXPERTS, GT]); ge = sb("gelu", [D, 4, GT]); oht = sb("oht", [EXPERTS, GT])
        oh = sb("oh", [PT, GROUP, EXPERTS]); rank = sb("rank", [PT, GROUP, EXPERTS]); top = sb("top", [PT, GROUP])
        y = sb("y", [PT, GROUP, D]); sq = sb("ysq", [PT, GROUP, D])
        st = [sb(f"st{k}", [PT, GROUP])[:] for k in range(5)]
        small = ps("small", [D, 512]); spread = ps("spread", [D, 2, 512]); inner = ps("inner", [D, 4, 512]); outer = ps("outer", [D, 512])
        with nc.Block() as block:
            @block.sync
            def _(sp):
                for dst, drm in ((wr[:], a["L0_ffn_router"]), (w1[:], a["L0_ffn_w1"]), (b1[:], a["L0_ffn_b1"]),
                                 (wo[:], a["L0_ffn_wo"]), (pick[:], C["pick"]), (early[:], C["earlier"])):
                    sp.dma_start(dst, drm).then_inc(s["loaded"], 16)
                for k in range(3):
                    sp.dma_start(rows[:, k, :], bc(a["L0_ffn_rows"][k:k + 1, :], [PT, D])).then_inc(s["loaded"], 16)

            @block.tensor
            def _(pe):
                pe.wait_ge(s["loaded"], 144)
                with pe.Fori(0, 4) as c:
                    n = c + 1
                    wait(pe, s, n, "staged")
                    for t in range(GROUP):
                        mm = pe.matmul(small[0:PT, t * EXPERTS:(t + 1) * EXPERTS], hs[:, t * PT:(t + 1) * PT], wr[:], start=True, stop=True)
                    mm.then_inc(s["r_logits"], 1)
                    wait(pe, s, n, "r_picked")
                    for t in range(GROUP):
                        mm = pe.transpose(spread[0:EXPERTS, 0, t * PT:(t + 1) * PT],
                                          oh[:, t, :], ident[0:PT, 0:PT])
                    mm.then_inc(s["picked_t"], 1)
                    wait(pe, s, n, "mask_t")
                    for e in range(EXPERTS):
                        if e >= 2:
                            pe.wait_ge(s["masked"], c * EXPERTS + (e - 1))
                        pe.matmul(spread[:, e % 2, 0:GT], pick[:, e, :], oht[:], start=True, stop=True).then_inc(s["spread"], 1)
                    pe.wait_ge(s["masked"], n * EXPERTS)
                    for f in range(4):
                        for e in range(EXPERTS):
                            pe.matmul(inner[:, f, 0:GT], w1[:, e, f * D:(f + 1) * D], xm[:, e, :], start=(e == 0), stop=False)
                        pe.matmul(inner[:, f, 0:GT], b1[:, f * D:(f + 1) * D], oht[:], start=False, stop=True).then_inc(s["inner"], 1)
                    pe.wait_ge(s["gelu"], n * 4)
                    for t in range(GROUP):
                        for f in range(4):
                            mm = pe.matmul(outer[0:PT, t * D:(t + 1) * D], ge[:, f, t * PT:(t + 1) * PT], wo[:, f, :],
                                           start=(f == 0), stop=(f == 3))
                    mm.then_inc(s["outer"], 1)

            @block.scalar
            def _(act):
                with act.Fori(0, 4) as c:
                    n = c + 1
                    act.wait_ge(s["done"], c)
                    act.activation(hs[:], h_t[:, bass.ts(c, GT)], ACT.Copy).then_inc(s["staged"], 1)
                    wait(act, s, n, "picked_t")
                    act.activation(oht[:], spread[0:EXPERTS, 0, 0:GT], ACT.Copy).then_inc(s["mask_t"], 1)
                    for f in range(4):
                        act.wait_ge(s["inner"], c * 4 + (f + 1))
                        act.activation(ge[:, f, :], inner[:, f, 0:GT], ACT.Gelu).then_inc(s["gelu"], 1)

            @block.vector
            def _(v):
                v.wait_ge(s["loaded"], 144)
                with v.Fori(0, 4) as c:
                    n = c + 1
                    wait(v, s, n, "r_logits")
                    argmax_vector(v, s, n, "r", small[0:PT, 0:GROUP * EXPERTS].rearrange("t (a e) -> t a e", e=EXPERTS),
                                  top[:], rank[:], early, oh[:])
                    for e in range(EXPERTS):
                        v.wait_ge(s["spread"], c * EXPERTS + (e + 1))
                        v.tensor_tensor(xm[:, e, :], hs[:], spread[:, e % 2, 0:GT], ALU.mult).then_inc(s["masked"], 1)
                    wait(v, s, n, "outer")
                    v.tensor_tensor(y[:], outer[0:PT, :].rearrange("t (a d) -> t a d", a=GROUP), h_n[:, bass.ts(c, GROUP), :], ALU.add)\
                        .then_inc(s["sum1"], 1)
                    wait(v, s, n, "sum1")
                    v.tensor_tensor(y[:], y[:], bc(rows[:, 0:1, :], [PT, GROUP, D]), ALU.add).then_inc(s["sum2"], 1)
                    wait(v, s, n, "sum2")
                    norm_vector(v, s, n, y[:], sq[:], st, D, 1e-12)
                    wait(v, s, n, "n_normed")
                    v.tensor_tensor(y[:], y[:], bc(rows[:, 1:2, :], [PT, GROUP, D]), ALU.mult).then_inc(s["gained"], 1)
                    wait(v, s, n, "gained")
                    v.tensor_tensor(y[:], y[:], bc(rows[:, 2:3, :], [PT, GROUP, D]), ALU.add).then_inc(s["shifted"], 1)
                    wait(v, s, n, "shifted")
                    v.tensor_tensor(x[:, bass.ts(c, GROUP), :], x[:, bass.ts(c, GROUP), :], y[:], ALU.add).then_inc(s["done"], 1)

            @block.gpsimd
            def _(pool):
                with pool.Fori(0, 4) as c:
                    norm_pool(pool, s, c + 1, st, g["half"][0:PT, 0:GROUP])



def l1_attention(nc, g, a):
    normalise(nc, g, "n3", [("layer", 1e-5)])
    ident, x, h_t = g["ident"], g["x"], g["h_t"]
    LEVELS = len(HALVES)
    names = ("loaded cleared staged xx xxx mix tanh m mixed xs proj_rkg proj_d proj_v d_tanh w_t decay rk v_copied scan diffs cut exps factors "
             "g_exp g_one g_inv gate a_ready a_masked a_sum y_ready y_copied y_turned y_affine gated out_ready done " + NORM_STEPS)
    with stage(nc, "r1", names) as (s, sb, ps):
        maa = sb("maa", [D, 6]); w1 = sb("w1", [D, 160]); w2 = sb("w2", [32, 5, D]); td = sb("decay", [D, 1]); dw1 = sb("dw1", [D, 64]); dw2 = sb("dw2", [64, D])
        bonus = sb("bonus", [D, 1]); w = sb("w", [D, 5, D]); lnw = sb("ln", [D, 2]); lm = sb("level_mask", [PT, LEVELS + 1, PT])
        hs = sb("hs", [D, 2, SEQ]); xx = sb("xx", [D, 2, SEQ]); x3 = sb("xxx", [D, 2, SEQ]); mix = sb("mix", [32, 5, PT]); xs = sb("xs", [D, 5, PT])
        dh = sb("dh", [64, PT]); e = sb("e", [D, 2, SEQ]); cum = sb("cum", [D, 2, 65]); on = sb("on", [D, SEQ])
        rk = sb("rk", [D, 2, PT]); vs = sb("vs", [PT, D]); ex = sb("ex", [D, 2, LEVELS, 2, 64]); fac = sb("fac", [D, 2, LEVELS + 1, PT])
        gt = sb("gate", [D, PT]); am = sb("am", [PT, 2, LEVELS + 1, PT]); at = sb("at", [PT, 2, PT])
        y = sb("y", [PT, 2, 64]); sq = sb("ysq", [PT, 2, 64]); yt = sb("yt", [D, PT])
        st = [sb(f"st{k}", [PT, 2])[:] for k in range(5)]
        lo = ps("lo", [D, 2, 512]); mp = ps("mp", [D, 2, 512]); pa = ps("pa", [D, 4, 512])
        flat = lambda buf: buf.rearrange("d a b -> d (a b)")
        slot = lambda buf, k, rows=slice(0, D): buf[rows, k // 4, (k % 4) * PT:(k % 4 + 1) * PT]
        with nc.Block() as block:
            @block.sync
            def _(sp):
                loads = [(maa[:, k:k + 1], a[f"L1_maa_{c}"]) for k, c in enumerate("xwkvrg")]
                loads += [(w1[:], a["L1_maa_w1"]), (w2[:], a["L1_maa_w2"]), (td[:], a["L1_decay"]), (dw1[:], a["L1_decay_w1"]), (dw2[:], a["L1_decay_w2"]),
                          (bonus[:], a["L1_bonus"]), (w[:], a["L1_w"]), (lnw[:, 0:1], a["L1_ln_w"]), (lnw[:, 1:2], a["L1_ln_b"]), (lm[:], g["consts"]["level_mask"])]
                assert len(loads) == 16
                for dst, drm in loads:
                    sp.dma_start(dst, drm).then_inc(s["loaded"], 16)

            @block.tensor
            def _(pe):
                pe.wait_ge(s["loaded"], 256)
                with pe.Fori(0, PAIRS) as i:
                    n = i + 1
                    wait(pe, s, n, "xxx")
                    for k in range(5):
                        mm = pe.matmul(slot(lo, k, slice(0, 32)), w1[:, 32 * k:32 * k + 32], flat(x3), start=True, stop=True)
                    mm.then_inc(s["mix"], 1)
                    pe.wait_ge(s["tanh"], n * 2)
                    for k in range(5):
                        mm = pe.matmul(slot(mp, k), w2[:, k, :], mix[:, k, :], start=True, stop=True)
                    mm.then_inc(s["m"], 1)
                    wait(pe, s, n, "xs")
                    pe.matmul(lo[0:64, 0, 0:PT], dw1[:], xs[:, 0, :], start=True, stop=True).then_inc(s["proj_d"], 1)
                    pe.matmul(slot(mp, 0), w[:, 0, :], xs[:, 3, :], start=True, stop=True)
                    pe.matmul(slot(mp, 1), w[:, 1, :], xs[:, 1, :], start=True, stop=True)
                    pe.matmul(slot(mp, 2), w[:, 3, :], xs[:, 4, :], start=True, stop=True).then_inc(s["proj_rkg"], 1)
                    pe.matmul(mp[0:PT, 1, 0:D], xs[:, 2, :], w[:, 2, :], start=True, stop=True).then_inc(s["proj_v"], 1)
                    wait(pe, s, n, "d_tanh")
                    pe.matmul(lo[:, 1, 0:PT], dw2[:], dh[:], start=True, stop=True).then_inc(s["w_t"], 1)
                    pe.wait_ge(s["factors"], n * 4)
                    for h in range(2):
                        rows = slice(64 * h, 64 * h + 64)
                        for l in range(LEVELS + 1):
                            mm = pe.matmul(pa[0:PT, 2 * h + l // 4, (l % 4) * PT:(l % 4 + 1) * PT], fac[rows, 1, l, :], fac[rows, 0, l, :], start=True, stop=True)
                        mm.then_inc(s["a_ready"], 1)
                    pe.wait_ge(s["a_sum"], n * 2)
                    wait(pe, s, n, "v_copied")
                    for h in range(2):
                        mm = pe.matmul(lo[0:PT, 0, 64 * h:64 * h + 64], at[:, h, :], vs[:, 64 * h:64 * h + 64], start=True, stop=True)
                    mm.then_inc(s["y_ready"], 1)
                    wait(pe, s, n, "n_normed")
                    pe.transpose(lo[:, 1, 0:PT], flat(y), ident[0:PT, 0:PT]).then_inc(s["y_turned"], 1)
                    wait(pe, s, n, "gated")
                    pe.matmul(mp[0:PT, 1, 0:D], yt[:], w[:, 4, :], start=True, stop=True).then_inc(s["out_ready"], 1)

            @block.scalar
            def _(act):
                act.wait_ge(s["loaded"], 256)
                with act.Fori(0, PAIRS) as i:
                    n = i + 1
                    act.wait_ge(s["done"], i)
                    act.activation(flat(hs), h_t[:, bass.ts(i, PT)], ACT.Copy).then_inc(s["staged"], 1)
                    wait(act, s, n, "mix")
                    act.activation(mix[:, 0:4, :].rearrange("k a t -> k (a t)"), lo[0:32, 0, 0:4 * PT], ACT.Tanh).then_inc(s["tanh"], 1)
                    act.activation(mix[:, 4, :], lo[0:32, 1, 0:PT], ACT.Tanh).then_inc(s["tanh"], 1)
                    wait(act, s, n, "proj_d")
                    act.activation(dh[:], lo[0:64, 0, 0:PT], ACT.Tanh).then_inc(s["d_tanh"], 1)
                    wait(act, s, n, "proj_rkg")
                    act.activation(flat(rk), mp[:, 0, 0:2 * PT], ACT.Copy).then_inc(s["rk"], 1)
                    act.activation(gt[:], slot(mp, 2), ACT.Exp, scale=-1.0).then_inc(s["g_exp"], 1)
                    wait(act, s, n, "w_t")
                    act.activation(flat(e), lo[:, 1, 0:PT], ACT.Exp, bias=td[:, 0:1]).then_inc(s["decay"], 1)
                    wait(act, s, n, "proj_v")
                    act.activation(vs[:], mp[0:PT, 1, 0:D], ACT.Copy).then_inc(s["v_copied"], 1)
                    wait(act, s, n, "cut")
                    act.activation(ex[:], ex[:], ACT.Exp).then_inc(s["exps"], 1)
                    wait(act, s, n, "y_turned", "gate")
                    act.activation(yt[:], lo[:, 1, 0:PT], ACT.Identity, scale=lnw[:, 0:1], bias=lnw[:, 1:2]).then_inc(s["y_affine"], 1)

            @block.vector
            def _(v):
                v.memset(on[:], 1.0).then_inc(s["cleared"], 1)
                v.memset(cum[:], 0.0).then_inc(s["cleared"], 1)
                v.wait_ge(s["cleared"], 2)
                v.wait_ge(s["loaded"], 256)
                with v.Fori(0, PAIRS) as i:
                    n = i + 1
                    wait(v, s, n, "staged")
                    v.tensor_tensor(xx[:, :, 1:SEQ], hs[:, :, 0:SEQ - 1], hs[:, :, 1:SEQ], ALU.subtract).then_inc(s["xx"], 1)
                    v.tensor_scalar(xx[:, :, 0:1], hs[:, :, 0:1], -1.0, None, ALU.mult).then_inc(s["xx"], 1)
                    v.wait_ge(s["xx"], n * 2)
                    v.scalar_tensor_tensor(flat(x3), flat(xx), maa[:, 0:1], flat(hs), ALU.mult, ALU.add).then_inc(s["xxx"], 1)
                    wait(v, s, n, "m")
                    for k in range(5):
                        v.scalar_tensor_tensor(xs[:, k, :], slot(mp, k), maa[:, k + 1:k + 2], flat(xx), ALU.add, ALU.mult).then_inc(s["mixed"], 1)
                    v.wait_ge(s["mixed"], n * 5)
                    v.tensor_tensor(xs[:], xs[:], bc(flat(hs)[:, None, :], [D, 5, PT]), ALU.add).then_inc(s["xs"], 1)
                    wait(v, s, n, "g_exp")
                    v.tensor_scalar(gt[:], gt[:], 1.0, None, ALU.add).then_inc(s["g_one"], 1)
                    wait(v, s, n, "g_one")
                    v.reciprocal(gt[:], gt[:]).then_inc(s["g_inv"], 1)
                    wait(v, s, n, "g_inv")
                    v.tensor_tensor(gt[:], gt[:], slot(mp, 2), ALU.mult).then_inc(s["gate"], 1)
                    wait(v, s, n, "decay")
                    for b in range(2):
                        v.tensor_tensor_scan(cum[:, b, 1:SEQ + 1], on[:], e[:, b, :], 0.0, ALU.mult, ALU.add).then_inc(s["scan"], 1)
                    v.wait_ge(s["scan"], n * 2)
                    for l, m in enumerate(HALVES):
                        shape = [D, 2, 64 // (2 * m), 2 * m]
                        blocks = lambda buf: buf.rearrange("d b (c u) -> d b c u", u=2 * m)
                        ref = bc(blocks(cum[:, :, 0:64])[:, :, :, m:m + 1], shape)
                        v.tensor_tensor(blocks(ex[:, 0, l, :, :]), ref, blocks(cum[:, :, 0:64]), ALU.subtract).then_inc(s["diffs"], 1)
                        v.tensor_tensor(blocks(ex[:, 1, l, :, :]), blocks(cum[:, :, 1:65]), ref, ALU.subtract).then_inc(s["diffs"], 1)
                    v.wait_ge(s["diffs"], n * 2 * LEVELS)
                    v.tensor_scalar(ex[:], ex[:], 0.0, None, ALU.min).then_inc(s["cut"], 1)
                    wait(v, s, n, "exps", "rk")
                    for q in range(2):
                        v.tensor_tensor(fac[:, q, 0:LEVELS, :].rearrange("d l (b t) -> d l b t", b=2), ex[:, q, :, :, 0:SEQ],
                                        bc(rk[:, q, :].rearrange("d (b t) -> d b t", b=2)[:, None, :, :], [D, LEVELS, 2, SEQ]), ALU.mult)\
                            .then_inc(s["factors"], 1)
                    v.tensor_scalar(fac[:, 0, LEVELS, :], rk[:, 0, :], bonus[:, 0:1], None, ALU.mult).then_inc(s["factors"], 1)
                    v.tensor_copy(fac[:, 1, LEVELS, :], rk[:, 1, :]).then_inc(s["factors"], 1)
                    for h in range(2):
                        v.wait_ge(s["a_ready"], i * 2 + (h + 1))
                        for q, (lo_l, hi_l) in enumerate(((0, 4), (4, LEVELS + 1))):
                            v.tensor_tensor(am[:, h, lo_l:hi_l, :], pa[0:PT, 2 * h + q, 0:(hi_l - lo_l) * PT].rearrange("s (l t) -> s l t", t=PT),
                                            lm[:, lo_l:hi_l, :], ALU.mult).then_inc(s["a_masked"], 1)
                        v.wait_ge(s["a_masked"], i * 4 + (2 * h + 2))
                        v.tensor_reduce(at[:, h, :], am[:, h, :, :].rearrange("s l t -> s t l"), AX.X, ALU.add).then_inc(s["a_sum"], 1)
                    wait(v, s, n, "y_ready")
                    v.tensor_copy(flat(y), lo[0:PT, 0, 0:D]).then_inc(s["y_copied"], 1)
                    wait(v, s, n, "y_copied")
                    norm_vector(v, s, n, y[:], sq[:], st, 64, 1e-5 * 64)
                    wait(v, s, n, "y_affine")
                    v.tensor_tensor(yt[:], yt[:], gt[:], ALU.mult).then_inc(s["gated"], 1)
                    wait(v, s, n, "out_ready")
                    v.tensor_tensor(x[:, i, :], mp[0:PT, 1, 0:D], x[:, i, :], ALU.add).then_inc(s["done"], 1)

            @block.gpsimd
            def _(pool):
                with pool.Fori(0, PAIRS) as i:
                    norm_pool(pool, s, i + 1, st, g["half"][0:PT, 0:2])



def l1_cross(nc, g, a):
    normalise(nc, g, "n4", [("layer", 1e-5)])
    ident, ones, x, h_t = g["ident"], g["ones"], g["x"], g["h_t"]
    C, S, KV = HEADS * SEQ // D, SEQ, 6
    TURNS = KV + 3 * C
    Q4 = 4 * SEQ
    names = ("loaded bq_scaled q_made q_t ctxt0 ctxt1 mask0 mask1 q_ready turned freed0 freed1 scores masked negmax probs inverse diag pv oz_copied "
             "spread o_norm picked u_sum u_ready out_ready out_sum done")
    with stage(nc, "x1", names) as (s, sb, ps):
        wq = sb("wq", [D, D]); wkv = sb("wkv", [D, 2 * D]); wp = sb("wp", [D, D]); bias = sb("bias", [D, 4]); bp = sb("bp", [PT, D]); hm = sb("hm", [D, HEADS]); hm4 = sb("hm4", [D, 4])
        qt = sb("q_t", [D, TOK]); ct = [sb(f"ctx_t{j}", [D, CTX]) for j in range(2)]; mk = [sb(f"mask{j}", [D, CTX]) for j in range(2)]
        qb = [sb(f"q{j}", [D, HEADS, S]) for j in range(2)]; kt = sb("k_t", [D, CTX]); vv = sb("v", [TP, TILES, D])
        pr = [sb(f"pr{k}", [D, CTX]) for k in range(3)]; pt = sb("pt", [TP, TILES, C * D])
        mx = sb("mx", [D, 2]); nm = sb("nm", [D, 2]); l = sb("l", [D, C]); rl = sb("rl", [D, C]); dg = sb("dg", [D, C * D])
        o1 = sb("o1", [D, 4, SEQ]); ub = sb("ub", [D, S]); ut = sb("ut", [D, PT]); acc = sb("acc", [PT, D])
        sc = ps("sc", [D, 6, 512]); turn = ps("turn", [D, 2, 512])
        oz, spread, out = sc[:, 3, :], sc[:, 4, :], sc[:, 5, :]

        def cnt(i, j, per, k):
            return i * (2 * per) + (j * per + k)

        with nc.Block() as block:
            @block.sync
            def _(sp):
                for dst, drm in ((wq[:], a["L1_xattn_wq"]), (wkv[:], a["L1_xattn_wkv"]), (wp[:], a["L1_xattn_wp"]), (bias[:, 0:1], a["L1_xattn_bq"]),
                                 (bias[:, 1:2], a["L1_xattn_bk"]), (bias[:, 2:3], a["L1_xattn_bv"]), (bp[:], bc(a["L1_xattn_bp"], [PT, D])),
                                 (hm[:], g["headmask"]), (hm4[:], g["consts"]["headmask4"])):
                    sp.dma_start(dst, drm).then_inc(s["loaded"], 16)

                def body(i):
                    for j in range(2):
                        if not (isinstance(i, int) and i == 0):
                            sp.wait_ge(s["turned"], cnt(i - 1, j, TURNS, KV))
                            apart(sp)
                            sp.wait_ge(s["masked"], cnt(i - 1, j, C, C))
                        sp.dma_start(ct[j][:], a["ctx_t"][bass.ds(i * 2 + j, 1), :, :].rearrange("o d c -> (o d) c")).then_inc(s[f"ctxt{j}"], 16)
                        sp.dma_start(mk[j][:], bc(a["ctx_mask"][bass.ds(i * 2 + j, 1), :, :].rearrange("o r c -> (o r) c"), [D, CTX]))\
                            .then_inc(s[f"mask{j}"], 16)
                rounds(sp, body)

            @block.tensor
            def _(pe):
                pe.wait_ge(s["loaded"], 144)
                for b in range(4):
                    pe.matmul(sc[:, b, 0:GT], wq[:], h_t[:, b * GT:(b + 1) * GT], start=True, stop=True).then_inc(s["q_made"], 1)
                pe.wait_ge(s["q_t"], 4)

                def group(i, j, k, emit):
                    n = TURNS * j + k
                    if not (isinstance(i, int) and i == 0 and n < 2):
                        pe.wait_ge(s[f"freed{n % 2}"], i * TURNS + n // 2)
                    emit(turn[:, n % 2, :]).then_inc(s["turned"], 1)

                def copied(i, j, k):
                    n = TURNS * j + k
                    pe.wait_ge(s["freed0"], i * TURNS + (n + 1) // 2)
                    pe.wait_ge(s["freed1"], i * TURNS + n // 2)

                def pair_out(i):
                    pe.wait_ge(s["u_ready"], cnt(i, 1, 1, 1))
                    pe.matmul(out[0:PT, 0:D], ut[:], wp[:], start=True, stop=True).then_inc(s["out_ready"], 1)

                def body(i):
                    for j in range(2):
                        first = isinstance(i, int) and i == 0 and j == 0
                        pe.wait_ge(s[f"ctxt{j}"], i * 16 + 16)
                        for b in range(3):
                            group(i, j, b, lambda bank: pe.matmul(bank[:, 0:BANKC], wkv[:, 0:D], ct[j][:, b * BANKC:(b + 1) * BANKC], start=True, stop=True))

                        def values(b, bank):
                            for t in range(4):
                                mm = pe.matmul(bank[0:TP, t * D:(t + 1) * D], ct[j][:, (4 * b + t) * TP:(4 * b + t + 1) * TP], wkv[:, D:2 * D],
                                               start=True, stop=True)
                            return mm
                        for b in range(3):
                            group(i, j, 3 + b, lambda bank: values(b, bank))
                        copied(i, j, 3)
                        pe.wait_ge(s["q_ready"], cnt(i, j, 1, 1))

                        def score(c, turned=None):
                            if c >= 2:
                                pe.wait_ge(s["masked"], cnt(i, j, C, c - 1))
                            elif c == 0 and not first:
                                pe.wait_ge(s["masked"], cnt(i, j, C, 0))
                            elif not first:
                                pe.wait_ge(s["oz_copied"], cnt(i, j, 1, 0))
                                pe.wait_ge(s["o_norm"], cnt(i, j, 1, 0))
                                if j == 0:
                                    pe.wait_ge(s["out_sum"], i)
                            for b in range(3):
                                mm = pe.matmul(sc[:, 3 * (c % 2) + b, 0:BANKC], qb[j].rearrange("d h t -> d (h t)")[:, c * D:(c + 1) * D],
                                               kt[:, b * BANKC:(b + 1) * BANKC], start=True, stop=True)
                                if turned is not None and b < 2:
                                    turn_group(turned, b)
                            mm.then_inc(s["scores"], 1)

                        def turn_group(c, b):
                            def tiles(bank):
                                for t in range(4):
                                    mm = pe.transpose(bank[0:TP, t * D:(t + 1) * D], pr[c % 3][:, (4 * b + t) * TP:(4 * b + t + 1) * TP], ident[:])
                                return mm
                            if b == 0:
                                pe.wait_ge(s["probs"], cnt(i, j, C, c + 1))
                            group(i, j, KV + 3 * c + b, tiles)

                        score(0)
                        if j == 0 and not first:
                            pair_out(i - 1)
                        score(1)
                        for c in range(C):
                            if c + 2 < C:
                                score(c + 2, c)
                                turn_group(c, 2)
                            else:
                                for b in range(3):
                                    turn_group(c, b)
                        copied(i, j, TURNS)
                        for t in range(TILES):
                            for q in range(4):
                                mm = pe.matmul(oz[32 * q:32 * q + 32, 0:Q4], vv[:, t, 32 * q:32 * q + 32], pt[:, t, Q4 * q:Q4 * (q + 1)],
                                               start=(t == 0), stop=(t == TILES - 1), tile_position=(0, 32 * q))
                        mm.then_inc(s["pv"], 1)
                        pe.wait_ge(s["diag"], cnt(i, j, 1, 1))
                        for q in range(4):
                            mm = pe.matmul(spread[32 * q:32 * q + 32, 0:Q4], ones[:, 32 * q:32 * q + 32], dg[:, Q4 * q:Q4 * (q + 1)],
                                           start=True, stop=True, tile_position=(0, 32 * q))
                        mm.then_inc(s["spread"], 1)

                rounds(pe, body)
                pair_out(PAIRS - 1)

            @block.scalar
            def _(act):
                act.wait_ge(s["bq_scaled"], 1)
                for b in range(4):
                    act.wait_ge(s["q_made"], b + 1)
                    act.activation(qt[:, b * GT:(b + 1) * GT], sc[:, b, 0:GT], ACT.Identity, scale=8 ** -0.5, bias=bias[:, 3:4]).then_inc(s["q_t"], 1)

                def body(i):
                    for j in range(2):
                        first = isinstance(i, int) and i == 0 and j == 0

                        def copy_group(k, dst, src, **kw):
                            if (TURNS * j + k) % 2 == 0:
                                act.wait_ge(s["turned"], cnt(i, j, TURNS, k + 1))
                                act.activation(dst, src, ACT.Identity if kw else ACT.Copy, **kw).then_inc(s["freed0"], 1)

                        for k in range(3):
                            copy_group(k, kt[:, k * BANKC:(k + 1) * BANKC], turn[:, 0, 0:BANKC], bias=bias[:, 1:2])
                        for k in range(3):
                            copy_group(3 + k, vv[:, 4 * k:4 * k + 4, :], turn[0:TP, 0, :].rearrange("p (t d) -> p t d", d=D))

                        def exps(c):
                            act.wait_ge(s["negmax"], cnt(i, j, C, c + 1))
                            if c == 0 and not first:
                                act.wait_ge(s["inverse"], cnt(i, j, 1, 0))
                            act.activation(pr[c % 3][:], pr[c % 3][:], ACT.Exp, bias=nm[:, c % 2:c % 2 + 1], accum_out=l[:, c:c + 1]).then_inc(s["probs"], 1)

                        exps(0)
                        exps(1)
                        for c in range(C):
                            for b in range(3):
                                copy_group(KV + 3 * c + b, pt[:, 4 * b:4 * b + 4, c * D:(c + 1) * D], turn[0:TP, 0, :].rearrange("p (t q) -> p t q", t=4))
                            if c + 2 < C:
                                exps(c + 2)
                        act.wait_ge(s["pv"], cnt(i, j, 1, 1))
                        if not first:
                            act.wait_ge(s["u_sum"], cnt(i, j, 1, 0))
                        act.activation(o1.rearrange("d h t -> d (h t)"), oz[:, 0:Q4], ACT.Copy).then_inc(s["oz_copied"], 1)

                rounds(act, body)

            @block.gpsimd
            def _(pool):
                pool.wait_ge(s["q_t"], 4)
                pool.wait_ge(s["loaded"], 144)

                def body(i):
                    for j in range(2):
                        if not (isinstance(i, int) and i == 0):
                            pool.wait_ge(s["scores"], cnt(i - 1, j, C, C))
                        pool.tensor_tensor(qb[j][:], bc(qt[:, bass.ds((i * 2 + j) * S, S)][:, None, :], [D, HEADS, S]),
                                           bc(hm[:, :, None], [D, HEADS, S]), ALU.mult).then_inc(s["q_ready"], 1)
                rounds(pool, body)

            @block.vector
            def _(v):
                v.wait_ge(s["loaded"], 144)
                v.tensor_scalar(bias[:, 3:4], bias[:, 0:1], 8 ** -0.5, None, ALU.mult).then_inc(s["bq_scaled"], 1)

                def add_out(i):
                    v.wait_ge(s["out_ready"], i + 1)
                    v.tensor_tensor(acc[:], out[0:PT, 0:D], bp[:], ALU.add).then_inc(s["out_sum"], 1)
                    v.wait_ge(s["out_sum"], i + 1)
                    v.tensor_tensor(x[:, i, :], acc[:], x[:, i, :], ALU.add).then_inc(s["done"], 1)

                def body(i):
                    for j in range(2):
                        first = isinstance(i, int) and i == 0 and j == 0

                        def copy_group(k, emit):
                            if (TURNS * j + k) % 2:
                                v.wait_ge(s["turned"], cnt(i, j, TURNS, k + 1))
                                emit().then_inc(s["freed1"], 1)

                        for k in range(3):
                            copy_group(k, lambda: v.tensor_scalar(kt[:, k * BANKC:(k + 1) * BANKC], turn[:, 1, 0:BANKC], bias[:, 1:2], None, ALU.add))
                        for k in range(3):
                            copy_group(3 + k, lambda: v.tensor_copy(vv[:, 4 * k:4 * k + 4, :], turn[0:TP, 1, :].rearrange("p (t d) -> p t d", d=D)))

                        def maxima(c):
                            v.wait_ge(s["scores"], cnt(i, j, C, c + 1))
                            if c == 0:
                                v.wait_ge(s[f"mask{j}"], i * 16 + 16)
                            if c >= 3:
                                v.wait_ge(s["turned"], cnt(i, j, TURNS, KV + 3 * (c - 2)))
                            elif not first:
                                v.wait_ge(s["turned"], cnt(i, j, TURNS, 0))
                            if not (first and c < 2):
                                v.wait_ge(s["probs"], cnt(i, j, C, c - 1))
                            apart(v)
                            v.tensor_tensor_reduce(pr[c % 3].rearrange("q (a b) -> q a b", a=3), sc[:, 3 * (c % 2):3 * (c % 2) + 3, 0:BANKC],
                                                   mk[j].rearrange("q (a b) -> q a b", a=3), 1.0, -3.0e38, ALU.add, ALU.max, mx[:, c % 2:c % 2 + 1])\
                                .then_inc(s["masked"], 1)
                            v.wait_ge(s["masked"], cnt(i, j, C, c + 1))
                            v.tensor_scalar(nm[:, c % 2:c % 2 + 1], mx[:, c % 2:c % 2 + 1], -1.0, None, ALU.mult).then_inc(s["negmax"], 1)

                        maxima(0)
                        if j == 0 and not first:
                            add_out(i - 1)
                        maxima(1)
                        for c in range(C):
                            for b in range(3):
                                copy_group(KV + 3 * c + b, lambda: v.tensor_copy(pt[:, 4 * b:4 * b + 4, c * D:(c + 1) * D],
                                                                                 turn[0:TP, 1, :].rearrange("p (t q) -> p t q", t=4)))
                            if c + 2 < C:
                                maxima(c + 2)
                        v.wait_ge(s["probs"], cnt(i, j, C, C))
                        v.reciprocal(rl[:], l[:]).then_inc(s["inverse"], 1)
                        v.wait_ge(s["inverse"], cnt(i, j, 1, 1))
                        v.tensor_tensor(dg.rearrange("p (c q) -> p c q", c=C), bc(ident[:, None, :], [D, C, D]), bc(rl[:, :, None], [D, C, D]), ALU.mult)\
                            .then_inc(s["diag"], 1)
                        v.wait_ge(s["spread"], cnt(i, j, 1, 1))
                        v.wait_ge(s["oz_copied"], cnt(i, j, 1, 1))
                        v.tensor_tensor(o1.rearrange("d h t -> d (h t)"), o1.rearrange("d h t -> d (h t)"), spread[:, 0:Q4], ALU.mult).then_inc(s["o_norm"], 1)
                        v.wait_ge(s["o_norm"], cnt(i, j, 1, 1))
                        v.tensor_tensor(o1[:], o1[:], bc(hm4[:, :, None], [D, 4, SEQ]), ALU.mult).then_inc(s["picked"], 1)
                        v.wait_ge(s["picked"], cnt(i, j, 1, 1))
                        v.tensor_reduce(ub[:], o1.rearrange("d h t -> d t h"), AX.X, ALU.add).then_inc(s["u_sum"], 1)
                        v.wait_ge(s["u_sum"], cnt(i, j, 1, 1))
                        if j == 0 and not first:
                            v.wait_ge(s["out_ready"], i)
                        v.tensor_scalar(ut[:, j * S:(j + 1) * S], ub[:], bias[:, 2:3], None, ALU.add).then_inc(s["u_ready"], 1)

                rounds(v, body)
                add_out(PAIRS - 1)



def l1_ffn(nc, g, a):
    normalise(nc, g, "n5", [("layer", 1e-5)])
    ident, x, h_n, h_t, C = g["ident"], g["x"], g["h_n"], g["h_t"], g["consts"]
    names = ("loaded staged gate_exp gate_one gate picked_t mask_t copied_n normed_t turned_n spread affine masked inner relu outer "
             "weighed summed biased bias_in gated resid done " + NORM_STEPS + ROUTE_STEPS)
    with stage(nc, "f1", names) as (s, sb, ps):
        wc = sb("centroids", [D, EXPERTS]); lg = sb("ln_g", [D, EXPERTS]); lb = sb("ln_b", [D, EXPERTS])
        w1 = sb("w1", [D, EXPERTS, 512]); b1 = sb("b1", [EXPERTS, 512]); w2 = sb("w2", [D, 4, EXPERTS, D]); b2 = sb("b2", [EXPERTS, D])
        pick = sb("pick", [EXPERTS, EXPERTS, D]); early = sb("earlier", [D, EXPERTS])
        hs = sb("hs", [D, GT]); xn = sb("xn", [D, GT]); xa = sb("xa", [D, GT]); xm = sb("xm", [D, EXPERTS, GT])
        re = sb("relu", [D, 4, GT]); oht = sb("oht", [EXPERTS, GT])
        oh = sb("oh", [PT, GROUP, EXPERTS]); rank = sb("rank", [PT, GROUP, EXPERTS]); top = sb("top", [PT, GROUP]); gate = sb("gate", [PT, GROUP])
        y = sb("y", [PT, GROUP, D]); sq = sb("ysq", [PT, GROUP, D]); wy = sb("wy", [PT, EXPERTS, D]); fo = sb("fo", [PT, D])
        st = [sb(f"st{k}", [PT, GROUP])[:] for k in range(5)]
        small = ps("small", [D, 512]); spread = ps("spread", [D, 2, 512]); inner = ps("inner", [D, 4, 512]); bias = ps("bias", [D, 512])
        with nc.Block() as block:
            @block.sync
            def _(sp):
                for dst, drm in ((wc[:], a["L1_ffn_centroids"]), (lg[:], a["L1_ffn_g"]), (lb[:], a["L1_ffn_b"]), (w1[:], a["L1_ffn_w1"]),
                                 (b1[:], a["L1_ffn_b1"]), (w2[:], a["L1_ffn_w2"]), (b2[:], a["L1_ffn_b2"]),
                                 (pick[:], C["pick"]), (early[:], C["earlier"])):
                    sp.dma_start(dst, drm).then_inc(s["loaded"], 16)

            @block.tensor
            def _(pe):
                pe.wait_ge(s["loaded"], 144)
                with pe.Fori(0, 4) as c:
                    n = c + 1
                    wait(pe, s, n, "staged")
                    for t in range(GROUP):
                        mm = pe.matmul(small[0:PT, t * EXPERTS:(t + 1) * EXPERTS], hs[:, t * PT:(t + 1) * PT], wc[:], start=True, stop=True)
                    mm.then_inc(s["r_logits"], 1)
                    wait(pe, s, n, "r_picked")
                    for t in range(GROUP):
                        mm = pe.transpose(spread[0:EXPERTS, 0, t * PT:(t + 1) * PT], oh[:, t, :], ident[0:PT, 0:PT])
                    mm.then_inc(s["picked_t"], 1)
                    wait(pe, s, n, "n_normed")
                    for t in range(GROUP):
                        mm = pe.transpose(spread[:, 1, t * PT:(t + 1) * PT], y[:, t, :], ident[0:PT, 0:PT])
                    mm.then_inc(s["turned_n"], 1)
                    wait(pe, s, n, "mask_t", "copied_n")
                    for e in range(EXPERTS):
                        if e >= 2:
                            pe.wait_ge(s["masked"], c * EXPERTS + (e - 1))
                        pe.matmul(spread[:, e % 2, 0:GT], pick[:, e, :], oht[:], start=True, stop=True).then_inc(s["spread"], 1)
                    pe.wait_ge(s["masked"], n * EXPERTS)
                    for f in range(4):
                        for e in range(EXPERTS):
                            pe.matmul(inner[:, f, 0:GT], w1[:, e, f * D:(f + 1) * D], xm[:, e, :], start=(e == 0), stop=False)
                        pe.matmul(inner[:, f, 0:GT], b1[:, f * D:(f + 1) * D], oht[:], start=False, stop=True).then_inc(s["inner"], 1)
                    pe.wait_ge(s["relu"], n * 4)
                    for t in range(GROUP):
                        pe.matmul(bias[0:PT, t * D:(t + 1) * D], oht[:, t * PT:(t + 1) * PT], b2[:], start=True, stop=True)
                    for t in range(GROUP):
                        if t:
                            pe.wait_ge(s["weighed"], c * GROUP + t)
                        for q in range(2):
                            for f in range(4):
                                mm = pe.matmul(inner[0:PT, q, :], re[:, f, t * PT:(t + 1) * PT], w2[:, f, 4 * q:4 * q + 4, :],
                                               start=(f == 0), stop=(f == 3))
                        mm.then_inc(s["outer"], 1)

            @block.scalar
            def _(act):
                with act.Fori(0, 4) as c:
                    n = c + 1
                    act.wait_ge(s["done"], c)
                    act.activation(hs[:], h_t[:, bass.ts(c, GT)], ACT.Copy).then_inc(s["staged"], 1)
                    act.activation(y[:], h_n[:, bass.ts(c, GROUP), :], ACT.Copy).then_inc(s["resid"], 1)
                    wait(act, s, n, "r_logits", "r_max")
                    act.activation(gate[:], top[:], ACT.Exp, scale=-1.0).then_inc(s["gate_exp"], 1)
                    wait(act, s, n, "picked_t")
                    act.activation(oht[:], spread[0:EXPERTS, 0, 0:GT], ACT.Copy).then_inc(s["mask_t"], 1)
                    wait(act, s, n, "turned_n")
                    act.activation(xn[:], spread[:, 1, 0:GT], ACT.Copy).then_inc(s["copied_n"], 1)
                    for f in range(4):
                        act.wait_ge(s["inner"], c * 4 + (f + 1))
                        act.activation(re[:, f, :], inner[:, f, 0:GT], ACT.Relu).then_inc(s["relu"], 1)

            @block.vector
            def _(v):
                v.wait_ge(s["loaded"], 144)
                with v.Fori(0, 4) as c:
                    n = c + 1
                    wait(v, s, n, "r_logits")
                    logits = small[0:PT, 0:GROUP * EXPERTS].rearrange("t (a e) -> t a e", e=EXPERTS)
                    v.tensor_reduce(top[:], logits, AX.X, ALU.max).then_inc(s["r_max"], 1)
                    wait(v, s, n, "r_max")
                    v.tensor_tensor(rank[:], logits, bc(top[:, :, None], [PT, GROUP, EXPERTS]), ALU.is_equal).then_inc(s["r_best"], 1)
                    wait(v, s, n, "r_best")
                    v.tensor_tensor(rank[:], rank[:], bc(early[0:PT, None, :], [PT, GROUP, EXPERTS]), ALU.mult).then_inc(s["r_order"], 1)
                    wait(v, s, n, "r_order", "gate_exp")
                    v.tensor_reduce(top[:], rank[:], AX.X, ALU.max).then_inc(s["r_first"], 1)
                    wait(v, s, n, "r_first")
                    v.tensor_tensor(oh[:], rank[:], bc(top[:, :, None], [PT, GROUP, EXPERTS]), ALU.is_equal).then_inc(s["r_picked"], 1)
                    v.tensor_scalar(gate[:], gate[:], 1.0, None, ALU.add).then_inc(s["gate_one"], 1)
                    wait(v, s, n, "gate_one")
                    v.reciprocal(gate[:], gate[:]).then_inc(s["gate"], 1)
                    wait(v, s, n, "resid")
                    norm_vector(v, s, n, y[:], sq[:], st, D, 1e-5)
                    wait(v, s, n, "copied_n")
                    for e in range(EXPERTS):
                        if e:
                            v.wait_ge(s["masked"], c * EXPERTS + e)
                        v.tensor_scalar(xa[:], xn[:], lg[:, e:e + 1], lb[:, e:e + 1], ALU.mult, ALU.add).then_inc(s["affine"], 1)
                        v.wait_ge(s["affine"], c * EXPERTS + (e + 1))
                        v.wait_ge(s["spread"], c * EXPERTS + (e + 1))
                        v.tensor_tensor(xm[:, e, :], xa[:], spread[:, e % 2, 0:GT], ALU.mult).then_inc(s["masked"], 1)
                    for t in range(GROUP):
                        m = c * GROUP + (t + 1)
                        wait(v, s, m, "outer")
                        v.tensor_tensor(wy.rearrange("t (q e) d -> t q e d", q=2), inner[0:PT, 0:2, :].rearrange("t q (e d) -> t q e d", e=4),
                                        bc(oh[:, t, :].rearrange("t (q e) -> t q e", q=2)[:, :, :, None], [PT, 2, 4, D]), ALU.mult)\
                            .then_inc(s["weighed"], 1)
                        wait(v, s, m, "weighed")
                        v.tensor_reduce(fo[:], wy.rearrange("t e d -> t d e"), AX.X, ALU.add).then_inc(s["summed"], 1)
                        wait(v, s, m, "summed")
                        v.tensor_tensor(fo[:], fo[:], bias[0:PT, t * D:(t + 1) * D], ALU.add).then_inc(s["biased"], 1)
                        wait(v, s, m, "biased")
                        v.scalar_tensor_tensor(sq[:, t, :], fo[:], gate[:, t:t + 1], h_n[:, c * GROUP + t, :], ALU.mult, ALU.add)\
                            .then_inc(s["gated"], 1)
                    v.wait_ge(s["gated"], n * GROUP)
                    v.tensor_tensor(x[:, bass.ts(c, GROUP), :], x[:, bass.ts(c, GROUP), :], sq[:], ALU.add).then_inc(s["done"], 1)

            @block.gpsimd
            def _(pool):
                with pool.Fori(0, 4) as c:
                    norm_pool(pool, s, c + 1, st, g["half"][0:PT, 0:GROUP])



STATES = 16


def l2_attention(nc, g, a):
    normalise(nc, g, "n6", [("layer", 1e-5)])
    ident, x, h_t = g["ident"], g["x"], g["h_t"]
    names = ("loaded alog_exp a_ready dt_proj biased absed exped logged dt_ready du_ready y_start spread_w dA0 dA1 reset0 reset1 b_ready c_ready "
             "ub scan0 scan1 hc0 hc1 acc0 acc1 turned added")
    with stage(nc, "s2", names) as (s, sb, ps):
        wd = sb("w_dt", [D, D]); bd = sb("b_dt", [D, 1]); wbc = sb("w_bc", [D, 2, STATES]); an = sb("a", [D, STATES]); dd = sb("d", [D, 1])
        dt = sb("dt", [D, TOK]); ab = sb("abs", [D, TOK]); du = sb("du", [D, TOK]); y = sb("y", [D, TOK]); ub = sb("ub", [D, TOK])
        dA = [sb(f"dA{j}", [D, TOK]) for j in range(2)]; hc = [sb(f"hc{j}", [D, TOK]) for j in range(2)]
        wb = sb("wb", [D, 2, D])
        pb = ps("pb", [D, 4, 512]); pc = ps("pc", [D, 4, 512])
        four = lambda buf: buf.rearrange("d (a b) -> d a b", a=4)
        with nc.Block() as block:
            @block.sync
            def _(sp):
                for dst, drm in ((wd[:], a["L2_dt"]), (bd[:], a["L2_bdt"]), (wbc[:], a["L2_bc"]), (an[:], a["L2_alog"]), (dd[:], a["L2_d"])):
                    sp.dma_start(dst, drm).then_inc(s["loaded"], 16)

            @block.tensor
            def _(pe):
                pe.wait_ge(s["loaded"], 80)
                for b in range(4):
                    mm = pe.matmul(pb[:, b, 0:GT], wd[:], h_t[:, b * GT:(b + 1) * GT], start=True, stop=True)
                mm.then_inc(s["dt_proj"], 1)
                pe.wait_ge(s["biased"], 1)
                with pe.Fori(0, STATES // 2) as i:
                    for j in range(2):
                        m = i * 2 + (j + 1)
                        wait(pe, s, m, "spread_w")
                        pe.wait_ge(s["ub"], i * 2 + j)
                        for b in range(4):
                            mm = pe.matmul(pb[:, b, 0:GT], wb[:, 0, :], h_t[:, b * GT:(b + 1) * GT], start=True, stop=True)
                        mm.then_inc(s["b_ready"], 1)
                        pe.wait_ge(s[f"hc{1 - j}"], i + j)
                        for b in range(4):
                            mm = pe.matmul(pc[:, b, 0:GT], wb[:, 1, :], h_t[:, b * GT:(b + 1) * GT], start=True, stop=True)
                        mm.then_inc(s["c_ready"], 1)
                pe.wait_ge(s["acc1"], STATES // 2)
                pe.wait_ge(s["hc1"], STATES // 2)
                for t in range(PAIRS):
                    mm = pe.transpose(pb[0:PT, t // 4, (t % 4) * D:(t % 4 + 1) * D], y[:, t * PT:(t + 1) * PT], ident[:])
                mm.then_inc(s["turned"], 1)

            @block.scalar
            def _(act):
                act.wait_ge(s["loaded"], 80)
                act.activation(an[:], an[:], ACT.Exp).then_inc(s["alog_exp"], 1)
                act.wait_ge(s["absed"], 1)
                act.activation(ab[:], ab[:], ACT.Exp, scale=-1.0).then_inc(s["exped"], 1)
                act.wait_ge(s["exped"], 1)
                act.activation(ab[:], ab[:], ACT.Ln, bias=1.0).then_inc(s["logged"], 1)
                act.wait_ge(s["dt_ready"], 1)
                act.wait_ge(s["a_ready"], 1)
                with act.Fori(0, STATES // 2) as i:
                    for j in range(2):
                        m = i * 2 + (j + 1)
                        n = i * 2 + j
                        act.wait_ge(s["c_ready"], i * 2 + j)
                        act.activation(wb[:], bc(wbc[:, :, bass.ds(n, 1)], [D, 2, D]), ACT.Copy).then_inc(s["spread_w"], 1)
                        act.wait_ge(s[f"scan{j}"], i)
                        act.activation(dA[j][:], dt[:], ACT.Exp, scale=an[:, bass.ds(n, 1)]).then_inc(s[f"dA{j}"], 1)

            @block.vector
            def _(v):
                v.wait_ge(s["loaded"], 80)
                v.wait_ge(s["dt_proj"], 1)
                v.tensor_scalar(four(dt), pb[:, :, 0:GT], bd[:, 0:1], None, ALU.add).then_inc(s["biased"], 1)
                v.wait_ge(s["biased"], 1)
                v.scalar_tensor_tensor(ab[:], dt[:], -1.0, dt[:], ALU.mult, ALU.max).then_inc(s["absed"], 1)
                v.wait_ge(s["alog_exp"], 1)
                v.tensor_scalar(an[:], an[:], -1.0, None, ALU.mult).then_inc(s["a_ready"], 1)
                v.wait_ge(s["logged"], 1)
                v.scalar_tensor_tensor(dt[:], dt[:], 0.0, ab[:], ALU.max, ALU.add).then_inc(s["dt_ready"], 1)
                v.wait_ge(s["dt_ready"], 1)
                v.tensor_tensor(du[:], dt[:], h_t[:], ALU.mult).then_inc(s["du_ready"], 1)
                v.wait_ge(s["du_ready"], 1)
                with v.Fori(0, STATES // 2) as i:
                    for j in range(2):
                        m = i * 2 + (j + 1)
                        wait(v, s, m, "b_ready")
                        v.wait_ge(s[f"scan{1 - j}"], i + j)
                        v.tensor_tensor(four(ub), four(du), pb[:, :, 0:GT], ALU.mult).then_inc(s["ub"], 1)
                        v.wait_ge(s[f"reset{j}"], i + 1)
                        v.wait_ge(s[f"acc{j}"], i)
                        wait(v, s, m, "ub")
                        v.tensor_tensor_scan(hc[j][:], dA[j][:], ub[:], 0.0, ALU.mult, ALU.add).then_inc(s[f"scan{j}"], 1)
                        v.wait_ge(s[f"scan{j}"], i + 1)
                        wait(v, s, m, "c_ready")
                        v.tensor_tensor(four(hc[j]), four(hc[j]), pc[:, :, 0:GT], ALU.mult).then_inc(s[f"hc{j}"], 1)
                v.wait_ge(s["turned"], 1)
                v.tensor_tensor(x.rearrange("t (a b) d -> t a (b d)", a=4), x.rearrange("t (a b) d -> t a (b d)", a=4), pb[0:PT, :, :], ALU.add)\
                    .then_inc(s["added"], 1)

            @block.gpsimd
            def _(pool):
                pool.wait_ge(s["loaded"], 80)
                pool.tensor_scalar(y[:], h_t[:], dd[:, 0:1], None, ALU.mult).then_inc(s["y_start"], 1)
                pool.wait_ge(s["y_start"], 1)
                with pool.Fori(0, STATES // 2) as i:
                    for j in range(2):
                        pool.wait_ge(s[f"dA{j}"], i + 1)
                        apart(pool)
                        pool.memset(dA[j].rearrange("d (b t) -> d b t", t=SEQ)[:, :, 0:1], 0.0).then_inc(s[f"reset{j}"], 1)
                        pool.wait_ge(s[f"acc{1 - j}"], i + j)
                        pool.wait_ge(s[f"hc{j}"], i + 1)
                        pool.tensor_tensor(y[:], y[:], hc[j][:], ALU.add).then_inc(s[f"acc{j}"], 1)



def l2_cross(nc, g, a):
    normalise(nc, g, "n7", [("layer", 1e-5)])
    ident, ones, x, h_t, csum = g["ident"], g["ones"], g["x"], g["h_t"], g["ctx_sum"]
    names = ("loaded cs biassum cqw_ready c_w scores rowmax negmax probs inverse diag turned copied pv pv_copied spread c2q "
             "own own_col own_row own_max own_neg own_exp own_inv own_norm own_bc weighted q2c prod1 prod2 out_ready out_sum done summed "
             "ctx0 ctx1 ctxt0 ctxt1 half own_copied biassum2")
    with stage(nc, "x2", names) as (s, sb, ps):
        cols = sb("cols", [D, 3]); bias = sb("bias", [SEQ, 3]); bsum = sb("bsum", [SEQ, 1]); wl = sb("wl", [D, 4, D]); bl = sb("bl", [PT, D])
        ct = [sb(f"ctx_t{j}", [D, CTX]) for j in range(2)]; cn = [sb(f"ctx_n{j}", [TP, TILES, D]) for j in range(2)]
        feat = sb("feat", [D, 4, PT]); cq = sb("cq", [D, PT]); pr = sb("pr", [SEQ, CTX]); pt = sb("pt", [TP, TILES, SEQ])
        mx = sb("mx", [SEQ, 1]); nm = sb("nm", [SEQ, 1]); l = sb("l", [SEQ, 1]); il = sb("il", [SEQ, 1]); dg = sb("dg", [SEQ, SEQ])
        pvs = sb("pvs", [D, SEQ]); own = sb("own", [SEQ, 1]); row = sb("row", [1, SEQ]); r1 = sb("r1", [1, 4]); wc = sb("wc", [D, SEQ]); q2c = sb("q2c", [D, 1])
        acc = sb("acc", [PT, D])
        sc = ps("sc", [D, 3, 512]); turn = ps("turn", [D, 2, 512]); pv = ps("pv", [D, 512]); mi = ps("mi", [D, 512]); out = ps("out", [D, 512])
        with nc.Block() as block:
            @block.sync
            def _(sp):
                for dst, drm in ((cols[:], a["L2_x_cols"]), (bias[:], bc(a["L2_x_bias"], [SEQ, 3])), (wl[:], a["L2_x_wl"]), (bl[:], bc(a["L2_x_bl"], [PT, D]))):
                    sp.dma_start(dst, drm).then_inc(s["loaded"], 16)
                with sp.Fori(0, PAIRS) as i:
                    for j in range(2):
                        sp.wait_ge(s["pv"], i * 2)
                        sp.wait_ge(s["summed"], i * 2)
                        sp.dma_start(ct[j][:], a["ctx_t"][bass.ds(i * 2 + j, 1), :, :].rearrange("o d c -> (o d) c")).then_inc(s[f"ctxt{j}"], 16)
                        sp.dma_start(cn[j][:], a["ctx"][bass.ds(i * 2 + j, 1), :, :, :].rearrange("o p t d -> (o p) t d")).then_inc(s[f"ctx{j}"], 16)

            @block.tensor
            def _(pe):
                pe.wait_ge(s["loaded"], 64)
                with pe.Fori(0, PAIRS) as i:
                    for j in range(2):
                        m = i * 2 + (j + 1)
                        own_cols = slice(j * SEQ, (j + 1) * SEQ)
                        wait(pe, s, i + 1, "cqw_ready")
                        pe.wait_ge(s[f"ctxt{j}"], (i + 1) * 16)
                        for b in range(3):
                            mm = pe.matmul(sc[0:SEQ, b, 0:BANKC], cq[:, own_cols], ct[j][:, b * BANKC:(b + 1) * BANKC], start=True, stop=True)
                        mm.then_inc(s["scores"], 1)
                        pe.matmul(out[0:SEQ, 128:129], feat[:, 0, own_cols], cols[:, 1:2], start=True, stop=True).then_inc(s["c_w"], 1)
                        wait(pe, s, m, "probs")
                        apart(pe)
                        for b in range(3):
                            if b == 2:
                                pe.wait_ge(s["copied"], i * 6 + (3 * j + 1))
                                apart(pe)
                            for t in range(4):
                                mm = pe.transpose(turn[0:TP, b % 2, t * SEQ:(t + 1) * SEQ], pr[:, (4 * b + t) * TP:(4 * b + t + 1) * TP], ident[0:SEQ, 0:SEQ])
                            mm.then_inc(s["turned"], 1)
                        pe.wait_ge(s[f"ctx{j}"], (i + 1) * 16)
                        pe.wait_ge(s["copied"], i * 6 + (3 * j + 3))
                        for t in range(TILES):
                            mm = pe.matmul(pv[:, 0:SEQ], cn[j][:, t, :], pt[:, t, :], start=(t == 0), stop=(t == TILES - 1))
                        mm.then_inc(s["pv"], 1)
                        wait(pe, s, m, "diag", "pv_copied")
                        pe.matmul(pv[:, 64:64 + SEQ], ones[0:SEQ, :], dg[:], start=True, stop=True).then_inc(s["spread"], 1)
                        wait(pe, s, m, "own")
                        apart(pe)
                        pe.transpose(mi[0:1, 64:64 + SEQ], own[:], ident[0:SEQ, 0:SEQ]).then_inc(s["own_row"], 1)
                        wait(pe, s, m, "own_norm")
                        pe.matmul(mi[:, 128:128 + SEQ], ones[0:1, :], row[:], start=True, stop=True).then_inc(s["own_bc"], 1)
                    wait(pe, s, i + 1, "prod2")
                    for k in range(4):
                        mm = pe.matmul(out[0:PT, 0:D], feat[:, k, :], wl[:, k, :], start=(k == 0), stop=(k == 3))
                    mm.then_inc(s["out_ready"], 1)

            @block.scalar
            def _(act):
                act.wait_ge(s["loaded"], 64)
                with act.Fori(0, PAIRS) as i:
                    act.wait_ge(s["done"], i)
                    act.activation(feat[:, 0, :], h_t[:, bass.ts(i, PT)], ACT.Copy).then_inc(s["cs"], 1)
                    act.activation(cq[:], h_t[:, bass.ts(i, PT)], ACT.Identity, scale=cols[:, 0:1], bias=cols[:, 2:3]).then_inc(s["cqw_ready"], 1)
                    for j in range(2):
                        m = i * 2 + (j + 1)
                        wait(act, s, m, "negmax")
                        act.activation(pr.rearrange("q (a b) -> q a b", a=3), sc[0:SEQ, :, 0:BANKC], ACT.Exp, bias=nm[:, 0:1], accum_out=l[:, 0:1])\
                            .then_inc(s["probs"], 1)
                        for b in range(3):
                            act.wait_ge(s["turned"], i * 6 + (3 * j + b + 1))
                            act.activation(pt[:, 4 * b:4 * b + 4, :], turn[0:TP, b % 2, 0:4 * SEQ].rearrange("p (t q) -> p t q", t=4), ACT.Copy)\
                                .then_inc(s["copied"], 1)
                        wait(act, s, m, "pv")
                        act.activation(pvs[:], pv[:, 0:SEQ], ACT.Copy).then_inc(s["pv_copied"], 1)
                        wait(act, s, m, "own_neg")
                        act.activation(row[:], mi[0:1, 64:64 + SEQ], ACT.Exp, bias=r1[:, 1:2], accum_out=r1[:, 2:3]).then_inc(s["own_exp"], 1)

            @block.vector
            def _(v):
                v.wait_ge(s["loaded"], 64)
                v.tensor_tensor(bsum[:], bias[:, 0:1], bias[:, 1:2], ALU.add).then_inc(s["biassum"], 1)
                v.wait_ge(s["biassum"], 1)
                v.tensor_tensor(bsum[:], bsum[:], bias[:, 2:3], ALU.add).then_inc(s["biassum2"], 1)
                v.wait_ge(s["biassum2"], 1)
                with v.Fori(0, PAIRS) as i:
                    for j in range(2):
                        m = i * 2 + (j + 1)
                        oc = slice(j * SEQ, (j + 1) * SEQ)
                        wait(v, s, m, "scores")
                        v.tensor_reduce(mx[:], sc[0:SEQ, :, 0:BANKC], AX.XY, ALU.max).then_inc(s["rowmax"], 1)
                        wait(v, s, m, "rowmax", "c_w")
                        v.tensor_scalar(nm[:], mx[:], -1.0, None, ALU.mult).then_inc(s["negmax"], 1)
                        v.scalar_tensor_tensor(own[:], mx[:], bsum[:, 0:1], out[0:SEQ, 128:129], ALU.add, ALU.add).then_inc(s["own"], 1)
                        v.wait_ge(s[f"ctxt{j}"], (i + 1) * 16)
                        v.tensor_reduce(csum[:, bass.ds(i * 2 + j, 1)], ct[j][:], AX.X, ALU.add).then_inc(s["summed"], 1)
                        wait(v, s, m, "probs")
                        v.reciprocal(il[:], l[:]).then_inc(s["inverse"], 1)
                        wait(v, s, m, "inverse")
                        v.tensor_scalar(dg[:], ident[0:SEQ, 0:SEQ], il[:, 0:1], None, ALU.mult).then_inc(s["diag"], 1)
                        wait(v, s, m, "spread", "pv_copied")
                        v.tensor_tensor(feat[:, 1, oc], pvs[:], pv[:, 64:64 + SEQ], ALU.mult).then_inc(s["c2q"], 1)
                        wait(v, s, m, "own_row")
                        v.tensor_reduce(r1[:, 0:1], mi[0:1, 64:64 + SEQ], AX.X, ALU.max).then_inc(s["own_max"], 1)
                        wait(v, s, m, "own_max")
                        v.tensor_scalar(r1[:, 1:2], r1[:, 0:1], -1.0, None, ALU.mult).then_inc(s["own_neg"], 1)
                        wait(v, s, m, "own_exp")
                        v.reciprocal(r1[:, 3:4], r1[:, 2:3]).then_inc(s["own_inv"], 1)
                        wait(v, s, m, "own_inv")
                        v.tensor_scalar(row[:], row[:], r1[:, 3:4], None, ALU.mult).then_inc(s["own_norm"], 1)
                        wait(v, s, m, "own_bc", "c2q")
                        v.tensor_tensor(wc[:], feat[:, 0, oc], mi[:, 128:128 + SEQ], ALU.mult).then_inc(s["weighted"], 1)
                        wait(v, s, m, "weighted")
                        v.tensor_reduce(q2c[:], wc[:], AX.X, ALU.add).then_inc(s["q2c"], 1)
                        v.tensor_tensor(feat[:, 2, oc], feat[:, 0, oc], feat[:, 1, oc], ALU.mult).then_inc(s["prod1"], 1)
                        wait(v, s, m, "q2c", "prod1")
                        last = v.tensor_scalar(feat[:, 3, oc], feat[:, 0, oc], q2c[:, 0:1], None, ALU.mult)
                        if j:
                            last.then_inc(s["prod2"], 1)
                    wait(v, s, i + 1, "out_ready")
                    v.tensor_tensor(acc[:], out[0:PT, 0:D], bl[:], ALU.add).then_inc(s["out_sum"], 1)
                    wait(v, s, i + 1, "out_sum")
                    v.tensor_tensor(x[:, i, :], acc[:], x[:, i, :], ALU.add).then_inc(s["done"], 1)



HEAD_AT = [2 * (k % 8) + k // 8 for k in range(16)]


def l3_attention(nc, g, a):
    normalise(nc, g, "n9", [("layer", 1e-5), ("rms", 1e-6)], a["L3_scale"])
    ident, x, h_t = g["ident"], g["x"], g["h_t"]
    names = ("loaded staged_h qk qk_copied v_ready v_copied scores masked rowmax shifted probs rowsum inverse turned "
             "pt_act pt_vec pv o_ready o_turned o_copied out_ready out_sum done")
    R, BLOCKS = PT, 8
    with stage(nc, "a3", names) as (s, sb, ps):
        w = sb("w", [D, 3 * 1024]); wo = sb("wo", [D, BLOCKS, D]); mk = sb("mask", [R, R]); bo = sb("bo", [R, D])
        hs = sb("hs", [D, R]); qk = sb("qk", [D, 16, R]); vs = sb("vs", [R, 1024])
        pr = sb("pr", [R, HEADS, R]); pt = sb("pt", [R, HEADS, R]); on = sb("on", [R, 1024]); ot = sb("ot", [D, BLOCKS, R]); acc = sb("acc", [R, D])
        mx = sb("mx", [R, HEADS]); ls = sb("ls", [R, HEADS]); rl = sb("rl", [R, HEADS])
        scores = ps("scores", [D, 4, 512]); pv = ps("pv", [D, 2, 512]); mi = ps("mi", [D, 2, 512])
        with nc.Block() as block:
            @block.sync
            def _(sp):
                for dst, drm in ((w[:], a["L3_wqkv"]), (wo[:], a["L3_wout"]), (mk[:], g["consts"]["batch_mask"]),
                                 (bo[:], bc(a["L3_bout"], [R, D]))):
                    sp.dma_start(dst, drm).then_inc(s["loaded"], 16)

            @block.tensor
            def _(pe):
                pe.wait_ge(s["loaded"], 64)
                with pe.Fori(0, PAIRS) as i:
                    n = i + 1
                    wait(pe, s, n, "staged_h")
                    for b in range(16):
                        mm = pe.matmul(scores[:, b // 4, (b % 4) * R:(b % 4 + 1) * R], w[:, b * D:(b + 1) * D], hs[:], start=True, stop=True)
                    mm.then_inc(s["qk"], 1)
                    for b in range(2):
                        mm = pe.matmul(pv[0:R, b, :], hs[:], w[:, 2048 + b * 512:2560 + b * 512], start=True, stop=True)
                    mm.then_inc(s["v_ready"], 1)
                    wait(pe, s, n, "qk_copied")
                    for k in range(HEADS):
                        half = slice(64 * (k // 8), 64 * (k // 8) + 64)
                        mm = pe.matmul(scores[0:R, k // 4, (k % 4) * R:(k % 4 + 1) * R], qk[half, k % 8, :], qk[half, 8 + k % 8, :],
                                       start=True, stop=True)
                    mm.then_inc(s["scores"], 1)
                    wait(pe, s, n, "masked")
                    turn_probs(pe, s, n, R, scores, pr, ident)
                    wait(pe, s, n, "pt_act", "pt_vec", "v_copied")
                    for k in range(HEADS):
                        h = HEAD_AT[k]
                        mm = pe.matmul(pv[0:R, k // 8, (k % 8) * 64:(k % 8 + 1) * 64], pt[:, k, :], vs[:, 64 * h:64 * h + 64], start=True, stop=True)
                    mm.then_inc(s["pv"], 1)
                    wait(pe, s, n, "o_ready")
                    for b in range(BLOCKS):
                        mm = pe.transpose(mi[:, b // 4, (b % 4) * R:(b % 4 + 1) * R], on[:, b * D:(b + 1) * D], ident[0:R, 0:R])
                    mm.then_inc(s["o_turned"], 1)
                    wait(pe, s, n, "o_copied")
                    for b in range(BLOCKS):
                        mm = pe.matmul(pv[0:R, 0, 0:D], ot[:, b, :], wo[:, b, :], start=(b == 0), stop=(b == BLOCKS - 1))
                    mm.then_inc(s["out_ready"], 1)

            @block.scalar
            def _(act):
                with act.Fori(0, PAIRS) as i:
                    n = i + 1
                    act.wait_ge(s["done"], i)
                    act.activation(hs[:], h_t[:, bass.ts(i, PT)], ACT.Copy).then_inc(s["staged_h"], 1)
                    wait(act, s, n, "qk")
                    act.activation(qk[:, 0:8, :].rearrange("d (a b) t -> d a (b t)", a=2), scores[:, 0:2, 0:4 * R], ACT.Copy, scale=64 ** -0.5)
                    act.activation(qk[:, 8:16, :].rearrange("d (a b) t -> d a (b t)", a=2), scores[:, 2:4, 0:4 * R], ACT.Copy)\
                        .then_inc(s["qk_copied"], 1)
                    wait(act, s, n, "v_ready")
                    act.activation(vs.rearrange("t (a b) -> t a b", a=2), pv[0:R, :, :], ACT.Copy).then_inc(s["v_copied"], 1)
                    wait(act, s, n, "shifted")
                    act.activation(pr[:], pr[:], ACT.Exp).then_inc(s["probs"], 1)
                    wait(act, s, n, "turned")
                    act.activation(pt[:, 0:8, :].rearrange("k (a b) q -> k a (b q)", a=2), scores[0:R, 0:2, 0:4 * R], ACT.Copy)\
                        .then_inc(s["pt_act"], 1)
                    wait(act, s, n, "o_turned")
                    act.activation(ot.rearrange("d (a b) t -> d a (b t)", a=2), mi[:, :, 0:4 * R], ACT.Copy).then_inc(s["o_copied"], 1)

            @block.vector
            def _(v):
                v.wait_ge(s["loaded"], 64)
                with v.Fori(0, PAIRS) as i:
                    n = i + 1
                    softmax_vector(v, s, n, R, scores, mk, pr[:], mx[:], ls[:], rl[:])
                    wait(v, s, n, "turned")
                    v.tensor_copy(pt[:, 8:16, :].rearrange("k (a b) q -> k a (b q)", a=2), scores[0:R, 2:4, 0:4 * R])\
                        .then_inc(s["pt_vec"], 1)
                    wait(v, s, n, "pv", "inverse")
                    v.tensor_tensor(on.rearrange("q (h e) -> q h e", h=HEADS), pv[0:R, :, :].rearrange("q a (h e) -> q (a h) e", e=64),
                                    bc(rl[:, :, None], [R, HEADS, 64]), ALU.mult).then_inc(s["o_ready"], 1)
                    wait(v, s, n, "out_ready")
                    v.tensor_tensor(acc[:], pv[0:R, 0, 0:D], bo[:], ALU.add).then_inc(s["out_sum"], 1)
                    wait(v, s, n, "out_sum")
                    v.tensor_tensor(x[:, i, :], acc[:], x[:, i, :], ALU.add).then_inc(s["done"], 1)



def l3_cross(nc, g, a):
    normalise(nc, g, "n10", [("layer", 1e-5)])
    x, h_t, csum = g["x"], g["h_t"], g["ctx_sum"]
    with stage(nc, "c3", "loaded spread part biased added") as (s, sb, ps):
        w = sb("w", [D, 2, D]); b = sb("b", [PT, D]); cs = sb("cs", [D, BATCH, SEQ]); y = sb("y", [PT, PAIRS, D])
        acc = ps("acc", [D, 4, 512])
        with nc.Block() as block:
            @block.sync
            def _(sp):
                sp.dma_start(w[:], a["L3_x_w"]).then_inc(s["loaded"], 16)
                sp.dma_start(b[:], bc(a["L3_x_b"], [PT, D])).then_inc(s["loaded"], 16)

            @block.scalar
            def _(act):
                act.activation(cs[:], bc(csum[:, :, None], [D, BATCH, SEQ]), ACT.Copy, scale=1.0 / CTX).then_inc(s["spread"], 1)

            @block.tensor
            def _(pe):
                pe.wait_ge(s["loaded"], 32)
                pe.wait_ge(s["spread"], 1)
                for t in range(PAIRS):
                    dst = acc[0:PT, t // 4, (t % 4) * D:(t % 4 + 1) * D]
                    pe.matmul(dst, h_t[:, t * PT:(t + 1) * PT], w[:, 0, :], start=True, stop=False)
                    mm = pe.matmul(dst, cs[:, 2 * t:2 * t + 2, :], w[:, 1, :], start=False, stop=True)
                mm.then_inc(s["part"], 1)

            @block.vector
            def _(v):
                v.wait_ge(s["loaded"], 32)
                v.wait_ge(s["part"], 1)
                v.tensor_tensor(y.rearrange("t (a c) d -> t a c d", a=4), acc[0:PT, :, :].rearrange("t a (c d) -> t a c d", d=D),
                                bc(b[:, None, None, :], [PT, 4, 4, D]), ALU.add).then_inc(s["biased"], 1)
                v.wait_ge(s["biased"], 1)
                v.tensor_tensor(x[:], x[:], y[:], ALU.add).then_inc(s["added"], 1)


def l3_ffn(nc, g, a):
    normalise(nc, g, "n11", [("layer", 1e-5)])
    x, h_t = g["x"], g["h_t"]
    with stage(nc, "f3", "loaded inner relu outer biased done") as (s, sb, ps):
        w1 = sb("w1", [D, 256]); b1 = sb("b1", [D, 2]); w2 = sb("w2", [D, 2, D]); b2 = sb("b2", [PT, D])
        re = sb("relu", [D, 2, 2, GT]); y = sb("y", [PT, 2, GROUP * D])
        inner = ps("inner", [D, 2, 2, 512]); outer = ps("outer", [D, 2, 512])
        with nc.Block() as block:
            @block.sync
            def _(sp):
                for dst, drm in ((w1[:], a["L3_ffn_w1"]), (b1[:], a["L3_ffn_b1"]), (w2[:], a["L3_ffn_w2"]), (b2[:], bc(a["L3_ffn_b2"], [PT, D]))):
                    sp.dma_start(dst, drm).then_inc(s["loaded"], 16)

            @block.tensor
            def _(pe):
                pe.wait_ge(s["loaded"], 64)

                def second(c):
                    pe.wait_ge(s["relu"], 2 * (c + 1))
                    if c >= 2:
                        pe.wait_ge(s["biased"], c - 1)
                    for t in range(GROUP):
                        for f in range(2):
                            mm = pe.matmul(outer[0:PT, c % 2, t * D:(t + 1) * D], re[:, c % 2, f, t * PT:(t + 1) * PT], w2[:, f, :],
                                           start=(f == 0), stop=(f == 1))
                    mm.then_inc(s["outer"], 1)

                for c in range(4):
                    if c >= 2:
                        pe.wait_ge(s["relu"], 2 * (c - 1))
                    for f in range(2):
                        pe.matmul(inner[:, c % 2, f, 0:GT], w1[:, f * D:(f + 1) * D], h_t[:, c * GT:(c + 1) * GT], start=True, stop=True)\
                            .then_inc(s["inner"], 1)
                    if c:
                        second(c - 1)
                second(3)

            @block.scalar
            def _(act):
                act.wait_ge(s["loaded"], 64)
                for c in range(4):
                    if c >= 2:
                        act.wait_ge(s["outer"], c - 1)
                    for f in range(2):
                        act.wait_ge(s["inner"], 2 * c + f + 1)
                        act.activation(re[:, c % 2, f, :], inner[:, c % 2, f, 0:GT], ACT.Relu, bias=b1[:, f:f + 1]).then_inc(s["relu"], 1)

            @block.vector
            def _(v):
                v.wait_ge(s["loaded"], 64)
                for c in range(4):
                    v.wait_ge(s["outer"], c + 1)
                    if c >= 2:
                        v.wait_ge(s["done"], c - 1)
                    v.tensor_tensor(y[:, c % 2, :].rearrange("t (a d) -> t a d", d=D), outer[0:PT, c % 2, :].rearrange("t (a d) -> t a d", d=D),
                                    bc(b2[:, None, :], [PT, GROUP, D]), ALU.add).then_inc(s["biased"], 1)
                    v.wait_ge(s["biased"], c + 1)
                    v.tensor_tensor(x[:, c * GROUP:(c + 1) * GROUP, :], x[:, c * GROUP:(c + 1) * GROUP, :],
                                    y[:, c % 2, :].rearrange("t (a d) -> t a d", d=D), ALU.add).then_inc(s["done"], 1)



def l2_ffn(nc, g, a):
    ident, x, h_n, h_t, C = g["ident"], g["x"], g["h_n"], g["h_t"], g["consts"]
    with ExitStack() as es:
        base = es.enter_context(nc.sbuf_tensor("m2_base", [PT, PAIRS, D], F32))
        normalise(nc, g, "n8a", [("layer", 1e-5)])
        with stage(nc, "m2keep", "kept") as (s, _, _):
            with nc.Block() as block:
                @block.vector
                def _(v):
                    v.tensor_copy(base[:], x[:]).then_inc(s["kept"], 1)
                    v.wait_ge(s["kept"], 1)
                    v.tensor_copy(x[:], h_n[:])
        normalise(nc, g, "n8b", [("layer", 1e-5)], a["L2_ln1_weight"], a["L2_ln1_bias"])
        narrow_attention(nc, g, "a2", D, SEQ // 4, SequenceTokens, C["sequence_mask"], 8 ** -0.5, a["L2_qkv"], a["L2_proj"],
                         order=SequenceTokens.part)
        normalise(nc, g, "n8c", [("layer", 1e-5)], a["L2_ln2_weight"], a["L2_ln2_bias"])
        names = ("loaded staged shifted gates gate_sum gate_inv first_gone weighed weight inner gelu outer added done "
                 "r_logits g_max p_max p_best p_order p_first p_picked q_max q_best q_order q_first q_picked both normal")
        with stage(nc, "m2", names) as (s, sb, ps):
            wr = sb("router", [D, EXPERTS]); w1 = sb("w1", [D, EXPERTS, 256]); w2 = sb("w2", [D, EXPERTS, 2, D]); early = sb("earlier", [D, EXPERTS])
            hs = sb("hs", [D, GT]); ge = sb("gelu", [D, 2, 2, GT]); top = sb("top", [PT, GROUP])
            e3 = [PT, GROUP, EXPERTS]
            gt = sb("gates", e3); rest = sb("rest", e3); rank = sb("rank", e3); p1 = sb("p1", e3); p2 = sb("p2", e3)
            y = sb("y", [PT, GROUP, D])
            small = ps("small", [D, 512]); inner = ps("inner", [D, 4, 512]); outer = ps("outer", [D, 2, 512])
            with nc.Block() as block:
                @block.sync
                def _(sp):
                    for dst, drm in ((wr[:], a["L2_router"]), (w1[:], a["L2_moe_w1"]), (w2[:], a["L2_moe_w2"]), (early[:], C["earlier"])):
                        sp.dma_start(dst, drm).then_inc(s["loaded"], 16)

                @block.tensor
                def _(pe):
                    pe.wait_ge(s["loaded"], 64)
                    with pe.Fori(0, 4) as c:
                        wait(pe, s, c + 1, "staged")
                        for t in range(GROUP):
                            mm = pe.matmul(small[0:PT, t * EXPERTS:(t + 1) * EXPERTS], hs[:, t * PT:(t + 1) * PT], wr[:], start=True, stop=True)
                        mm.then_inc(s["r_logits"], 1)

                        def second(e):
                            pe.wait_ge(s["gelu"], c * EXPERTS + (e + 1))
                            if e >= 2:
                                pe.wait_ge(s["added"], c * EXPERTS + (e - 1))
                            for t in range(GROUP):
                                for f in range(2):
                                    mm = pe.matmul(outer[0:PT, e % 2, t * D:(t + 1) * D], ge[:, e % 2, f, t * PT:(t + 1) * PT], w2[:, e, f, :],
                                                   start=(f == 0), stop=(f == 1))
                            mm.then_inc(s["outer"], 1)

                        for e in range(EXPERTS):
                            if e >= 2:
                                pe.wait_ge(s["gelu"], c * EXPERTS + (e - 1))
                            for f in range(2):
                                mm = pe.matmul(inner[:, 2 * (e % 2) + f, 0:GT], w1[:, e, f * D:(f + 1) * D], hs[:], start=True, stop=True)
                            mm.then_inc(s["inner"], 1)
                            if e:
                                second(e - 1)
                        second(EXPERTS - 1)

                @block.scalar
                def _(act):
                    with act.Fori(0, 4) as c:
                        n = c + 1
                        act.wait_ge(s["done"], c)
                        act.activation(hs[:], h_t[:, bass.ts(c, GT)], ACT.Copy).then_inc(s["staged"], 1)
                        wait(act, s, n, "shifted")
                        act.activation(gt[:], gt[:], ACT.Exp).then_inc(s["gates"], 1)
                        for e in range(EXPERTS):
                            act.wait_ge(s["inner"], c * EXPERTS + (e + 1))
                            if e >= 2:
                                act.wait_ge(s["outer"], c * EXPERTS + (e - 1))
                            act.activation(ge[:, e % 2, :, :], inner[:, 2 * (e % 2):2 * (e % 2) + 2, 0:GT], ACT.Gelu_apprx_tanh)\
                                .then_inc(s["gelu"], 1)

                @block.vector
                def _(v):
                    v.wait_ge(s["loaded"], 64)
                    with v.Fori(0, 4) as c:
                        n = c + 1
                        wait(v, s, n, "r_logits")
                        logits = small[0:PT, 0:GROUP * EXPERTS].rearrange("t (a e) -> t a e", e=EXPERTS)
                        v.tensor_reduce(top[:], logits, AX.X, ALU.max).then_inc(s["g_max"], 1)
                        wait(v, s, n, "g_max")
                        v.tensor_tensor(gt[:], logits, bc(top[:, :, None], e3), ALU.subtract).then_inc(s["shifted"], 1)
                        wait(v, s, n, "gates")
                        v.tensor_reduce(top[:], gt[:], AX.X, ALU.add).then_inc(s["gate_sum"], 1)
                        wait(v, s, n, "gate_sum")
                        v.reciprocal(top[:], top[:]).then_inc(s["gate_inv"], 1)
                        wait(v, s, n, "gate_inv")
                        v.tensor_tensor(gt[:], gt[:], bc(top[:, :, None], e3), ALU.mult).then_inc(s["normal"], 1)
                        wait(v, s, n, "normal")
                        argmax_vector(v, s, n, "p", gt[:], top[:], rank[:], early, p1[:])
                        wait(v, s, n, "p_picked")
                        v.scalar_tensor_tensor(rest[:], p1[:], -4.0, gt[:], ALU.mult, ALU.add).then_inc(s["first_gone"], 1)
                        wait(v, s, n, "first_gone")
                        argmax_vector(v, s, n, "q", rest[:], top[:], rank[:], early, p2[:])
                        wait(v, s, n, "q_picked")
                        v.tensor_tensor(p1[:], p1[:], p2[:], ALU.add).then_inc(s["both"], 1)
                        wait(v, s, n, "both")
                        v.tensor_tensor(gt[:], gt[:], p1[:], ALU.mult).then_inc(s["weight"], 1)
                        wait(v, s, n, "weight")
                        for e in range(EXPERTS):
                            v.wait_ge(s["outer"], c * EXPERTS + (e + 1))
                            for t in range(GROUP):
                                part = outer[0:PT, e % 2, t * D:(t + 1) * D]
                                if e == 0:
                                    last = v.tensor_scalar(y[:, t, :], part, gt[:, t, e:e + 1], None, ALU.mult)
                                else:
                                    if t == 0:
                                        v.wait_ge(s["added"], c * EXPERTS + e)
                                    last = v.scalar_tensor_tensor(y[:, t, :], part, gt[:, t, e:e + 1], y[:, t, :], ALU.mult, ALU.add)
                            last.then_inc(s["added"], 1)
                        v.wait_ge(s["added"], n * EXPERTS)
                        v.tensor_tensor(y[:], y[:], base[:, bass.ts(c, GROUP), :], ALU.add).then_inc(s["weighed"], 1)
                        wait(v, s, n, "weighed")
                        v.tensor_tensor(x[:, bass.ts(c, GROUP), :], x[:, bass.ts(c, GROUP), :], y[:], ALU.add).then_inc(s["done"], 1)



PARTS = [l0_attention, l0_cross, l0_ffn, l1_attention, l1_cross, l1_ffn, l2_attention, l2_cross, l2_ffn, l3_attention, l3_cross, l3_ffn]


def laid_out(v):
    col = lambda name: v[name].reshape(-1, 1)
    kb = lambda w: w.reshape(-1, 128, w.shape[-1]).transpose(1, 0, 2)
    r = {}
    r["x"] = v["x"].reshape(TOK, D)
    c = v["ctx_1024"].reshape(BATCH, TP, TILES, D)
    r["ctx"] = c
    r["ctx_t"] = c.transpose(0, 3, 2, 1).reshape(BATCH, D, CTX)
    r["ctx_mask"] = v["mask_Bx1x1xS2_ff0"].reshape(BATCH, TP, TILES).transpose(0, 2, 1).reshape(BATCH, 1, CTX)
    r["L0_attn_in_proj_weight"] = v["L0_attn_in_proj_weight"].T
    r["L0_attn_out_proj_weight"] = v["L0_attn_out_proj_weight"].T
    for k in ("L0_xattn_ln_m_w", "L0_xattn_ln_m_b", "L0_xattn_ln_l_w", "L0_xattn_ln_l_b"):
        r[k] = col(k)
    r["L0_xattn_wq_t"] = v["L0_xattn_Wq"].reshape(D, 8, 64).transpose(2, 1, 0)
    r["L0_xattn_wk_t"] = v["L0_xattn_Wkv"][:, :512].reshape(D, 8, 64).transpose(2, 1, 0)
    r["L0_xattn_wv"] = v["L0_xattn_Wkv"][:, 512:]
    r["L0_xattn_wout"] = kb(v["L0_xattn_Wout"])
    r["L0_ffn_router"] = v["L0_ffn_Wr"].T
    r["L0_ffn_w1"] = v["L0_ffn_W1"].transpose(1, 0, 2)
    r["L0_ffn_b1"] = v["L0_ffn_b1"]
    r["L0_ffn_wo"] = kb(v["L0_ffn_Wo"])
    r["L0_ffn_rows"] = np.stack([v["L0_ffn_bo"], v["L0_ffn_gamma"], v["L0_ffn_beta"]])
    for k in "xwkvrg":
        r[f"L1_maa_{k}"] = col(f"L1_attn_time_maa_{k}")
    r["L1_maa_w1"] = v["L1_attn_time_maa_w1"]
    r["L1_maa_w2"] = v["L1_attn_time_maa_w2"].transpose(1, 0, 2)
    r["L1_decay"] = col("L1_attn_time_decay")
    r["L1_decay_w1"] = v["L1_attn_time_decay_w1"]
    r["L1_decay_w2"] = v["L1_attn_time_decay_w2"]
    r["L1_bonus"] = v["L1_attn_time_faaaa"].reshape(D, 1)
    r["L1_w"] = np.stack([v[f"L1_attn_W{k}"] for k in "rkvgo"], 1)
    r["L1_ln_w"], r["L1_ln_b"] = col("L1_attn_ln_w"), col("L1_attn_ln_b")
    r["L1_xattn_wq"], r["L1_xattn_wkv"], r["L1_xattn_wp"] = v["L1_xattn_Wq"], v["L1_xattn_Wkv"], v["L1_xattn_Wp"]
    r["L1_xattn_bq"] = col("L1_xattn_bq")
    r["L1_xattn_bk"] = v["L1_xattn_bkv"][:D].reshape(D, 1)
    r["L1_xattn_bv"] = v["L1_xattn_bkv"][D:].reshape(D, 1)
    r["L1_xattn_bp"] = v["L1_xattn_bp"].reshape(1, D)
    r["L1_ffn_centroids"] = v["L1_ffn_centroids"].T
    r["L1_ffn_g"], r["L1_ffn_b"] = v["L1_ffn_ln_g"].T, v["L1_ffn_ln_b"].T
    r["L1_ffn_w1"] = v["L1_ffn_w1"].transpose(1, 0, 2)
    r["L1_ffn_b1"], r["L1_ffn_b2"] = v["L1_ffn_b1"], v["L1_ffn_b2"]
    r["L1_ffn_w2"] = v["L1_ffn_w2"].reshape(EXPERTS, 4, 128, D).transpose(2, 1, 0, 3)
    r["L2_dt"], r["L2_bdt"] = v["L2_attn_W_dt"].T, col("L2_attn_b_dt")
    r["L2_bc"] = np.stack([v["L2_attn_W_B"].T, v["L2_attn_W_C"].T], 1)
    r["L2_alog"], r["L2_d"] = v["L2_attn_A_log"], col("L2_attn_D")
    r["L2_x_cols"] = np.stack([v["L2_xattn_w_cq"], v["L2_xattn_w_c"], v["L2_xattn_w_q"]], 1)
    r["L2_x_bias"] = np.stack([v["L2_xattn_b_cq"], v["L2_xattn_b_c"], v["L2_xattn_b_q"]]).reshape(1, 3)
    r["L2_x_wl"] = kb(v["L2_xattn_W_l"].T)
    r["L2_x_bl"] = v["L2_xattn_b_l"].reshape(1, D)
    for k in ("ln1_weight", "ln1_bias", "ln2_weight", "ln2_bias"):
        r[f"L2_{k}"] = col(f"L2_ffn_{k}")
    w = v["L2_ffn_qkv_weight"]
    rep = lambda m: np.repeat(m.reshape(4, 8, D), 4, axis=0).reshape(D, D)
    r["L2_qkv"] = np.concatenate([w[:128], rep(w[128:160]), rep(w[160:192])]).T
    r["L2_proj"] = v["L2_ffn_proj_weight"].T
    r["L2_router"] = v["L2_ffn_router_weight"].T
    r["L2_moe_w1"] = v["L2_ffn_moe_w1"].transpose(1, 0, 2)
    r["L2_moe_w2"] = v["L2_ffn_moe_w2"].reshape(EXPERTS, 2, 128, D).transpose(2, 0, 1, 3)
    r["L3_scale"] = col("L3_attn_norm_scale")
    r["L3_wqkv"] = np.concatenate([v[f"L3_attn_w{k}"].reshape(D, 1024) for k in "qkv"], 1)
    r["L3_wout"] = kb(v["L3_attn_w_out"][HEAD_AT].reshape(1024, D))
    r["L3_bout"] = v["L3_attn_b_out"].reshape(1, D)
    r["L3_x_w"] = np.stack([v["L3_xattn_W"][:, :D].T, v["L3_xattn_W"][:, D:].T], 1)
    r["L3_x_b"] = v["L3_xattn_b"].reshape(1, D)
    r["L3_ffn_w1"] = v["L3_ffn_W1"][1]
    r["L3_ffn_b1"] = v["L3_ffn_b1"][1].reshape(2, 128).T
    r["L3_ffn_w2"] = kb(v["L3_ffn_W2"][1])
    r["L3_ffn_b2"] = v["L3_ffn_b2"][1].reshape(1, D)
    return r


def build(nc, a, out, consts):
    with ExitStack() as es:
        def sb(label, shape):
            return es.enter_context(nc.sbuf_tensor(label, shape, F32))

        g = {"x": sb("x_sb", [PT, PAIRS, D]), "h_n": sb("h_n", [PT, PAIRS, D]), "h_t": sb("h_t", [D, TOK]),
             "sq": sb("sq", [PT, PAIRS, D]), "ident": sb("ident", [D, D]), "half": sb("half", [D, 16]),
             "ones": sb("ones", [D, D]), "ctx_sum": sb("ctx_sum", [D, BATCH]), "headmask": consts["headmask"],
             "consts": consts}
        with stage(nc, "start", "x_in const_in") as (s, _, _):
            with nc.Block() as block:
                @block.sync
                def _(sp):
                    sp.dma_start(g["x"][:], a["x"].rearrange("(n p) d -> p n d", p=PT)).then_inc(s["x_in"], 16)
                    sp.dma_start(g["ident"][:], consts["ident"]).then_inc(s["x_in"], 16)
                    sp.wait_ge(s["x_in"], 32)

                @block.vector
                def _(v):
                    v.memset(g["half"][:], -0.5)
                    v.memset(g["ones"][:], 1.0).then_inc(s["const_in"], 1)
                    v.wait_ge(s["const_in"], 1)
        for part in PARTS:
            part(nc, g, a)
        with stage(nc, "end", "stored") as (s, _, _):
            with nc.Block() as block:
                @block.sync
                def _(sp):
                    sp.dma_start(out.rearrange("(n p) d -> p n d", p=PT), g["x"][:]).then_inc(s["stored"], 16)
                    sp.wait_ge(s["stored"], 16)


def shape_constants():
    f = np.float32
    p = np.arange(PT)
    same = p[:, None] // SEQ == p[None, :] // SEQ
    q, t = np.arange(D)[:, None], np.arange(D)[None, :]
    src, dst = (p % SEQ)[:, None], (p % SEQ)[None, :]
    levels = [same & (src // (2 * m) == dst // (2 * m)) & (src // m < dst // m) for m in HALVES] + [same & (src == dst)]
    pick = np.zeros((EXPERTS, EXPERTS, D), f)
    for e in range(EXPERTS):
        pick[e, e] = 1
    return {
        "ident": np.eye(D, dtype=f),
        "headmask": (np.arange(D)[:, None] // 8 == np.arange(HEADS)[None, :]).astype(f),
        "headmask4": (np.arange(D)[:, None] % 32 // 8 == np.arange(4)[None, :]).astype(f),
        "causal_mask": np.where(same & (p[:, None] >= p[None, :]), 0, NEG).astype(f),
        "batch_mask": np.where(same, 0, NEG).astype(f),
        "sequence_mask": np.where((q // BATCH == t // BATCH) & (q >= t), 0, NEG).astype(f),
        "level_mask": np.stack(levels, 1).astype(f),
        "pick": pick,
        "earlier": np.tile(np.arange(EXPERTS, 0, -1).astype(f), (D, 1)),
    }


HALVES = (1, 2, 4, 8, 16, 32)


def kernel(**inputs):
    from concourse import bacc
    from concourse.bass_utils import run_bass_kernel_spmd

    nc = bacc.Bacc("TRN2", target_bir_lowering=False, num_devices=1)
    arrays = laid_out({k: np.asarray(v) for k, v in inputs.items()})
    consts = shape_constants()
    named = {**{f"in_{k}": v for k, v in arrays.items()}, **{f"c_{k}": v for k, v in consts.items()}}
    named = {k: np.ascontiguousarray(v) for k, v in named.items()}
    aps = {k: nc.dram_tensor(k, v.shape, F32, kind="ExternalInput").ap() for k, v in named.items()}
    out = nc.dram_tensor("out", (TOK, D), F32, kind="ExternalOutput").ap()
    build(nc, {k[3:]: ap for k, ap in aps.items() if k.startswith("in_")}, out,
          {k[2:]: ap for k, ap in aps.items() if k.startswith("c_")})
    got = run_bass_kernel_spmd(nc, [named], core_ids=[0])
    return got.results[0]["out"].reshape(BATCH, SEQ, D)
```

```python
from contextlib import ExitStack, contextmanager

import numpy as np

import concourse.bass as bass
from concourse import mybir

F32 = mybir.dt.float32
ALU = mybir.AluOpType
ACT = mybir.ActivationFunctionType
AX = mybir.AxisListType

BATCH, SEQ, D = 32, 56, 128
PAIRS = BATCH // 2
PT = 2 * SEQ
TOK = BATCH * SEQ
GROUP = 4
GT = GROUP * PT
CTX, TILES = 1500, 12
TP = CTX // TILES
BANKC = 4 * TP
NEG = -1.0e30
EXPERTS = 8


@contextmanager
def stage(nc, name, sems):
    with ExitStack() as es:
        handles = [nc.alloc_semaphore(f"{name}_{s}") for s in sems.split()]
        s = dict(zip(sems.split(), handles))

        def sb(label, shape):
            return es.enter_context(nc.sbuf_tensor(f"{name}_{label}", shape, F32))

        def ps(label, shape):
            return es.enter_context(nc.psum_tensor(f"{name}_{label}", shape, F32))

        yield s, sb, ps
        nc.clear_and_free_semaphores(handles)
        nc.all_engine_barrier()


def bc(ap, shape):
    return ap.to_broadcast(shape)


def wait(eng, s, n, *names):
    for name in names:
        eng.wait_ge(s[name], n)


def apart(eng):
    eng.nop(nofuse=True)



def normalise(nc, g, name, rounds, gain=None, shift=None):
    x, h_n, h_t, sq, ident, half = g["x"], g["h_n"], g["h_t"], g["sq"], g["ident"], g["half"]
    full = [PT, PAIRS, D]
    with stage(nc, name, "loaded summed mean centred squared sumsq var rstd normed turned copied") as (s, sb, ps):
        sums, mean, ssq, var, rstd = (sb(f"s{k}", [PT, PAIRS]) for k in range(5))
        aff = sb("affine", [D, 2])
        turn = ps("turn", [D, 4, 512])
        with nc.Block() as block:
            @block.sync
            def _(sp):
                if gain is not None:
                    sp.dma_start(aff[:, 0:1], gain).then_inc(s["loaded"], 16)
                if shift is not None:
                    sp.dma_start(aff[:, 1:2], shift).then_inc(s["loaded"], 16)

            @block.vector
            def _(v):
                for k, (kind, eps) in enumerate(rounds):
                    src = x if k == 0 else h_n
                    n = k + 1
                    if k:
                        v.wait_ge(s["normed"], k)
                    if kind == "layer":
                        v.tensor_reduce(sums[:], src[:], AX.X, ALU.add).then_inc(s["summed"], 1)
                        v.wait_ge(s["summed"], n)
                        v.tensor_scalar(mean[:], sums[:], 1.0 / D, None, ALU.mult).then_inc(s["mean"], 1)
                        v.wait_ge(s["mean"], n)
                        v.tensor_tensor(h_n[:], src[:], bc(mean[:, :, None], full), ALU.subtract).then_inc(s["centred"], 1)
                        src = h_n
                    v.wait_ge(s["squared"], n)
                    v.tensor_reduce(ssq[:], sq[:], AX.X, ALU.add).then_inc(s["sumsq"], 1)
                    v.wait_ge(s["sumsq"], n)
                    v.tensor_scalar(var[:], ssq[:], 1.0 / D, eps, ALU.mult, ALU.add).then_inc(s["var"], 1)
                    v.wait_ge(s["rstd"], n)
                    v.tensor_tensor(h_n[:], src[:], bc(rstd[:, :, None], full), ALU.mult).then_inc(s["normed"], 1)

            @block.gpsimd
            def _(pool):
                for k in range(len(rounds)):
                    pool.wait_ge(s["var"], k + 1)
                    pool.tensor_tensor(rstd[:], var[:], half[0:PT, 0:PAIRS], ALU.pow).then_inc(s["rstd"], 1)

            @block.scalar
            def _(act):
                centred = 0
                for k, (kind, eps) in enumerate(rounds):
                    if kind == "layer":
                        centred += 1
                        act.wait_ge(s["centred"], centred)
                        src = h_n
                    else:
                        if k:
                            act.wait_ge(s["normed"], k)
                        src = x if k == 0 else h_n
                    act.activation(sq[:], src[:], ACT.Square).then_inc(s["squared"], 1)
                loads = (gain is not None) + (shift is not None)
                if loads:
                    act.wait_ge(s["loaded"], 16 * loads)
                for b in range(4):
                    act.wait_ge(s["turned"], b + 1)
                    act.activation(h_t[:, b * GT:(b + 1) * GT], turn[:, b, 0:GT], ACT.Identity,
                                   scale=aff[:, 0:1] if gain is not None else 1.0,
                                   bias=aff[:, 1:2] if shift is not None else 0.0).then_inc(s["copied"], 1)

            @block.tensor
            def _(pe):
                pe.wait_ge(s["normed"], len(rounds))
                for t in range(PAIRS):
                    mm = pe.transpose(turn[:, t // 4, (t % 4) * PT:(t % 4 + 1) * PT], h_n[:, t, :], ident[0:PT, 0:PT])
                    if t % 4 == 3:
                        mm.then_inc(s["turned"], 1)



HEADS = 16


class PairTokens:
    fixed = staticmethod(lambda buf: buf[:])
    part = staticmethod(lambda buf, i: buf[:, bass.ts(i, PT)])
    heads = staticmethod(lambda buf: buf[:])
    all_heads = staticmethod(lambda buf, i: bc(buf[:, bass.ts(i, PT)][:, None, :], [D, HEADS, PT]))
    mask = staticmethod(lambda hm: bc(hm[:, :, None], [D, HEADS, PT]))


class SequenceTokens:
    fixed = staticmethod(lambda buf: buf.rearrange("d (b t) -> d b t", t=BATCH))
    part = staticmethod(lambda buf, i: buf.rearrange("d (t b) -> d b t", t=BATCH)[:, bass.ts(i, 4), :])
    heads = staticmethod(lambda buf: buf.rearrange("d h (b t) -> d h b t", t=BATCH))
    all_heads = staticmethod(lambda buf, i: bc(SequenceTokens.part(buf, i)[:, None, :, :], [D, HEADS, 4, BATCH]))
    mask = staticmethod(lambda hm: bc(hm[:, :, None, None], [D, HEADS, 4, BATCH]))


def walk(eng, count, body):
    body(0, 0)
    body(1, 1)
    with eng.Fori(1, count // 2 - 1) as q:
        body(q * 2, 0)
        body(q * 2 + 1, 1)
    body(count - 2, 0)
    body(count - 1, 1)


def early(i, n):
    return isinstance(i, int) and i < n


def narrow_attention(nc, g, name, R, count, src, mask, scale, wqkv, wo_add, order=None):
    ident, h_t, x = g["ident"], g["h_t"], g["x"]
    names = ("loaded cleared projected evacuated staged_q staged_k staged_h v_ready v_copied scores masked rowmax shifted "
             "probs turned pt_act pt_vec pv inverse o_ready o_turned o_copied out_ready done out2 added")
    E = 9
    with stage(nc, name, names) as (s, sb, ps):
        w = sb("w", [D, 3 * D]); wo = sb("wo", [D, D]); mk = sb("mask", [R, R]); hm = sb("hm", [D, HEADS])
        q_t = sb("q_t", [D, TOK]); k_t = sb("k_t", [D, TOK])
        qs, hs = ([sb(f"{n}{p}", [D, R]) for p in range(2)] for n in ("qs", "hs"))
        kb = [sb(f"kb{p}", [D, HEADS, R]) for p in range(2)]; vs = [sb(f"vs{p}", [R, HEADS, E]) for p in range(2)]
        pr = [sb(f"pr{p}", [R, HEADS, R]) for p in range(2)]; pt = sb("pt", [R, HEADS, R]); on = sb("on", [R, D]); ot = sb("ot", [D, R])
        mx = sb("mx", [R, HEADS]); rl = sb("rl", [R, HEADS])
        o_t = sb("o_t", [D, TOK]) if order else None
        scores = ps("scores", [D, 4, 512]); turn = ps("turn", [D, 2, 512]); pv = ps("pv", [D, 512]); mi = ps("mi", [D, 512])
        last = count - 1
        is_last = lambda i: isinstance(i, int) and i == last
        with nc.Block() as block:
            @block.sync
            def _(sp):
                for dst, drm in ((w[:], wqkv), (wo[:], wo_add), (mk[:], mask), (hm[:], g["headmask"])):
                    sp.dma_start(dst, drm).then_inc(s["loaded"], 16)

            @block.tensor
            def _(pe):
                pe.wait_ge(s["loaded"], 64)
                for m in range(2):
                    for b in range(4):
                        if m:
                            pe.wait_ge(s["evacuated"], b + 1)
                        pe.matmul(scores[:, b, 0:GT], w[:, m * D:(m + 1) * D], h_t[:, b * GT:(b + 1) * GT],
                                  start=True, stop=True).then_inc(s["projected"], 1)
                pe.wait_ge(s["evacuated"], 8)

                def score(i, p, b):
                    if b == 0:
                        pe.wait_ge(s["staged_q"], i + 1)
                        pe.wait_ge(s["staged_k"], i + 1)
                    mm = pe.matmul(scores[0:R, b, 0:4 * R], qs[p][:], kb[p][:, 4 * b:4 * b + 4, :], start=True, stop=True)
                    if b % 2:
                        mm.then_inc(s["scores"], 1)

                def values(i, p):
                    pe.wait_ge(s["staged_h"], i + 1)
                    if not early(i, 2):
                        pe.wait_ge(s["o_copied"], i - 1)
                    pe.matmul(mi[0:R, 0:D], hs[p][:], w[:, 2 * D:3 * D], start=True, stop=True).then_inc(s["v_ready"], 1)

                def turn_group(i, p, b):
                    if b % 2 == 0:
                        pe.wait_ge(s["probs"], i * 2 + (b // 2 + 1))
                    if b >= 2:
                        pe.wait_ge(s["pt_act" if b == 2 else "pt_vec"], i * 2 + 1)
                    apart(pe)
                    for k in range(4):
                        mm = pe.transpose(turn[0:R, b % 2, k * R:(k + 1) * R], pr[p][:, 4 * b + k, :], ident[0:R, 0:R])
                    mm.then_inc(s["turned"], 1)

                def turn_output(i):
                    wait(pe, s, i + 1, "o_ready")
                    if not is_last(i):
                        pe.wait_ge(s["v_copied"], i + 2)
                    apart(pe)
                    pe.transpose(mi[:, 256:256 + R], on[:], ident[0:R, 0:R]).then_inc(s["o_turned"], 1)

                def project(i):
                    wait(pe, s, i + 1, "o_copied")
                    pe.matmul(pv[0:R, 256:256 + D], ot[:], wo[:], start=True, stop=True).then_inc(s["out_ready"], 1)

                def body(i, p):
                    def next_score(b):
                        if not is_last(i):
                            score(i + 1, 1 - p, b)

                    turn_group(i, p, 0)
                    next_score(0)
                    turn_group(i, p, 1)
                    if not early(i, 1):
                        turn_output(i - 1)
                    next_score(1)
                    turn_group(i, p, 2)
                    next_score(2)
                    if not order and not early(i, 1):
                        project(i - 1)
                    turn_group(i, p, 3)
                    next_score(3)
                    if not is_last(i):
                        values(i + 1, 1 - p)
                    pe.wait_ge(s["pt_act"], i * 2 + 2)
                    pe.wait_ge(s["pt_vec"], i * 2 + 2)
                    wait(pe, s, i + 1, "v_copied")
                    if not order and not early(i, 1):
                        pe.wait_ge(s["done"], i)
                    for h in range(HEADS):
                        mm = pe.matmul(pv[0:R, E * h:E * h + E], pt[:, h, :], vs[p][:, h, :], start=True, stop=True)
                    mm.then_inc(s["pv"], 1)

                for b in range(4):
                    score(0, 0, b)
                values(0, 0)
                walk(pe, count, body)
                turn_output(last)
                if order:
                    pe.wait_ge(s["o_copied"], count)
                    for t in range(PAIRS):
                        mm = pe.matmul(scores[0:PT, t // 4, (t % 4) * D:(t % 4 + 1) * D], o_t[:, t * PT:(t + 1) * PT],
                                       wo[:], start=True, stop=True)
                    mm.then_inc(s["out2"], 1)
                else:
                    project(last)

            @block.scalar
            def _(act):
                for b in range(8):
                    act.wait_ge(s["projected"], b + 1)
                    dst = (q_t if b < 4 else k_t)[:, (b % 4) * GT:(b % 4 + 1) * GT]
                    act.activation(dst, scores[:, b % 4, 0:GT], ACT.Copy, scale=scale if b < 4 else 1.0)\
                        .then_inc(s["evacuated"], 1)
                act.wait_ge(s["evacuated"], 8)
                act.wait_ge(s["loaded"], 64)

                def stage_rows(i, p):
                    if not early(i, 2):
                        act.wait_ge(s["scores"], (i - 1) * 2)
                        act.wait_ge(s["v_ready"], i - 1)
                    act.activation(src.fixed(qs[p]), src.part(q_t, i), ACT.Copy).then_inc(s["staged_q"], 1)
                    act.activation(src.fixed(hs[p]), src.part(h_t, i), ACT.Copy).then_inc(s["staged_h"], 1)

                def copy_values(i, p):
                    wait(act, s, i + 1, "v_ready")
                    if early(i, 2):
                        act.wait_ge(s["cleared"], 2)
                    act.activation(vs[p][:, :, 0:8], mi[0:R, 0:D].rearrange("t (h e) -> t h e", h=HEADS), ACT.Copy).then_inc(s["v_copied"], 1)

                def exps(i, p, h):
                    act.wait_ge(s["shifted"], i * 2 + (h + 1))
                    act.activation(pr[p][:, 8 * h:8 * h + 8, :], pr[p][:, 8 * h:8 * h + 8, :], ACT.Exp).then_inc(s["probs"], 1)

                def copy_output(i):
                    wait(act, s, i + 1, "o_turned")
                    if order:
                        act.activation(order(o_t, i), mi[:, 256:256 + R].rearrange("d (b t) -> d b t", t=BATCH), ACT.Copy)\
                            .then_inc(s["o_copied"], 1)
                    else:
                        if not early(i, 1):
                            act.wait_ge(s["out_ready"], i)
                        act.activation(ot[:], mi[:, 256:256 + R], ACT.Copy).then_inc(s["o_copied"], 1)

                def body(i, p):
                    def copy_group(b):
                        act.wait_ge(s["turned"], i * 4 + (b + 1))
                        act.activation(pt[:, 4 * b:4 * b + 4, :].rearrange("k a q -> k (a q)"), turn[0:R, b % 2, 0:4 * R], ACT.Copy)\
                            .then_inc(s["pt_act"], 1)

                    copy_group(0)
                    if not early(i, 1):
                        copy_output(i - 1)
                    copy_group(2)
                    if not isinstance(i, int) or i + 2 < count:
                        stage_rows(i + 2, p)
                    if not is_last(i):
                        exps(i + 1, 1 - p, 0)
                        copy_values(i + 1, 1 - p)
                        exps(i + 1, 1 - p, 1)

                stage_rows(0, 0)
                stage_rows(1, 1)
                exps(0, 0, 0)
                copy_values(0, 0)
                exps(0, 0, 1)
                walk(act, count, body)
                copy_output(last)

            @block.gpsimd
            def _(pool):
                for p in range(2):
                    pool.memset(vs[p][:, :, 8:E], 1.0).then_inc(s["cleared"], 1)
                pool.wait_ge(s["evacuated"], 8)
                pool.wait_ge(s["loaded"], 64)

                def spread_keys(i, p):
                    if not early(i, 2):
                        pool.wait_ge(s["scores"], (i - 1) * 2)
                    pool.tensor_tensor(src.heads(kb[p]), src.all_heads(k_t, i), src.mask(hm), ALU.mult).then_inc(s["staged_k"], 1)

                walk(pool, count, spread_keys)

            @block.vector
            def _(v):
                v.wait_ge(s["evacuated"], 8)
                v.wait_ge(s["loaded"], 64)

                def mask_scores(i, p, h):
                    heads = slice(8 * h, 8 * h + 8)
                    n = i * 2 + (h + 1)
                    v.wait_ge(s["scores"], n)
                    v.tensor_tensor(pr[p][:, heads, :].rearrange("q (a b) k -> q a b k", a=2),
                                    scores[0:R, 2 * h:2 * h + 2, 0:4 * R].rearrange("q a (b k) -> q a b k", b=4),
                                    bc(mk[:, None, None, :], [R, 2, 4, R]), ALU.add).then_inc(s["masked"], 1)
                    v.wait_ge(s["masked"], n)
                    if not early(i, 1):
                        v.wait_ge(s["shifted"], i * 2 + (h - 1))
                    v.tensor_reduce(mx[:, heads], pr[p][:, heads, :], AX.X, ALU.max).then_inc(s["rowmax"], 1)

                def shift_scores(i, p, h):
                    heads = slice(8 * h, 8 * h + 8)
                    v.wait_ge(s["rowmax"], i * 2 + (h + 1))
                    v.tensor_tensor(pr[p][:, heads, :], pr[p][:, heads, :], bc(mx[:, heads, None], [R, 8, R]), ALU.subtract).then_inc(s["shifted"], 1)

                def add_output(i):
                    wait(v, s, i + 1, "out_ready")
                    v.tensor_tensor(x[:, i, :], pv[0:R, 256:256 + D], x[:, i, :], ALU.add).then_inc(s["done"], 1)

                def body(i, p):
                    def copy_group(b):
                        v.wait_ge(s["turned"], i * 4 + (b + 1))
                        v.tensor_copy(pt[:, 4 * b:4 * b + 4, :].rearrange("k a q -> k (a q)"), turn[0:R, b % 2, 0:4 * R]).then_inc(s["pt_vec"], 1)

                    copy_group(1)
                    if not is_last(i):
                        mask_scores(i + 1, 1 - p, 0)
                        shift_scores(i + 1, 1 - p, 0)
                    if not order and not early(i, 1):
                        add_output(i - 1)
                    copy_group(3)
                    if not is_last(i):
                        mask_scores(i + 1, 1 - p, 1)
                        shift_scores(i + 1, 1 - p, 1)
                    wait(v, s, i + 1, "pv")
                    if not early(i, 1):
                        v.wait_ge(s["o_ready"], i)
                    sums = pv[0:R, 0:HEADS * E].rearrange("q (h e) -> q h e", h=HEADS)
                    v.reciprocal(rl[:, :, None], sums[:, :, 8:E]).then_inc(s["inverse"], 1)
                    wait(v, s, i + 1, "inverse")
                    if not early(i, 1):
                        v.wait_ge(s["o_turned"], i)
                    v.tensor_tensor(on.rearrange("q (h e) -> q h e", h=HEADS), sums[:, :, 0:8],
                                    bc(rl[:, :, None], [R, HEADS, 8]), ALU.mult).then_inc(s["o_ready"], 1)

                for h in range(2):
                    mask_scores(0, 0, h)
                    shift_scores(0, 0, h)
                walk(v, count, body)
                if order:
                    v.wait_ge(s["out2"], 1)
                    v.tensor_tensor(x.rearrange("t (a b) d -> t a (b d)", a=4), scores[0:PT, :, :],
                                    x.rearrange("t (a b) d -> t a (b d)", a=4), ALU.add).then_inc(s["added"], 1)
                else:
                    add_output(last)


def softmax_vector(v, s, n, R, scores, mask, pr, mx, ls, rl):
    full, four = [R, HEADS, R], [R, 4, 4, R]
    v.wait_ge(s["scores"], n)
    v.tensor_tensor(pr.rearrange("q (a b) k -> q a b k", a=4), scores[0:R, :, 0:4 * R].rearrange("q a (b k) -> q a b k", b=4),
                    bc(mask[:, None, None, :], four), ALU.add).then_inc(s["masked"], 1)
    v.wait_ge(s["masked"], n)
    v.tensor_reduce(mx, pr, AX.X, ALU.max).then_inc(s["rowmax"], 1)
    v.wait_ge(s["rowmax"], n)
    v.tensor_tensor(pr, pr, bc(mx[:, :, None], full), ALU.subtract).then_inc(s["shifted"], 1)
    v.wait_ge(s["probs"], n)
    v.tensor_reduce(ls, pr, AX.X, ALU.add).then_inc(s["rowsum"], 1)
    v.wait_ge(s["rowsum"], n)
    v.reciprocal(rl, ls).then_inc(s["inverse"], 1)


def turn_probs(pe, s, n, R, scores, pr, ident):
    pe.wait_ge(s["probs"], n)
    for h in range(HEADS):
        mm = pe.transpose(scores[0:R, h // 4, (h % 4) * R:(h % 4 + 1) * R], pr[:, h, :], ident[0:R, 0:R])
    mm.then_inc(s["turned"], 1)


def l0_attention(nc, g, a):
    normalise(nc, g, "n0", [("layer", 1e-5)])
    narrow_attention(nc, g, "a0", PT, PAIRS, PairTokens, g["consts"]["causal_mask"], 8 ** -0.5,
                     a["L0_attn_in_proj_weight"], a["L0_attn_out_proj_weight"])



def rounds(eng, body):
    body(0)
    with eng.Fori(1, PAIRS - 1) as i:
        body(i)
    body(PAIRS - 1)


def l0_cross(nc, g, a):
    normalise(nc, g, "n1", [("layer", 1e-5), ("layer", 1e-5)], a["L0_xattn_ln_l_w"], a["L0_xattn_ln_l_b"])
    ident, ones, x, h_t, half = g["ident"], g["ones"], g["x"], g["h_t"], g["half"]
    QH, C, S = 8, 4, SEQ
    names = ("loaded negb heads heads_copied q_made q_act q_vec ctx0 ctx1 stats mv var rstd centred z_ready "
             "lat_ready q_ready turned freed0 freed1 scores max_ctx max_lat negmax probs sums inverse diag pl pv ol_copied mixed "
             "o_norm o_ready out_ready done")
    with stage(nc, "x0", names) as (s, sb, ps):
        wqt = sb("wq_t", [64, QH, D]); wkt = sb("wk_t", [64, QH, D]); wv = sb("wv", [D, 512]); wout = sb("wout", [D, C, D])
        ab = sb("gain_shift", [D, 3]); mh = sb("heads", [D, QH, D]); q = sb("q", [D, QH, TOK])
        cx = [sb(f"ctx{j}", [TP, TILES, D]) for j in range(2)]; z = [sb(f"z{j}", [TP, TILES, D]) for j in range(2)]
        bst = sb("bst", [TP, TILES, 6]); mv = [sb(f"mv{j}", [TP, TILES, 2]) for j in range(2)]; rstd = sb("rstd", [TP, TILES, 1])
        zt = sb("z_t", [D, CTX]); lt = [sb(f"lat_t{j}", [D, S]) for j in range(2)]; ln = [sb(f"lat{j}", [S, D]) for j in range(2)]
        ql = [sb(f"q_lat{j}", [D, QH, S]) for j in range(2)]; qz = [sb(f"q_ctx{j}", [D, QH, S]) for j in range(2)]
        pr = [sb(f"pr{k}", [PT, CTX + S]) for k in range(C)]; sl = [sb(f"lat_scores{j}", [PT, C, S]) for j in range(2)]; pt = sb("pt", [TP, TILES, C * PT]); ptl = sb("ptl", [S, C * PT])
        mx = sb("mx", [PT, 2]); nm = sb("nm", [PT, 2]); l = [sb(f"l{j}", [PT, C, 2]) for j in range(2)]; ls = sb("ls", [PT, C]); rl = sb("rl", [PT, C])
        dg = sb("dg", [PT, C, PT]); ols = sb("ols", [D, C * PT]); o1 = sb("o1", [D, C * PT]); ut = sb("ut", [D, C, PT])
        sc = ps("sc", [D, 6, 512]); turn = ps("turn", [D, 2, 512])
        oz, ol, spread = (sc[:, b, :] for b in (3, 4, 5))
        FRONT = 4
        TURNS = 4 * C + FRONT + 2
        SHIFT = FRONT - 2
        OUT = C * S + D

        def cnt(i, j, per, k):
            return i * (2 * per) + (j * per + k)

        def is_first(i, j):
            return isinstance(i, int) and i == 0 and j == 0

        def is_last(i, j):
            return isinstance(i, int) and i == PAIRS - 1 and j == 1

        def chunk_group(i, j, c, b):
            if c == 0:
                return (i, j, 2 + b if is_first(i, j) or b >= 2 else b)
            return (i, j, 2 + 4 * c + b + (0 if c < 2 or is_last(i, j) else 2 if c == 2 else 4))

        def front_group(i, j, b):
            if is_first(i, j):
                return (i, j, b - SHIFT)
            return (*((i, 0) if j else (i - 1, 1)), (10, 11, 16, 17)[b])

        def project_group(i, j, r):
            return (i, j, 2 + 4 * C + r) if is_last(i, j) else (*after_of(i, j), 2 + r)

        def after_of(i, j):
            return (i, 1) if j == 0 else (i + 1, 0)

        def emitted(i, j, k):
            return i * (2 * TURNS) + (SHIFT + TURNS * j + k + 1)

        def half_of(i, j, k):
            n = SHIFT + TURNS * j + k + 1
            return i * TURNS + (n + 1) // 2, i * TURNS + n // 2

        def lat_scored(eng, i, j):
            eng.wait_ge(s["freed1"], half_of(*front_group(i, j, 3))[1])

        with nc.Block() as block:
            @block.sync
            def _(sp):
                for dst, drm in ((wqt[:], a["L0_xattn_wq_t"]), (wkt[:], a["L0_xattn_wk_t"]), (wv[:], a["L0_xattn_wv"]), (wout[:], a["L0_xattn_wout"]),
                                 (ab[:, 0:1], a["L0_xattn_ln_m_w"]), (ab[:, 1:2], a["L0_xattn_ln_m_b"])):
                    sp.dma_start(dst, drm).then_inc(s["loaded"], 16)

                def body(i):
                    for j in range(2):
                        if not (isinstance(i, int) and i == 0):
                            sp.wait_ge(s["centred"], cnt(i, j, 1, -1))
                        sp.dma_start(cx[j][:], a["ctx"][bass.ds(i * 2 + j, 1), :, :, :].rearrange("o p t d -> (o p) t d")).then_inc(s[f"ctx{j}"], 16)
                rounds(sp, body)

            @block.tensor
            def _(pe):
                pe.wait_ge(s["loaded"], 96)
                for h in range(QH):
                    mm = pe.matmul(sc[:, h // 4, (h % 4) * D:(h % 4 + 1) * D], wqt[:, h, :], wkt[:, h, :], start=True, stop=True)
                mm.then_inc(s["heads"], 1)
                pe.wait_ge(s["heads_copied"], 1)
                for k in range(4 * QH):
                    if k >= 2:
                        pe.wait_ge(s["q_act" if k % 2 == 0 else "q_vec"], k // 2)
                    pe.matmul(sc[:, k % 2, 0:GT], mh[:, k // 4, :], h_t[:, (k % 4) * GT:(k % 4 + 1) * GT], start=True, stop=True)\
                        .then_inc(s["q_made"], 1)
                pe.wait_ge(s["q_act"], 2 * QH)
                pe.wait_ge(s["q_vec"], 2 * QH)

                def group(i, j, k, emit):
                    bank = (SHIFT + k) % 2
                    if not (is_first(i, j) and SHIFT + k < 2):
                        pe.wait_ge(s[f"freed{bank}"], half_of(i, j, k - 2)[bank])
                    apart(pe)
                    emit(turn[:, bank, :]).then_inc(s["turned"], 1)

                def copied(i, j, k):
                    bank = (SHIFT + k) % 2
                    pe.wait_ge(s[f"freed{bank}"], half_of(i, j, k)[bank])

                def project(i, j, r):
                    def half_heads(bank):
                        for c in range(2 * r, 2 * r + 2):
                            mm = pe.matmul(bank[:, (c % 2) * PT:(c % 2 + 1) * PT], wv[:, c * D:(c + 1) * D], o1[:, c * PT:(c + 1) * PT], start=True, stop=True)
                        return mm
                    pe.wait_ge(s["o_ready"], cnt(i, j, 1, 1))
                    group(*project_group(i, j, r), half_heads)

                def pair_out(i, bank):
                    for c in range(C):
                        mm = pe.matmul(bank[0:PT, OUT:OUT + D], ut[:, c, :], wout[:, c, :], start=(c == 0), stop=(c == C - 1))
                    return mm

                def front(i, j, b):
                    def turn_context(bank):
                        for t in range(4):
                            mm = pe.transpose(bank[:, t * TP:(t + 1) * TP], z[j][:, 4 * b + t, :], ident[0:TP, 0:TP])
                        return mm

                    def latents(bank):
                        pe.transpose(bank[0:S, C * S:C * S + D], lt[j][:], ident[:])
                        for c in range(C):
                            mm = pe.matmul(bank[0:PT, c * S:(c + 1) * S], ql[j][:, 2 * c:2 * c + 2, :], lt[j][:], start=True, stop=True)
                        if j == 1 and not (isinstance(i, int) and i == 0):
                            mm = pair_out(i - 1, bank)
                        return mm

                    if b == 0:
                        pe.wait_ge(s["z_ready"], cnt(i, j, 1, 1))
                    if b < 3:
                        group(*front_group(i, j, b), turn_context)
                    else:
                        pe.wait_ge(s["lat_ready"], cnt(i, j, 1, 1))
                        pe.wait_ge(s["q_ready"], cnt(i, j, 1, 1))
                        group(*front_group(i, j, 3), latents)

                def score(i, j, c, turned=None):
                    if c >= 2:
                        pe.wait_ge(s["probs"], cnt(i, j, C, c - 1))
                    elif not (isinstance(i, int) and i == 0 and j == 0):
                        if c == 0:
                            pe.wait_ge(s["probs"], cnt(i, j, C, -1))
                        else:
                            pe.wait_ge(s["o_norm"], cnt(i, j, 1, 0))
                    if c == 0:
                        for b in (1, 2):
                            copied(*front_group(i, j, b))
                    for b in range(3):
                        mm = pe.matmul(sc[0:PT, 3 * (c % 2) + b, 0:BANKC], qz[j][:, 2 * c:2 * c + 2, :], zt[:, b * BANKC:(b + 1) * BANKC],
                                       start=True, stop=True)
                        if turned is not None and b < 2:
                            turned(b)
                    mm.then_inc(s["scores"], 1)

                def body(i):
                    for j in range(2):
                        first = isinstance(i, int) and i == 0 and j == 0
                        last = isinstance(i, int) and i == PAIRS - 1 and j == 1
                        before = (i, 0) if j else (i - 1, 1)
                        after = after_of(i, j)

                        def turn_group(c, b):
                            def tiles(bank):
                                if b == 3:
                                    return pe.transpose(bank[0:S, 0:PT], pr[c][:, CTX:CTX + S], ident[0:PT, 0:PT])
                                for t in range(4):
                                    mm = pe.transpose(bank[0:TP, t * PT:(t + 1) * PT], pr[c][:, (4 * b + t) * TP:(4 * b + t + 1) * TP], ident[0:PT, 0:PT])
                                return mm
                            if b == 0:
                                pe.wait_ge(s["probs"], cnt(i, j, C, c + 1))
                            group(*chunk_group(i, j, c, b), tiles)

                        def sums(b, tiles):
                            if tiles[0] % 4 == 0:
                                copied(*chunk_group(i, j, C - 1, b))
                            for t in tiles:
                                mm = pe.matmul(oz[:, 0:C * PT], z[j][:, t, :], pt[:, t, :], start=(t == 0), stop=(t == TILES - 1))
                            return mm

                        def later(b):
                            if not last:
                                front(*after, b)

                        if not first:
                            turn_group(0, 0)
                            turn_group(0, 1)
                        score(i, j, 1, None if first else lambda b: project(*before, b))
                        if first:
                            turn_group(0, 0)
                            turn_group(0, 1)
                        score(i, j, 2, lambda b: turn_group(0, 2 + b))
                        turn_group(1, 0)
                        turn_group(1, 1)
                        score(i, j, 3, lambda b: turn_group(1, 2 + b))
                        later(0)
                        later(1)
                        for b in range(4):
                            turn_group(2, b)
                        later(2)
                        later(3)
                        if not last:
                            score(*after, 0)
                        turn_group(3, 0)
                        turn_group(3, 1)
                        sums(0, (0, 1))
                        turn_group(3, 2)
                        sums(0, (2, 3))
                        turn_group(3, 3)
                        sums(1, (4, 5, 6, 7))
                        copied(*chunk_group(i, j, C - 1, 3))
                        pe.matmul(ol[:, 0:C * PT], ln[j][:], ptl[:], start=True, stop=True).then_inc(s["pl"], 1)
                        pe.wait_ge(s["diag"], cnt(i, j, 1, 1))
                        pe.matmul(spread[:, 0:C * PT], ones[0:PT, :], dg[:], start=True, stop=True)
                        mm = sums(2, (8, 9, 10, 11))
                        mm.then_inc(s["pv"], 1)

                for b in range(FRONT):
                    front(0, 0, b)
                score(0, 0, 0)
                rounds(pe, body)
                for r in range(2):
                    project(PAIRS - 1, 1, r)
                for r in range(2):
                    copied(*project_group(PAIRS - 1, 1, r))
                pair_out(PAIRS - 1, turn[:, 0, :]).then_inc(s["out_ready"], 1)

            @block.scalar
            def _(act):
                act.wait_ge(s["heads"], 1)
                act.activation(mh.rearrange("k (a b) d -> k a (b d)", a=2), sc[:, 0:2, :], ACT.Copy, scale=64 ** -0.5).then_inc(s["heads_copied"], 1)
                for k in range(0, 4 * QH, 2):
                    act.wait_ge(s["q_made"], k + 1)
                    act.activation(q[:, k // 4, (k % 4) * GT:(k % 4 + 1) * GT], sc[:, 0, 0:GT], ACT.Copy).then_inc(s["q_act"], 1)
                act.wait_ge(s["q_act"], 2 * QH)
                act.wait_ge(s["q_vec"], 2 * QH)
                act.wait_ge(s["negb"], 1)

                def stage_queries(i, j):
                    cols = bass.ds((i * 2 + j) * S, S)
                    act.activation(lt[j][:], h_t[:, cols], ACT.Identity, bias=ab[:, 2:3]).then_inc(s["lat_ready"], 1)
                    act.activation(ql[j][:], q[:, :, cols], ACT.Copy)
                    act.activation(qz[j][:], q[:, :, cols], ACT.Identity, scale=ab[:, 0:1]).then_inc(s["q_ready"], 1)

                def shift_sums(i, j):
                    act.wait_ge(s["o_norm"], cnt(i, j, 1, 1))
                    act.activation(o1[:], o1[:], ACT.Identity, bias=ab[:, 1:2]).then_inc(s["o_ready"], 1)

                def exps(i, j, c):
                    act.wait_ge(s["negmax"], cnt(i, j, C, c + 1))
                    if c == 0:
                        lat_scored(act, i, j)
                    act.activation(pr[c][:, CTX:CTX + S], sl[j][:, c, :], ACT.Exp, bias=nm[:, c % 2:c % 2 + 1], accum_out=l[j][:, c, 1:2])
                    act.activation(pr[c][:, 0:CTX].rearrange("q (a b) -> q a b", a=3), sc[0:PT, 3 * (c % 2):3 * (c % 2) + 3, 0:BANKC], ACT.Exp,
                                   bias=nm[:, c % 2:c % 2 + 1], accum_out=l[j][:, c, 0:1]).then_inc(s["probs"], 1)

                def group_ready(i, j, k):
                    act.wait_ge(s["turned"], emitted(i, j, k))

                def front_copies(i, j, b):
                    group_ready(*front_group(i, j, b))
                    act.activation(zt[:, b * BANKC:(b + 1) * BANKC], turn[:, 0, 0:BANKC], ACT.Copy).then_inc(s["freed0"], 1)

                def copy_heads(i, j):
                    group_ready(*project_group(i, j, 0))
                    for e in range(2):
                        ins = act.activation(ut[64 * e:64 * e + 64, 0:2, j * S:(j + 1) * S],
                                             turn[64 * e:64 * e + 64, 0, 0:2 * PT].rearrange("d (c t) -> d c t", c=2)[:, :, e * S:(e + 1) * S], ACT.Copy)
                    ins.then_inc(s["freed0"], 1)

                stage_queries(0, 0)
                front_copies(0, 0, 0)
                front_copies(0, 0, 2)
                exps(0, 0, 0)

                def body(i):
                    for j in range(2):
                        first = isinstance(i, int) and i == 0 and j == 0
                        last = isinstance(i, int) and i == PAIRS - 1 and j == 1
                        before = (i, 0) if j else (i - 1, 1)
                        after = after_of(i, j)

                        def copy(c, b):
                            group_ready(*chunk_group(i, j, c, b))
                            act.activation(pt[:, 4 * b:4 * b + 4, c * PT:(c + 1) * PT], turn[0:TP, 0, 0:4 * PT].rearrange("p (t q) -> p t q", t=4),
                                           ACT.Copy).then_inc(s["freed0"], 1)

                        copy(0, 0)
                        if not first:
                            copy_heads(*before)
                        exps(i, j, 1)
                        copy(0, 2)
                        copy(1, 0)
                        exps(i, j, 2)
                        copy(1, 2)
                        if not last:
                            stage_queries(*after)
                            front_copies(*after, 0)
                        copy(2, 0)
                        exps(i, j, 3)
                        copy(2, 2)
                        if not last:
                            front_copies(*after, 2)
                        copy(3, 0)
                        if not last:
                            exps(*after, 0)
                        copy(3, 2)
                        act.wait_ge(s["pl"], cnt(i, j, 1, 1))
                        act.activation(ols[:], ol[:, 0:C * PT], ACT.Copy).then_inc(s["ol_copied"], 1)
                        shift_sums(i, j)

                rounds(act, body)
                copy_heads(PAIRS - 1, 1)

            @block.gpsimd
            def _(pool):
                shape = [TP, TILES, D]

                def body(i):
                    for j in range(2):
                        pool.wait_ge(s["mv"], cnt(i, j, 1, 1))
                        if not is_first(i, j):
                            pool.wait_ge(s["z_ready"], cnt(i, j, 1, 0))
                        apart(pool)
                        pool.tensor_scalar(rstd[:], mv[j][:, :, 1:2], 1e-5, None, ALU.add).then_inc(s["var"], 1)
                        pool.wait_ge(s["var"], cnt(i, j, 1, 1))
                        pool.tensor_tensor(rstd[:], rstd[:], half[0:TP, 0:TILES].rearrange("p (t o) -> p t o", o=1), ALU.pow).then_inc(s["rstd"], 1)
                        if not (isinstance(i, int) and i == 0):
                            pool.wait_ge(s["pv"], cnt(i, j, 1, -1))
                        pool.tensor_tensor(z[j][:], cx[j][:], bc(mv[j][:, :, 0:1], shape), ALU.subtract).then_inc(s["centred"], 1)
                        pool.wait_ge(s["centred"], cnt(i, j, 1, 1))
                        pool.wait_ge(s["rstd"], cnt(i, j, 1, 1))
                        pool.tensor_tensor(z[j][:], z[j][:], bc(rstd[:], shape), ALU.mult).then_inc(s["z_ready"], 1)
                rounds(pool, body)

            @block.vector
            def _(v):
                v.wait_ge(s["loaded"], 96)
                v.tensor_scalar(ab[:, 2:3], ab[:, 1:2], -1.0, None, ALU.mult).then_inc(s["negb"], 1)
                for k in range(1, 4 * QH, 2):
                    v.wait_ge(s["q_made"], k + 1)
                    v.tensor_copy(q[:, k // 4, (k % 4) * GT:(k % 4 + 1) * GT], sc[:, 1, 0:GT]).then_inc(s["q_vec"], 1)

                def statistics(i, j):
                    v.wait_ge(s[f"ctx{j}"], i * 16 + 16)
                    if not is_first(i, j):
                        v.wait_ge(s["mv"], cnt(i, j, 1, 0))
                    if not (isinstance(i, int) and i == 0):
                        v.wait_ge(s["z_ready"], cnt(i, j, 1, -1))
                    for t in range(TILES):
                        v.bn_stats(bst[:, t, :], cx[j][:, t, :]).then_inc(s["stats"], 1)
                    v.wait_ge(s["stats"], cnt(i, j, TILES, TILES))
                    apart(v)
                    for t in range(TILES):
                        ins = v.bn_aggr(mv[j][:, t, :], bst[:, t, :])
                    ins.then_inc(s["mv"], 1)

                def group_ready(i, j, k):
                    v.wait_ge(s["turned"], emitted(i, j, k))

                def add_out(i, bank):
                    v.tensor_tensor(x[:, i, :], turn[0:PT, bank, OUT:OUT + D], x[:, i, :], ALU.add).then_inc(s["done"], 1)

                def front_context(i, j):
                    group_ready(*front_group(i, j, 1))
                    v.tensor_copy(zt[:, BANKC:2 * BANKC], turn[:, 1, 0:BANKC]).then_inc(s["freed1"], 1)

                def front_latents(i, j):
                    group_ready(*front_group(i, j, 3))
                    if j == 1 and not (isinstance(i, int) and i == 0):
                        add_out(i - 1, 1)
                    v.tensor_copy(ln[j][:], turn[0:S, 1, C * S:C * S + D])
                    v.tensor_copy(sl[j][:], turn[0:PT, 1, 0:C * S].rearrange("q (c t) -> q c t", c=C)).then_inc(s["freed1"], 1)

                def copy_heads(i, j):
                    group_ready(*project_group(i, j, 1))
                    for e in range(2):
                        ins = v.tensor_copy(ut[64 * e:64 * e + 64, 2:4, j * S:(j + 1) * S],
                                            turn[64 * e:64 * e + 64, 1, 0:2 * PT].rearrange("d (c t) -> d c t", c=2)[:, :, e * S:(e + 1) * S])
                    ins.then_inc(s["freed1"], 1)

                def maxima(i, j, c):
                    first = isinstance(i, int) and i == 0 and j == 0
                    v.wait_ge(s["scores"], cnt(i, j, C, c + 1))
                    if not (first and c < 2):
                        v.wait_ge(s["probs"], cnt(i, j, C, c - 1))
                    if not (first and c == 0):
                        v.wait_ge(s["negmax"], cnt(i, j, C, c))
                    v.tensor_reduce(mx[:, 0:1], sc[0:PT, 3 * (c % 2):3 * (c % 2) + 3, 0:BANKC], AX.XY, ALU.max).then_inc(s["max_ctx"], 1)
                    if c == 0:
                        lat_scored(v, i, j)
                    v.tensor_reduce(mx[:, 1:2], sl[j][:, c, :], AX.X, ALU.max).then_inc(s["max_lat"], 1)
                    v.wait_ge(s["max_ctx"], cnt(i, j, C, c + 1))
                    v.wait_ge(s["max_lat"], cnt(i, j, C, c + 1))
                    v.tensor_reduce(nm[:, c % 2:c % 2 + 1], mx[:], AX.X, ALU.max, negate=True).then_inc(s["negmax"], 1)

                statistics(0, 0)
                statistics(0, 1)
                front_context(0, 0)
                front_latents(0, 0)
                maxima(0, 0, 0)

                def body(i):
                    for j in range(2):
                        first = isinstance(i, int) and i == 0 and j == 0
                        last = isinstance(i, int) and i == PAIRS - 1 and j == 1
                        before = (i, 0) if j else (i - 1, 1)
                        after = after_of(i, j)

                        def copy_context(c):
                            group_ready(*chunk_group(i, j, c, 1))
                            v.tensor_copy(pt[:, 4:8, c * PT:(c + 1) * PT], turn[0:TP, 1, 0:4 * PT].rearrange("p (t q) -> p t q", t=4)).then_inc(s["freed1"], 1)

                        def copy_latents(c):
                            group_ready(*chunk_group(i, j, c, 3))
                            v.tensor_copy(ptl[:, c * PT:(c + 1) * PT], turn[0:S, 1, 0:PT]).then_inc(s["freed1"], 1)

                        copy_context(0)
                        if not first:
                            copy_heads(*before)
                        maxima(i, j, 1)
                        copy_latents(0)
                        maxima(i, j, 2)
                        copy_context(1)
                        copy_latents(1)
                        maxima(i, j, 3)
                        if not last:
                            front_context(*after)
                        copy_context(2)
                        copy_latents(2)
                        if not last:
                            front_latents(*after)
                            maxima(*after, 0)
                        copy_context(3)
                        copy_latents(3)
                        v.wait_ge(s["probs"], cnt(i, j, C, C))
                        v.tensor_reduce(ls[:], l[j][:], AX.X, ALU.add).then_inc(s["sums"], 1)
                        v.wait_ge(s["sums"], cnt(i, j, 1, 1))
                        v.reciprocal(rl[:], ls[:]).then_inc(s["inverse"], 1)
                        v.wait_ge(s["inverse"], cnt(i, j, 1, 1))
                        v.tensor_tensor(dg[:], bc(ident[0:PT, None, 0:PT], [PT, C, PT]), bc(rl[:, :, None], [PT, C, PT]), ALU.mult).then_inc(s["diag"], 1)
                        if not last and not is_last(*after):
                            statistics(*after_of(*after))
                        v.wait_ge(s["ol_copied"], cnt(i, j, 1, 1))
                        v.wait_ge(s["pv"], cnt(i, j, 1, 1))
                        v.scalar_tensor_tensor(o1[:], oz[:, 0:C * PT], ab[:, 0:1], ols[:], ALU.mult, ALU.add).then_inc(s["mixed"], 1)
                        v.wait_ge(s["mixed"], cnt(i, j, 1, 1))
                        v.tensor_tensor(o1[:], o1[:], spread[:, 0:C * PT], ALU.mult).then_inc(s["o_norm"], 1)

                rounds(v, body)
                copy_heads(PAIRS - 1, 1)
                v.wait_ge(s["out_ready"], 1)
                add_out(PAIRS - 1, 0)



NORM_STEPS = "n_sum n_mean n_centred n_squared n_sumsq n_var n_rstd n_normed "
ROUTE_STEPS = "r_logits r_max r_best r_order r_first r_picked "


def norm_vector(v, s, n, y, sq, st, size, eps):
    norm_start(v, s, n, y, sq, st, size, eps)
    norm_end(v, s, n, y, st)


def norm_start(v, s, n, y, sq, st, size, eps):
    shape = list(y.shape)
    v.tensor_reduce(st[0], y, AX.X, ALU.add).then_inc(s["n_sum"], 1)
    wait(v, s, n, "n_sum")
    v.tensor_scalar(st[1], st[0], 1.0 / size, None, ALU.mult).then_inc(s["n_mean"], 1)
    wait(v, s, n, "n_mean")
    v.tensor_tensor(y, y, bc(st[1][:, :, None], shape), ALU.subtract).then_inc(s["n_centred"], 1)
    wait(v, s, n, "n_centred")
    v.tensor_tensor(sq, y, y, ALU.mult).then_inc(s["n_squared"], 1)
    wait(v, s, n, "n_squared")
    v.tensor_reduce(st[2], sq, AX.X, ALU.add).then_inc(s["n_sumsq"], 1)
    wait(v, s, n, "n_sumsq")
    v.tensor_scalar(st[3], st[2], 1.0 / size, eps, ALU.mult, ALU.add).then_inc(s["n_var"], 1)


def norm_end(v, s, n, y, st):
    wait(v, s, n, "n_rstd")
    v.tensor_tensor(y, y, bc(st[4][:, :, None], list(y.shape)), ALU.mult).then_inc(s["n_normed"], 1)


def norm_pool(pool, s, n, st, half):
    wait(pool, s, n, "n_var")
    pool.tensor_tensor(st[4], st[3], half, ALU.pow).then_inc(s["n_rstd"], 1)


def argmax_vector(v, s, n, p, value, top, rank, earlier, picked):
    shape = list(value.shape)
    v.tensor_reduce(top, value, AX.X, ALU.max).then_inc(s[p + "_max"], 1)
    wait(v, s, n, p + "_max")
    v.tensor_tensor(rank, value, bc(top[:, :, None], shape), ALU.is_equal).then_inc(s[p + "_best"], 1)
    wait(v, s, n, p + "_best")
    v.tensor_tensor(rank, rank, bc(earlier[0:shape[0], None, :], shape), ALU.mult).then_inc(s[p + "_order"], 1)
    wait(v, s, n, p + "_order")
    v.tensor_reduce(top, rank, AX.X, ALU.max).then_inc(s[p + "_first"], 1)
    wait(v, s, n, p + "_first")
    v.tensor_tensor(picked, rank, bc(top[:, :, None], shape), ALU.is_equal).then_inc(s[p + "_picked"], 1)



def l0_ffn(nc, g, a):
    normalise(nc, g, "n2", [("layer", 1e-5)])
    ident, x, h_n, h_t, C = g["ident"], g["x"], g["h_n"], g["h_t"], g["consts"]
    names = ("loaded staged picked_t mask_t spread masked inner gelu outer sum1 sum2 gained shifted done "
             + NORM_STEPS + ROUTE_STEPS)
    with stage(nc, "f0", names) as (s, sb, ps):
        wr = sb("router", [D, EXPERTS]); w1 = sb("w1", [D, EXPERTS, 512]); b1 = sb("b1", [EXPERTS, 512])
        wo = sb("wo", [D, 4, D]); rows = sb("rows", [PT, 3, D]); pick = sb("pick", [EXPERTS, EXPERTS, D])
        early = sb("earlier", [D, EXPERTS])
        hs = sb("hs", [D, GT]); xm = sb("xm", [D, EXPERTS, GT]); ge = sb("gelu", [D, 4, GT]); oht = sb("oht", [EXPERTS, GT])
        oh = sb("oh", [PT, GROUP, EXPERTS]); rank = sb("rank", [PT, GROUP, EXPERTS]); top = sb("top", [PT, GROUP])
        y = sb("y", [PT, GROUP, D]); sq = sb("ysq", [PT, GROUP, D])
        st = [sb(f"st{k}", [PT, GROUP])[:] for k in range(5)]
        small = ps("small", [D, 512]); spread = ps("spread", [D, 2, 512]); inner = ps("inner", [D, 4, 512]); outer = ps("outer", [D, 512])
        with nc.Block() as block:
            @block.sync
            def _(sp):
                for dst, drm in ((wr[:], a["L0_ffn_router"]), (w1[:], a["L0_ffn_w1"]), (b1[:], a["L0_ffn_b1"]),
                                 (wo[:], a["L0_ffn_wo"]), (pick[:], C["pick"]), (early[:], C["earlier"])):
                    sp.dma_start(dst, drm).then_inc(s["loaded"], 16)
                for k in range(3):
                    sp.dma_start(rows[:, k, :], bc(a["L0_ffn_rows"][k:k + 1, :], [PT, D])).then_inc(s["loaded"], 16)

            @block.tensor
            def _(pe):
                pe.wait_ge(s["loaded"], 144)
                with pe.Fori(0, 4) as c:
                    n = c + 1
                    wait(pe, s, n, "staged")
                    for t in range(GROUP):
                        mm = pe.matmul(small[0:PT, t * EXPERTS:(t + 1) * EXPERTS], hs[:, t * PT:(t + 1) * PT], wr[:], start=True, stop=True)
                    mm.then_inc(s["r_logits"], 1)
                    wait(pe, s, n, "r_picked")
                    for t in range(GROUP):
                        mm = pe.transpose(spread[0:EXPERTS, 0, t * PT:(t + 1) * PT],
                                          oh[:, t, :], ident[0:PT, 0:PT])
                    mm.then_inc(s["picked_t"], 1)
                    wait(pe, s, n, "mask_t")
                    for e in range(EXPERTS):
                        if e >= 2:
                            pe.wait_ge(s["masked"], c * EXPERTS + (e - 1))
                        pe.matmul(spread[:, e % 2, 0:GT], pick[:, e, :], oht[:], start=True, stop=True).then_inc(s["spread"], 1)
                    pe.wait_ge(s["masked"], n * EXPERTS)
                    for f in range(4):
                        for e in range(EXPERTS):
                            pe.matmul(inner[:, f, 0:GT], w1[:, e, f * D:(f + 1) * D], xm[:, e, :], start=(e == 0), stop=False)
                        pe.matmul(inner[:, f, 0:GT], b1[:, f * D:(f + 1) * D], oht[:], start=False, stop=True).then_inc(s["inner"], 1)
                    pe.wait_ge(s["gelu"], n * 4)
                    for t in range(GROUP):
                        for f in range(4):
                            mm = pe.matmul(outer[0:PT, t * D:(t + 1) * D], ge[:, f, t * PT:(t + 1) * PT], wo[:, f, :],
                                           start=(f == 0), stop=(f == 3))
                    mm.then_inc(s["outer"], 1)

            @block.scalar
            def _(act):
                with act.Fori(0, 4) as c:
                    n = c + 1
                    act.wait_ge(s["done"], c)
                    act.activation(hs[:], h_t[:, bass.ts(c, GT)], ACT.Copy).then_inc(s["staged"], 1)
                    wait(act, s, n, "picked_t")
                    act.activation(oht[:], spread[0:EXPERTS, 0, 0:GT], ACT.Copy).then_inc(s["mask_t"], 1)
                    for f in range(4):
                        act.wait_ge(s["inner"], c * 4 + (f + 1))
                        act.activation(ge[:, f, :], inner[:, f, 0:GT], ACT.Gelu).then_inc(s["gelu"], 1)

            @block.vector
            def _(v):
                v.wait_ge(s["loaded"], 144)
                with v.Fori(0, 4) as c:
                    n = c + 1
                    wait(v, s, n, "r_logits")
                    argmax_vector(v, s, n, "r", small[0:PT, 0:GROUP * EXPERTS].rearrange("t (a e) -> t a e", e=EXPERTS),
                                  top[:], rank[:], early, oh[:])
                    for e in range(EXPERTS):
                        v.wait_ge(s["spread"], c * EXPERTS + (e + 1))
                        v.tensor_tensor(xm[:, e, :], hs[:], spread[:, e % 2, 0:GT], ALU.mult).then_inc(s["masked"], 1)
                    wait(v, s, n, "outer")
                    v.tensor_tensor(y[:], outer[0:PT, :].rearrange("t (a d) -> t a d", a=GROUP), h_n[:, bass.ts(c, GROUP), :], ALU.add)\
                        .then_inc(s["sum1"], 1)
                    wait(v, s, n, "sum1")
                    v.tensor_tensor(y[:], y[:], bc(rows[:, 0:1, :], [PT, GROUP, D]), ALU.add).then_inc(s["sum2"], 1)
                    wait(v, s, n, "sum2")
                    norm_vector(v, s, n, y[:], sq[:], st, D, 1e-12)
                    wait(v, s, n, "n_normed")
                    v.tensor_tensor(y[:], y[:], bc(rows[:, 1:2, :], [PT, GROUP, D]), ALU.mult).then_inc(s["gained"], 1)
                    wait(v, s, n, "gained")
                    v.tensor_tensor(y[:], y[:], bc(rows[:, 2:3, :], [PT, GROUP, D]), ALU.add).then_inc(s["shifted"], 1)
                    wait(v, s, n, "shifted")
                    v.tensor_tensor(x[:, bass.ts(c, GROUP), :], x[:, bass.ts(c, GROUP), :], y[:], ALU.add).then_inc(s["done"], 1)

            @block.gpsimd
            def _(pool):
                with pool.Fori(0, 4) as c:
                    norm_pool(pool, s, c + 1, st, g["half"][0:PT, 0:GROUP])



def l1_attention(nc, g, a):
    normalise(nc, g, "n3", [("layer", 1e-5)])
    ident, x, h_t = g["ident"], g["x"], g["h_t"]
    LEVELS = len(HALVES)
    names = ("loaded cleared staged xx xxx mix tanh m mixed xs proj_rkg proj_d proj_v d_tanh w_t decay rk v_copied scan diffs cut exps factors "
             "g_exp g_one g_inv gate a_ready a_masked a_sum y_ready y_copied y_turned y_affine gated out_ready done " + NORM_STEPS)
    with stage(nc, "r1", names) as (s, sb, ps):
        maa = sb("maa", [D, 6]); w1 = sb("w1", [D, 160]); w2 = sb("w2", [32, 5, D]); td = sb("decay", [D, 1]); dw1 = sb("dw1", [D, 64]); dw2 = sb("dw2", [64, D])
        bonus = sb("bonus", [D, 1]); w = sb("w", [D, 5, D]); lnw = sb("ln", [D, 2]); lm = sb("level_mask", [PT, LEVELS + 1, PT])
        hs = [sb(f"hs{p}", [D, 2, SEQ]) for p in range(2)]; xx = sb("xx", [D, 2, SEQ]); x3 = sb("xxx", [D, 2, SEQ]); mix = sb("mix", [32, 5, PT]); xs = sb("xs", [D, 5, PT])
        dh = sb("dh", [64, PT]); e = sb("e", [D, 2, SEQ]); cum = sb("cum", [D, 2, 65]); on = sb("on", [D, SEQ])
        rk = sb("rk", [D, 2, PT]); vs = sb("vs", [PT, D]); ex = sb("ex", [D, 2, LEVELS, 2, 64]); fac = sb("fac", [D, 2, LEVELS + 1, PT])
        gt = [sb(f"gate{p}", [D, PT]) for p in range(2)]; am = sb("am", [PT, 2, LEVELS + 1, PT]); at = sb("at", [PT, 2, PT])
        y = sb("y", [PT, 2, 64]); sq = sb("ysq", [PT, 2, 64]); yt = sb("yt", [D, PT])
        st = [sb(f"st{k}", [PT, 2])[:] for k in range(5)]
        lo = ps("lo", [D, 2, 512]); mp = ps("mp", [D, 2, 512]); pa = ps("pa", [D, 4, 512])
        flat = lambda buf: buf.rearrange("d a b -> d (a b)")
        slot = lambda buf, k, rows=slice(0, D): buf[rows, k // 4, (k % 4) * PT:(k % 4 + 1) * PT]
        is_last = lambda i: isinstance(i, int) and i == PAIRS - 1
        with nc.Block() as block:
            @block.sync
            def _(sp):
                loads = [(maa[:, k:k + 1], a[f"L1_maa_{c}"]) for k, c in enumerate("xwkvrg")]
                loads += [(w1[:], a["L1_maa_w1"]), (w2[:], a["L1_maa_w2"]), (td[:], a["L1_decay"]), (dw1[:], a["L1_decay_w1"]), (dw2[:], a["L1_decay_w2"]),
                          (bonus[:], a["L1_bonus"]), (w[:], a["L1_w"]), (lnw[:, 0:1], a["L1_ln_w"]), (lnw[:, 1:2], a["L1_ln_b"]), (lm[:], g["consts"]["level_mask"])]
                assert len(loads) == 16
                for dst, drm in loads:
                    sp.dma_start(dst, drm).then_inc(s["loaded"], 16)

            @block.tensor
            def _(pe):
                pe.wait_ge(s["loaded"], 256)

                def mix_products(i):
                    wait(pe, s, i + 1, "xxx")
                    for k in range(5):
                        mm = pe.matmul(slot(lo, k, slice(0, 32)), w1[:, 32 * k:32 * k + 32], flat(x3), start=True, stop=True)
                    mm.then_inc(s["mix"], 1)

                def shift_products(i):
                    pe.wait_ge(s["tanh"], i * 2 + 2)
                    if not early(i, 1):
                        wait(pe, s, i, "v_copied", "gate")
                    for k in range(5):
                        mm = pe.matmul(slot(mp, k), w2[:, k, :], mix[:, k, :], start=True, stop=True)
                    mm.then_inc(s["m"], 1)

                def projections(i):
                    wait(pe, s, i + 1, "xs")
                    pe.matmul(lo[0:64, 0, 0:PT], dw1[:], xs[:, 0, :], start=True, stop=True).then_inc(s["proj_d"], 1)
                    pe.matmul(slot(mp, 0), w[:, 0, :], xs[:, 3, :], start=True, stop=True)
                    pe.matmul(slot(mp, 1), w[:, 1, :], xs[:, 1, :], start=True, stop=True)
                    pe.matmul(slot(mp, 2), w[:, 3, :], xs[:, 4, :], start=True, stop=True).then_inc(s["proj_rkg"], 1)
                    pe.matmul(mp[0:PT, 1, 0:D], xs[:, 2, :], w[:, 2, :], start=True, stop=True).then_inc(s["proj_v"], 1)
                    wait(pe, s, i + 1, "d_tanh")
                    pe.matmul(lo[:, 1, 0:PT], dw2[:], dh[:], start=True, stop=True).then_inc(s["w_t"], 1)

                def pair_products(i, h):
                    rows = slice(64 * h, 64 * h + 64)
                    for l in range(LEVELS + 1):
                        mm = pe.matmul(pa[0:PT, 2 * h + l // 4, (l % 4) * PT:(l % 4 + 1) * PT], fac[rows, 1, l, :], fac[rows, 0, l, :], start=True, stop=True)
                    mm.then_inc(s["a_ready"], 1)

                def body(i, p):
                    pe.wait_ge(s["factors"], i * 4 + 4)
                    if not early(i, 1):
                        wait(pe, s, i, "done")
                    pair_products(i, 0)
                    if not is_last(i):
                        mix_products(i + 1)
                    pair_products(i, 1)
                    if not is_last(i):
                        shift_products(i + 1)
                    pe.wait_ge(s["a_sum"], i * 2 + 2)
                    wait(pe, s, i + 1, "v_copied")
                    for h in range(2):
                        mm = pe.matmul(pa[0:PT, 3, 64 * h:64 * h + 64], at[:, h, :], vs[:, 64 * h:64 * h + 64], start=True, stop=True)
                    mm.then_inc(s["y_ready"], 1)
                    if not is_last(i):
                        projections(i + 1)
                    wait(pe, s, i + 1, "n_normed")
                    pe.transpose(pa[:, 3, D:D + PT], flat(y), ident[0:PT, 0:PT]).then_inc(s["y_turned"], 1)
                    wait(pe, s, i + 1, "gated")
                    pe.matmul(pa[0:PT, 3, 2 * D:3 * D], yt[:], w[:, 4, :], start=True, stop=True).then_inc(s["out_ready"], 1)

                mix_products(0)
                shift_products(0)
                projections(0)
                walk(pe, PAIRS, body)

            @block.scalar
            def _(act):
                act.wait_ge(s["loaded"], 256)

                def stage_rows(i, p):
                    if not early(i, 2):
                        wait(act, s, i - 1, "xs")
                    act.activation(flat(hs[p]), h_t[:, bass.ds(i * PT, PT)], ACT.Copy).then_inc(s["staged"], 1)

                def first_part(i, p):
                    n = i + 1
                    wait(act, s, n, "mix")
                    act.activation(mix[:, 0:4, :].rearrange("k a t -> k (a t)"), lo[0:32, 0, 0:4 * PT], ACT.Tanh).then_inc(s["tanh"], 1)
                    act.activation(mix[:, 4, :], lo[0:32, 1, 0:PT], ACT.Tanh).then_inc(s["tanh"], 1)
                    wait(act, s, n, "proj_d")
                    act.activation(dh[:], lo[0:64, 0, 0:PT], ACT.Tanh).then_inc(s["d_tanh"], 1)
                    wait(act, s, n, "proj_rkg")
                    act.activation(flat(rk), mp[:, 0, 0:2 * PT], ACT.Copy).then_inc(s["rk"], 1)
                    act.activation(gt[p][:], slot(mp, 2), ACT.Exp, scale=-1.0).then_inc(s["g_exp"], 1)
                    wait(act, s, n, "w_t")
                    act.activation(flat(e), lo[:, 1, 0:PT], ACT.Exp, bias=td[:, 0:1]).then_inc(s["decay"], 1)
                    wait(act, s, n, "proj_v")
                    act.activation(vs[:], mp[0:PT, 1, 0:D], ACT.Copy).then_inc(s["v_copied"], 1)

                def exps(i):
                    wait(act, s, i + 1, "cut")
                    act.activation(ex[:], ex[:], ACT.Exp).then_inc(s["exps"], 1)

                def body(i, p):
                    if not is_last(i):
                        first_part(i + 1, 1 - p)
                    wait(act, s, i + 1, "y_turned")
                    if not early(i, 1):
                        wait(act, s, i, "out_ready")
                    act.activation(yt[:], pa[:, 3, D:D + PT], ACT.Identity, scale=lnw[:, 0:1], bias=lnw[:, 1:2]).then_inc(s["y_affine"], 1)
                    if not isinstance(i, int) or i + 2 < PAIRS:
                        stage_rows(i + 2, p)
                    if not is_last(i):
                        exps(i + 1)

                stage_rows(0, 0)
                stage_rows(1, 1)
                first_part(0, 0)
                exps(0)
                walk(act, PAIRS, body)

            @block.vector
            def _(v):
                v.memset(on[:], 1.0).then_inc(s["cleared"], 1)
                v.memset(cum[:], 0.0).then_inc(s["cleared"], 1)
                v.wait_ge(s["cleared"], 2)
                v.wait_ge(s["loaded"], 256)

                def differences(i, p):
                    n = i + 1
                    wait(v, s, n, "staged")
                    if not early(i, 1):
                        v.wait_ge(s["mixed"], i * 5)
                    v.tensor_tensor(xx[:, :, 1:SEQ], hs[p][:, :, 0:SEQ - 1], hs[p][:, :, 1:SEQ], ALU.subtract).then_inc(s["xx"], 1)
                    v.tensor_scalar(xx[:, :, 0:1], hs[p][:, :, 0:1], -1.0, None, ALU.mult).then_inc(s["xx"], 1)
                    v.wait_ge(s["xx"], n * 2)
                    if not early(i, 1):
                        wait(v, s, i, "mix")
                    v.scalar_tensor_tensor(flat(x3), flat(xx), maa[:, 0:1], flat(hs[p]), ALU.mult, ALU.add).then_inc(s["xxx"], 1)

                def mixtures(i, p):
                    n = i + 1
                    wait(v, s, n, "m")
                    if not early(i, 1):
                        wait(v, s, i, "proj_v")
                    for k in range(5):
                        v.scalar_tensor_tensor(xs[:, k, :], slot(mp, k), maa[:, k + 1:k + 2], flat(xx), ALU.add, ALU.mult).then_inc(s["mixed"], 1)
                    v.wait_ge(s["mixed"], n * 5)
                    v.tensor_tensor(xs[:], xs[:], bc(flat(hs[p])[:, None, :], [D, 5, PT]), ALU.add).then_inc(s["xs"], 1)

                def gate_and_sums(i, p):
                    n = i + 1
                    wait(v, s, n, "g_exp")
                    v.tensor_scalar(gt[p][:], gt[p][:], 1.0, None, ALU.add).then_inc(s["g_one"], 1)
                    wait(v, s, n, "g_one")
                    v.reciprocal(gt[p][:], gt[p][:]).then_inc(s["g_inv"], 1)
                    wait(v, s, n, "g_inv", "rk")
                    v.tensor_tensor(gt[p][:], gt[p][:], slot(mp, 2), ALU.mult).then_inc(s["gate"], 1)
                    wait(v, s, n, "decay")
                    if not early(i, 1):
                        v.wait_ge(s["diffs"], i * (2 * LEVELS))
                    for b in range(2):
                        v.tensor_tensor_scan(cum[:, b, 1:SEQ + 1], on[:], e[:, b, :], 0.0, ALU.mult, ALU.add).then_inc(s["scan"], 1)

                def exponents(i):
                    v.wait_ge(s["scan"], i * 2 + 2)
                    if not early(i, 1):
                        v.wait_ge(s["factors"], i * 4)
                    for l, m in enumerate(HALVES):
                        shape = [D, 2, 64 // (2 * m), 2 * m]
                        blocks = lambda buf: buf.rearrange("d b (c u) -> d b c u", u=2 * m)
                        ref = bc(blocks(cum[:, :, 0:64])[:, :, :, m:m + 1], shape)
                        v.tensor_tensor(blocks(ex[:, 0, l, :, :]), ref, blocks(cum[:, :, 0:64]), ALU.subtract).then_inc(s["diffs"], 1)
                        v.tensor_tensor(blocks(ex[:, 1, l, :, :]), blocks(cum[:, :, 1:65]), ref, ALU.subtract).then_inc(s["diffs"], 1)
                    v.wait_ge(s["diffs"], i * (2 * LEVELS) + 2 * LEVELS)
                    v.tensor_scalar(ex[:], ex[:], 0.0, None, ALU.min).then_inc(s["cut"], 1)

                def factors(i):
                    wait(v, s, i + 1, "exps", "rk")
                    if not early(i, 1):
                        v.wait_ge(s["a_ready"], i * 2)
                    for q in range(2):
                        v.tensor_tensor(fac[:, q, 0:LEVELS, :].rearrange("d l (b t) -> d l b t", b=2), ex[:, q, :, :, 0:SEQ],
                                        bc(rk[:, q, :].rearrange("d (b t) -> d b t", b=2)[:, None, :, :], [D, LEVELS, 2, SEQ]), ALU.mult)\
                            .then_inc(s["factors"], 1)
                    v.tensor_scalar(fac[:, 0, LEVELS, :], rk[:, 0, :], bonus[:, 0:1], None, ALU.mult).then_inc(s["factors"], 1)
                    v.tensor_copy(fac[:, 1, LEVELS, :], rk[:, 1, :]).then_inc(s["factors"], 1)

                def body(i, p):
                    n = i + 1

                    def ahead(step, *args):
                        if not is_last(i):
                            step(i + 1, *args)

                    ahead(differences, 1 - p)
                    for h in range(2):
                        v.wait_ge(s["a_ready"], i * 2 + (h + 1))
                        if not early(i, 1):
                            v.wait_ge(s["a_sum"], (i - 1) * 2 + (h + 1))
                            v.wait_ge(s["y_ready"], i)
                        for q, (lo_l, hi_l) in enumerate(((0, 4), (4, LEVELS + 1))):
                            v.tensor_tensor(am[:, h, lo_l:hi_l, :], pa[0:PT, 2 * h + q, 0:(hi_l - lo_l) * PT].rearrange("s (l t) -> s l t", t=PT),
                                            lm[:, lo_l:hi_l, :], ALU.mult).then_inc(s["a_masked"], 1)
                        v.wait_ge(s["a_masked"], i * 4 + (2 * h + 2))
                        v.tensor_reduce(at[:, h, :], am[:, h, :, :].rearrange("s l t -> s t l"), AX.X, ALU.add).then_inc(s["a_sum"], 1)
                    ahead(mixtures, 1 - p)
                    wait(v, s, n, "y_ready")
                    if not early(i, 1):
                        wait(v, s, i, "y_turned")
                    v.tensor_copy(flat(y), pa[0:PT, 3, 0:D]).then_inc(s["y_copied"], 1)
                    wait(v, s, n, "y_copied")
                    norm_start(v, s, n, y[:], sq[:], st, 64, 1e-5 * 64)
                    ahead(gate_and_sums, 1 - p)
                    norm_end(v, s, n, y[:], st)
                    ahead(exponents)
                    wait(v, s, n, "y_affine")
                    v.tensor_tensor(yt[:], yt[:], gt[p][:], ALU.mult).then_inc(s["gated"], 1)
                    ahead(factors)
                    wait(v, s, n, "out_ready")
                    v.tensor_tensor(x[:, i, :], pa[0:PT, 3, 2 * D:3 * D], x[:, i, :], ALU.add).then_inc(s["done"], 1)

                differences(0, 0)
                mixtures(0, 0)
                gate_and_sums(0, 0)
                exponents(0)
                factors(0)
                walk(v, PAIRS, body)

            @block.gpsimd
            def _(pool):
                walk(pool, PAIRS, lambda i, p: norm_pool(pool, s, i + 1, st, g["half"][0:PT, 0:2]))



def l1_cross(nc, g, a):
    normalise(nc, g, "n4", [("layer", 1e-5)])
    ident, ones, x, h_t = g["ident"], g["ones"], g["x"], g["h_t"]
    C, S, KV = HEADS * SEQ // D, SEQ, 6
    TURNS = KV + 3 * C
    Q4 = 4 * SEQ
    names = ("loaded bq_scaled q_made q_t ctxt0 ctxt1 mask0 mask1 q_ready turned freed0 freed1 scores masked negmax probs inverse diag pv oz_copied "
             "spread o_norm picked u_sum u_ready out_ready out_sum done")
    with stage(nc, "x1", names) as (s, sb, ps):
        wq = sb("wq", [D, D]); wkv = sb("wkv", [D, 2 * D]); wp = sb("wp", [D, D]); bias = sb("bias", [D, 4]); bp = sb("bp", [PT, D]); hm = sb("hm", [D, HEADS]); hm4 = sb("hm4", [D, 4])
        qt = sb("q_t", [D, TOK]); ct = [sb(f"ctx_t{j}", [D, CTX]) for j in range(2)]; mk = [sb(f"mask{j}", [D, CTX]) for j in range(2)]
        qb = [sb(f"q{j}", [D, HEADS, S]) for j in range(2)]; kt = sb("k_t", [D, CTX]); vv = [sb(f"v{j}", [TP, TILES, D]) for j in range(2)]
        pr = [sb(f"pr{k}", [D, CTX]) for k in range(4)]; pt = sb("pt", [TP, TILES, C * D])
        mx = sb("mx", [D, 3]); nm = sb("nm", [D, 3]); l = [sb(f"l{j}", [D, C]) for j in range(2)]; rl = sb("rl", [D, C]); dg = sb("dg", [D, C * D])
        o1 = sb("o1", [D, 4, SEQ]); ub = sb("ub", [D, S]); ut = sb("ut", [D, PT]); acc = sb("acc", [PT, D])
        sc = ps("sc", [D, 6, 512]); turn = ps("turn", [D, 2, 512])
        oz, spread, out = sc[:, 3, :], sc[:, 4, :], sc[:, 5, :]

        def cnt(i, j, per, k):
            return i * (2 * per) + (j * per + k)

        is_first = lambda i, j: isinstance(i, int) and i == 0 and j == 0
        is_last = lambda i, j: isinstance(i, int) and i == PAIRS - 1 and j == 1
        before_of = lambda i, j: (i, 0) if j else (i - 1, 1)
        after_of = lambda i, j: (i, 1) if j == 0 else (i + 1, 0)
        buf_of = lambda c: 3 if c == C - 1 else c % 3
        slot_of = lambda c: slice(2, 3) if c == C - 1 else slice(c % 2, c % 2 + 1)

        def chunk_place(i, j, c, b):
            if c == C - 2 and not is_last(i, j):
                k = 3 * c + 2 * b
            else:
                k = 3 * c + b + (KV if c == C - 1 and not is_last(i, j) else 0)
            return i, KV + TURNS * j + k

        def keys_place(i, j, b):
            if is_first(i, j):
                return 0, b
            q, p = before_of(i, j)
            return q, KV + TURNS * p + 3 * (C - 2) + 2 * b + 1

        def values_place(i, j, b):
            if is_first(i, j):
                return 0, 3 + b
            q, p = before_of(i, j)
            return q, KV + TURNS * p + 3 * (C - 1) + 3 + b

        def emitted(place):
            i, n = place
            return i * (2 * TURNS) + (n + 1)

        def freed(place):
            i, n = place
            return s[f"freed{n % 2}"], i * TURNS + (n // 2 + 1)

        with nc.Block() as block:
            @block.sync
            def _(sp):
                for dst, drm in ((wq[:], a["L1_xattn_wq"]), (wkv[:], a["L1_xattn_wkv"]), (wp[:], a["L1_xattn_wp"]), (bias[:, 0:1], a["L1_xattn_bq"]),
                                 (bias[:, 1:2], a["L1_xattn_bk"]), (bias[:, 2:3], a["L1_xattn_bv"]), (bp[:], bc(a["L1_xattn_bp"], [PT, D])),
                                 (hm[:], g["headmask"]), (hm4[:], g["consts"]["headmask4"])):
                    sp.dma_start(dst, drm).then_inc(s["loaded"], 16)

                def body(i):
                    for j in range(2):
                        if not (isinstance(i, int) and i == 0):
                            sp.wait_ge(s["turned"], emitted(values_place(i - 1, j, 2)))
                            apart(sp)
                            sp.wait_ge(s["masked"], cnt(i - 1, j, C, C))
                        sp.dma_start(ct[j][:], a["ctx_t"][bass.ds(i * 2 + j, 1), :, :].rearrange("o d c -> (o d) c")).then_inc(s[f"ctxt{j}"], 16)
                        sp.dma_start(mk[j][:], bc(a["ctx_mask"][bass.ds(i * 2 + j, 1), :, :].rearrange("o r c -> (o r) c"), [D, CTX]))\
                            .then_inc(s[f"mask{j}"], 16)
                rounds(sp, body)

            @block.tensor
            def _(pe):
                pe.wait_ge(s["loaded"], 144)
                for b in range(4):
                    pe.matmul(sc[:, b, 0:GT], wq[:], h_t[:, b * GT:(b + 1) * GT], start=True, stop=True).then_inc(s["q_made"], 1)
                pe.wait_ge(s["q_t"], 4)

                def group(place, emit):
                    i, n = place
                    if not (isinstance(i, int) and i == 0 and n < 2):
                        pe.wait_ge(s[f"freed{n % 2}"], i * TURNS + n // 2)
                    emit(turn[:, n % 2, :]).then_inc(s["turned"], 1)

                def keys(i, j, b):
                    if b == 0:
                        pe.wait_ge(s[f"ctxt{j}"], i * 16 + 16)
                    group(keys_place(i, j, b), lambda bank: pe.matmul(bank[:, 0:BANKC], wkv[:, 0:D], ct[j][:, b * BANKC:(b + 1) * BANKC], start=True, stop=True))

                def values(i, j, b):
                    def tiles(bank):
                        for t in range(4):
                            mm = pe.matmul(bank[0:TP, t * D:(t + 1) * D], ct[j][:, (4 * b + t) * TP:(4 * b + t + 1) * TP], wkv[:, D:2 * D],
                                           start=True, stop=True)
                        return mm
                    group(values_place(i, j, b), tiles)

                def pair_out(i):
                    pe.wait_ge(s["u_ready"], cnt(i, 1, 1, 1))
                    pe.matmul(out[0:PT, 0:D], ut[:], wp[:], start=True, stop=True).then_inc(s["out_ready"], 1)

                def score(i, j, c, fill=None):
                    if c >= 2:
                        pe.wait_ge(s["masked"], cnt(i, j, C, c - 1))
                    elif c == 0:
                        if not is_first(i, j):
                            pe.wait_ge(s["masked"], cnt(i, j, C, 0))
                        for b in (1, 2) if is_first(i, j) else (2,):
                            pe.wait_ge(*freed(keys_place(i, j, b)))
                        pe.wait_ge(s["q_ready"], cnt(i, j, 1, 1))
                    elif not is_first(i, j):
                        pe.wait_ge(s["oz_copied"], cnt(i, j, 1, 0))
                        pe.wait_ge(s["o_norm"], cnt(i, j, 1, 0))
                        if j == 1 and not (isinstance(i, int) and i == 0):
                            pe.wait_ge(s["out_sum"], i)
                    for b in range(3):
                        mm = pe.matmul(sc[:, 3 * (c % 2) + b, 0:BANKC], qb[j].rearrange("d h t -> d (h t)")[:, c * D:(c + 1) * D],
                                       kt[:, b * BANKC:(b + 1) * BANKC], start=True, stop=True)
                        if fill is not None and b < 2:
                            fill(b)
                    mm.then_inc(s["scores"], 1)

                def body(i):
                    for j in range(2):
                        after = after_of(i, j)
                        more = not is_last(i, j)

                        def turn_group(c, b):
                            def tiles(bank):
                                for t in range(4):
                                    mm = pe.transpose(bank[0:TP, t * D:(t + 1) * D], pr[buf_of(c)][:, (4 * b + t) * TP:(4 * b + t + 1) * TP], ident[:])
                                return mm
                            if b == 0:
                                pe.wait_ge(s["probs"], cnt(i, j, C, c + 1))
                            group(chunk_place(i, j, c, b), tiles)

                        turn_group(0, 0)
                        turn_group(0, 1)
                        score(i, j, 1)
                        turn_group(0, 2)
                        score(i, j, 2)
                        for c in range(1, C - 2):
                            score(i, j, c + 2, lambda b: turn_group(c, b))
                            turn_group(c, 2)
                        for b in range(3):
                            turn_group(C - 2, b)
                            if more:
                                keys(*after, b)
                        if more:
                            for b in range(3):
                                values(*after, b)
                            score(*after, 0)
                        for b in range(3):
                            turn_group(C - 1, b)
                        if j == 0 and not (isinstance(i, int) and i == 0):
                            pair_out(i - 1)
                        for b in (1, 2):
                            pe.wait_ge(*freed(chunk_place(i, j, C - 1, b)))
                        for t in range(TILES):
                            for q in range(4):
                                mm = pe.matmul(oz[32 * q:32 * q + 32, 0:Q4], vv[j][:, t, 32 * q:32 * q + 32], pt[:, t, Q4 * q:Q4 * (q + 1)],
                                               start=(t == 0), stop=(t == TILES - 1), tile_position=(0, 32 * q))
                        mm.then_inc(s["pv"], 1)
                        pe.wait_ge(s["diag"], cnt(i, j, 1, 1))
                        for q in range(4):
                            mm = pe.matmul(spread[32 * q:32 * q + 32, 0:Q4], ones[:, 32 * q:32 * q + 32], dg[:, Q4 * q:Q4 * (q + 1)],
                                           start=True, stop=True, tile_position=(0, 32 * q))
                        mm.then_inc(s["spread"], 1)

                for b in range(3):
                    keys(0, 0, b)
                for b in range(3):
                    values(0, 0, b)
                score(0, 0, 0)
                rounds(pe, body)
                pair_out(PAIRS - 1)

            @block.scalar
            def _(act):
                act.wait_ge(s["bq_scaled"], 1)
                for b in range(4):
                    act.wait_ge(s["q_made"], b + 1)
                    act.activation(qt[:, b * GT:(b + 1) * GT], sc[:, b, 0:GT], ACT.Identity, scale=8 ** -0.5, bias=bias[:, 3:4]).then_inc(s["q_t"], 1)

                def copy_group(place, dst, src, **kw):
                    if place[1] % 2 == 0:
                        act.wait_ge(s["turned"], emitted(place))
                        act.activation(dst, src, ACT.Identity if kw else ACT.Copy, **kw).then_inc(s["freed0"], 1)

                def copy_keys(i, j, b):
                    copy_group(keys_place(i, j, b), kt[:, b * BANKC:(b + 1) * BANKC], turn[:, 0, 0:BANKC], bias=bias[:, 1:2])

                def copy_values(i, j):
                    for b in range(3):
                        copy_group(values_place(i, j, b), vv[j][:, 4 * b:4 * b + 4, :], turn[0:TP, 0, :].rearrange("p (t d) -> p t d", d=D))

                def copy_probs(i, j, c, b):
                    copy_group(chunk_place(i, j, c, b), pt[:, 4 * b:4 * b + 4, c * D:(c + 1) * D], turn[0:TP, 0, :].rearrange("p (t q) -> p t q", t=4))

                def exps(i, j, c):
                    act.wait_ge(s["negmax"], cnt(i, j, C, c + 1))
                    act.activation(pr[buf_of(c)][:], pr[buf_of(c)][:], ACT.Exp, bias=nm[:, slot_of(c)], accum_out=l[j][:, c:c + 1]).then_inc(s["probs"], 1)

                def body(i):
                    for j in range(2):
                        after = after_of(i, j)
                        more = not is_last(i, j)
                        for c in range(C - 2):
                            copy_probs(i, j, c, 0)
                            exps(i, j, c + 1)
                            copy_probs(i, j, c, 1)
                            copy_probs(i, j, c, 2)
                        for b in range(3):
                            if b == 2:
                                exps(i, j, C - 1)
                            copy_probs(i, j, C - 2, b)
                            if more:
                                copy_keys(*after, b)
                        if more:
                            copy_values(*after)
                        for b in range(3):
                            copy_probs(i, j, C - 1, b)
                        if more:
                            exps(*after, 0)
                        act.wait_ge(s["pv"], cnt(i, j, 1, 1))
                        if not is_first(i, j):
                            act.wait_ge(s["u_sum"], cnt(i, j, 1, 0))
                        act.activation(o1.rearrange("d h t -> d (h t)"), oz[:, 0:Q4], ACT.Copy).then_inc(s["oz_copied"], 1)

                for b in range(3):
                    copy_keys(0, 0, b)
                copy_values(0, 0)
                exps(0, 0, 0)
                rounds(act, body)

            @block.gpsimd
            def _(pool):
                pool.wait_ge(s["q_t"], 4)
                pool.wait_ge(s["loaded"], 144)

                def body(i):
                    for j in range(2):
                        if not (isinstance(i, int) and i == 0):
                            pool.wait_ge(s["scores"], cnt(i - 1, j, C, C))
                        pool.tensor_tensor(qb[j][:], bc(qt[:, bass.ds((i * 2 + j) * S, S)][:, None, :], [D, HEADS, S]),
                                           bc(hm[:, :, None], [D, HEADS, S]), ALU.mult).then_inc(s["q_ready"], 1)
                rounds(pool, body)

            @block.vector
            def _(v):
                v.wait_ge(s["loaded"], 144)
                v.tensor_scalar(bias[:, 3:4], bias[:, 0:1], 8 ** -0.5, None, ALU.mult).then_inc(s["bq_scaled"], 1)

                def add_out(i):
                    v.wait_ge(s["out_ready"], i + 1)
                    v.tensor_tensor(acc[:], out[0:PT, 0:D], bp[:], ALU.add).then_inc(s["out_sum"], 1)
                    v.wait_ge(s["out_sum"], i + 1)
                    v.tensor_tensor(x[:, i, :], acc[:], x[:, i, :], ALU.add).then_inc(s["done"], 1)

                def copy_group(place, emit):
                    if place[1] % 2:
                        v.wait_ge(s["turned"], emitted(place))
                        emit().then_inc(s["freed1"], 1)

                def copy_keys(i, j, b):
                    copy_group(keys_place(i, j, b), lambda: v.tensor_scalar(kt[:, b * BANKC:(b + 1) * BANKC], turn[:, 1, 0:BANKC], bias[:, 1:2], None, ALU.add))

                def copy_values(i, j):
                    for b in range(3):
                        copy_group(values_place(i, j, b), lambda: v.tensor_copy(vv[j][:, 4 * b:4 * b + 4, :], turn[0:TP, 1, :].rearrange("p (t d) -> p t d", d=D)))

                def copy_probs(i, j, c, b):
                    copy_group(chunk_place(i, j, c, b), lambda: v.tensor_copy(pt[:, 4 * b:4 * b + 4, c * D:(c + 1) * D],
                                                                              turn[0:TP, 1, :].rearrange("p (t q) -> p t q", t=4)))

                def maxima(i, j, c):
                    v.wait_ge(s["scores"], cnt(i, j, C, c + 1))
                    if c == 0:
                        v.wait_ge(s[f"mask{j}"], i * 16 + 16)
                    if c == C - 1:
                        v.wait_ge(s["turned"], emitted(chunk_place(i, j, 0, 0)))
                    elif c >= 3:
                        v.wait_ge(s["turned"], emitted(chunk_place(i, j, c - 3, 2)))
                    elif not is_first(i, j):
                        v.wait_ge(s["turned"], emitted(chunk_place(*before_of(i, j), c + 3, 2)))
                    if c >= 2:
                        v.wait_ge(s["probs"], cnt(i, j, C, c - 1))
                    elif not is_first(i, j):
                        v.wait_ge(s["probs"], cnt(i, j, C, c - 2))
                    apart(v)
                    v.tensor_tensor_reduce(pr[buf_of(c)].rearrange("q (a b) -> q a b", a=3), sc[:, 3 * (c % 2):3 * (c % 2) + 3, 0:BANKC],
                                           mk[j].rearrange("q (a b) -> q a b", a=3), 1.0, -3.0e38, ALU.add, ALU.max, mx[:, slot_of(c)])\
                        .then_inc(s["masked"], 1)
                    v.wait_ge(s["masked"], cnt(i, j, C, c + 1))
                    v.tensor_scalar(nm[:, slot_of(c)], mx[:, slot_of(c)], -1.0, None, ALU.mult).then_inc(s["negmax"], 1)

                for b in range(3):
                    copy_keys(0, 0, b)
                copy_values(0, 0)
                maxima(0, 0, 0)

                def body(i):
                    for j in range(2):
                        first = is_first(i, j)
                        after = after_of(i, j)
                        more = not is_last(i, j)
                        for b in range(3):
                            copy_probs(i, j, 0, b)
                        maxima(i, j, 1)
                        maxima(i, j, 2)
                        for c in range(1, C - 2):
                            for b in range(3):
                                copy_probs(i, j, c, b)
                            if c + 2 < C - 1:
                                maxima(i, j, c + 2)
                        for b in range(3):
                            copy_probs(i, j, C - 2, b)
                            if more:
                                copy_keys(*after, b)
                            if b == 0:
                                maxima(i, j, C - 1)
                        if more:
                            copy_values(*after)
                        for b in range(3):
                            copy_probs(i, j, C - 1, b)
                        if more:
                            maxima(*after, 0)
                        if j == 0 and not (isinstance(i, int) and i == 0):
                            add_out(i - 1)
                        v.wait_ge(s["probs"], cnt(i, j, C, C))
                        v.reciprocal(rl[:], l[j][:]).then_inc(s["inverse"], 1)
                        v.wait_ge(s["inverse"], cnt(i, j, 1, 1))
                        v.tensor_tensor(dg.rearrange("p (c q) -> p c q", c=C), bc(ident[:, None, :], [D, C, D]), bc(rl[:, :, None], [D, C, D]), ALU.mult)\
                            .then_inc(s["diag"], 1)
                        v.wait_ge(s["spread"], cnt(i, j, 1, 1))
                        v.wait_ge(s["oz_copied"], cnt(i, j, 1, 1))
                        v.tensor_tensor(o1.rearrange("d h t -> d (h t)"), o1.rearrange("d h t -> d (h t)"), spread[:, 0:Q4], ALU.mult).then_inc(s["o_norm"], 1)
                        v.wait_ge(s["o_norm"], cnt(i, j, 1, 1))
                        v.tensor_tensor(o1[:], o1[:], bc(hm4[:, :, None], [D, 4, SEQ]), ALU.mult).then_inc(s["picked"], 1)
                        v.wait_ge(s["picked"], cnt(i, j, 1, 1))
                        v.tensor_reduce(ub[:], o1.rearrange("d h t -> d t h"), AX.X, ALU.add).then_inc(s["u_sum"], 1)
                        v.wait_ge(s["u_sum"], cnt(i, j, 1, 1))
                        if j == 0 and not first:
                            v.wait_ge(s["out_ready"], i)
                        v.tensor_scalar(ut[:, j * S:(j + 1) * S], ub[:], bias[:, 2:3], None, ALU.add).then_inc(s["u_ready"], 1)

                rounds(v, body)
                add_out(PAIRS - 1)



def l1_ffn(nc, g, a):
    normalise(nc, g, "n5", [("layer", 1e-5)])
    ident, x, h_n, h_t, C = g["ident"], g["x"], g["h_n"], g["h_t"], g["consts"]
    names = ("loaded staged gate_exp gate_one gate picked_t mask_t copied_n normed_t turned_n spread affine masked inner relu outer "
             "weighed summed biased bias_in gated resid done " + NORM_STEPS + ROUTE_STEPS)
    with stage(nc, "f1", names) as (s, sb, ps):
        wc = sb("centroids", [D, EXPERTS]); lg = sb("ln_g", [D, EXPERTS]); lb = sb("ln_b", [D, EXPERTS])
        w1 = sb("w1", [D, EXPERTS, 512]); b1 = sb("b1", [EXPERTS, 512]); w2 = sb("w2", [D, 4, EXPERTS, D]); b2 = sb("b2", [EXPERTS, D])
        pick = sb("pick", [EXPERTS, EXPERTS, D]); early = sb("earlier", [D, EXPERTS])
        hs = sb("hs", [D, GT]); xn = sb("xn", [D, GT]); xa = sb("xa", [D, GT]); xm = sb("xm", [D, EXPERTS, GT])
        re = sb("relu", [D, 4, GT]); oht = sb("oht", [EXPERTS, GT])
        oh = sb("oh", [PT, GROUP, EXPERTS]); rank = sb("rank", [PT, GROUP, EXPERTS]); top = sb("top", [PT, GROUP]); gate = sb("gate", [PT, GROUP])
        y = sb("y", [PT, GROUP, D]); sq = sb("ysq", [PT, GROUP, D]); wy = sb("wy", [PT, EXPERTS, D]); fo = sb("fo", [PT, D])
        st = [sb(f"st{k}", [PT, GROUP])[:] for k in range(5)]
        small = ps("small", [D, 512]); spread = ps("spread", [D, 2, 512]); inner = ps("inner", [D, 4, 512]); bias = ps("bias", [D, 512])
        with nc.Block() as block:
            @block.sync
            def _(sp):
                for dst, drm in ((wc[:], a["L1_ffn_centroids"]), (lg[:], a["L1_ffn_g"]), (lb[:], a["L1_ffn_b"]), (w1[:], a["L1_ffn_w1"]),
                                 (b1[:], a["L1_ffn_b1"]), (w2[:], a["L1_ffn_w2"]), (b2[:], a["L1_ffn_b2"]),
                                 (pick[:], C["pick"]), (early[:], C["earlier"])):
                    sp.dma_start(dst, drm).then_inc(s["loaded"], 16)

            @block.tensor
            def _(pe):
                pe.wait_ge(s["loaded"], 144)
                with pe.Fori(0, 4) as c:
                    n = c + 1
                    wait(pe, s, n, "staged")
                    for t in range(GROUP):
                        mm = pe.matmul(small[0:PT, t * EXPERTS:(t + 1) * EXPERTS], hs[:, t * PT:(t + 1) * PT], wc[:], start=True, stop=True)
                    mm.then_inc(s["r_logits"], 1)
                    wait(pe, s, n, "r_picked")
                    for t in range(GROUP):
                        mm = pe.transpose(spread[0:EXPERTS, 0, t * PT:(t + 1) * PT], oh[:, t, :], ident[0:PT, 0:PT])
                    mm.then_inc(s["picked_t"], 1)
                    wait(pe, s, n, "n_normed")
                    for t in range(GROUP):
                        mm = pe.transpose(spread[:, 1, t * PT:(t + 1) * PT], y[:, t, :], ident[0:PT, 0:PT])
                    mm.then_inc(s["turned_n"], 1)
                    wait(pe, s, n, "mask_t", "copied_n")
                    for e in range(EXPERTS):
                        if e >= 2:
                            pe.wait_ge(s["masked"], c * EXPERTS + (e - 1))
                        pe.matmul(spread[:, e % 2, 0:GT], pick[:, e, :], oht[:], start=True, stop=True).then_inc(s["spread"], 1)
                    pe.wait_ge(s["masked"], n * EXPERTS)
                    for f in range(4):
                        for e in range(EXPERTS):
                            pe.matmul(inner[:, f, 0:GT], w1[:, e, f * D:(f + 1) * D], xm[:, e, :], start=(e == 0), stop=False)
                        pe.matmul(inner[:, f, 0:GT], b1[:, f * D:(f + 1) * D], oht[:], start=False, stop=True).then_inc(s["inner"], 1)
                    pe.wait_ge(s["relu"], n * 4)
                    for t in range(GROUP):
                        pe.matmul(bias[0:PT, t * D:(t + 1) * D], oht[:, t * PT:(t + 1) * PT], b2[:], start=True, stop=True)
                    for t in range(GROUP):
                        if t:
                            pe.wait_ge(s["weighed"], c * GROUP + t)
                        for q in range(2):
                            for f in range(4):
                                mm = pe.matmul(inner[0:PT, q, :], re[:, f, t * PT:(t + 1) * PT], w2[:, f, 4 * q:4 * q + 4, :],
                                               start=(f == 0), stop=(f == 3))
                        mm.then_inc(s["outer"], 1)

            @block.scalar
            def _(act):
                with act.Fori(0, 4) as c:
                    n = c + 1
                    act.wait_ge(s["done"], c)
                    act.activation(hs[:], h_t[:, bass.ts(c, GT)], ACT.Copy).then_inc(s["staged"], 1)
                    act.activation(y[:], h_n[:, bass.ts(c, GROUP), :], ACT.Copy).then_inc(s["resid"], 1)
                    wait(act, s, n, "r_logits", "r_max")
                    act.activation(gate[:], top[:], ACT.Exp, scale=-1.0).then_inc(s["gate_exp"], 1)
                    wait(act, s, n, "picked_t")
                    act.activation(oht[:], spread[0:EXPERTS, 0, 0:GT], ACT.Copy).then_inc(s["mask_t"], 1)
                    wait(act, s, n, "turned_n")
                    act.activation(xn[:], spread[:, 1, 0:GT], ACT.Copy).then_inc(s["copied_n"], 1)
                    for f in range(4):
                        act.wait_ge(s["inner"], c * 4 + (f + 1))
                        act.activation(re[:, f, :], inner[:, f, 0:GT], ACT.Relu).then_inc(s["relu"], 1)

            @block.vector
            def _(v):
                v.wait_ge(s["loaded"], 144)
                with v.Fori(0, 4) as c:
                    n = c + 1
                    wait(v, s, n, "r_logits")
                    logits = small[0:PT, 0:GROUP * EXPERTS].rearrange("t (a e) -> t a e", e=EXPERTS)
                    v.tensor_reduce(top[:], logits, AX.X, ALU.max).then_inc(s["r_max"], 1)
                    wait(v, s, n, "r_max")
                    v.tensor_tensor(rank[:], logits, bc(top[:, :, None], [PT, GROUP, EXPERTS]), ALU.is_equal).then_inc(s["r_best"], 1)
                    wait(v, s, n, "r_best")
                    v.tensor_tensor(rank[:], rank[:], bc(early[0:PT, None, :], [PT, GROUP, EXPERTS]), ALU.mult).then_inc(s["r_order"], 1)
                    wait(v, s, n, "r_order", "gate_exp")
                    v.tensor_reduce(top[:], rank[:], AX.X, ALU.max).then_inc(s["r_first"], 1)
                    wait(v, s, n, "r_first")
                    v.tensor_tensor(oh[:], rank[:], bc(top[:, :, None], [PT, GROUP, EXPERTS]), ALU.is_equal).then_inc(s["r_picked"], 1)
                    v.tensor_scalar(gate[:], gate[:], 1.0, None, ALU.add).then_inc(s["gate_one"], 1)
                    wait(v, s, n, "gate_one")
                    v.reciprocal(gate[:], gate[:]).then_inc(s["gate"], 1)
                    wait(v, s, n, "resid")
                    norm_vector(v, s, n, y[:], sq[:], st, D, 1e-5)
                    wait(v, s, n, "copied_n")
                    for e in range(EXPERTS):
                        if e:
                            v.wait_ge(s["masked"], c * EXPERTS + e)
                        v.tensor_scalar(xa[:], xn[:], lg[:, e:e + 1], lb[:, e:e + 1], ALU.mult, ALU.add).then_inc(s["affine"], 1)
                        v.wait_ge(s["affine"], c * EXPERTS + (e + 1))
                        v.wait_ge(s["spread"], c * EXPERTS + (e + 1))
                        v.tensor_tensor(xm[:, e, :], xa[:], spread[:, e % 2, 0:GT], ALU.mult).then_inc(s["masked"], 1)
                    for t in range(GROUP):
                        m = c * GROUP + (t + 1)
                        wait(v, s, m, "outer")
                        v.tensor_tensor(wy.rearrange("t (q e) d -> t q e d", q=2), inner[0:PT, 0:2, :].rearrange("t q (e d) -> t q e d", e=4),
                                        bc(oh[:, t, :].rearrange("t (q e) -> t q e", q=2)[:, :, :, None], [PT, 2, 4, D]), ALU.mult)\
                            .then_inc(s["weighed"], 1)
                        wait(v, s, m, "weighed")
                        v.tensor_reduce(fo[:], wy.rearrange("t e d -> t d e"), AX.X, ALU.add).then_inc(s["summed"], 1)
                        wait(v, s, m, "summed")
                        v.tensor_tensor(fo[:], fo[:], bias[0:PT, t * D:(t + 1) * D], ALU.add).then_inc(s["biased"], 1)
                        wait(v, s, m, "biased")
                        v.scalar_tensor_tensor(sq[:, t, :], fo[:], gate[:, t:t + 1], h_n[:, c * GROUP + t, :], ALU.mult, ALU.add)\
                            .then_inc(s["gated"], 1)
                    v.wait_ge(s["gated"], n * GROUP)
                    v.tensor_tensor(x[:, bass.ts(c, GROUP), :], x[:, bass.ts(c, GROUP), :], sq[:], ALU.add).then_inc(s["done"], 1)

            @block.gpsimd
            def _(pool):
                with pool.Fori(0, 4) as c:
                    norm_pool(pool, s, c + 1, st, g["half"][0:PT, 0:GROUP])



STATES = 16


def l2_attention(nc, g, a):
    normalise(nc, g, "n6", [("layer", 1e-5)])
    ident, x, h_t = g["ident"], g["x"], g["h_t"]
    names = ("loaded alog_exp a_ready dt_proj biased absed exped logged dt_ready du_ready y_start spread_w dA0 dA1 reset0 reset1 b_ready c_ready "
             "ub scan0 scan1 hc0 hc1 acc0 acc1 turned added")
    with stage(nc, "s2", names) as (s, sb, ps):
        wd = sb("w_dt", [D, D]); bd = sb("b_dt", [D, 1]); wbc = sb("w_bc", [D, 2, STATES]); an = sb("a", [D, STATES]); dd = sb("d", [D, 1])
        dt = sb("dt", [D, TOK]); ab = sb("abs", [D, TOK]); du = sb("du", [D, TOK]); y = sb("y", [D, TOK]); ub = sb("ub", [D, TOK])
        dA = [sb(f"dA{j}", [D, TOK]) for j in range(2)]; hc = [sb(f"hc{j}", [D, TOK]) for j in range(2)]
        wb = sb("wb", [D, 2, D])
        pb = ps("pb", [D, 4, 512]); pc = ps("pc", [D, 4, 512])
        four = lambda buf: buf.rearrange("d (a b) -> d a b", a=4)
        with nc.Block() as block:
            @block.sync
            def _(sp):
                for dst, drm in ((wd[:], a["L2_dt"]), (bd[:], a["L2_bdt"]), (wbc[:], a["L2_bc"]), (an[:], a["L2_alog"]), (dd[:], a["L2_d"])):
                    sp.dma_start(dst, drm).then_inc(s["loaded"], 16)

            @block.tensor
            def _(pe):
                pe.wait_ge(s["loaded"], 80)
                for b in range(4):
                    mm = pe.matmul(pb[:, b, 0:GT], wd[:], h_t[:, b * GT:(b + 1) * GT], start=True, stop=True)
                mm.then_inc(s["dt_proj"], 1)
                pe.wait_ge(s["biased"], 1)
                with pe.Fori(0, STATES // 2) as i:
                    for j in range(2):
                        m = i * 2 + (j + 1)
                        wait(pe, s, m, "spread_w")
                        pe.wait_ge(s["ub"], i * 2 + j)
                        for b in range(4):
                            mm = pe.matmul(pb[:, b, 0:GT], wb[:, 0, :], h_t[:, b * GT:(b + 1) * GT], start=True, stop=True)
                        mm.then_inc(s["b_ready"], 1)
                        pe.wait_ge(s[f"hc{1 - j}"], i + j)
                        for b in range(4):
                            mm = pe.matmul(pc[:, b, 0:GT], wb[:, 1, :], h_t[:, b * GT:(b + 1) * GT], start=True, stop=True)
                        mm.then_inc(s["c_ready"], 1)
                pe.wait_ge(s["acc1"], STATES // 2)
                pe.wait_ge(s["hc1"], STATES // 2)
                for t in range(PAIRS):
                    mm = pe.transpose(pb[0:PT, t // 4, (t % 4) * D:(t % 4 + 1) * D], y[:, t * PT:(t + 1) * PT], ident[:])
                mm.then_inc(s["turned"], 1)

            @block.scalar
            def _(act):
                act.wait_ge(s["loaded"], 80)
                act.activation(an[:], an[:], ACT.Exp).then_inc(s["alog_exp"], 1)
                act.wait_ge(s["absed"], 1)
                act.activation(ab[:], ab[:], ACT.Exp, scale=-1.0).then_inc(s["exped"], 1)
                act.wait_ge(s["exped"], 1)
                act.activation(ab[:], ab[:], ACT.Ln, bias=1.0).then_inc(s["logged"], 1)
                act.wait_ge(s["dt_ready"], 1)
                act.wait_ge(s["a_ready"], 1)
                with act.Fori(0, STATES // 2) as i:
                    for j in range(2):
                        m = i * 2 + (j + 1)
                        n = i * 2 + j
                        act.wait_ge(s["c_ready"], i * 2 + j)
                        act.activation(wb[:], bc(wbc[:, :, bass.ds(n, 1)], [D, 2, D]), ACT.Copy).then_inc(s["spread_w"], 1)
                        act.wait_ge(s[f"scan{j}"], i)
                        act.activation(dA[j][:], dt[:], ACT.Exp, scale=an[:, bass.ds(n, 1)]).then_inc(s[f"dA{j}"], 1)

            @block.vector
            def _(v):
                v.wait_ge(s["loaded"], 80)
                v.wait_ge(s["dt_proj"], 1)
                v.tensor_scalar(four(dt), pb[:, :, 0:GT], bd[:, 0:1], None, ALU.add).then_inc(s["biased"], 1)
                v.wait_ge(s["biased"], 1)
                v.scalar_tensor_tensor(ab[:], dt[:], -1.0, dt[:], ALU.mult, ALU.max).then_inc(s["absed"], 1)
                v.wait_ge(s["alog_exp"], 1)
                v.tensor_scalar(an[:], an[:], -1.0, None, ALU.mult).then_inc(s["a_ready"], 1)
                v.wait_ge(s["logged"], 1)
                v.scalar_tensor_tensor(dt[:], dt[:], 0.0, ab[:], ALU.max, ALU.add).then_inc(s["dt_ready"], 1)
                v.wait_ge(s["dt_ready"], 1)
                v.tensor_tensor(du[:], dt[:], h_t[:], ALU.mult).then_inc(s["du_ready"], 1)
                v.wait_ge(s["du_ready"], 1)
                with v.Fori(0, STATES // 2) as i:
                    for j in range(2):
                        m = i * 2 + (j + 1)
                        wait(v, s, m, "b_ready")
                        v.wait_ge(s[f"scan{1 - j}"], i + j)
                        v.tensor_tensor(four(ub), four(du), pb[:, :, 0:GT], ALU.mult).then_inc(s["ub"], 1)
                        v.wait_ge(s[f"reset{j}"], i + 1)
                        v.wait_ge(s[f"acc{j}"], i)
                        wait(v, s, m, "ub")
                        v.tensor_tensor_scan(hc[j][:], dA[j][:], ub[:], 0.0, ALU.mult, ALU.add).then_inc(s[f"scan{j}"], 1)
                        v.wait_ge(s[f"scan{j}"], i + 1)
                        wait(v, s, m, "c_ready")
                        v.tensor_tensor(four(hc[j]), four(hc[j]), pc[:, :, 0:GT], ALU.mult).then_inc(s[f"hc{j}"], 1)
                v.wait_ge(s["turned"], 1)
                v.tensor_tensor(x.rearrange("t (a b) d -> t a (b d)", a=4), x.rearrange("t (a b) d -> t a (b d)", a=4), pb[0:PT, :, :], ALU.add)\
                    .then_inc(s["added"], 1)

            @block.gpsimd
            def _(pool):
                pool.wait_ge(s["loaded"], 80)
                pool.tensor_scalar(y[:], h_t[:], dd[:, 0:1], None, ALU.mult).then_inc(s["y_start"], 1)
                pool.wait_ge(s["y_start"], 1)
                with pool.Fori(0, STATES // 2) as i:
                    for j in range(2):
                        pool.wait_ge(s[f"dA{j}"], i + 1)
                        apart(pool)
                        pool.memset(dA[j].rearrange("d (b t) -> d b t", t=SEQ)[:, :, 0:1], 0.0).then_inc(s[f"reset{j}"], 1)
                        pool.wait_ge(s[f"acc{1 - j}"], i + j)
                        pool.wait_ge(s[f"hc{j}"], i + 1)
                        pool.tensor_tensor(y[:], y[:], hc[j][:], ALU.add).then_inc(s[f"acc{j}"], 1)



def l2_cross(nc, g, a):
    normalise(nc, g, "n7", [("layer", 1e-5)])
    ident, ones, x, h_t, csum = g["ident"], g["ones"], g["x"], g["h_t"], g["ctx_sum"]
    names = ("loaded cleared biassum cs cqw_ready scores rowmax negmax probs inverse turned copied pv c2q_normed c2q_turned c2q "
             "own own_row own_max own_shifted own_exp own_sum own_inv own_norm own_bc weighted q2c prod1 features out_ready out_sum done summed "
             "ctx0 ctx1 ctxt0 ctxt1")
    HALF = 64
    with stage(nc, "x2", names) as (s, sb, ps):
        cols = sb("cols", [D, 3]); bias = sb("bias", [D, 3]); bsum = sb("bsum", [D, 2]); wl = sb("wl", [D, 4, D]); bl = sb("bl", [PT, D])
        ct = [sb(f"ctx_t{p}", [D, 2, CTX]) for p in range(2)]; cn = [sb(f"ctx_n{p}", [TP, 2, TILES, D]) for p in range(2)]
        feat = [sb(f"feat{p}", [D, 4, 2, SEQ]) for p in range(2)]; cq = sb("cq", [D, 2, HALF]); hp = sb("hp", [D, 2, HALF]); pr = sb("pr", [D, CTX]); pt = sb("pt", [TP, TILES, D])
        mx = sb("mx", [D, 1]); nm = sb("nm", [D, 1]); l = sb("l", [D, 1]); il = sb("il", [D, 1]); c2n = sb("c2n", [D, D])
        own = sb("own", [D, 1]); row = sb("row", [1, 2, HALF]); r1 = sb("r1", [1, 3, 2]); wc = sb("wc", [D, 2, SEQ]); q2c = sb("q2c", [D, 2])
        acc = sb("acc", [PT, D])
        sc = ps("sc", [D, 3, 512]); turn = ps("turn", [D, 2, 512]); pv = ps("pv", [D, 512]); mi = ps("mi", [D, 512]); out = ps("out", [D, 512])
        flat = lambda buf: buf.rearrange("d j t -> d (j t)")

        def walk(eng, body):
            def two(q):
                for p in range(2):
                    body(q * 2 + p, p, q)
            two(0)
            with eng.Fori(1, PAIRS // 2 - 1) as q:
                two(q)
            two(PAIRS // 2 - 1)

        is_last = lambda i: isinstance(i, int) and i == PAIRS - 1
        at_start = lambda i, n: isinstance(i, int) and i < n

        with nc.Block() as block:
            @block.sync
            def _(sp):
                for dst, drm in ((cols[:], a["L2_x_cols"]), (bias[:], bc(a["L2_x_bias"], [D, 3])), (wl[:], a["L2_x_wl"]), (bl[:], bc(a["L2_x_bl"], [PT, D]))):
                    sp.dma_start(dst, drm).then_inc(s["loaded"], 16)

                def body(i, p, q):
                    if not at_start(i, 2):
                        sp.wait_ge(s["scores"], i - 1)
                        apart(sp)
                        sp.wait_ge(s["summed"], (i - 1) * 2)
                    for j in range(2):
                        sp.dma_start(ct[p][:, j, :], a["ctx_t"][bass.ds(i * 2 + j, 1), :, :].rearrange("o d c -> (o d) c")).then_inc(s[f"ctxt{p}"], 16)
                    if not at_start(i, 2):
                        sp.wait_ge(s["pv"], i - 1)
                        apart(sp)
                    for j in range(2):
                        sp.dma_start(cn[p][:, j, :, :], a["ctx"][bass.ds(i * 2 + j, 1), :, :, :].rearrange("o p t d -> (o p) t d")).then_inc(s[f"ctx{p}"], 16)
                walk(sp, body)

            @block.tensor
            def _(pe):
                pe.wait_ge(s["loaded"], 64)

                def scores(i, p, q):
                    pe.wait_ge(s["cqw_ready"], i + 1)
                    pe.wait_ge(s[f"ctxt{p}"], (q + 1) * 32)
                    for b in range(3):
                        for j in range(2):
                            pe.matmul(sc[HALF * j:HALF * (j + 1), b, 0:BANKC], cq[:, j, :], ct[p][:, j, b * BANKC:(b + 1) * BANKC],
                                      start=True, stop=True, tile_position=(0, HALF * j))
                    pe.matmul(sc[:, 0, BANKC:BANKC + 1], flat(hp), cols[:, 1:2], start=True, stop=True).then_inc(s["scores"], 1)

                def turn_group(i, b):
                    apart(pe)
                    for t in range(4):
                        mm = pe.transpose(turn[0:TP, b % 2, t * D:(t + 1) * D], pr[:, (4 * b + t) * TP:(4 * b + t + 1) * TP], ident[:])
                    mm.then_inc(s["turned"], 1)

                def output(i, p):
                    pe.wait_ge(s["features"], i + 1)
                    if not at_start(i, 1):
                        pe.wait_ge(s["out_sum"], i)
                    for k in range(4):
                        mm = pe.matmul(out[0:PT, 0:D], feat[p][:, k], wl[:, k, :], start=(k == 0), stop=(k == 3))
                    mm.then_inc(s["out_ready"], 1)

                def body(i, p, q):
                    pe.wait_ge(s["probs"], i + 1)
                    turn_group(i, 0)
                    turn_group(i, 1)
                    if not at_start(i, 1):
                        output(i - 1, 1 - p)
                    pe.wait_ge(s["copied"], i * 3 + 1)
                    turn_group(i, 2)
                    pe.wait_ge(s["own"], i + 1)
                    if not at_start(i, 1):
                        pe.wait_ge(s["weighted"], i)
                    apart(pe)
                    pe.transpose(mi[0:1, 0:D], own[:], ident[:]).then_inc(s["own_row"], 1)
                    if not is_last(i):
                        scores(i + 1, 1 - p, q + p)
                    pe.wait_ge(s[f"ctx{p}"], (q + 1) * 32)
                    pe.wait_ge(s["copied"], i * 3 + 3)
                    if not at_start(i, 1):
                        pe.wait_ge(s["c2q"], i)
                    for t in range(TILES):
                        for j in range(2):
                            mm = pe.matmul(pv[HALF * j:HALF * (j + 1), 0:D], pt[:, t, HALF * j:HALF * (j + 1)], cn[p][:, j, t, :],
                                           start=(t == 0), stop=(t == TILES - 1), tile_position=(0, HALF * j))
                    mm.then_inc(s["pv"], 1)
                    pe.wait_ge(s["own_norm"], i + 1)
                    pe.matmul(mi[:, D:2 * D], ones[0:1, :], row.rearrange("o j t -> o (j t)"), start=True, stop=True).then_inc(s["own_bc"], 1)
                    pe.wait_ge(s["c2q_normed"], i + 1)
                    apart(pe)
                    pe.transpose(pv[:, D:2 * D], c2n[:], ident[:]).then_inc(s["c2q_turned"], 1)

                scores(0, 0, 0)
                walk(pe, body)
                output(PAIRS - 1, 1)

            @block.scalar
            def _(act):
                act.wait_ge(s["loaded"], 64)
                act.wait_ge(s["cleared"], 3)

                def stage_rows(i, p):
                    if not at_start(i, 2):
                        act.wait_ge(s["out_ready"], i - 1)
                    if not at_start(i, 1):
                        act.wait_ge(s["scores"], i)
                    here = h_t[:, bass.ds(i * PT, PT)].rearrange("d (j t) -> d j t", j=2)
                    act.activation(feat[p][:, 0], here, ACT.Copy).then_inc(s["cs"], 1)
                    act.activation(hp[:, :, 0:SEQ], here, ACT.Copy)
                    act.activation(cq[:, :, 0:SEQ], here, ACT.Identity, scale=cols[:, 0:1], bias=cols[:, 2:3]).then_inc(s["cqw_ready"], 1)

                def exps(i):
                    act.wait_ge(s["negmax"], i + 1)
                    act.wait_ge(s["own"], i + 1)
                    if not at_start(i, 1):
                        act.wait_ge(s["inverse"], i)
                    act.activation(pr.rearrange("q (a b) -> q a b", a=3), sc[:, :, 0:BANKC], ACT.Exp, bias=nm[:, 0:1], accum_out=l[:, 0:1])\
                        .then_inc(s["probs"], 1)

                def body(i, p, q):
                    def copy(b):
                        act.wait_ge(s["turned"], i * 3 + (b + 1))
                        act.activation(pt[:, 4 * b:4 * b + 4, :], turn[0:TP, b % 2, :].rearrange("p (t q) -> p t q", t=4), ACT.Copy)\
                            .then_inc(s["copied"], 1)
                    copy(0)
                    copy(1)
                    if not is_last(i):
                        stage_rows(i + 1, 1 - p)
                    copy(2)
                    act.wait_ge(s["own_shifted"], i + 1)
                    act.activation(row[:, :, 0:SEQ], row[:, :, 0:SEQ], ACT.Exp).then_inc(s["own_exp"], 1)
                    if not is_last(i):
                        exps(i + 1)

                stage_rows(0, 0)
                exps(0)
                walk(act, body)

            @block.vector
            def _(v):
                for buf in (cq, hp, row):
                    v.memset(buf[:], 0.0).then_inc(s["cleared"], 1)
                v.wait_ge(s["cleared"], 3)
                v.wait_ge(s["loaded"], 64)
                v.tensor_reduce(bsum[:, 0:1], bias[:], AX.X, ALU.add).then_inc(s["biassum"], 1)
                v.wait_ge(s["biassum"], 1)

                def maxima(i, p, q):
                    v.wait_ge(s["scores"], i + 1)
                    if not at_start(i, 1):
                        v.wait_ge(s["own_row"], i)
                        v.wait_ge(s["probs"], i)
                    v.tensor_reduce(mx[:], sc[:, :, 0:BANKC], AX.XY, ALU.max).then_inc(s["rowmax"], 1)
                    v.wait_ge(s["rowmax"], i + 1)
                    v.scalar_tensor_tensor(own[:], mx[:], bsum[:, 0:1], sc[:, 0, BANKC:BANKC + 1], ALU.add, ALU.add).then_inc(s["own"], 1)
                    v.tensor_scalar(nm[:], mx[:], -1.0, None, ALU.mult).then_inc(s["negmax"], 1)
                    v.wait_ge(s[f"ctxt{p}"], (q + 1) * 32)
                    for j in range(2):
                        v.tensor_reduce(csum[:, bass.ds(i * 2 + j, 1)], ct[p][:, j, :], AX.X, ALU.add).then_inc(s["summed"], 1)

                def output(i):
                    v.wait_ge(s["out_ready"], i + 1)
                    if not at_start(i, 1):
                        v.wait_ge(s["done"], i)
                    v.tensor_tensor(acc[:], out[0:PT, 0:D], bl[:], ALU.add).then_inc(s["out_sum"], 1)
                    v.wait_ge(s["out_sum"], i + 1)
                    v.tensor_tensor(x[:, i, :], acc[:], x[:, i, :], ALU.add).then_inc(s["done"], 1)

                def body(i, p, q):
                    n = i + 1
                    f = feat[p]
                    wait(v, s, n, "probs")
                    if not at_start(i, 1):
                        v.wait_ge(s["c2q_normed"], i)
                    v.reciprocal(il[:], l[:]).then_inc(s["inverse"], 1)
                    if not at_start(i, 1):
                        output(i - 1)
                    if not at_start(i, 1):
                        v.wait_ge(s["own_bc"], i)
                    wait(v, s, n, "own_row")
                    rows = mi[0:1, 0:D].rearrange("o (j t) -> o j t", j=2)[:, :, 0:SEQ]
                    v.tensor_reduce(r1[:, 0, :], rows, AX.X, ALU.max).then_inc(s["own_max"], 1)
                    wait(v, s, n, "own_max")
                    v.tensor_tensor(row[:, :, 0:SEQ], rows, bc(r1[:, 0, :, None], [1, 2, SEQ]), ALU.subtract).then_inc(s["own_shifted"], 1)
                    wait(v, s, n, "own_exp")
                    v.tensor_reduce(r1[:, 1, :], row[:, :, 0:SEQ], AX.X, ALU.add).then_inc(s["own_sum"], 1)
                    wait(v, s, n, "own_sum")
                    v.reciprocal(r1[:, 2, :], r1[:, 1, :]).then_inc(s["own_inv"], 1)
                    wait(v, s, n, "own_inv")
                    v.tensor_tensor(row[:, :, 0:SEQ], row[:, :, 0:SEQ], bc(r1[:, 2, :, None], [1, 2, SEQ]), ALU.mult).then_inc(s["own_norm"], 1)
                    if not is_last(i):
                        maxima(i + 1, 1 - p, q + p)
                    wait(v, s, n, "pv")
                    if not at_start(i, 1):
                        v.wait_ge(s["c2q_turned"], i)
                    v.tensor_scalar(c2n[:], pv[:, 0:D], il[:, 0:1], None, ALU.mult).then_inc(s["c2q_normed"], 1)
                    wait(v, s, n, "own_bc")
                    v.tensor_tensor(wc[:], f[:, 0], mi[:, D:2 * D].rearrange("d (j t) -> d j t", j=2)[:, :, 0:SEQ], ALU.mult).then_inc(s["weighted"], 1)
                    wait(v, s, n, "weighted")
                    v.tensor_reduce(q2c[:], wc[:], AX.X, ALU.add).then_inc(s["q2c"], 1)
                    wait(v, s, n, "q2c")
                    v.tensor_tensor(f[:, 3], f[:, 0], bc(q2c[:, :, None], [D, 2, SEQ]), ALU.mult)
                    wait(v, s, n, "c2q_turned")
                    v.tensor_copy(f[:, 1], pv[:, D:2 * D].rearrange("d (j t) -> d j t", j=2)[:, :, 0:SEQ]).then_inc(s["c2q"], 1)
                    wait(v, s, n, "c2q")
                    v.tensor_tensor(f[:, 2], f[:, 0], f[:, 1], ALU.mult).then_inc(s["features"], 1)

                maxima(0, 0, 0)
                walk(v, body)
                output(PAIRS - 1)



def l3_attention(nc, g, a):
    normalise(nc, g, "n9", [("layer", 1e-5), ("rms", 1e-6)], a["L3_scale"])
    ident, ones, x, h_t = g["ident"], g["ones"], g["x"], g["h_t"]
    names = ("loaded staged grouped copied0 copied1 scores masked rowmax shifted probs sums inverse o_ready out_ready out_sum done")
    R, BLOCKS, HALF = PT, 8, 64
    GROUPS = 10
    AHEAD = 6
    with stage(nc, "a3", names) as (s, sb, ps):
        w = sb("w", [D, 3 * 1024]); wo = sb("wo", [D, BLOCKS, D]); mk = sb("mask", [R, R]); bo = sb("bo", [R, D])
        hs = [sb(f"hs{p}", [D, R]) for p in range(2)]; qk = sb("qk", [D, 2 * BLOCKS, R]); vs = [sb(f"vs{p}", [R, 1024]) for p in range(2)]
        pr = sb("pr", [R, HEADS, R]); pt = sb("pt", [R, HEADS, R]); ot = sb("ot", [D, BLOCKS, R]); acc = sb("acc", [R, D])
        mx = sb("mx", [R, HEADS]); rl = sb("rl", [D, 4 * R])
        scores = ps("scores", [D, 4, 512]); ring = ps("ring", [D, 2, 512]); osum = ps("osum", [D, 512]); lsum = ps("lsum", [D, 512])
        last = PAIRS - 1
        is_last = lambda i: isinstance(i, int) and i == last

        def place(i, k):
            return i * GROUPS + (AHEAD + k)

        def ahead(i, b):
            return (0, b - AHEAD) if early(i, 1) else (i - 1, b)

        def turned(i, b):
            return (i, b if is_last(i) else AHEAD + b)

        def in_bank(i, k):
            bank = k % 2
            return bank, i * (GROUPS // 2) + ((AHEAD + k - bank) // 2 + 1)

        with nc.Block() as block:
            @block.sync
            def _(sp):
                for dst, drm in ((w[:], a["L3_wqkv"]), (wo[:], a["L3_wout"]), (mk[:], g["consts"]["batch_mask"]),
                                 (bo[:], bc(a["L3_bout"], [R, D]))):
                    sp.dma_start(dst, drm).then_inc(s["loaded"], 16)

            @block.tensor
            def _(pe):
                pe.wait_ge(s["loaded"], 64)

                def group(i, k, emit):
                    bank, n = in_bank(i, k)
                    if not (early(i, 1) and n == 1):
                        pe.wait_ge(s[f"copied{bank}"], n - 1)
                    apart(pe)
                    emit(ring[:, bank, :]).then_inc(s["grouped"], 1)

                def copied(i, k):
                    bank, n = in_bank(i, k)
                    pe.wait_ge(s[f"copied{bank}"], n)

                def project(i, p, b):
                    def blocks(bank):
                        for k in range(4):
                            mm = pe.matmul(bank[:, k * R:(k + 1) * R], w[:, (4 * b + k) * D:(4 * b + k + 1) * D], hs[p][:], start=True, stop=True)
                        return mm

                    def values(bank):
                        return pe.matmul(bank[0:R, :], hs[p][:], w[:, 2048 + (b - 4) * 512:2560 + (b - 4) * 512], start=True, stop=True)

                    if b == 0:
                        wait(pe, s, i + 1, "staged")
                    group(*ahead(i, b), blocks if b < 4 else values)

                def score(i, half):
                    if half == 0:
                        for b in (2, 3):
                            copied(*ahead(i, b))
                    for k in range(4):
                        for e in range(2):
                            rows = slice(HALF * e, HALF * (e + 1))
                            mm = pe.matmul(scores[0:R, 2 * half + e, k * R:(k + 1) * R], qk[rows, 4 * half + k, :], qk[rows, BLOCKS + 4 * half + k, :],
                                           start=True, stop=True)
                    mm.then_inc(s["scores"], 1)

                def turn_group(i, b):
                    def tiles(bank):
                        for k in range(4):
                            mm = pe.transpose(bank[0:R, k * R:(k + 1) * R], pr[:, 4 * b + k, :], ident[0:R, 0:R])
                        return mm
                    if b % 2 == 0:
                        pe.wait_ge(s["probs"], i * 2 + (b // 2 + 1))
                    group(*turned(i, b), tiles)

                def weigh(i, p, half):
                    for e in range(2):
                        copied(*turned(i, 2 * half + e))
                    if not early(i, 1) or half:
                        pe.wait_ge(s["o_ready"], i * 2 + half)
                    if half == 0:
                        copied(*ahead(i, 4))
                        copied(*ahead(i, 5))
                        if not early(i, 1):
                            pe.wait_ge(s["out_sum"], i)
                    for e in range(2):
                        rows = slice(HALF * e, HALF * (e + 1))
                        pe.matmul(lsum[rows, 0:4 * R], ones[0:R, 0:HALF], pt[:, 4 * (2 * half + e):4 * (2 * half + e) + 4, :],
                                  start=True, stop=True, tile_position=(0, HALF * e))
                    for k in range(4):
                        for e in range(2):
                            rows = slice(HALF * e, HALF * (e + 1))
                            head = 2 * (4 * half + k) + e
                            mm = pe.matmul(osum[rows, k * R:(k + 1) * R], vs[p][:, HALF * head:HALF * (head + 1)], pt[:, 4 * (2 * half + e) + k, :],
                                           start=True, stop=True, tile_position=(0, HALF * e))
                    mm.then_inc(s["sums"], 1)

                def output(i):
                    pe.wait_ge(s["o_ready"], i * 2 + 2)
                    for b in range(BLOCKS):
                        mm = pe.matmul(lsum[0:R, 0:D], ot[:, b, :], wo[:, b, :], start=(b == 0), stop=(b == BLOCKS - 1))
                    mm.then_inc(s["out_ready"], 1)

                def body(i, p):
                    if not is_last(i):
                        for b in range(4):
                            project(i + 1, 1 - p, b)
                    if not early(i, 1):
                        output(i - 1)
                    if not is_last(i):
                        for b in (4, 5):
                            project(i + 1, 1 - p, b)
                    for half in range(2):
                        turn_group(i, 2 * half)
                        turn_group(i, 2 * half + 1)
                        if not is_last(i):
                            score(i + 1, half)
                        weigh(i, p, half)

                for b in range(AHEAD):
                    project(0, 0, b)
                for half in range(2):
                    score(0, half)
                walk(pe, PAIRS, body)
                output(last)

            @block.scalar
            def _(act):
                def stage_rows(i, p):
                    if not early(i, 2):
                        bank, n = in_bank(*ahead(i - 2, 5))
                        act.wait_ge(s["grouped"], place(*ahead(i - 2, 5)) + 1)
                    act.activation(hs[p][:], h_t[:, bass.ds(i * PT, PT)], ACT.Copy).then_inc(s["staged"], 1)

                def made(i, k):
                    act.wait_ge(s["grouped"], place(i, k) + 1)

                def exps(i, half):
                    act.wait_ge(s["shifted"], i * 2 + (half + 1))
                    act.activation(pr[:, 8 * half:8 * half + 8, :], pr[:, 8 * half:8 * half + 8, :], ACT.Exp).then_inc(s["probs"], 1)

                def rows_ahead(i, p, groups):
                    for b in groups:
                        made(*ahead(i, b))
                        if b < 4:
                            act.activation(qk[:, 4 * b:4 * b + 4, :].rearrange("d b t -> d (b t)"), ring[:, b % 2, 0:4 * R], ACT.Copy,
                                           scale=HALF ** -0.5 if b == 0 else 1.0).then_inc(s[f"copied{b % 2}"], 1)
                        else:
                            act.activation(vs[p][:, (b - 4) * 512:(b - 3) * 512], ring[0:R, b % 2, :], ACT.Copy).then_inc(s[f"copied{b % 2}"], 1)

                def body(i, p):
                    if not is_last(i):
                        rows_ahead(i + 1, 1 - p, (0,))
                    exps(i, 1)
                    if not is_last(i):
                        rows_ahead(i + 1, 1 - p, (2, 3, 4, 5))
                    for half in range(2):
                        made(*turned(i, 2 * half))
                        act.activation(pt[:, 8 * half:8 * half + 4, :].rearrange("k a q -> k (a q)"), ring[0:R, 0, 0:4 * R], ACT.Copy)\
                            .then_inc(s["copied0"], 1)
                        if half == 0 and (not isinstance(i, int) or i + 2 <= last):
                            stage_rows(i + 2, p)
                    if not is_last(i):
                        exps(i + 1, 0)

                stage_rows(0, 0)
                stage_rows(1, 1)
                rows_ahead(0, 0, (0, 2, 3, 4, 5))
                exps(0, 0)
                walk(act, PAIRS, body)

            @block.vector
            def _(v):
                v.wait_ge(s["loaded"], 64)

                def made(i, k):
                    v.wait_ge(s["grouped"], place(i, k) + 1)

                def queries_ahead(i):
                    made(*ahead(i, 1))
                    v.tensor_scalar(qk[:, 4:8, :].rearrange("d b t -> d (b t)"), ring[:, 1, 0:4 * R], HALF ** -0.5, None, ALU.mult).then_inc(s["copied1"], 1)

                def mask_scores(i, half):
                    heads = slice(8 * half, 8 * half + 8)
                    n = i * 2 + (half + 1)
                    v.wait_ge(s["scores"], n)
                    v.tensor_tensor(pr[:, heads, :].rearrange("q (a b) k -> q a b k", a=2),
                                    scores[0:R, 2 * half:2 * half + 2, 0:4 * R].rearrange("q a (b k) -> q a b k", b=4),
                                    bc(mk[:, None, None, :], [R, 2, 4, R]), ALU.add).then_inc(s["masked"], 1)
                    v.wait_ge(s["masked"], n)
                    if not early(i, 1):
                        v.wait_ge(s["shifted"], i * 2 + (half - 1))
                    v.tensor_reduce(mx[:, heads], pr[:, heads, :], AX.X, ALU.max).then_inc(s["rowmax"], 1)

                def shift_scores(i, half):
                    heads = slice(8 * half, 8 * half + 8)
                    v.wait_ge(s["rowmax"], i * 2 + (half + 1))
                    v.tensor_tensor(pr[:, heads, :], pr[:, heads, :], bc(mx[:, heads, None], [R, 8, R]), ALU.subtract).then_inc(s["shifted"], 1)

                def norm_sums(i, half):
                    n = i * 2 + (half + 1)
                    v.wait_ge(s["sums"], n)
                    if not (early(i, 1) and half == 0):
                        v.wait_ge(s["o_ready"], n - 1)
                    v.reciprocal(rl[:], lsum[:, 0:4 * R]).then_inc(s["inverse"], 1)
                    v.wait_ge(s["inverse"], n)
                    if half == 0 and not early(i, 1):
                        v.wait_ge(s["out_ready"], i)
                    v.tensor_tensor(ot[:, 4 * half:4 * half + 4, :].rearrange("d b t -> d (b t)"), osum[:, 0:4 * R], rl[:], ALU.mult).then_inc(s["o_ready"], 1)

                def add_output(i):
                    wait(v, s, i + 1, "out_ready")
                    if not early(i, 1):
                        v.wait_ge(s["done"], i)
                    v.tensor_tensor(acc[:], lsum[0:R, 0:D], bo[:], ALU.add).then_inc(s["out_sum"], 1)
                    wait(v, s, i + 1, "out_sum")
                    v.tensor_tensor(x[:, i, :], acc[:], x[:, i, :], ALU.add).then_inc(s["done"], 1)

                def body(i, p):
                    if not is_last(i):
                        queries_ahead(i + 1)
                    shift_scores(i, 1)
                    if not early(i, 1):
                        add_output(i - 1)
                    for half in range(2):
                        made(*turned(i, 2 * half + 1))
                        v.tensor_copy(pt[:, 8 * half + 4:8 * half + 8, :].rearrange("k a q -> k (a q)"), ring[0:R, 1, 0:4 * R]).then_inc(s["copied1"], 1)
                        if half and not is_last(i):
                            shift_scores(i + 1, 0)
                        if not is_last(i):
                            mask_scores(i + 1, half)
                        norm_sums(i, half)

                queries_ahead(0)
                mask_scores(0, 0)
                shift_scores(0, 0)
                mask_scores(0, 1)
                walk(v, PAIRS, body)
                add_output(last)



def l3_cross(nc, g, a):
    normalise(nc, g, "n10", [("layer", 1e-5)])
    x, h_t, csum = g["x"], g["h_t"], g["ctx_sum"]
    with stage(nc, "c3", "loaded spread part biased added") as (s, sb, ps):
        w = sb("w", [D, 2, D]); b = sb("b", [PT, D]); cs = sb("cs", [D, BATCH, SEQ]); y = sb("y", [PT, PAIRS, D])
        acc = ps("acc", [D, 4, 512])
        with nc.Block() as block:
            @block.sync
            def _(sp):
                sp.dma_start(w[:], a["L3_x_w"]).then_inc(s["loaded"], 16)
                sp.dma_start(b[:], bc(a["L3_x_b"], [PT, D])).then_inc(s["loaded"], 16)

            @block.scalar
            def _(act):
                act.activation(cs[:], bc(csum[:, :, None], [D, BATCH, SEQ]), ACT.Copy, scale=1.0 / CTX).then_inc(s["spread"], 1)

            @block.tensor
            def _(pe):
                pe.wait_ge(s["loaded"], 32)
                pe.wait_ge(s["spread"], 1)
                for t in range(PAIRS):
                    dst = acc[0:PT, t // 4, (t % 4) * D:(t % 4 + 1) * D]
                    pe.matmul(dst, h_t[:, t * PT:(t + 1) * PT], w[:, 0, :], start=True, stop=False)
                    mm = pe.matmul(dst, cs[:, 2 * t:2 * t + 2, :], w[:, 1, :], start=False, stop=True)
                mm.then_inc(s["part"], 1)

            @block.vector
            def _(v):
                v.wait_ge(s["loaded"], 32)
                v.wait_ge(s["part"], 1)
                v.tensor_tensor(y.rearrange("t (a c) d -> t a c d", a=4), acc[0:PT, :, :].rearrange("t a (c d) -> t a c d", d=D),
                                bc(b[:, None, None, :], [PT, 4, 4, D]), ALU.add).then_inc(s["biased"], 1)
                v.wait_ge(s["biased"], 1)
                v.tensor_tensor(x[:], x[:], y[:], ALU.add).then_inc(s["added"], 1)


def l3_ffn(nc, g, a):
    normalise(nc, g, "n11", [("layer", 1e-5)])
    x, h_t = g["x"], g["h_t"]
    with stage(nc, "f3", "loaded inner relu outer biased done") as (s, sb, ps):
        w1 = sb("w1", [D, 256]); b1 = sb("b1", [D, 2]); w2 = sb("w2", [D, 2, D]); b2 = sb("b2", [PT, D])
        re = sb("relu", [D, 2, 2, GT]); y = sb("y", [PT, 2, GROUP * D])
        inner = ps("inner", [D, 2, 2, 512]); outer = ps("outer", [D, 2, 512])
        with nc.Block() as block:
            @block.sync
            def _(sp):
                for dst, drm in ((w1[:], a["L3_ffn_w1"]), (b1[:], a["L3_ffn_b1"]), (w2[:], a["L3_ffn_w2"]), (b2[:], bc(a["L3_ffn_b2"], [PT, D]))):
                    sp.dma_start(dst, drm).then_inc(s["loaded"], 16)

            @block.tensor
            def _(pe):
                pe.wait_ge(s["loaded"], 64)

                def second(c):
                    pe.wait_ge(s["relu"], 2 * (c + 1))
                    if c >= 2:
                        pe.wait_ge(s["biased"], c - 1)
                    for t in range(GROUP):
                        for f in range(2):
                            mm = pe.matmul(outer[0:PT, c % 2, t * D:(t + 1) * D], re[:, c % 2, f, t * PT:(t + 1) * PT], w2[:, f, :],
                                           start=(f == 0), stop=(f == 1))
                    mm.then_inc(s["outer"], 1)

                for c in range(4):
                    if c >= 2:
                        pe.wait_ge(s["relu"], 2 * (c - 1))
                    for f in range(2):
                        pe.matmul(inner[:, c % 2, f, 0:GT], w1[:, f * D:(f + 1) * D], h_t[:, c * GT:(c + 1) * GT], start=True, stop=True)\
                            .then_inc(s["inner"], 1)
                    if c:
                        second(c - 1)
                second(3)

            @block.scalar
            def _(act):
                act.wait_ge(s["loaded"], 64)
                for c in range(4):
                    if c >= 2:
                        act.wait_ge(s["outer"], c - 1)
                    for f in range(2):
                        act.wait_ge(s["inner"], 2 * c + f + 1)
                        act.activation(re[:, c % 2, f, :], inner[:, c % 2, f, 0:GT], ACT.Relu, bias=b1[:, f:f + 1]).then_inc(s["relu"], 1)

            @block.vector
            def _(v):
                v.wait_ge(s["loaded"], 64)
                for c in range(4):
                    v.wait_ge(s["outer"], c + 1)
                    if c >= 2:
                        v.wait_ge(s["done"], c - 1)
                    v.tensor_tensor(y[:, c % 2, :].rearrange("t (a d) -> t a d", d=D), outer[0:PT, c % 2, :].rearrange("t (a d) -> t a d", d=D),
                                    bc(b2[:, None, :], [PT, GROUP, D]), ALU.add).then_inc(s["biased"], 1)
                    v.wait_ge(s["biased"], c + 1)
                    v.tensor_tensor(x[:, c * GROUP:(c + 1) * GROUP, :], x[:, c * GROUP:(c + 1) * GROUP, :],
                                    y[:, c % 2, :].rearrange("t (a d) -> t a d", d=D), ALU.add).then_inc(s["done"], 1)



def l2_ffn(nc, g, a):
    ident, x, h_n, h_t, C = g["ident"], g["x"], g["h_n"], g["h_t"], g["consts"]
    with ExitStack() as es:
        base = es.enter_context(nc.sbuf_tensor("m2_base", [PT, PAIRS, D], F32))
        normalise(nc, g, "n8a", [("layer", 1e-5)])
        with stage(nc, "m2keep", "kept") as (s, _, _):
            with nc.Block() as block:
                @block.vector
                def _(v):
                    v.tensor_copy(base[:], x[:]).then_inc(s["kept"], 1)
                    v.wait_ge(s["kept"], 1)
                    v.tensor_copy(x[:], h_n[:])
        normalise(nc, g, "n8b", [("layer", 1e-5)], a["L2_ln1_weight"], a["L2_ln1_bias"])
        narrow_attention(nc, g, "a2", D, SEQ // 4, SequenceTokens, C["sequence_mask"], 8 ** -0.5, a["L2_qkv"], a["L2_proj"],
                         order=SequenceTokens.part)
        normalise(nc, g, "n8c", [("layer", 1e-5)], a["L2_ln2_weight"], a["L2_ln2_bias"])
        names = ("loaded staged shifted gates gate_sum gate_inv first_gone weighed weight inner gelu outer added done "
                 "r_logits g_max p_max p_best p_order p_first p_picked q_max q_best q_order q_first q_picked both normal")
        with stage(nc, "m2", names) as (s, sb, ps):
            wr = sb("router", [D, EXPERTS]); w1 = sb("w1", [D, EXPERTS, 256]); w2 = sb("w2", [D, EXPERTS, 2, D]); early = sb("earlier", [D, EXPERTS])
            hs = sb("hs", [D, GT]); ge = sb("gelu", [D, 2, 2, GT]); top = sb("top", [PT, GROUP])
            e3 = [PT, GROUP, EXPERTS]
            gt = sb("gates", e3); rest = sb("rest", e3); rank = sb("rank", e3); p1 = sb("p1", e3); p2 = sb("p2", e3)
            y = sb("y", [PT, GROUP, D])
            small = ps("small", [D, 512]); inner = ps("inner", [D, 4, 512]); outer = ps("outer", [D, 2, 512])
            with nc.Block() as block:
                @block.sync
                def _(sp):
                    for dst, drm in ((wr[:], a["L2_router"]), (w1[:], a["L2_moe_w1"]), (w2[:], a["L2_moe_w2"]), (early[:], C["earlier"])):
                        sp.dma_start(dst, drm).then_inc(s["loaded"], 16)

                @block.tensor
                def _(pe):
                    pe.wait_ge(s["loaded"], 64)
                    with pe.Fori(0, 4) as c:
                        wait(pe, s, c + 1, "staged")
                        for t in range(GROUP):
                            mm = pe.matmul(small[0:PT, t * EXPERTS:(t + 1) * EXPERTS], hs[:, t * PT:(t + 1) * PT], wr[:], start=True, stop=True)
                        mm.then_inc(s["r_logits"], 1)

                        def second(e):
                            pe.wait_ge(s["gelu"], c * EXPERTS + (e + 1))
                            if e >= 2:
                                pe.wait_ge(s["added"], c * EXPERTS + (e - 1))
                            for t in range(GROUP):
                                for f in range(2):
                                    mm = pe.matmul(outer[0:PT, e % 2, t * D:(t + 1) * D], ge[:, e % 2, f, t * PT:(t + 1) * PT], w2[:, e, f, :],
                                                   start=(f == 0), stop=(f == 1))
                            mm.then_inc(s["outer"], 1)

                        for e in range(EXPERTS):
                            if e >= 2:
                                pe.wait_ge(s["gelu"], c * EXPERTS + (e - 1))
                            for f in range(2):
                                mm = pe.matmul(inner[:, 2 * (e % 2) + f, 0:GT], w1[:, e, f * D:(f + 1) * D], hs[:], start=True, stop=True)
                            mm.then_inc(s["inner"], 1)
                            if e:
                                second(e - 1)
                        second(EXPERTS - 1)

                @block.scalar
                def _(act):
                    with act.Fori(0, 4) as c:
                        n = c + 1
                        act.wait_ge(s["done"], c)
                        act.activation(hs[:], h_t[:, bass.ts(c, GT)], ACT.Copy).then_inc(s["staged"], 1)
                        wait(act, s, n, "shifted")
                        act.activation(gt[:], gt[:], ACT.Exp).then_inc(s["gates"], 1)
                        for e in range(EXPERTS):
                            act.wait_ge(s["inner"], c * EXPERTS + (e + 1))
                            if e >= 2:
                                act.wait_ge(s["outer"], c * EXPERTS + (e - 1))
                            act.activation(ge[:, e % 2, :, :], inner[:, 2 * (e % 2):2 * (e % 2) + 2, 0:GT], ACT.Gelu_apprx_tanh)\
                                .then_inc(s["gelu"], 1)

                @block.vector
                def _(v):
                    v.wait_ge(s["loaded"], 64)
                    with v.Fori(0, 4) as c:
                        n = c + 1
                        wait(v, s, n, "r_logits")
                        logits = small[0:PT, 0:GROUP * EXPERTS].rearrange("t (a e) -> t a e", e=EXPERTS)
                        v.tensor_reduce(top[:], logits, AX.X, ALU.max).then_inc(s["g_max"], 1)
                        wait(v, s, n, "g_max")
                        v.tensor_tensor(gt[:], logits, bc(top[:, :, None], e3), ALU.subtract).then_inc(s["shifted"], 1)
                        wait(v, s, n, "gates")
                        v.tensor_reduce(top[:], gt[:], AX.X, ALU.add).then_inc(s["gate_sum"], 1)
                        wait(v, s, n, "gate_sum")
                        v.reciprocal(top[:], top[:]).then_inc(s["gate_inv"], 1)
                        wait(v, s, n, "gate_inv")
                        v.tensor_tensor(gt[:], gt[:], bc(top[:, :, None], e3), ALU.mult).then_inc(s["normal"], 1)
                        wait(v, s, n, "normal")
                        argmax_vector(v, s, n, "p", gt[:], top[:], rank[:], early, p1[:])
                        wait(v, s, n, "p_picked")
                        v.scalar_tensor_tensor(rest[:], p1[:], -4.0, gt[:], ALU.mult, ALU.add).then_inc(s["first_gone"], 1)
                        wait(v, s, n, "first_gone")
                        argmax_vector(v, s, n, "q", rest[:], top[:], rank[:], early, p2[:])
                        wait(v, s, n, "q_picked")
                        v.tensor_tensor(p1[:], p1[:], p2[:], ALU.add).then_inc(s["both"], 1)
                        wait(v, s, n, "both")
                        v.tensor_tensor(gt[:], gt[:], p1[:], ALU.mult).then_inc(s["weight"], 1)
                        wait(v, s, n, "weight")
                        for e in range(EXPERTS):
                            v.wait_ge(s["outer"], c * EXPERTS + (e + 1))
                            for t in range(GROUP):
                                part = outer[0:PT, e % 2, t * D:(t + 1) * D]
                                if e == 0:
                                    last = v.tensor_scalar(y[:, t, :], part, gt[:, t, e:e + 1], None, ALU.mult)
                                else:
                                    if t == 0:
                                        v.wait_ge(s["added"], c * EXPERTS + e)
                                    last = v.scalar_tensor_tensor(y[:, t, :], part, gt[:, t, e:e + 1], y[:, t, :], ALU.mult, ALU.add)
                            last.then_inc(s["added"], 1)
                        v.wait_ge(s["added"], n * EXPERTS)
                        v.tensor_tensor(y[:], y[:], base[:, bass.ts(c, GROUP), :], ALU.add).then_inc(s["weighed"], 1)
                        wait(v, s, n, "weighed")
                        v.tensor_tensor(x[:, bass.ts(c, GROUP), :], x[:, bass.ts(c, GROUP), :], y[:], ALU.add).then_inc(s["done"], 1)



PARTS = [l0_attention, l0_cross, l0_ffn, l1_attention, l1_cross, l1_ffn, l2_attention, l2_cross, l2_ffn, l3_attention, l3_cross, l3_ffn]


def laid_out(v):
    col = lambda name: v[name].reshape(-1, 1)
    kb = lambda w: w.reshape(-1, 128, w.shape[-1]).transpose(1, 0, 2)
    r = {}
    r["x"] = v["x"].reshape(TOK, D)
    c = v["ctx_1024"].reshape(BATCH, TP, TILES, D)
    r["ctx"] = c
    r["ctx_t"] = c.transpose(0, 3, 2, 1).reshape(BATCH, D, CTX)
    r["ctx_mask"] = v["mask_Bx1x1xS2_ff0"].reshape(BATCH, TP, TILES).transpose(0, 2, 1).reshape(BATCH, 1, CTX)
    r["L0_attn_in_proj_weight"] = v["L0_attn_in_proj_weight"].T
    r["L0_attn_out_proj_weight"] = v["L0_attn_out_proj_weight"].T
    for k in ("L0_xattn_ln_m_w", "L0_xattn_ln_m_b", "L0_xattn_ln_l_w", "L0_xattn_ln_l_b"):
        r[k] = col(k)
    r["L0_xattn_wq_t"] = v["L0_xattn_Wq"].reshape(D, 8, 64).transpose(2, 1, 0)
    r["L0_xattn_wk_t"] = v["L0_xattn_Wkv"][:, :512].reshape(D, 8, 64).transpose(2, 1, 0)
    r["L0_xattn_wv"] = v["L0_xattn_Wkv"][:, 512:]
    r["L0_xattn_wout"] = kb(v["L0_xattn_Wout"])
    r["L0_ffn_router"] = v["L0_ffn_Wr"].T
    r["L0_ffn_w1"] = v["L0_ffn_W1"].transpose(1, 0, 2)
    r["L0_ffn_b1"] = v["L0_ffn_b1"]
    r["L0_ffn_wo"] = kb(v["L0_ffn_Wo"])
    r["L0_ffn_rows"] = np.stack([v["L0_ffn_bo"], v["L0_ffn_gamma"], v["L0_ffn_beta"]])
    for k in "xwkvrg":
        r[f"L1_maa_{k}"] = col(f"L1_attn_time_maa_{k}")
    r["L1_maa_w1"] = v["L1_attn_time_maa_w1"]
    r["L1_maa_w2"] = v["L1_attn_time_maa_w2"].transpose(1, 0, 2)
    r["L1_decay"] = col("L1_attn_time_decay")
    r["L1_decay_w1"] = v["L1_attn_time_decay_w1"]
    r["L1_decay_w2"] = v["L1_attn_time_decay_w2"]
    r["L1_bonus"] = v["L1_attn_time_faaaa"].reshape(D, 1)
    r["L1_w"] = np.stack([v[f"L1_attn_W{k}"] for k in "rkvgo"], 1)
    r["L1_ln_w"], r["L1_ln_b"] = col("L1_attn_ln_w"), col("L1_attn_ln_b")
    r["L1_xattn_wq"], r["L1_xattn_wkv"], r["L1_xattn_wp"] = v["L1_xattn_Wq"], v["L1_xattn_Wkv"], v["L1_xattn_Wp"]
    r["L1_xattn_bq"] = col("L1_xattn_bq")
    r["L1_xattn_bk"] = v["L1_xattn_bkv"][:D].reshape(D, 1)
    r["L1_xattn_bv"] = v["L1_xattn_bkv"][D:].reshape(D, 1)
    r["L1_xattn_bp"] = v["L1_xattn_bp"].reshape(1, D)
    r["L1_ffn_centroids"] = v["L1_ffn_centroids"].T
    r["L1_ffn_g"], r["L1_ffn_b"] = v["L1_ffn_ln_g"].T, v["L1_ffn_ln_b"].T
    r["L1_ffn_w1"] = v["L1_ffn_w1"].transpose(1, 0, 2)
    r["L1_ffn_b1"], r["L1_ffn_b2"] = v["L1_ffn_b1"], v["L1_ffn_b2"]
    r["L1_ffn_w2"] = v["L1_ffn_w2"].reshape(EXPERTS, 4, 128, D).transpose(2, 1, 0, 3)
    r["L2_dt"], r["L2_bdt"] = v["L2_attn_W_dt"].T, col("L2_attn_b_dt")
    r["L2_bc"] = np.stack([v["L2_attn_W_B"].T, v["L2_attn_W_C"].T], 1)
    r["L2_alog"], r["L2_d"] = v["L2_attn_A_log"], col("L2_attn_D")
    r["L2_x_cols"] = np.stack([v["L2_xattn_w_cq"], v["L2_xattn_w_c"], v["L2_xattn_w_q"]], 1)
    r["L2_x_bias"] = np.stack([v["L2_xattn_b_cq"], v["L2_xattn_b_c"], v["L2_xattn_b_q"]]).reshape(1, 3)
    r["L2_x_wl"] = kb(v["L2_xattn_W_l"].T)
    r["L2_x_bl"] = v["L2_xattn_b_l"].reshape(1, D)
    for k in ("ln1_weight", "ln1_bias", "ln2_weight", "ln2_bias"):
        r[f"L2_{k}"] = col(f"L2_ffn_{k}")
    w = v["L2_ffn_qkv_weight"]
    rep = lambda m: np.repeat(m.reshape(4, 8, D), 4, axis=0).reshape(D, D)
    r["L2_qkv"] = np.concatenate([w[:128], rep(w[128:160]), rep(w[160:192])]).T
    r["L2_proj"] = v["L2_ffn_proj_weight"].T
    r["L2_router"] = v["L2_ffn_router_weight"].T
    r["L2_moe_w1"] = v["L2_ffn_moe_w1"].transpose(1, 0, 2)
    r["L2_moe_w2"] = v["L2_ffn_moe_w2"].reshape(EXPERTS, 2, 128, D).transpose(2, 0, 1, 3)
    r["L3_scale"] = col("L3_attn_norm_scale")
    r["L3_wqkv"] = np.concatenate([v[f"L3_attn_w{k}"].reshape(D, 1024) for k in "qkv"], 1)
    r["L3_wout"] = kb(v["L3_attn_w_out"].reshape(1024, D))
    r["L3_bout"] = v["L3_attn_b_out"].reshape(1, D)
    r["L3_x_w"] = np.stack([v["L3_xattn_W"][:, :D].T, v["L3_xattn_W"][:, D:].T], 1)
    r["L3_x_b"] = v["L3_xattn_b"].reshape(1, D)
    r["L3_ffn_w1"] = v["L3_ffn_W1"][1]
    r["L3_ffn_b1"] = v["L3_ffn_b1"][1].reshape(2, 128).T
    r["L3_ffn_w2"] = kb(v["L3_ffn_W2"][1])
    r["L3_ffn_b2"] = v["L3_ffn_b2"][1].reshape(1, D)
    return r


def build(nc, a, out, consts):
    with ExitStack() as es:
        def sb(label, shape):
            return es.enter_context(nc.sbuf_tensor(label, shape, F32))

        g = {"x": sb("x_sb", [PT, PAIRS, D]), "h_n": sb("h_n", [PT, PAIRS, D]), "h_t": sb("h_t", [D, TOK]),
             "sq": sb("sq", [PT, PAIRS, D]), "ident": sb("ident", [D, D]), "half": sb("half", [D, 16]),
             "ones": sb("ones", [D, D]), "ctx_sum": sb("ctx_sum", [D, BATCH]), "headmask": consts["headmask"],
             "consts": consts}
        with stage(nc, "start", "x_in const_in") as (s, _, _):
            with nc.Block() as block:
                @block.sync
                def _(sp):
                    sp.dma_start(g["x"][:], a["x"].rearrange("(n p) d -> p n d", p=PT)).then_inc(s["x_in"], 16)
                    sp.dma_start(g["ident"][:], consts["ident"]).then_inc(s["x_in"], 16)
                    sp.wait_ge(s["x_in"], 32)

                @block.vector
                def _(v):
                    v.memset(g["half"][:], -0.5)
                    v.memset(g["ones"][:], 1.0).then_inc(s["const_in"], 1)
                    v.wait_ge(s["const_in"], 1)
        for part in PARTS:
            part(nc, g, a)
        with stage(nc, "end", "stored") as (s, _, _):
            with nc.Block() as block:
                @block.sync
                def _(sp):
                    sp.dma_start(out.rearrange("(n p) d -> p n d", p=PT), g["x"][:]).then_inc(s["stored"], 16)
                    sp.wait_ge(s["stored"], 16)


def shape_constants():
    f = np.float32
    p = np.arange(PT)
    same = p[:, None] // SEQ == p[None, :] // SEQ
    q, t = np.arange(D)[:, None], np.arange(D)[None, :]
    src, dst = (p % SEQ)[:, None], (p % SEQ)[None, :]
    levels = [same & (src // (2 * m) == dst // (2 * m)) & (src // m < dst // m) for m in HALVES] + [same & (src == dst)]
    pick = np.zeros((EXPERTS, EXPERTS, D), f)
    for e in range(EXPERTS):
        pick[e, e] = 1
    return {
        "ident": np.eye(D, dtype=f),
        "headmask": (np.arange(D)[:, None] // 8 == np.arange(HEADS)[None, :]).astype(f),
        "headmask4": (np.arange(D)[:, None] % 32 // 8 == np.arange(4)[None, :]).astype(f),
        "causal_mask": np.where(same & (p[:, None] >= p[None, :]), 0, NEG).astype(f),
        "batch_mask": np.where(same, 0, NEG).astype(f),
        "sequence_mask": np.where((q // BATCH == t // BATCH) & (q >= t), 0, NEG).astype(f),
        "level_mask": np.stack(levels, 1).astype(f),
        "pick": pick,
        "earlier": np.tile(np.arange(EXPERTS, 0, -1).astype(f), (D, 1)),
    }


HALVES = (1, 2, 4, 8, 16, 32)


def kernel(**inputs):
    from concourse import bacc
    from concourse.bass_utils import run_bass_kernel_spmd

    nc = bacc.Bacc("TRN2", target_bir_lowering=False, num_devices=1)
    arrays = laid_out({k: np.asarray(v) for k, v in inputs.items()})
    consts = shape_constants()
    named = {**{f"in_{k}": v for k, v in arrays.items()}, **{f"c_{k}": v for k, v in consts.items()}}
    named = {k: np.ascontiguousarray(v) for k, v in named.items()}
    aps = {k: nc.dram_tensor(k, v.shape, F32, kind="ExternalInput").ap() for k, v in named.items()}
    out = nc.dram_tensor("out", (TOK, D), F32, kind="ExternalOutput").ap()
    build(nc, {k[3:]: ap for k, ap in aps.items() if k.startswith("in_")}, out,
          {k[2:]: ap for k, ap in aps.items() if k.startswith("c_")})
    got = run_bass_kernel_spmd(nc, [named], core_ids=[0])
    return got.results[0]["out"].reshape(BATCH, SEQ, D)
```

```python
from contextlib import ExitStack, contextmanager

import numpy as np

import concourse.bass as bass
from concourse import mybir

F32 = mybir.dt.float32
ALU = mybir.AluOpType
ACT = mybir.ActivationFunctionType
AX = mybir.AxisListType

BATCH, SEQ, D = 32, 56, 128
PAIRS = BATCH // 2
PT = 2 * SEQ
TOK = BATCH * SEQ
GROUP = 4
GT = GROUP * PT
CTX, TILES = 1500, 12
TP = CTX // TILES
BANKC = 4 * TP
NEG = -1.0e30
EXPERTS = 8


@contextmanager
def stage(nc, name, sems):
    with ExitStack() as es:
        handles = [nc.alloc_semaphore(f"{name}_{s}") for s in sems.split()]
        s = dict(zip(sems.split(), handles))

        def sb(label, shape):
            return es.enter_context(nc.sbuf_tensor(f"{name}_{label}", shape, F32))

        def ps(label, shape):
            return es.enter_context(nc.psum_tensor(f"{name}_{label}", shape, F32))

        yield s, sb, ps
        nc.clear_and_free_semaphores(handles)
        nc.all_engine_barrier()


def bc(ap, shape):
    return ap.to_broadcast(shape)


def wait(eng, s, n, *names):
    for name in names:
        eng.wait_ge(s[name], n)


def apart(eng):
    eng.nop(nofuse=True)



def normalise(nc, g, name, rounds, gain=None, shift=None, loads=(), loaded=None):
    x, h_n, h_t, ident, half = g["x"], g["h_n"], g["h_t"], g["ident"], g["half"]
    with stage(nc, name, "loaded stats mv mean_sq mean_of_sq var rstd normed turned copied") as (s, sb, ps):
        bst = sb("bst", [PT, PAIRS, 6]); mv = sb("mv", [PT, PAIRS, 2]); msq, rstd = (sb(f"s{k}", [PT, PAIRS, 1]) for k in range(2))
        aff = sb("affine", [D, 2])
        turn = ps("turn", [D, 4, 512])
        with nc.Block() as block:
            @block.sync
            def _(sp):
                if gain is not None:
                    sp.dma_start(aff[:, 0:1], gain).then_inc(s["loaded"], 16)
                if shift is not None:
                    sp.dma_start(aff[:, 1:2], shift).then_inc(s["loaded"], 16)
                for dst, drm in loads:
                    sp.dma_start(dst, drm).then_inc(loaded, 16)

            @block.vector
            def _(v):
                squares = 0
                for k, (kind, eps) in enumerate(rounds):
                    src = x if k == 0 else h_n
                    if k:
                        v.wait_ge(s["normed"], k * PAIRS)
                    for t in range(PAIRS):
                        v.bn_stats(bst[:, t, :], src[:, t, :]).then_inc(s["stats"], 1)
                    for t in range(PAIRS):
                        v.wait_ge(s["stats"], k * PAIRS + t + 1)
                        v.bn_aggr(mv[:, t, :], bst[:, t, :]).then_inc(s["mv"], 1)
                    if kind == "rms":
                        squares += 1
                        v.wait_ge(s["mv"], (k + 1) * PAIRS)
                        v.tensor_tensor(msq[:], mv[:, :, 0:1], mv[:, :, 0:1], ALU.mult).then_inc(s["mean_sq"], 1)
                        v.wait_ge(s["mean_sq"], squares)
                        v.tensor_tensor(mv[:, :, 1:2], mv[:, :, 1:2], msq[:], ALU.add).then_inc(s["mean_of_sq"], 1)
                    for b in range(2):
                        v.wait_ge(s["rstd"], k * 2 + b + 1)
                        for t in range(PAIRS // 2 * b, PAIRS // 2 * (b + 1)):
                            if kind == "layer":
                                v.tensor_scalar(h_n[:, t, :], src[:, t, :], mv[:, t, 0:1], rstd[:, t, :], ALU.subtract, ALU.mult).then_inc(s["normed"], 1)
                            else:
                                v.tensor_scalar(h_n[:, t, :], src[:, t, :], rstd[:, t, :], None, ALU.mult).then_inc(s["normed"], 1)

            @block.gpsimd
            def _(pool):
                squares = 0
                for k, (kind, eps) in enumerate(rounds):
                    if k:
                        pool.wait_ge(s["normed"], k * PAIRS)
                    if kind == "rms":
                        squares += 1
                        pool.wait_ge(s["mean_of_sq"], squares)
                    for b in range(2):
                        part = slice(PAIRS // 2 * b, PAIRS // 2 * (b + 1))
                        pool.wait_ge(s["mv"], k * PAIRS + PAIRS // 2 * (b + 1))
                        pool.tensor_scalar(rstd[:, part, :], mv[:, part, 1:2], eps, None, ALU.add).then_inc(s["var"], 1)
                        pool.wait_ge(s["var"], k * 2 + b + 1)
                        pool.tensor_tensor(rstd[:, part, :], rstd[:, part, :], half[0:PT, part, None], ALU.pow).then_inc(s["rstd"], 1)

            @block.scalar
            def _(act):
                loads = (gain is not None) + (shift is not None)
                if loads:
                    act.wait_ge(s["loaded"], 16 * loads)
                for b in range(4):
                    act.wait_ge(s["turned"], b + 1)
                    act.activation(h_t[:, b * GT:(b + 1) * GT], turn[:, b, 0:GT], ACT.Identity,
                                   scale=aff[:, 0:1] if gain is not None else 1.0,
                                   bias=aff[:, 1:2] if shift is not None else 0.0).then_inc(s["copied"], 1)

            @block.tensor
            def _(pe):
                for t in range(PAIRS):
                    pe.wait_ge(s["normed"], (len(rounds) - 1) * PAIRS + t + 1)
                    mm = pe.transpose(turn[:, t // 4, (t % 4) * PT:(t % 4 + 1) * PT], h_n[:, t, :], ident[0:PT, 0:PT])
                    if t % 4 == 3:
                        mm.then_inc(s["turned"], 1)



HEADS = 16


class PairTokens:
    fixed = staticmethod(lambda buf: buf[:])
    part = staticmethod(lambda buf, i: buf[:, bass.ts(i, PT)])
    heads = staticmethod(lambda buf: buf[:])
    all_heads = staticmethod(lambda buf, i: bc(buf[:, bass.ts(i, PT)][:, None, :], [D, HEADS, PT]))
    mask = staticmethod(lambda hm: bc(hm[:, :, None], [D, HEADS, PT]))


class SequenceTokens:
    fixed = staticmethod(lambda buf: buf.rearrange("d (b t) -> d b t", t=BATCH))
    part = staticmethod(lambda buf, i: buf.rearrange("d (t b) -> d b t", t=BATCH)[:, bass.ts(i, 4), :])
    heads = staticmethod(lambda buf: buf.rearrange("d h (b t) -> d h b t", t=BATCH))
    all_heads = staticmethod(lambda buf, i: bc(SequenceTokens.part(buf, i)[:, None, :, :], [D, HEADS, 4, BATCH]))
    mask = staticmethod(lambda hm: bc(hm[:, :, None, None], [D, HEADS, 4, BATCH]))


def walk(eng, count, body):
    body(0, 0)
    body(1, 1)
    if count > 4:
        with eng.Fori(1, count // 2 - 1) as q:
            body(q * 2, 0)
            body(q * 2 + 1, 1)
    body(count - 2, 0)
    body(count - 1, 1)


def early(i, n):
    return isinstance(i, int) and i < n


def narrow_attention(nc, g, name, R, count, src, mask, scale, wqkv, wo_add, norm, order=None):
    ident, h_t, x = g["ident"], g["h_t"], g["x"]
    names = ("loaded cleared projected evacuated staged_q staged_k staged_h v_ready v_copied scores masked rowmax shifted "
             "probs turned pt_act pt_vec pv inverse o_ready o_turned o_copied out_ready done out2 added")
    E = 9
    with stage(nc, name, names) as (s, sb, ps):
        w = sb("w", [D, 3 * D]); wo = sb("wo", [D, D]); mk = sb("mask", [R, R]); hm = sb("hm", [D, HEADS])
        q_t = sb("q_t", [D, TOK]); k_t = sb("k_t", [D, TOK])
        qs, hs = ([sb(f"{n}{p}", [D, R]) for p in range(2)] for n in ("qs", "hs"))
        kb = [sb(f"kb{p}", [D, HEADS, R]) for p in range(2)]; vs = [sb(f"vs{p}", [R, HEADS, E]) for p in range(2)]
        pr = [sb(f"pr{p}", [R, HEADS, R]) for p in range(2)]; pt = sb("pt", [R, HEADS, R]); on = sb("on", [R, D]); ot = sb("ot", [D, R])
        mx = sb("mx", [R, HEADS]); rl = sb("rl", [R, HEADS])
        o_t = sb("o_t", [D, TOK]) if order else None
        normalise(nc, g, *norm, loads=((w[:], wqkv), (wo[:], wo_add), (mk[:], mask), (hm[:], g["headmask"])), loaded=s["loaded"])
        scores = ps("scores", [D, 4, 512]); turn = ps("turn", [D, 2, 512]); pv = ps("pv", [D, 512]); mi = ps("mi", [D, 512])
        last = count - 1
        is_last = lambda i: isinstance(i, int) and i == last
        with nc.Block() as block:
            @block.tensor
            def _(pe):
                pe.wait_ge(s["loaded"], 64)
                for m in range(2):
                    for b in range(4):
                        if m:
                            pe.wait_ge(s["evacuated"], b + 1)
                        pe.matmul(scores[:, b, 0:GT], w[:, m * D:(m + 1) * D], h_t[:, b * GT:(b + 1) * GT],
                                  start=True, stop=True).then_inc(s["projected"], 1)
                pe.wait_ge(s["evacuated"], 8)

                def score(i, p, b):
                    if b == 0:
                        pe.wait_ge(s["staged_q"], i + 1)
                        pe.wait_ge(s["staged_k"], i + 1)
                    mm = pe.matmul(scores[0:R, b, 0:4 * R], qs[p][:], kb[p][:, 4 * b:4 * b + 4, :], start=True, stop=True)
                    if b % 2:
                        mm.then_inc(s["scores"], 1)

                def values(i, p):
                    pe.wait_ge(s["staged_h"], i + 1)
                    if not early(i, 2):
                        pe.wait_ge(s["o_copied"], i - 1)
                    pe.matmul(mi[0:R, 0:D], hs[p][:], w[:, 2 * D:3 * D], start=True, stop=True).then_inc(s["v_ready"], 1)

                def turn_group(i, p, b):
                    if b % 2 == 0:
                        pe.wait_ge(s["probs"], i * 2 + (b // 2 + 1))
                    if b >= 2:
                        pe.wait_ge(*((s["pt_act"], i * 3 + 1) if b == 2 else (s["pt_vec"], i + 1)))
                    apart(pe)
                    for k in range(4):
                        mm = pe.transpose(turn[0:R, b % 2, k * R:(k + 1) * R], pr[p][:, 4 * b + k, :], ident[0:R, 0:R])
                    mm.then_inc(s["turned"], 1)

                def turn_output(i):
                    wait(pe, s, i + 1, "o_ready")
                    if not is_last(i):
                        pe.wait_ge(s["v_copied"], i + 2)
                    apart(pe)
                    pe.transpose(mi[:, 256:256 + R], on[:], ident[0:R, 0:R]).then_inc(s["o_turned"], 1)

                def project(i):
                    wait(pe, s, i + 1, "o_copied")
                    pe.matmul(pv[0:R, 256:256 + D], ot[:], wo[:], start=True, stop=True).then_inc(s["out_ready"], 1)

                def body(i, p):
                    def next_score(b):
                        if not is_last(i):
                            score(i + 1, 1 - p, b)

                    turn_group(i, p, 0)
                    next_score(0)
                    turn_group(i, p, 1)
                    if not early(i, 1):
                        turn_output(i - 1)
                    next_score(1)
                    turn_group(i, p, 2)
                    next_score(2)
                    if not order and not early(i, 1):
                        project(i - 1)
                    turn_group(i, p, 3)
                    next_score(3)
                    if not is_last(i):
                        values(i + 1, 1 - p)
                    pe.wait_ge(s["pt_act"], i * 3 + 3)
                    pe.wait_ge(s["pt_vec"], i + 1)
                    wait(pe, s, i + 1, "v_copied")
                    if not order and not early(i, 1):
                        pe.wait_ge(s["done"], i)
                    for h in range(HEADS):
                        mm = pe.matmul(pv[0:R, E * h:E * h + E], pt[:, h, :], vs[p][:, h, :], start=True, stop=True)
                    mm.then_inc(s["pv"], 1)

                for b in range(4):
                    score(0, 0, b)
                values(0, 0)
                walk(pe, count, body)
                turn_output(last)
                if order:
                    pe.wait_ge(s["o_copied"], count)
                    for t in range(PAIRS):
                        mm = pe.matmul(scores[0:PT, t // 4, (t % 4) * D:(t % 4 + 1) * D], o_t[:, t * PT:(t + 1) * PT],
                                       wo[:], start=True, stop=True)
                    mm.then_inc(s["out2"], 1)
                else:
                    project(last)

            @block.scalar
            def _(act):
                for b in range(8):
                    act.wait_ge(s["projected"], b + 1)
                    dst = (q_t if b < 4 else k_t)[:, (b % 4) * GT:(b % 4 + 1) * GT]
                    act.activation(dst, scores[:, b % 4, 0:GT], ACT.Copy, scale=scale if b < 4 else 1.0)\
                        .then_inc(s["evacuated"], 1)
                act.wait_ge(s["evacuated"], 8)
                act.wait_ge(s["loaded"], 64)

                def stage_rows(i, p):
                    if not early(i, 2):
                        act.wait_ge(s["scores"], (i - 1) * 2)
                        act.wait_ge(s["v_ready"], i - 1)
                    act.activation(src.fixed(qs[p]), src.part(q_t, i), ACT.Copy).then_inc(s["staged_q"], 1)
                    act.activation(src.fixed(hs[p]), src.part(h_t, i), ACT.Copy).then_inc(s["staged_h"], 1)

                def copy_values(i, p):
                    wait(act, s, i + 1, "v_ready")
                    if early(i, 2):
                        act.wait_ge(s["cleared"], 2)
                    act.activation(vs[p][:, :, 0:8], mi[0:R, 0:D].rearrange("t (h e) -> t h e", h=HEADS), ACT.Copy).then_inc(s["v_copied"], 1)

                def exps(i, p, h):
                    act.wait_ge(s["shifted"], i * 2 + (h + 1))
                    act.activation(pr[p][:, 8 * h:8 * h + 8, :], pr[p][:, 8 * h:8 * h + 8, :], ACT.Exp).then_inc(s["probs"], 1)

                def copy_output(i):
                    wait(act, s, i + 1, "o_turned")
                    if order:
                        act.activation(order(o_t, i), mi[:, 256:256 + R].rearrange("d (b t) -> d b t", t=BATCH), ACT.Copy)\
                            .then_inc(s["o_copied"], 1)
                    else:
                        if not early(i, 1):
                            act.wait_ge(s["out_ready"], i)
                        act.activation(ot[:], mi[:, 256:256 + R], ACT.Copy).then_inc(s["o_copied"], 1)

                def body(i, p):
                    def copy_group(b):
                        act.wait_ge(s["turned"], i * 4 + (b + 1))
                        act.activation(pt[:, 4 * b:4 * b + 4, :].rearrange("k a q -> k (a q)"), turn[0:R, b % 2, 0:4 * R], ACT.Copy)\
                            .then_inc(s["pt_act"], 1)

                    copy_group(0)
                    if not early(i, 1):
                        copy_output(i - 1)
                    copy_group(2)
                    copy_group(3)
                    if not isinstance(i, int) or i + 2 < count:
                        stage_rows(i + 2, p)
                    if not is_last(i):
                        exps(i + 1, 1 - p, 0)
                        copy_values(i + 1, 1 - p)
                        exps(i + 1, 1 - p, 1)

                stage_rows(0, 0)
                stage_rows(1, 1)
                exps(0, 0, 0)
                copy_values(0, 0)
                exps(0, 0, 1)
                walk(act, count, body)
                copy_output(last)

            @block.gpsimd
            def _(pool):
                for p in range(2):
                    pool.memset(vs[p][:, :, 8:E], 1.0).then_inc(s["cleared"], 1)
                pool.wait_ge(s["evacuated"], 8)
                pool.wait_ge(s["loaded"], 64)

                def spread_keys(i, p):
                    if not early(i, 2):
                        pool.wait_ge(s["scores"], (i - 1) * 2)
                    pool.tensor_tensor(src.heads(kb[p]), src.all_heads(k_t, i), src.mask(hm), ALU.mult).then_inc(s["staged_k"], 1)

                walk(pool, count, spread_keys)

            @block.vector
            def _(v):
                v.wait_ge(s["evacuated"], 8)
                v.wait_ge(s["loaded"], 64)

                def mask_scores(i, p, h):
                    heads = slice(8 * h, 8 * h + 8)
                    n = i * 2 + (h + 1)
                    v.wait_ge(s["scores"], n)
                    v.tensor_tensor(pr[p][:, heads, :].rearrange("q (a b) k -> q a b k", a=2),
                                    scores[0:R, 2 * h:2 * h + 2, 0:4 * R].rearrange("q a (b k) -> q a b k", b=4),
                                    bc(mk[:, None, None, :], [R, 2, 4, R]), ALU.add).then_inc(s["masked"], 1)
                    v.wait_ge(s["masked"], n)
                    if not early(i, 1):
                        v.wait_ge(s["shifted"], i * 2 + (h - 1))
                    v.tensor_reduce(mx[:, heads], pr[p][:, heads, :], AX.X, ALU.max).then_inc(s["rowmax"], 1)

                def shift_scores(i, p, h):
                    heads = slice(8 * h, 8 * h + 8)
                    v.wait_ge(s["rowmax"], i * 2 + (h + 1))
                    v.tensor_tensor(pr[p][:, heads, :], pr[p][:, heads, :], bc(mx[:, heads, None], [R, 8, R]), ALU.subtract).then_inc(s["shifted"], 1)

                def add_output(i):
                    wait(v, s, i + 1, "out_ready")
                    v.tensor_tensor(x[:, i, :], pv[0:R, 256:256 + D], x[:, i, :], ALU.add).then_inc(s["done"], 1)

                def body(i, p):
                    v.wait_ge(s["turned"], i * 4 + 2)
                    v.tensor_copy(pt[:, 4:8, :].rearrange("k a q -> k (a q)"), turn[0:R, 1, 0:4 * R]).then_inc(s["pt_vec"], 1)
                    if not is_last(i):
                        mask_scores(i + 1, 1 - p, 0)
                        shift_scores(i + 1, 1 - p, 0)
                    if not order and not early(i, 1):
                        add_output(i - 1)
                    if not is_last(i):
                        mask_scores(i + 1, 1 - p, 1)
                        shift_scores(i + 1, 1 - p, 1)
                    wait(v, s, i + 1, "pv")
                    if not early(i, 1):
                        v.wait_ge(s["o_ready"], i)
                    sums = pv[0:R, 0:HEADS * E].rearrange("q (h e) -> q h e", h=HEADS)
                    v.reciprocal(rl[:, :, None], sums[:, :, 8:E]).then_inc(s["inverse"], 1)
                    wait(v, s, i + 1, "inverse")
                    if not early(i, 1):
                        v.wait_ge(s["o_turned"], i)
                    v.tensor_tensor(on.rearrange("q (h e) -> q h e", h=HEADS), sums[:, :, 0:8],
                                    bc(rl[:, :, None], [R, HEADS, 8]), ALU.mult).then_inc(s["o_ready"], 1)

                for h in range(2):
                    mask_scores(0, 0, h)
                    shift_scores(0, 0, h)
                walk(v, count, body)
                if order:
                    v.wait_ge(s["out2"], 1)
                    v.tensor_tensor(x.rearrange("t (a b) d -> t a (b d)", a=4), scores[0:PT, :, :],
                                    x.rearrange("t (a b) d -> t a (b d)", a=4), ALU.add).then_inc(s["added"], 1)
                else:
                    add_output(last)


def softmax_vector(v, s, n, R, scores, mask, pr, mx, ls, rl):
    full, four = [R, HEADS, R], [R, 4, 4, R]
    v.wait_ge(s["scores"], n)
    v.tensor_tensor(pr.rearrange("q (a b) k -> q a b k", a=4), scores[0:R, :, 0:4 * R].rearrange("q a (b k) -> q a b k", b=4),
                    bc(mask[:, None, None, :], four), ALU.add).then_inc(s["masked"], 1)
    v.wait_ge(s["masked"], n)
    v.tensor_reduce(mx, pr, AX.X, ALU.max).then_inc(s["rowmax"], 1)
    v.wait_ge(s["rowmax"], n)
    v.tensor_tensor(pr, pr, bc(mx[:, :, None], full), ALU.subtract).then_inc(s["shifted"], 1)
    v.wait_ge(s["probs"], n)
    v.tensor_reduce(ls, pr, AX.X, ALU.add).then_inc(s["rowsum"], 1)
    v.wait_ge(s["rowsum"], n)
    v.reciprocal(rl, ls).then_inc(s["inverse"], 1)


def turn_probs(pe, s, n, R, scores, pr, ident):
    pe.wait_ge(s["probs"], n)
    for h in range(HEADS):
        mm = pe.transpose(scores[0:R, h // 4, (h % 4) * R:(h % 4 + 1) * R], pr[:, h, :], ident[0:R, 0:R])
    mm.then_inc(s["turned"], 1)


def l0_attention(nc, g, a):
    narrow_attention(nc, g, "a0", PT, PAIRS, PairTokens, g["consts"]["causal_mask"], 8 ** -0.5,
                     a["L0_attn_in_proj_weight"], a["L0_attn_out_proj_weight"], ("n0", [("layer", 1e-5)]))



def rounds(eng, body):
    body(0)
    with eng.Fori(1, PAIRS - 1) as i:
        body(i)
    body(PAIRS - 1)


def l0_cross(nc, g, a):
    ident, ones, x, h_t, half = g["ident"], g["ones"], g["x"], g["h_t"], g["half"]
    QH, C, S = 8, 4, SEQ
    names = ("loaded negb heads heads_copied q_made q_act q_vec ctx0 ctx1 stats mv var rstd centred z_ready "
             "lat_ready q_ready turned freed0 freed1 scores max_ctx max_lat negmax probs sums inverse diag pl pv ol_copied mixed "
             "o_norm o_ready out_ready done")
    with stage(nc, "x0", names) as (s, sb, ps):
        wqt = sb("wq_t", [64, QH, D]); wkt = sb("wk_t", [64, QH, D]); wv = sb("wv", [D, 512]); wout = sb("wout", [D, C, D])
        ab = sb("gain_shift", [D, 3]); mh = sb("heads", [D, QH, D]); q = sb("q", [D, QH, TOK])
        cx = [sb(f"ctx{j}", [TP, TILES, D]) for j in range(2)]; z = [sb(f"z{j}", [TP, TILES, D]) for j in range(2)]
        bst = sb("bst", [TP, TILES, 6]); mv = [sb(f"mv{j}", [TP, TILES, 2]) for j in range(2)]; rstd = sb("rstd", [TP, TILES, 1])
        zt = sb("z_t", [D, CTX]); lt = [sb(f"lat_t{j}", [D, S]) for j in range(2)]; ln = [sb(f"lat{j}", [S, D]) for j in range(2)]
        ql = [sb(f"q_lat{j}", [D, QH, S]) for j in range(2)]; qz = [sb(f"q_ctx{j}", [D, QH, S]) for j in range(2)]
        pr = [sb(f"pr{k}", [PT, CTX + S]) for k in range(C)]; sl = [sb(f"lat_scores{j}", [PT, C, S]) for j in range(2)]; pt = sb("pt", [TP, TILES, C * PT]); ptl = sb("ptl", [S, C * PT])
        mx = sb("mx", [PT, 2]); nm = sb("nm", [PT, 2]); l = [sb(f"l{j}", [PT, C, 2]) for j in range(2)]; ls = sb("ls", [PT, C]); rl = sb("rl", [PT, C])
        dg = sb("dg", [PT, C, PT]); ols = sb("ols", [D, C * PT]); o1 = sb("o1", [D, C * PT]); ut = sb("ut", [D, C, PT])
        loads = ((wqt[:], a["L0_xattn_wq_t"]), (wkt[:], a["L0_xattn_wk_t"]), (wv[:], a["L0_xattn_wv"]), (wout[:], a["L0_xattn_wout"]),
                 (ab[:, 0:1], a["L0_xattn_ln_m_w"]), (ab[:, 1:2], a["L0_xattn_ln_m_b"]))
        normalise(nc, g, "n1", [("layer", 1e-5), ("layer", 1e-5)], a["L0_xattn_ln_l_w"], a["L0_xattn_ln_l_b"], loads=loads, loaded=s["loaded"])
        sc = ps("sc", [D, 6, 512]); turn = ps("turn", [D, 2, 512])
        oz, ol, spread = (sc[:, b, :] for b in (3, 4, 5))
        FRONT = 4
        TURNS = 4 * C + FRONT + 2
        SHIFT = FRONT - 2
        OUT = C * S + D

        def cnt(i, j, per, k):
            return i * (2 * per) + (j * per + k)

        def is_first(i, j):
            return isinstance(i, int) and i == 0 and j == 0

        def is_last(i, j):
            return isinstance(i, int) and i == PAIRS - 1 and j == 1

        def chunk_group(i, j, c, b):
            if c == 0:
                return (i, j, 2 + b if is_first(i, j) or b >= 2 else b)
            return (i, j, 2 + 4 * c + b + (0 if c < 2 or is_last(i, j) else 2 if c == 2 else 4))

        def front_group(i, j, b):
            if is_first(i, j):
                return (i, j, b - SHIFT)
            return (*((i, 0) if j else (i - 1, 1)), (10, 11, 16, 17)[b])

        def project_group(i, j, r):
            return (i, j, 2 + 4 * C + r) if is_last(i, j) else (*after_of(i, j), 2 + r)

        def after_of(i, j):
            return (i, 1) if j == 0 else (i + 1, 0)

        def emitted(i, j, k):
            return i * (2 * TURNS) + (SHIFT + TURNS * j + k + 1)

        def half_of(i, j, k):
            n = SHIFT + TURNS * j + k + 1
            return i * TURNS + (n + 1) // 2, i * TURNS + n // 2

        def lat_scored(eng, i, j):
            eng.wait_ge(s["freed1"], half_of(*front_group(i, j, 3))[1])

        with nc.Block() as block:
            @block.sync
            def _(sp):
                def body(i):
                    for j in range(2):
                        if not (isinstance(i, int) and i == 0):
                            sp.wait_ge(s["centred"], cnt(i, j, 1, -1))
                        sp.dma_start(cx[j][:], a["ctx"][bass.ds(i * 2 + j, 1), :, :, :].rearrange("o p t d -> (o p) t d")).then_inc(s[f"ctx{j}"], 16)
                rounds(sp, body)

            @block.tensor
            def _(pe):
                pe.wait_ge(s["loaded"], 96)
                for h in range(QH):
                    mm = pe.matmul(sc[:, h // 4, (h % 4) * D:(h % 4 + 1) * D], wqt[:, h, :], wkt[:, h, :], start=True, stop=True)
                mm.then_inc(s["heads"], 1)
                pe.wait_ge(s["heads_copied"], 1)
                for k in range(4 * QH):
                    if k >= 2:
                        pe.wait_ge(s["q_act" if k % 2 == 0 else "q_vec"], k // 2)
                    pe.matmul(sc[:, k % 2, 0:GT], mh[:, k // 4, :], h_t[:, (k % 4) * GT:(k % 4 + 1) * GT], start=True, stop=True)\
                        .then_inc(s["q_made"], 1)
                pe.wait_ge(s["q_act"], 2 * QH)
                pe.wait_ge(s["q_vec"], 2 * QH)

                def group(i, j, k, emit):
                    bank = (SHIFT + k) % 2
                    if not (is_first(i, j) and SHIFT + k < 2):
                        pe.wait_ge(s[f"freed{bank}"], half_of(i, j, k - 2)[bank])
                    apart(pe)
                    emit(turn[:, bank, :]).then_inc(s["turned"], 1)

                def copied(i, j, k):
                    bank = (SHIFT + k) % 2
                    pe.wait_ge(s[f"freed{bank}"], half_of(i, j, k)[bank])

                def project(i, j, r):
                    def half_heads(bank):
                        for c in range(2 * r, 2 * r + 2):
                            mm = pe.matmul(bank[:, (c % 2) * PT:(c % 2 + 1) * PT], wv[:, c * D:(c + 1) * D], o1[:, c * PT:(c + 1) * PT], start=True, stop=True)
                        return mm
                    pe.wait_ge(s["o_ready"], cnt(i, j, 1, 1))
                    group(*project_group(i, j, r), half_heads)

                def pair_out(i, bank):
                    for c in range(C):
                        mm = pe.matmul(bank[0:PT, OUT:OUT + D], ut[:, c, :], wout[:, c, :], start=(c == 0), stop=(c == C - 1))
                    return mm

                def front(i, j, b):
                    def turn_context(bank):
                        for t in range(4):
                            mm = pe.transpose(bank[:, t * TP:(t + 1) * TP], z[j][:, 4 * b + t, :], ident[0:TP, 0:TP])
                        return mm

                    def latents(bank):
                        pe.transpose(bank[0:S, C * S:C * S + D], lt[j][:], ident[:])
                        for c in range(C):
                            mm = pe.matmul(bank[0:PT, c * S:(c + 1) * S], ql[j][:, 2 * c:2 * c + 2, :], lt[j][:], start=True, stop=True)
                        if j == 1 and not (isinstance(i, int) and i == 0):
                            mm = pair_out(i - 1, bank)
                        return mm

                    if b == 0:
                        pe.wait_ge(s["z_ready"], cnt(i, j, 1, 1))
                    if b < 3:
                        group(*front_group(i, j, b), turn_context)
                    else:
                        pe.wait_ge(s["lat_ready"], cnt(i, j, 1, 1))
                        pe.wait_ge(s["q_ready"], cnt(i, j, 1, 1))
                        group(*front_group(i, j, 3), latents)

                def score(i, j, c, turned=None):
                    if c >= 2:
                        pe.wait_ge(s["probs"], cnt(i, j, C, c - 1))
                    elif not (isinstance(i, int) and i == 0 and j == 0):
                        if c == 0:
                            pe.wait_ge(s["probs"], cnt(i, j, C, -1))
                        else:
                            pe.wait_ge(s["o_norm"], cnt(i, j, 1, 0))
                    if c == 0:
                        for b in (1, 2):
                            copied(*front_group(i, j, b))
                    for b in range(3):
                        mm = pe.matmul(sc[0:PT, 3 * (c % 2) + b, 0:BANKC], qz[j][:, 2 * c:2 * c + 2, :], zt[:, b * BANKC:(b + 1) * BANKC],
                                       start=True, stop=True)
                        if turned is not None and b < 2:
                            turned(b)
                    mm.then_inc(s["scores"], 1)

                def body(i):
                    for j in range(2):
                        first = isinstance(i, int) and i == 0 and j == 0
                        last = isinstance(i, int) and i == PAIRS - 1 and j == 1
                        before = (i, 0) if j else (i - 1, 1)
                        after = after_of(i, j)

                        def turn_group(c, b):
                            def tiles(bank):
                                if b == 3:
                                    return pe.transpose(bank[0:S, 0:PT], pr[c][:, CTX:CTX + S], ident[0:PT, 0:PT])
                                for t in range(4):
                                    mm = pe.transpose(bank[0:TP, t * PT:(t + 1) * PT], pr[c][:, (4 * b + t) * TP:(4 * b + t + 1) * TP], ident[0:PT, 0:PT])
                                return mm
                            if b == 0:
                                pe.wait_ge(s["probs"], cnt(i, j, C, c + 1))
                            group(*chunk_group(i, j, c, b), tiles)

                        def sums(b, tiles):
                            if tiles[0] % 4 == 0:
                                copied(*chunk_group(i, j, C - 1, b))
                            for t in tiles:
                                mm = pe.matmul(oz[:, 0:C * PT], z[j][:, t, :], pt[:, t, :], start=(t == 0), stop=(t == TILES - 1))
                            return mm

                        def later(b):
                            if not last:
                                front(*after, b)

                        if not first:
                            turn_group(0, 0)
                            turn_group(0, 1)
                        score(i, j, 1, None if first else lambda b: project(*before, b))
                        if first:
                            turn_group(0, 0)
                            turn_group(0, 1)
                        score(i, j, 2, lambda b: turn_group(0, 2 + b))
                        turn_group(1, 0)
                        turn_group(1, 1)
                        score(i, j, 3, lambda b: turn_group(1, 2 + b))
                        later(0)
                        later(1)
                        for b in range(4):
                            turn_group(2, b)
                        later(2)
                        later(3)
                        if not last:
                            score(*after, 0)
                        turn_group(3, 0)
                        turn_group(3, 1)
                        sums(0, (0, 1))
                        turn_group(3, 2)
                        sums(0, (2, 3))
                        turn_group(3, 3)
                        sums(1, (4, 5, 6, 7))
                        copied(*chunk_group(i, j, C - 1, 3))
                        pe.matmul(ol[:, 0:C * PT], ln[j][:], ptl[:], start=True, stop=True).then_inc(s["pl"], 1)
                        pe.wait_ge(s["diag"], cnt(i, j, 1, 1))
                        pe.matmul(spread[:, 0:C * PT], ones[0:PT, :], dg[:], start=True, stop=True)
                        mm = sums(2, (8, 9, 10, 11))
                        mm.then_inc(s["pv"], 1)

                for b in range(FRONT):
                    front(0, 0, b)
                score(0, 0, 0)
                rounds(pe, body)
                for r in range(2):
                    project(PAIRS - 1, 1, r)
                for r in range(2):
                    copied(*project_group(PAIRS - 1, 1, r))
                pair_out(PAIRS - 1, turn[:, 0, :]).then_inc(s["out_ready"], 1)

            @block.scalar
            def _(act):
                act.wait_ge(s["heads"], 1)
                act.activation(mh.rearrange("k (a b) d -> k a (b d)", a=2), sc[:, 0:2, :], ACT.Copy, scale=64 ** -0.5).then_inc(s["heads_copied"], 1)
                for k in range(0, 4 * QH, 2):
                    act.wait_ge(s["q_made"], k + 1)
                    act.activation(q[:, k // 4, (k % 4) * GT:(k % 4 + 1) * GT], sc[:, 0, 0:GT], ACT.Copy).then_inc(s["q_act"], 1)
                act.wait_ge(s["q_act"], 2 * QH)
                act.wait_ge(s["q_vec"], 2 * QH)
                act.wait_ge(s["negb"], 1)

                def stage_queries(i, j):
                    cols = bass.ds((i * 2 + j) * S, S)
                    act.activation(lt[j][:], h_t[:, cols], ACT.Identity, bias=ab[:, 2:3]).then_inc(s["lat_ready"], 1)
                    act.activation(ql[j][:], q[:, :, cols], ACT.Copy)
                    act.activation(qz[j][:], q[:, :, cols], ACT.Identity, scale=ab[:, 0:1]).then_inc(s["q_ready"], 1)

                def shift_sums(i, j):
                    act.wait_ge(s["o_norm"], cnt(i, j, 1, 1))
                    act.activation(o1[:], o1[:], ACT.Identity, bias=ab[:, 1:2]).then_inc(s["o_ready"], 1)

                def exps(i, j, c):
                    act.wait_ge(s["negmax"], cnt(i, j, C, c + 1))
                    if c == 0:
                        lat_scored(act, i, j)
                    act.activation(pr[c][:, CTX:CTX + S], sl[j][:, c, :], ACT.Exp, bias=nm[:, c % 2:c % 2 + 1], accum_out=l[j][:, c, 1:2])
                    act.activation(pr[c][:, 0:CTX].rearrange("q (a b) -> q a b", a=3), sc[0:PT, 3 * (c % 2):3 * (c % 2) + 3, 0:BANKC], ACT.Exp,
                                   bias=nm[:, c % 2:c % 2 + 1], accum_out=l[j][:, c, 0:1]).then_inc(s["probs"], 1)

                def group_ready(i, j, k):
                    act.wait_ge(s["turned"], emitted(i, j, k))

                def front_copies(i, j, b):
                    group_ready(*front_group(i, j, b))
                    act.activation(zt[:, b * BANKC:(b + 1) * BANKC], turn[:, 0, 0:BANKC], ACT.Copy).then_inc(s["freed0"], 1)

                def copy_heads(i, j):
                    group_ready(*project_group(i, j, 0))
                    for e in range(2):
                        ins = act.activation(ut[64 * e:64 * e + 64, 0:2, j * S:(j + 1) * S],
                                             turn[64 * e:64 * e + 64, 0, 0:2 * PT].rearrange("d (c t) -> d c t", c=2)[:, :, e * S:(e + 1) * S], ACT.Copy)
                    ins.then_inc(s["freed0"], 1)

                stage_queries(0, 0)
                front_copies(0, 0, 0)
                front_copies(0, 0, 2)
                exps(0, 0, 0)

                def body(i):
                    for j in range(2):
                        first = isinstance(i, int) and i == 0 and j == 0
                        last = isinstance(i, int) and i == PAIRS - 1 and j == 1
                        before = (i, 0) if j else (i - 1, 1)
                        after = after_of(i, j)

                        def copy(c, b):
                            group_ready(*chunk_group(i, j, c, b))
                            act.activation(pt[:, 4 * b:4 * b + 4, c * PT:(c + 1) * PT], turn[0:TP, 0, 0:4 * PT].rearrange("p (t q) -> p t q", t=4),
                                           ACT.Copy).then_inc(s["freed0"], 1)

                        copy(0, 0)
                        if not first:
                            copy_heads(*before)
                        exps(i, j, 1)
                        copy(0, 2)
                        copy(1, 0)
                        exps(i, j, 2)
                        copy(1, 2)
                        if not last:
                            stage_queries(*after)
                            front_copies(*after, 0)
                        copy(2, 0)
                        exps(i, j, 3)
                        copy(2, 2)
                        if not last:
                            front_copies(*after, 2)
                        copy(3, 0)
                        if not last:
                            exps(*after, 0)
                        copy(3, 2)
                        act.wait_ge(s["pl"], cnt(i, j, 1, 1))
                        act.activation(ols[:], ol[:, 0:C * PT], ACT.Copy).then_inc(s["ol_copied"], 1)
                        shift_sums(i, j)

                rounds(act, body)
                copy_heads(PAIRS - 1, 1)

            @block.gpsimd
            def _(pool):
                shape = [TP, TILES, D]

                def body(i):
                    for j in range(2):
                        pool.wait_ge(s["mv"], cnt(i, j, 1, 1))
                        if not is_first(i, j):
                            pool.wait_ge(s["z_ready"], cnt(i, j, 1, 0))
                        apart(pool)
                        pool.tensor_scalar(rstd[:], mv[j][:, :, 1:2], 1e-5, None, ALU.add).then_inc(s["var"], 1)
                        pool.wait_ge(s["var"], cnt(i, j, 1, 1))
                        pool.tensor_tensor(rstd[:], rstd[:], half[0:TP, 0:TILES].rearrange("p (t o) -> p t o", o=1), ALU.pow).then_inc(s["rstd"], 1)
                        if not (isinstance(i, int) and i == 0):
                            pool.wait_ge(s["pv"], cnt(i, j, 1, -1))
                        pool.tensor_tensor(z[j][:], cx[j][:], bc(mv[j][:, :, 0:1], shape), ALU.subtract).then_inc(s["centred"], 1)
                        pool.wait_ge(s["centred"], cnt(i, j, 1, 1))
                        pool.wait_ge(s["rstd"], cnt(i, j, 1, 1))
                        pool.tensor_tensor(z[j][:], z[j][:], bc(rstd[:], shape), ALU.mult).then_inc(s["z_ready"], 1)
                rounds(pool, body)

            @block.vector
            def _(v):
                v.wait_ge(s["loaded"], 96)
                v.tensor_scalar(ab[:, 2:3], ab[:, 1:2], -1.0, None, ALU.mult).then_inc(s["negb"], 1)
                for k in range(1, 4 * QH, 2):
                    v.wait_ge(s["q_made"], k + 1)
                    v.tensor_copy(q[:, k // 4, (k % 4) * GT:(k % 4 + 1) * GT], sc[:, 1, 0:GT]).then_inc(s["q_vec"], 1)

                def statistics(i, j):
                    v.wait_ge(s[f"ctx{j}"], i * 16 + 16)
                    if not is_first(i, j):
                        v.wait_ge(s["mv"], cnt(i, j, 1, 0))
                    if not (isinstance(i, int) and i == 0):
                        v.wait_ge(s["z_ready"], cnt(i, j, 1, -1))
                    for t in range(TILES):
                        v.bn_stats(bst[:, t, :], cx[j][:, t, :]).then_inc(s["stats"], 1)
                    v.wait_ge(s["stats"], cnt(i, j, TILES, TILES))
                    apart(v)
                    for t in range(TILES):
                        ins = v.bn_aggr(mv[j][:, t, :], bst[:, t, :])
                    ins.then_inc(s["mv"], 1)

                def group_ready(i, j, k):
                    v.wait_ge(s["turned"], emitted(i, j, k))

                def add_out(i, bank):
                    v.tensor_tensor(x[:, i, :], turn[0:PT, bank, OUT:OUT + D], x[:, i, :], ALU.add).then_inc(s["done"], 1)

                def front_context(i, j):
                    group_ready(*front_group(i, j, 1))
                    v.tensor_copy(zt[:, BANKC:2 * BANKC], turn[:, 1, 0:BANKC]).then_inc(s["freed1"], 1)

                def front_latents(i, j):
                    group_ready(*front_group(i, j, 3))
                    if j == 1 and not (isinstance(i, int) and i == 0):
                        add_out(i - 1, 1)
                    v.tensor_copy(ln[j][:], turn[0:S, 1, C * S:C * S + D])
                    v.tensor_copy(sl[j][:], turn[0:PT, 1, 0:C * S].rearrange("q (c t) -> q c t", c=C)).then_inc(s["freed1"], 1)

                def copy_heads(i, j):
                    group_ready(*project_group(i, j, 1))
                    for e in range(2):
                        ins = v.tensor_copy(ut[64 * e:64 * e + 64, 2:4, j * S:(j + 1) * S],
                                            turn[64 * e:64 * e + 64, 1, 0:2 * PT].rearrange("d (c t) -> d c t", c=2)[:, :, e * S:(e + 1) * S])
                    ins.then_inc(s["freed1"], 1)

                def maxima(i, j, c):
                    first = isinstance(i, int) and i == 0 and j == 0
                    v.wait_ge(s["scores"], cnt(i, j, C, c + 1))
                    if not (first and c < 2):
                        v.wait_ge(s["probs"], cnt(i, j, C, c - 1))
                    if not (first and c == 0):
                        v.wait_ge(s["negmax"], cnt(i, j, C, c))
                    v.tensor_reduce(mx[:, 0:1], sc[0:PT, 3 * (c % 2):3 * (c % 2) + 3, 0:BANKC], AX.XY, ALU.max).then_inc(s["max_ctx"], 1)
                    if c == 0:
                        lat_scored(v, i, j)
                    v.tensor_reduce(mx[:, 1:2], sl[j][:, c, :], AX.X, ALU.max).then_inc(s["max_lat"], 1)
                    v.wait_ge(s["max_ctx"], cnt(i, j, C, c + 1))
                    v.wait_ge(s["max_lat"], cnt(i, j, C, c + 1))
                    v.tensor_reduce(nm[:, c % 2:c % 2 + 1], mx[:], AX.X, ALU.max, negate=True).then_inc(s["negmax"], 1)

                statistics(0, 0)
                statistics(0, 1)
                front_context(0, 0)
                front_latents(0, 0)
                maxima(0, 0, 0)

                def body(i):
                    for j in range(2):
                        first = isinstance(i, int) and i == 0 and j == 0
                        last = isinstance(i, int) and i == PAIRS - 1 and j == 1
                        before = (i, 0) if j else (i - 1, 1)
                        after = after_of(i, j)

                        def copy_context(c):
                            group_ready(*chunk_group(i, j, c, 1))
                            v.tensor_copy(pt[:, 4:8, c * PT:(c + 1) * PT], turn[0:TP, 1, 0:4 * PT].rearrange("p (t q) -> p t q", t=4)).then_inc(s["freed1"], 1)

                        def copy_latents(c):
                            group_ready(*chunk_group(i, j, c, 3))
                            v.tensor_copy(ptl[:, c * PT:(c + 1) * PT], turn[0:S, 1, 0:PT]).then_inc(s["freed1"], 1)

                        copy_context(0)
                        if not first:
                            copy_heads(*before)
                        maxima(i, j, 1)
                        copy_latents(0)
                        maxima(i, j, 2)
                        copy_context(1)
                        copy_latents(1)
                        maxima(i, j, 3)
                        if not last:
                            front_context(*after)
                        copy_context(2)
                        copy_latents(2)
                        if not last:
                            front_latents(*after)
                            maxima(*after, 0)
                        copy_context(3)
                        copy_latents(3)
                        v.wait_ge(s["probs"], cnt(i, j, C, C))
                        v.tensor_reduce(ls[:], l[j][:], AX.X, ALU.add).then_inc(s["sums"], 1)
                        v.wait_ge(s["sums"], cnt(i, j, 1, 1))
                        v.reciprocal(rl[:], ls[:]).then_inc(s["inverse"], 1)
                        v.wait_ge(s["inverse"], cnt(i, j, 1, 1))
                        v.tensor_tensor(dg[:], bc(ident[0:PT, None, 0:PT], [PT, C, PT]), bc(rl[:, :, None], [PT, C, PT]), ALU.mult).then_inc(s["diag"], 1)
                        if not last and not is_last(*after):
                            statistics(*after_of(*after))
                        v.wait_ge(s["ol_copied"], cnt(i, j, 1, 1))
                        v.wait_ge(s["pv"], cnt(i, j, 1, 1))
                        v.scalar_tensor_tensor(o1[:], oz[:, 0:C * PT], ab[:, 0:1], ols[:], ALU.mult, ALU.add).then_inc(s["mixed"], 1)
                        v.wait_ge(s["mixed"], cnt(i, j, 1, 1))
                        v.tensor_tensor(o1[:], o1[:], spread[:, 0:C * PT], ALU.mult).then_inc(s["o_norm"], 1)

                rounds(v, body)
                copy_heads(PAIRS - 1, 1)
                v.wait_ge(s["out_ready"], 1)
                add_out(PAIRS - 1, 0)



NORM_STEPS = "n_sum n_mean n_centred n_squared n_sumsq n_var n_rstd n_normed "
ROUTE_STEPS = "r_logits r_max r_best r_order r_first r_picked "


def norm_vector(v, s, n, y, sq, st, size, eps):
    norm_start(v, s, n, y, sq, st, size, eps)
    norm_end(v, s, n, y, st)


def norm_start(v, s, n, y, sq, st, size, eps):
    shape = list(y.shape)
    v.tensor_reduce(st[0], y, AX.X, ALU.add).then_inc(s["n_sum"], 1)
    wait(v, s, n, "n_sum")
    v.tensor_scalar(st[1], st[0], 1.0 / size, None, ALU.mult).then_inc(s["n_mean"], 1)
    wait(v, s, n, "n_mean")
    v.tensor_tensor(y, y, bc(st[1][:, :, None], shape), ALU.subtract).then_inc(s["n_centred"], 1)
    wait(v, s, n, "n_centred")
    v.tensor_tensor(sq, y, y, ALU.mult).then_inc(s["n_squared"], 1)
    wait(v, s, n, "n_squared")
    v.tensor_reduce(st[2], sq, AX.X, ALU.add).then_inc(s["n_sumsq"], 1)
    wait(v, s, n, "n_sumsq")
    v.tensor_scalar(st[3], st[2], 1.0 / size, eps, ALU.mult, ALU.add).then_inc(s["n_var"], 1)


def norm_end(v, s, n, y, st):
    wait(v, s, n, "n_rstd")
    v.tensor_tensor(y, y, bc(st[4][:, :, None], list(y.shape)), ALU.mult).then_inc(s["n_normed"], 1)


def norm_pool(pool, s, n, st, half):
    wait(pool, s, n, "n_var")
    pool.tensor_tensor(st[4], st[3], half, ALU.pow).then_inc(s["n_rstd"], 1)


def argmax_vector(v, s, n, p, value, top, rank, earlier, picked):
    shape = list(value.shape)
    v.tensor_reduce(top, value, AX.X, ALU.max).then_inc(s[p + "_max"], 1)
    wait(v, s, n, p + "_max")
    v.tensor_tensor(rank, value, bc(top[:, :, None], shape), ALU.is_equal).then_inc(s[p + "_best"], 1)
    wait(v, s, n, p + "_best")
    v.tensor_tensor(rank, rank, bc(earlier[0:shape[0], None, :], shape), ALU.mult).then_inc(s[p + "_order"], 1)
    wait(v, s, n, p + "_order")
    v.tensor_reduce(top, rank, AX.X, ALU.max).then_inc(s[p + "_first"], 1)
    wait(v, s, n, p + "_first")
    v.tensor_tensor(picked, rank, bc(top[:, :, None], shape), ALU.is_equal).then_inc(s[p + "_picked"], 1)



def l0_ffn(nc, g, a):
    ident, x, h_n, h_t, C = g["ident"], g["x"], g["h_n"], g["h_t"], g["consts"]
    names = ("loaded staged picked_t mask_t spread masked inner gelu outer sum1 sum2 gained shifted done "
             + NORM_STEPS + ROUTE_STEPS)
    with stage(nc, "f0", names) as (s, sb, ps):
        wr = sb("router", [D, EXPERTS]); w1 = sb("w1", [D, EXPERTS, 512]); b1 = sb("b1", [EXPERTS, 512])
        wo = sb("wo", [D, 4, D]); rows = sb("rows", [PT, 3, D]); pick = sb("pick", [EXPERTS, EXPERTS, D])
        early_rank = sb("earlier", [D, EXPERTS])
        hs, oht = ([sb(f"{n}{p}", [rows, GT]) for p in range(2)] for n, rows in (("hs", D), ("oht", EXPERTS)))
        xm = [sb(f"xm{p}", [D, EXPERTS, GT]) for p in range(2)]; ge = sb("gelu", [D, 4, GT])
        oh = sb("oh", [PT, GROUP, EXPERTS]); rank = sb("rank", [PT, GROUP, EXPERTS]); top = sb("top", [PT, GROUP])
        y = sb("y", [PT, GROUP, D]); sq = sb("ysq", [PT, GROUP, D])
        st = [sb(f"st{k}", [PT, GROUP])[:] for k in range(5)]
        loads = ((wr[:], a["L0_ffn_router"]), (w1[:], a["L0_ffn_w1"]), (b1[:], a["L0_ffn_b1"]),
                 (wo[:], a["L0_ffn_wo"]), (pick[:], C["pick"]), (early_rank[:], C["earlier"]))
        loads += tuple((rows[:, k, :], bc(a["L0_ffn_rows"][k:k + 1, :], [PT, D])) for k in range(3))
        normalise(nc, g, "n2", [("layer", 1e-5)], loads=loads, loaded=s["loaded"])
        small = ps("small", [D, 512]); spread = ps("spread", [D, 2, 512]); inner = ps("inner", [D, 4, 512]); outer = ps("outer", [D, 512])
        with nc.Block() as block:
            @block.tensor
            def _(pe):
                pe.wait_ge(s["loaded"], 144)

                def route(c, p):
                    wait(pe, s, c + 1, "staged")
                    if not early(c, 1):
                        wait(pe, s, c, "r_best")
                    for t in range(GROUP):
                        mm = pe.matmul(small[0:PT, t * EXPERTS:(t + 1) * EXPERTS], hs[p][:, t * PT:(t + 1) * PT], wr[:], start=True, stop=True)
                    mm.then_inc(s["r_logits"], 1)

                def turn_mask(c, p):
                    wait(pe, s, c + 1, "r_picked")
                    if not early(c, 1):
                        pe.wait_ge(s["masked"], c * EXPERTS)
                    for t in range(GROUP):
                        mm = pe.transpose(spread[0:EXPERTS, 0, t * PT:(t + 1) * PT], oh[:, t, :], ident[0:PT, 0:PT])
                    mm.then_inc(s["picked_t"], 1)

                def spread_mask(c, p, e):
                    if e == 0:
                        wait(pe, s, c + 1, "mask_t")
                    if e >= 2:
                        pe.wait_ge(s["masked"], c * EXPERTS + (e - 1))
                    pe.matmul(spread[:, e % 2, 0:GT], pick[:, e, :], oht[p][:], start=True, stop=True).then_inc(s["spread"], 1)

                def body(c, p):
                    more = c < 3
                    if more:
                        route(c + 1, 1 - p)
                    pe.wait_ge(s["masked"], (c + 1) * EXPERTS)
                    for f in range(4):
                        if not early(c, 1):
                            pe.wait_ge(s["gelu"], (c - 1) * 4 + f + 1)
                        if f == 2 and more:
                            turn_mask(c + 1, 1 - p)
                        for e in range(EXPERTS):
                            pe.matmul(inner[:, f, 0:GT], w1[:, e, f * D:(f + 1) * D], xm[p][:, e, :], start=(e == 0), stop=False)
                            if f >= 2 and e % 2 and more:
                                spread_mask(c + 1, 1 - p, (f - 2) * 4 + e // 2)
                        pe.matmul(inner[:, f, 0:GT], b1[:, f * D:(f + 1) * D], oht[p][:], start=False, stop=True).then_inc(s["inner"], 1)
                    pe.wait_ge(s["gelu"], (c + 1) * 4)
                    if not early(c, 1):
                        wait(pe, s, c, "sum1")
                    for t in range(GROUP):
                        for f in range(4):
                            mm = pe.matmul(outer[0:PT, t * D:(t + 1) * D], ge[:, f, t * PT:(t + 1) * PT], wo[:, f, :],
                                           start=(f == 0), stop=(f == 3))
                    mm.then_inc(s["outer"], 1)

                route(0, 0)
                turn_mask(0, 0)
                for e in range(EXPERTS):
                    spread_mask(0, 0, e)
                walk(pe, 4, body)

            @block.scalar
            def _(act):
                def stage_rows(c, p):
                    if not early(c, 2):
                        act.wait_ge(s["masked"], (c - 1) * EXPERTS)
                    act.activation(hs[p][:], h_t[:, c * GT:(c + 1) * GT], ACT.Copy).then_inc(s["staged"], 1)

                def copy_mask(c, p):
                    wait(act, s, c + 1, "picked_t")
                    if not early(c, 2):
                        act.wait_ge(s["inner"], (c - 1) * 4)
                    act.activation(oht[p][:], spread[0:EXPERTS, 0, 0:GT], ACT.Copy).then_inc(s["mask_t"], 1)

                def body(c, p):
                    for f in range(4):
                        if f == 2 and c < 3:
                            copy_mask(c + 1, 1 - p)
                        act.wait_ge(s["inner"], c * 4 + (f + 1))
                        if f == 0 and not early(c, 1):
                            wait(act, s, c, "outer")
                        act.activation(ge[:, f, :], inner[:, f, 0:GT], ACT.Gelu).then_inc(s["gelu"], 1)
                    if c < 2:
                        stage_rows(c + 2, p)

                stage_rows(0, 0)
                stage_rows(1, 1)
                copy_mask(0, 0)
                walk(act, 4, body)

            @block.vector
            def _(v):
                v.wait_ge(s["loaded"], 144)

                def route(c, p):
                    wait(v, s, c + 1, "r_logits")
                    if not early(c, 1):
                        wait(v, s, c, "picked_t", "r_picked")
                    argmax_vector(v, s, c + 1, "r", small[0:PT, 0:GROUP * EXPERTS].rearrange("t (a e) -> t a e", e=EXPERTS),
                                  top[:], rank[:], early_rank, oh[:])

                def mask_rows(c, p):
                    for e in range(EXPERTS):
                        v.wait_ge(s["spread"], c * EXPERTS + (e + 1))
                        if e == 0 and not early(c, 2):
                            v.wait_ge(s["inner"], (c - 1) * 4)
                        v.tensor_tensor(xm[p][:, e, :], hs[p][:], spread[:, e % 2, 0:GT], ALU.mult).then_inc(s["masked"], 1)

                def body(c, p):
                    n = c + 1
                    if c < 3:
                        route(c + 1, 1 - p)
                        mask_rows(c + 1, 1 - p)
                    wait(v, s, n, "outer")
                    if not early(c, 1):
                        wait(v, s, c, "done")
                    here = slice(c * GROUP, (c + 1) * GROUP)
                    v.tensor_tensor(y[:], outer[0:PT, :].rearrange("t (a d) -> t a d", a=GROUP), h_n[:, here, :], ALU.add).then_inc(s["sum1"], 1)
                    wait(v, s, n, "sum1")
                    v.tensor_tensor(y[:], y[:], bc(rows[:, 0:1, :], [PT, GROUP, D]), ALU.add).then_inc(s["sum2"], 1)
                    wait(v, s, n, "sum2")
                    norm_vector(v, s, n, y[:], sq[:], st, D, 1e-12)
                    wait(v, s, n, "n_normed")
                    v.tensor_tensor(y[:], y[:], bc(rows[:, 1:2, :], [PT, GROUP, D]), ALU.mult).then_inc(s["gained"], 1)
                    wait(v, s, n, "gained")
                    v.tensor_tensor(y[:], y[:], bc(rows[:, 2:3, :], [PT, GROUP, D]), ALU.add).then_inc(s["shifted"], 1)
                    wait(v, s, n, "shifted")
                    v.tensor_tensor(x[:, here, :], x[:, here, :], y[:], ALU.add).then_inc(s["done"], 1)

                route(0, 0)
                mask_rows(0, 0)
                walk(v, 4, body)

            @block.gpsimd
            def _(pool):
                walk(pool, 4, lambda c, p: norm_pool(pool, s, c + 1, st, g["half"][0:PT, 0:GROUP]))



def l1_attention(nc, g, a):
    ident, x, h_t = g["ident"], g["x"], g["h_t"]
    LEVELS = len(HALVES)
    names = ("loaded cleared staged xx xxx mix tanh m mixed xs proj_rkg proj_d proj_v d_tanh w_t decay rk v_copied scan diffs cut exps factors "
             "g_exp g_one g_inv gate a_ready a_masked a_sum y_ready y_copied y_turned y_affine gated out_ready done " + NORM_STEPS)
    with stage(nc, "r1", names) as (s, sb, ps):
        maa = sb("maa", [D, 6]); w1 = sb("w1", [D, 160]); w2 = sb("w2", [32, 5, D]); td = sb("decay", [D, 1]); dw1 = sb("dw1", [D, 64]); dw2 = sb("dw2", [64, D])
        bonus = sb("bonus", [D, 1]); w = sb("w", [D, 5, D]); lnw = sb("ln", [D, 2]); lm = sb("level_mask", [PT, LEVELS + 1, PT])
        hs = [sb(f"hs{p}", [D, 2, SEQ]) for p in range(2)]; xx = sb("xx", [D, 2, SEQ]); x3 = sb("xxx", [D, 2, SEQ]); mix = sb("mix", [32, 5, PT]); xs = sb("xs", [D, 5, PT])
        dh = sb("dh", [64, PT]); e = sb("e", [D, 2, SEQ]); cum = sb("cum", [D, 2, 65]); on = sb("on", [D, SEQ])
        rk = sb("rk", [D, 2, PT]); vs = sb("vs", [PT, D]); ex = sb("ex", [D, 2, LEVELS, 2, 64]); fac = sb("fac", [D, 2, LEVELS + 1, PT])
        gt = [sb(f"gate{p}", [D, PT]) for p in range(2)]; am = sb("am", [PT, 2, LEVELS + 1, PT]); at = sb("at", [PT, 2, PT])
        y = sb("y", [PT, 2, 64]); sq = sb("ysq", [PT, 2, 64]); yt = sb("yt", [D, PT])
        st = [sb(f"st{k}", [PT, 2])[:] for k in range(5)]
        loads = [(maa[:, k:k + 1], a[f"L1_maa_{c}"]) for k, c in enumerate("xwkvrg")]
        loads += [(w1[:], a["L1_maa_w1"]), (w2[:], a["L1_maa_w2"]), (td[:], a["L1_decay"]), (dw1[:], a["L1_decay_w1"]), (dw2[:], a["L1_decay_w2"]),
                  (bonus[:], a["L1_bonus"]), (w[:], a["L1_w"]), (lnw[:, 0:1], a["L1_ln_w"]), (lnw[:, 1:2], a["L1_ln_b"]), (lm[:], g["consts"]["level_mask"])]
        normalise(nc, g, "n3", [("layer", 1e-5)], loads=loads, loaded=s["loaded"])
        lo = ps("lo", [D, 2, 512]); mp = ps("mp", [D, 2, 512]); pa = ps("pa", [D, 4, 512])
        flat = lambda buf: buf.rearrange("d a b -> d (a b)")
        slot = lambda buf, k, rows=slice(0, D): buf[rows, k // 4, (k % 4) * PT:(k % 4 + 1) * PT]
        is_last = lambda i: isinstance(i, int) and i == PAIRS - 1
        with nc.Block() as block:
            @block.tensor
            def _(pe):
                pe.wait_ge(s["loaded"], 256)

                def mix_products(i):
                    wait(pe, s, i + 1, "xxx")
                    for k in range(5):
                        mm = pe.matmul(slot(lo, k, slice(0, 32)), w1[:, 32 * k:32 * k + 32], flat(x3), start=True, stop=True)
                    mm.then_inc(s["mix"], 1)

                def shift_products(i):
                    pe.wait_ge(s["tanh"], i * 2 + 2)
                    if not early(i, 1):
                        wait(pe, s, i, "v_copied", "gate")
                    for k in range(5):
                        mm = pe.matmul(slot(mp, k), w2[:, k, :], mix[:, k, :], start=True, stop=True)
                    mm.then_inc(s["m"], 1)

                def projections(i):
                    wait(pe, s, i + 1, "xs")
                    pe.matmul(lo[0:64, 0, 0:PT], dw1[:], xs[:, 0, :], start=True, stop=True).then_inc(s["proj_d"], 1)
                    pe.matmul(slot(mp, 0), w[:, 0, :], xs[:, 3, :], start=True, stop=True)
                    pe.matmul(slot(mp, 1), w[:, 1, :], xs[:, 1, :], start=True, stop=True)
                    pe.matmul(slot(mp, 2), w[:, 3, :], xs[:, 4, :], start=True, stop=True).then_inc(s["proj_rkg"], 1)
                    pe.matmul(mp[0:PT, 1, 0:D], xs[:, 2, :], w[:, 2, :], start=True, stop=True).then_inc(s["proj_v"], 1)
                    wait(pe, s, i + 1, "d_tanh")
                    pe.matmul(lo[:, 1, 0:PT], dw2[:], dh[:], start=True, stop=True).then_inc(s["w_t"], 1)

                def pair_products(i, h):
                    rows = slice(64 * h, 64 * h + 64)
                    for l in range(LEVELS + 1):
                        mm = pe.matmul(pa[0:PT, 2 * h + l // 4, (l % 4) * PT:(l % 4 + 1) * PT], fac[rows, 1, l, :], fac[rows, 0, l, :], start=True, stop=True)
                    mm.then_inc(s["a_ready"], 1)

                def body(i, p):
                    pe.wait_ge(s["factors"], i * 4 + 4)
                    if not early(i, 1):
                        wait(pe, s, i, "done")
                    pair_products(i, 0)
                    if not is_last(i):
                        mix_products(i + 1)
                    pair_products(i, 1)
                    if not is_last(i):
                        shift_products(i + 1)
                    pe.wait_ge(s["a_sum"], i * 2 + 2)
                    wait(pe, s, i + 1, "v_copied")
                    for h in range(2):
                        mm = pe.matmul(pa[0:PT, 3, 64 * h:64 * h + 64], at[:, h, :], vs[:, 64 * h:64 * h + 64], start=True, stop=True)
                    mm.then_inc(s["y_ready"], 1)
                    if not is_last(i):
                        projections(i + 1)
                    wait(pe, s, i + 1, "n_normed")
                    pe.transpose(pa[:, 3, D:D + PT], flat(y), ident[0:PT, 0:PT]).then_inc(s["y_turned"], 1)
                    wait(pe, s, i + 1, "gated")
                    pe.matmul(pa[0:PT, 3, 2 * D:3 * D], yt[:], w[:, 4, :], start=True, stop=True).then_inc(s["out_ready"], 1)

                mix_products(0)
                shift_products(0)
                projections(0)
                walk(pe, PAIRS, body)

            @block.scalar
            def _(act):
                act.wait_ge(s["loaded"], 256)

                def stage_rows(i, p):
                    if not early(i, 2):
                        wait(act, s, i - 1, "xs")
                    act.activation(flat(hs[p]), h_t[:, bass.ds(i * PT, PT)], ACT.Copy).then_inc(s["staged"], 1)

                def first_part(i, p):
                    n = i + 1
                    wait(act, s, n, "mix")
                    act.activation(mix[:, 0:4, :].rearrange("k a t -> k (a t)"), lo[0:32, 0, 0:4 * PT], ACT.Tanh).then_inc(s["tanh"], 1)
                    act.activation(mix[:, 4, :], lo[0:32, 1, 0:PT], ACT.Tanh).then_inc(s["tanh"], 1)
                    wait(act, s, n, "proj_d")
                    act.activation(dh[:], lo[0:64, 0, 0:PT], ACT.Tanh).then_inc(s["d_tanh"], 1)
                    wait(act, s, n, "proj_rkg")
                    act.activation(flat(rk), mp[:, 0, 0:2 * PT], ACT.Copy).then_inc(s["rk"], 1)
                    act.activation(gt[p][:], slot(mp, 2), ACT.Exp, scale=-1.0).then_inc(s["g_exp"], 1)
                    wait(act, s, n, "w_t")
                    act.activation(flat(e), lo[:, 1, 0:PT], ACT.Exp, bias=td[:, 0:1]).then_inc(s["decay"], 1)
                    wait(act, s, n, "proj_v")
                    act.activation(vs[:], mp[0:PT, 1, 0:D], ACT.Copy).then_inc(s["v_copied"], 1)

                def exps(i):
                    wait(act, s, i + 1, "cut")
                    act.activation(ex[:], ex[:], ACT.Exp).then_inc(s["exps"], 1)

                def body(i, p):
                    if not is_last(i):
                        first_part(i + 1, 1 - p)
                    wait(act, s, i + 1, "y_turned")
                    if not early(i, 1):
                        wait(act, s, i, "out_ready")
                    act.activation(yt[:], pa[:, 3, D:D + PT], ACT.Identity, scale=lnw[:, 0:1], bias=lnw[:, 1:2]).then_inc(s["y_affine"], 1)
                    if not isinstance(i, int) or i + 2 < PAIRS:
                        stage_rows(i + 2, p)
                    if not is_last(i):
                        exps(i + 1)

                stage_rows(0, 0)
                stage_rows(1, 1)
                first_part(0, 0)
                exps(0)
                walk(act, PAIRS, body)

            @block.vector
            def _(v):
                v.memset(on[:], 1.0).then_inc(s["cleared"], 1)
                v.memset(cum[:], 0.0).then_inc(s["cleared"], 1)
                v.wait_ge(s["cleared"], 2)
                v.wait_ge(s["loaded"], 256)

                def differences(i, p):
                    n = i + 1
                    wait(v, s, n, "staged")
                    if not early(i, 1):
                        v.wait_ge(s["mixed"], i * 5)
                    v.tensor_tensor(xx[:, :, 1:SEQ], hs[p][:, :, 0:SEQ - 1], hs[p][:, :, 1:SEQ], ALU.subtract).then_inc(s["xx"], 1)
                    v.tensor_scalar(xx[:, :, 0:1], hs[p][:, :, 0:1], -1.0, None, ALU.mult).then_inc(s["xx"], 1)
                    v.wait_ge(s["xx"], n * 2)
                    if not early(i, 1):
                        wait(v, s, i, "mix")
                    v.scalar_tensor_tensor(flat(x3), flat(xx), maa[:, 0:1], flat(hs[p]), ALU.mult, ALU.add).then_inc(s["xxx"], 1)

                def mixtures(i, p):
                    n = i + 1
                    wait(v, s, n, "m")
                    if not early(i, 1):
                        wait(v, s, i, "proj_v")
                    for k in range(5):
                        v.scalar_tensor_tensor(xs[:, k, :], slot(mp, k), maa[:, k + 1:k + 2], flat(xx), ALU.add, ALU.mult).then_inc(s["mixed"], 1)
                    v.wait_ge(s["mixed"], n * 5)
                    v.tensor_tensor(xs[:], xs[:], bc(flat(hs[p])[:, None, :], [D, 5, PT]), ALU.add).then_inc(s["xs"], 1)

                def gate_and_sums(i, p):
                    n = i + 1
                    wait(v, s, n, "g_exp")
                    v.tensor_scalar(gt[p][:], gt[p][:], 1.0, None, ALU.add).then_inc(s["g_one"], 1)
                    wait(v, s, n, "g_one")
                    v.reciprocal(gt[p][:], gt[p][:]).then_inc(s["g_inv"], 1)
                    wait(v, s, n, "g_inv", "rk")
                    v.tensor_tensor(gt[p][:], gt[p][:], slot(mp, 2), ALU.mult).then_inc(s["gate"], 1)
                    wait(v, s, n, "decay")
                    if not early(i, 1):
                        v.wait_ge(s["diffs"], i * (2 * LEVELS))
                    for b in range(2):
                        v.tensor_tensor_scan(cum[:, b, 1:SEQ + 1], on[:], e[:, b, :], 0.0, ALU.mult, ALU.add).then_inc(s["scan"], 1)

                def exponents(i):
                    v.wait_ge(s["scan"], i * 2 + 2)
                    if not early(i, 1):
                        v.wait_ge(s["factors"], i * 4)
                    for l, m in enumerate(HALVES):
                        shape = [D, 2, 64 // (2 * m), 2 * m]
                        blocks = lambda buf: buf.rearrange("d b (c u) -> d b c u", u=2 * m)
                        ref = bc(blocks(cum[:, :, 0:64])[:, :, :, m:m + 1], shape)
                        v.tensor_tensor(blocks(ex[:, 0, l, :, :]), ref, blocks(cum[:, :, 0:64]), ALU.subtract).then_inc(s["diffs"], 1)
                        v.tensor_tensor(blocks(ex[:, 1, l, :, :]), blocks(cum[:, :, 1:65]), ref, ALU.subtract).then_inc(s["diffs"], 1)
                    v.wait_ge(s["diffs"], i * (2 * LEVELS) + 2 * LEVELS)
                    v.tensor_scalar(ex[:], ex[:], 0.0, None, ALU.min).then_inc(s["cut"], 1)

                def factors(i):
                    wait(v, s, i + 1, "exps", "rk")
                    if not early(i, 1):
                        v.wait_ge(s["a_ready"], i * 2)
                    for q in range(2):
                        v.tensor_tensor(fac[:, q, 0:LEVELS, :].rearrange("d l (b t) -> d l b t", b=2), ex[:, q, :, :, 0:SEQ],
                                        bc(rk[:, q, :].rearrange("d (b t) -> d b t", b=2)[:, None, :, :], [D, LEVELS, 2, SEQ]), ALU.mult)\
                            .then_inc(s["factors"], 1)
                    v.tensor_scalar(fac[:, 0, LEVELS, :], rk[:, 0, :], bonus[:, 0:1], None, ALU.mult).then_inc(s["factors"], 1)
                    v.tensor_copy(fac[:, 1, LEVELS, :], rk[:, 1, :]).then_inc(s["factors"], 1)

                def body(i, p):
                    n = i + 1

                    def ahead(step, *args):
                        if not is_last(i):
                            step(i + 1, *args)

                    ahead(differences, 1 - p)
                    for h in range(2):
                        v.wait_ge(s["a_ready"], i * 2 + (h + 1))
                        if not early(i, 1):
                            v.wait_ge(s["a_sum"], (i - 1) * 2 + (h + 1))
                            v.wait_ge(s["y_ready"], i)
                        for q, (lo_l, hi_l) in enumerate(((0, 4), (4, LEVELS + 1))):
                            v.tensor_tensor(am[:, h, lo_l:hi_l, :], pa[0:PT, 2 * h + q, 0:(hi_l - lo_l) * PT].rearrange("s (l t) -> s l t", t=PT),
                                            lm[:, lo_l:hi_l, :], ALU.mult).then_inc(s["a_masked"], 1)
                        v.wait_ge(s["a_masked"], i * 4 + (2 * h + 2))
                        v.tensor_reduce(at[:, h, :], am[:, h, :, :].rearrange("s l t -> s t l"), AX.X, ALU.add).then_inc(s["a_sum"], 1)
                    ahead(mixtures, 1 - p)
                    wait(v, s, n, "y_ready")
                    if not early(i, 1):
                        wait(v, s, i, "y_turned")
                    v.tensor_copy(flat(y), pa[0:PT, 3, 0:D]).then_inc(s["y_copied"], 1)
                    wait(v, s, n, "y_copied")
                    norm_start(v, s, n, y[:], sq[:], st, 64, 1e-5 * 64)
                    ahead(gate_and_sums, 1 - p)
                    norm_end(v, s, n, y[:], st)
                    ahead(exponents)
                    wait(v, s, n, "y_affine")
                    v.tensor_tensor(yt[:], yt[:], gt[p][:], ALU.mult).then_inc(s["gated"], 1)
                    ahead(factors)
                    wait(v, s, n, "out_ready")
                    v.tensor_tensor(x[:, i, :], pa[0:PT, 3, 2 * D:3 * D], x[:, i, :], ALU.add).then_inc(s["done"], 1)

                differences(0, 0)
                mixtures(0, 0)
                gate_and_sums(0, 0)
                exponents(0)
                factors(0)
                walk(v, PAIRS, body)

            @block.gpsimd
            def _(pool):
                walk(pool, PAIRS, lambda i, p: norm_pool(pool, s, i + 1, st, g["half"][0:PT, 0:2]))



def l1_cross(nc, g, a):
    ident, ones, x, h_t = g["ident"], g["ones"], g["x"], g["h_t"]
    C, S, KV = HEADS * SEQ // D, SEQ, 6
    TURNS = KV + 3 * C
    Q4 = 4 * SEQ
    names = ("loaded bq_scaled q_made q_t ctxt0 ctxt1 mask0 mask1 q_ready turned freed0 freed1 scores masked negmax probs inverse diag pv oz_copied "
             "spread o_norm picked u_sum u_ready out_ready out_sum done")
    with stage(nc, "x1", names) as (s, sb, ps):
        wq = sb("wq", [D, D]); wkv = sb("wkv", [D, 2 * D]); wp = sb("wp", [D, D]); bias = sb("bias", [D, 4]); bp = sb("bp", [PT, D]); hm = sb("hm", [D, HEADS]); hm4 = sb("hm4", [D, 4])
        qt = sb("q_t", [D, TOK]); ct = [sb(f"ctx_t{j}", [D, CTX]) for j in range(2)]; mk = [sb(f"mask{j}", [D, CTX]) for j in range(2)]
        qb = [sb(f"q{j}", [D, HEADS, S]) for j in range(2)]; kt = sb("k_t", [D, CTX]); vv = [sb(f"v{j}", [TP, TILES, D]) for j in range(2)]
        pr = [sb(f"pr{k}", [D, CTX]) for k in range(4)]; pt = sb("pt", [TP, TILES, C * D])
        mx = sb("mx", [D, 3]); nm = sb("nm", [D, 3]); l = [sb(f"l{j}", [D, C]) for j in range(2)]; rl = sb("rl", [D, C]); dg = sb("dg", [D, C * D])
        o1 = sb("o1", [D, 4, SEQ]); ub = sb("ub", [D, S]); ut = sb("ut", [D, PT]); acc = sb("acc", [PT, D])
        loads = ((wq[:], a["L1_xattn_wq"]), (wkv[:], a["L1_xattn_wkv"]), (wp[:], a["L1_xattn_wp"]), (bias[:, 0:1], a["L1_xattn_bq"]),
                 (bias[:, 1:2], a["L1_xattn_bk"]), (bias[:, 2:3], a["L1_xattn_bv"]), (bp[:], bc(a["L1_xattn_bp"], [PT, D])),
                 (hm[:], g["headmask"]), (hm4[:], g["consts"]["headmask4"]))
        normalise(nc, g, "n4", [("layer", 1e-5)], loads=loads, loaded=s["loaded"])
        sc = ps("sc", [D, 6, 512]); turn = ps("turn", [D, 2, 512])
        oz, spread, out = sc[:, 3, :], sc[:, 4, :], sc[:, 5, :]

        def cnt(i, j, per, k):
            return i * (2 * per) + (j * per + k)

        is_first = lambda i, j: isinstance(i, int) and i == 0 and j == 0
        is_last = lambda i, j: isinstance(i, int) and i == PAIRS - 1 and j == 1
        before_of = lambda i, j: (i, 0) if j else (i - 1, 1)
        after_of = lambda i, j: (i, 1) if j == 0 else (i + 1, 0)
        buf_of = lambda c: 3 if c == C - 1 else c % 3
        slot_of = lambda c: slice(2, 3) if c == C - 1 else slice(c % 2, c % 2 + 1)

        def chunk_place(i, j, c, b):
            if c == C - 2 and not is_last(i, j):
                k = 3 * c + 2 * b
            else:
                k = 3 * c + b + (KV if c == C - 1 and not is_last(i, j) else 0)
            return i, KV + TURNS * j + k

        def keys_place(i, j, b):
            if is_first(i, j):
                return 0, b
            q, p = before_of(i, j)
            return q, KV + TURNS * p + 3 * (C - 2) + 2 * b + 1

        def values_place(i, j, b):
            if is_first(i, j):
                return 0, 3 + b
            q, p = before_of(i, j)
            return q, KV + TURNS * p + 3 * (C - 1) + 3 + b

        def emitted(place):
            i, n = place
            return i * (2 * TURNS) + (n + 1)

        def freed(place):
            i, n = place
            return s[f"freed{n % 2}"], i * TURNS + (n // 2 + 1)

        with nc.Block() as block:
            @block.sync
            def _(sp):
                def body(i):
                    for j in range(2):
                        if not (isinstance(i, int) and i == 0):
                            sp.wait_ge(s["turned"], emitted(values_place(i - 1, j, 2)))
                            apart(sp)
                            sp.wait_ge(s["masked"], cnt(i - 1, j, C, C))
                        sp.dma_start(ct[j][:], a["ctx_t"][bass.ds(i * 2 + j, 1), :, :].rearrange("o d c -> (o d) c")).then_inc(s[f"ctxt{j}"], 16)
                        sp.dma_start(mk[j][:], bc(a["ctx_mask"][bass.ds(i * 2 + j, 1), :, :].rearrange("o r c -> (o r) c"), [D, CTX]))\
                            .then_inc(s[f"mask{j}"], 16)
                rounds(sp, body)

            @block.tensor
            def _(pe):
                pe.wait_ge(s["loaded"], 144)
                for b in range(4):
                    pe.matmul(sc[:, b, 0:GT], wq[:], h_t[:, b * GT:(b + 1) * GT], start=True, stop=True).then_inc(s["q_made"], 1)
                pe.wait_ge(s["q_t"], 4)

                def group(place, emit):
                    i, n = place
                    if not (isinstance(i, int) and i == 0 and n < 2):
                        pe.wait_ge(s[f"freed{n % 2}"], i * TURNS + n // 2)
                    emit(turn[:, n % 2, :]).then_inc(s["turned"], 1)

                def keys(i, j, b):
                    if b == 0:
                        pe.wait_ge(s[f"ctxt{j}"], i * 16 + 16)
                    group(keys_place(i, j, b), lambda bank: pe.matmul(bank[:, 0:BANKC], wkv[:, 0:D], ct[j][:, b * BANKC:(b + 1) * BANKC], start=True, stop=True))

                def values(i, j, b):
                    def tiles(bank):
                        for t in range(4):
                            mm = pe.matmul(bank[0:TP, t * D:(t + 1) * D], ct[j][:, (4 * b + t) * TP:(4 * b + t + 1) * TP], wkv[:, D:2 * D],
                                           start=True, stop=True)
                        return mm
                    group(values_place(i, j, b), tiles)

                def pair_out(i):
                    pe.wait_ge(s["u_ready"], cnt(i, 1, 1, 1))
                    pe.matmul(out[0:PT, 0:D], ut[:], wp[:], start=True, stop=True).then_inc(s["out_ready"], 1)

                def score(i, j, c, fill=None):
                    if c >= 2:
                        pe.wait_ge(s["masked"], cnt(i, j, C, c - 1))
                    elif c == 0:
                        if not is_first(i, j):
                            pe.wait_ge(s["masked"], cnt(i, j, C, 0))
                        for b in (1, 2) if is_first(i, j) else (2,):
                            pe.wait_ge(*freed(keys_place(i, j, b)))
                        pe.wait_ge(s["q_ready"], cnt(i, j, 1, 1))
                    elif not is_first(i, j):
                        pe.wait_ge(s["oz_copied"], cnt(i, j, 1, 0))
                        pe.wait_ge(s["o_norm"], cnt(i, j, 1, 0))
                        if j == 1 and not (isinstance(i, int) and i == 0):
                            pe.wait_ge(s["out_sum"], i)
                    for b in range(3):
                        mm = pe.matmul(sc[:, 3 * (c % 2) + b, 0:BANKC], qb[j].rearrange("d h t -> d (h t)")[:, c * D:(c + 1) * D],
                                       kt[:, b * BANKC:(b + 1) * BANKC], start=True, stop=True)
                        if fill is not None and b < 2:
                            fill(b)
                    mm.then_inc(s["scores"], 1)

                def body(i):
                    for j in range(2):
                        after = after_of(i, j)
                        more = not is_last(i, j)

                        def turn_group(c, b):
                            def tiles(bank):
                                for t in range(4):
                                    mm = pe.transpose(bank[0:TP, t * D:(t + 1) * D], pr[buf_of(c)][:, (4 * b + t) * TP:(4 * b + t + 1) * TP], ident[:])
                                return mm
                            if b == 0:
                                pe.wait_ge(s["probs"], cnt(i, j, C, c + 1))
                            group(chunk_place(i, j, c, b), tiles)

                        turn_group(0, 0)
                        turn_group(0, 1)
                        score(i, j, 1)
                        turn_group(0, 2)
                        score(i, j, 2)
                        for c in range(1, C - 2):
                            score(i, j, c + 2, lambda b: turn_group(c, b))
                            turn_group(c, 2)
                        for b in range(3):
                            turn_group(C - 2, b)
                            if more:
                                keys(*after, b)
                        if more:
                            for b in range(3):
                                values(*after, b)
                            score(*after, 0)
                        for b in range(3):
                            turn_group(C - 1, b)
                        if j == 0 and not (isinstance(i, int) and i == 0):
                            pair_out(i - 1)
                        for b in (1, 2):
                            pe.wait_ge(*freed(chunk_place(i, j, C - 1, b)))
                        for t in range(TILES):
                            for q in range(4):
                                mm = pe.matmul(oz[32 * q:32 * q + 32, 0:Q4], vv[j][:, t, 32 * q:32 * q + 32], pt[:, t, Q4 * q:Q4 * (q + 1)],
                                               start=(t == 0), stop=(t == TILES - 1), tile_position=(0, 32 * q))
                        mm.then_inc(s["pv"], 1)
                        pe.wait_ge(s["diag"], cnt(i, j, 1, 1))
                        for q in range(4):
                            mm = pe.matmul(spread[32 * q:32 * q + 32, 0:Q4], ones[:, 32 * q:32 * q + 32], dg[:, Q4 * q:Q4 * (q + 1)],
                                           start=True, stop=True, tile_position=(0, 32 * q))
                        mm.then_inc(s["spread"], 1)

                for b in range(3):
                    keys(0, 0, b)
                for b in range(3):
                    values(0, 0, b)
                score(0, 0, 0)
                rounds(pe, body)
                pair_out(PAIRS - 1)

            @block.scalar
            def _(act):
                act.wait_ge(s["bq_scaled"], 1)
                for b in range(4):
                    act.wait_ge(s["q_made"], b + 1)
                    act.activation(qt[:, b * GT:(b + 1) * GT], sc[:, b, 0:GT], ACT.Identity, scale=8 ** -0.5, bias=bias[:, 3:4]).then_inc(s["q_t"], 1)

                def copy_group(place, dst, src, **kw):
                    if place[1] % 2 == 0:
                        act.wait_ge(s["turned"], emitted(place))
                        act.activation(dst, src, ACT.Identity if kw else ACT.Copy, **kw).then_inc(s["freed0"], 1)

                def copy_keys(i, j, b):
                    copy_group(keys_place(i, j, b), kt[:, b * BANKC:(b + 1) * BANKC], turn[:, 0, 0:BANKC], bias=bias[:, 1:2])

                def copy_values(i, j):
                    for b in range(3):
                        copy_group(values_place(i, j, b), vv[j][:, 4 * b:4 * b + 4, :], turn[0:TP, 0, :].rearrange("p (t d) -> p t d", d=D))

                def copy_probs(i, j, c, b):
                    copy_group(chunk_place(i, j, c, b), pt[:, 4 * b:4 * b + 4, c * D:(c + 1) * D], turn[0:TP, 0, :].rearrange("p (t q) -> p t q", t=4))

                def exps(i, j, c):
                    act.wait_ge(s["negmax"], cnt(i, j, C, c + 1))
                    act.activation(pr[buf_of(c)][:], pr[buf_of(c)][:], ACT.Exp, bias=nm[:, slot_of(c)], accum_out=l[j][:, c:c + 1]).then_inc(s["probs"], 1)

                def body(i):
                    for j in range(2):
                        after = after_of(i, j)
                        more = not is_last(i, j)
                        for c in range(C - 2):
                            copy_probs(i, j, c, 0)
                            exps(i, j, c + 1)
                            copy_probs(i, j, c, 1)
                            copy_probs(i, j, c, 2)
                        for b in range(3):
                            if b == 2:
                                exps(i, j, C - 1)
                            copy_probs(i, j, C - 2, b)
                            if more:
                                copy_keys(*after, b)
                        if more:
                            copy_values(*after)
                        for b in range(3):
                            copy_probs(i, j, C - 1, b)
                        if more:
                            exps(*after, 0)
                        act.wait_ge(s["pv"], cnt(i, j, 1, 1))
                        if not is_first(i, j):
                            act.wait_ge(s["u_sum"], cnt(i, j, 1, 0))
                        act.activation(o1.rearrange("d h t -> d (h t)"), oz[:, 0:Q4], ACT.Copy).then_inc(s["oz_copied"], 1)

                for b in range(3):
                    copy_keys(0, 0, b)
                copy_values(0, 0)
                exps(0, 0, 0)
                rounds(act, body)

            @block.gpsimd
            def _(pool):
                pool.wait_ge(s["q_t"], 4)
                pool.wait_ge(s["loaded"], 144)

                def body(i):
                    for j in range(2):
                        if not (isinstance(i, int) and i == 0):
                            pool.wait_ge(s["scores"], cnt(i - 1, j, C, C))
                        pool.tensor_tensor(qb[j][:], bc(qt[:, bass.ds((i * 2 + j) * S, S)][:, None, :], [D, HEADS, S]),
                                           bc(hm[:, :, None], [D, HEADS, S]), ALU.mult).then_inc(s["q_ready"], 1)
                rounds(pool, body)

            @block.vector
            def _(v):
                v.wait_ge(s["loaded"], 144)
                v.tensor_scalar(bias[:, 3:4], bias[:, 0:1], 8 ** -0.5, None, ALU.mult).then_inc(s["bq_scaled"], 1)

                def add_out(i):
                    v.wait_ge(s["out_ready"], i + 1)
                    v.tensor_tensor(acc[:], out[0:PT, 0:D], bp[:], ALU.add).then_inc(s["out_sum"], 1)
                    v.wait_ge(s["out_sum"], i + 1)
                    v.tensor_tensor(x[:, i, :], acc[:], x[:, i, :], ALU.add).then_inc(s["done"], 1)

                def copy_group(place, emit):
                    if place[1] % 2:
                        v.wait_ge(s["turned"], emitted(place))
                        emit().then_inc(s["freed1"], 1)

                def copy_keys(i, j, b):
                    copy_group(keys_place(i, j, b), lambda: v.tensor_scalar(kt[:, b * BANKC:(b + 1) * BANKC], turn[:, 1, 0:BANKC], bias[:, 1:2], None, ALU.add))

                def copy_values(i, j):
                    for b in range(3):
                        copy_group(values_place(i, j, b), lambda: v.tensor_copy(vv[j][:, 4 * b:4 * b + 4, :], turn[0:TP, 1, :].rearrange("p (t d) -> p t d", d=D)))

                def copy_probs(i, j, c, b):
                    copy_group(chunk_place(i, j, c, b), lambda: v.tensor_copy(pt[:, 4 * b:4 * b + 4, c * D:(c + 1) * D],
                                                                              turn[0:TP, 1, :].rearrange("p (t q) -> p t q", t=4)))

                def maxima(i, j, c):
                    v.wait_ge(s["scores"], cnt(i, j, C, c + 1))
                    if c == 0:
                        v.wait_ge(s[f"mask{j}"], i * 16 + 16)
                    if c == C - 1:
                        v.wait_ge(s["turned"], emitted(chunk_place(i, j, 0, 0)))
                    elif c >= 3:
                        v.wait_ge(s["turned"], emitted(chunk_place(i, j, c - 3, 2)))
                    elif not is_first(i, j):
                        v.wait_ge(s["turned"], emitted(chunk_place(*before_of(i, j), c + 3, 2)))
                    if c >= 2:
                        v.wait_ge(s["probs"], cnt(i, j, C, c - 1))
                    elif not is_first(i, j):
                        v.wait_ge(s["probs"], cnt(i, j, C, c - 2))
                    apart(v)
                    v.tensor_tensor_reduce(pr[buf_of(c)].rearrange("q (a b) -> q a b", a=3), sc[:, 3 * (c % 2):3 * (c % 2) + 3, 0:BANKC],
                                           mk[j].rearrange("q (a b) -> q a b", a=3), 1.0, -3.0e38, ALU.add, ALU.max, mx[:, slot_of(c)])\
                        .then_inc(s["masked"], 1)
                    v.wait_ge(s["masked"], cnt(i, j, C, c + 1))
                    v.tensor_scalar(nm[:, slot_of(c)], mx[:, slot_of(c)], -1.0, None, ALU.mult).then_inc(s["negmax"], 1)

                for b in range(3):
                    copy_keys(0, 0, b)
                copy_values(0, 0)
                maxima(0, 0, 0)

                def body(i):
                    for j in range(2):
                        first = is_first(i, j)
                        after = after_of(i, j)
                        more = not is_last(i, j)
                        for b in range(3):
                            copy_probs(i, j, 0, b)
                        maxima(i, j, 1)
                        maxima(i, j, 2)
                        for c in range(1, C - 2):
                            for b in range(3):
                                copy_probs(i, j, c, b)
                            if c + 2 < C - 1:
                                maxima(i, j, c + 2)
                        for b in range(3):
                            copy_probs(i, j, C - 2, b)
                            if more:
                                copy_keys(*after, b)
                            if b == 0:
                                maxima(i, j, C - 1)
                        if more:
                            copy_values(*after)
                        for b in range(3):
                            copy_probs(i, j, C - 1, b)
                        if more:
                            maxima(*after, 0)
                        if j == 0 and not (isinstance(i, int) and i == 0):
                            add_out(i - 1)
                        v.wait_ge(s["probs"], cnt(i, j, C, C))
                        v.reciprocal(rl[:], l[j][:]).then_inc(s["inverse"], 1)
                        v.wait_ge(s["inverse"], cnt(i, j, 1, 1))
                        v.tensor_tensor(dg.rearrange("p (c q) -> p c q", c=C), bc(ident[:, None, :], [D, C, D]), bc(rl[:, :, None], [D, C, D]), ALU.mult)\
                            .then_inc(s["diag"], 1)
                        v.wait_ge(s["spread"], cnt(i, j, 1, 1))
                        v.wait_ge(s["oz_copied"], cnt(i, j, 1, 1))
                        v.tensor_tensor(o1.rearrange("d h t -> d (h t)"), o1.rearrange("d h t -> d (h t)"), spread[:, 0:Q4], ALU.mult).then_inc(s["o_norm"], 1)
                        v.wait_ge(s["o_norm"], cnt(i, j, 1, 1))
                        v.tensor_tensor(o1[:], o1[:], bc(hm4[:, :, None], [D, 4, SEQ]), ALU.mult).then_inc(s["picked"], 1)
                        v.wait_ge(s["picked"], cnt(i, j, 1, 1))
                        v.tensor_reduce(ub[:], o1.rearrange("d h t -> d t h"), AX.X, ALU.add).then_inc(s["u_sum"], 1)
                        v.wait_ge(s["u_sum"], cnt(i, j, 1, 1))
                        if j == 0 and not first:
                            v.wait_ge(s["out_ready"], i)
                        v.tensor_scalar(ut[:, j * S:(j + 1) * S], ub[:], bias[:, 2:3], None, ALU.add).then_inc(s["u_ready"], 1)

                rounds(v, body)
                add_out(PAIRS - 1)



def l1_ffn(nc, g, a):
    ident, x, h_n, h_t, C = g["ident"], g["x"], g["h_n"], g["h_t"], g["consts"]
    names = ("loaded staged gate_exp gate_one gate picked_t mask_t copied_n normed_t turned_n spread affine masked inner relu outer "
             "weighed summed biased bias_in gated resid done " + NORM_STEPS + ROUTE_STEPS)
    with stage(nc, "f1", names) as (s, sb, ps):
        wc = sb("centroids", [D, EXPERTS]); lg = sb("ln_g", [D, EXPERTS]); lb = sb("ln_b", [D, EXPERTS])
        w1 = sb("w1", [D, EXPERTS, 512]); b1 = sb("b1", [EXPERTS, 512]); w2 = sb("w2", [D, 4, EXPERTS, D]); b2 = sb("b2", [EXPERTS, D])
        pick = sb("pick", [EXPERTS, EXPERTS, D]); early_rank = sb("earlier", [D, EXPERTS])
        hs = [sb(f"hs{p}", [D, GT]) for p in range(2)]; xn = sb("xn", [D, GT]); xa = sb("xa", [D, GT]); xm = [sb(f"xm{p}", [D, EXPERTS, GT]) for p in range(2)]
        re = sb("relu", [D, 4, GT]); oht = [sb(f"oht{p}", [EXPERTS, GT]) for p in range(2)]
        oh = [sb(f"oh{p}", [PT, GROUP, EXPERTS]) for p in range(2)]; rank = sb("rank", [PT, GROUP, EXPERTS]); top = sb("top", [PT, GROUP]); gate = [sb(f"gate{p}", [PT, GROUP]) for p in range(2)]
        y = sb("y", [PT, GROUP, D]); sq = sb("ysq", [PT, GROUP, D]); res = sb("res", [PT, GROUP, D]); wy = sb("wy", [PT, EXPERTS, D]); fo = sb("fo", [PT, D])
        st = [sb(f"st{k}", [PT, GROUP])[:] for k in range(5)]
        loads = ((wc[:], a["L1_ffn_centroids"]), (lg[:], a["L1_ffn_g"]), (lb[:], a["L1_ffn_b"]), (w1[:], a["L1_ffn_w1"]),
                 (b1[:], a["L1_ffn_b1"]), (w2[:], a["L1_ffn_w2"]), (b2[:], a["L1_ffn_b2"]),
                 (pick[:], C["pick"]), (early_rank[:], C["earlier"]))
        normalise(nc, g, "n5", [("layer", 1e-5)], loads=loads, loaded=s["loaded"])
        small = ps("small", [D, 512]); spread = ps("spread", [D, 2, 512]); inner = ps("inner", [D, 4, 512]); bias = ps("bias", [D, 512])
        with nc.Block() as block:
            @block.tensor
            def _(pe):
                pe.wait_ge(s["loaded"], 144)

                def route(c, p):
                    wait(pe, s, c + 1, "staged")
                    if not early(c, 1):
                        wait(pe, s, c, "r_best")
                    for t in range(GROUP):
                        mm = pe.matmul(small[0:PT, t * EXPERTS:(t + 1) * EXPERTS], hs[p][:, t * PT:(t + 1) * PT], wc[:], start=True, stop=True)
                    mm.then_inc(s["r_logits"], 1)

                def turn_mask(c, p):
                    wait(pe, s, c + 1, "r_picked")
                    if not early(c, 1):
                        pe.wait_ge(s["masked"], c * EXPERTS)
                    for t in range(GROUP):
                        mm = pe.transpose(spread[0:EXPERTS, 0, t * PT:(t + 1) * PT], oh[p][:, t, :], ident[0:PT, 0:PT])
                    mm.then_inc(s["picked_t"], 1)
                    wait(pe, s, c + 1, "n_normed")
                    for t in range(GROUP):
                        mm = pe.transpose(spread[:, 1, t * PT:(t + 1) * PT], y[:, t, :], ident[0:PT, 0:PT])
                    mm.then_inc(s["turned_n"], 1)

                def spread_mask(c, p, e):
                    if e == 0:
                        wait(pe, s, c + 1, "mask_t", "copied_n")
                    if e >= 2:
                        pe.wait_ge(s["masked"], c * EXPERTS + (e - 1))
                    pe.matmul(spread[:, e % 2, 0:GT], pick[:, e, :], oht[p][:], start=True, stop=True).then_inc(s["spread"], 1)

                def body(c, p):
                    more = c < 3
                    if more:
                        route(c + 1, 1 - p)
                    pe.wait_ge(s["masked"], (c + 1) * EXPERTS)
                    if not early(c, 1):
                        pe.wait_ge(s["weighed"], c * GROUP)
                    for f in range(4):
                        if f == 2 and more:
                            turn_mask(c + 1, 1 - p)
                        for e in range(EXPERTS):
                            pe.matmul(inner[:, f, 0:GT], w1[:, e, f * D:(f + 1) * D], xm[p][:, e, :], start=(e == 0), stop=False)
                            if f >= 2 and e % 2 and more:
                                spread_mask(c + 1, 1 - p, (f - 2) * 4 + e // 2)
                        pe.matmul(inner[:, f, 0:GT], b1[:, f * D:(f + 1) * D], oht[p][:], start=False, stop=True).then_inc(s["inner"], 1)
                    pe.wait_ge(s["relu"], (c + 1) * 4)
                    if not early(c, 1):
                        pe.wait_ge(s["biased"], c * GROUP)
                    for t in range(GROUP):
                        pe.matmul(bias[0:PT, t * D:(t + 1) * D], oht[p][:, t * PT:(t + 1) * PT], b2[:], start=True, stop=True)
                    for t in range(GROUP):
                        if t >= 2:
                            pe.wait_ge(s["weighed"], c * GROUP + (t - 1))
                        for q in range(2):
                            for f in range(4):
                                mm = pe.matmul(inner[0:PT, 2 * (t % 2) + q, :], re[:, f, t * PT:(t + 1) * PT], w2[:, f, 4 * q:4 * q + 4, :],
                                               start=(f == 0), stop=(f == 3))
                        mm.then_inc(s["outer"], 1)

                route(0, 0)
                turn_mask(0, 0)
                for e in range(EXPERTS):
                    spread_mask(0, 0, e)
                walk(pe, 4, body)

            @block.scalar
            def _(act):
                def stage_rows(c, p):
                    if not early(c, 2):
                        act.wait_ge(s["r_logits"], c - 1)
                    act.activation(hs[p][:], h_t[:, c * GT:(c + 1) * GT], ACT.Copy).then_inc(s["staged"], 1)

                def gate_and_copies(c, p):
                    wait(act, s, c + 1, "r_logits", "r_max")
                    if not early(c, 2):
                        act.wait_ge(s["gated"], (c - 1) * GROUP)
                    act.activation(gate[p][:], top[:], ACT.Exp, scale=-1.0).then_inc(s["gate_exp"], 1)
                    wait(act, s, c + 1, "picked_t")
                    if not early(c, 2):
                        act.wait_ge(s["outer"], (c - 1) * GROUP)
                    act.activation(oht[p][:], spread[0:EXPERTS, 0, 0:GT], ACT.Copy).then_inc(s["mask_t"], 1)
                    wait(act, s, c + 1, "turned_n")
                    act.activation(xn[:], spread[:, 1, 0:GT], ACT.Copy).then_inc(s["copied_n"], 1)

                def body(c, p):
                    for f in range(4):
                        if f == 2 and c < 3:
                            gate_and_copies(c + 1, 1 - p)
                        act.wait_ge(s["inner"], c * 4 + (f + 1))
                        if f == 0 and not early(c, 1):
                            act.wait_ge(s["outer"], c * GROUP)
                        act.activation(re[:, f, :], inner[:, f, 0:GT], ACT.Relu).then_inc(s["relu"], 1)
                    if c < 2:
                        stage_rows(c + 2, p)

                stage_rows(0, 0)
                stage_rows(1, 1)
                gate_and_copies(0, 0)
                walk(act, 4, body)

            @block.vector
            def _(v):
                v.wait_ge(s["loaded"], 144)

                def route(c, p):
                    n = c + 1
                    wait(v, s, n, "r_logits")
                    if not early(c, 1):
                        wait(v, s, c, "r_picked")
                    if not early(c, 2):
                        wait(v, s, c - 1, "picked_t")
                        v.wait_ge(s["weighed"], (c - 1) * GROUP)
                    logits = small[0:PT, 0:GROUP * EXPERTS].rearrange("t (a e) -> t a e", e=EXPERTS)
                    v.tensor_reduce(top[:], logits, AX.X, ALU.max).then_inc(s["r_max"], 1)
                    wait(v, s, n, "r_max")
                    v.tensor_tensor(rank[:], logits, bc(top[:, :, None], [PT, GROUP, EXPERTS]), ALU.is_equal).then_inc(s["r_best"], 1)
                    wait(v, s, n, "r_best")
                    v.tensor_tensor(rank[:], rank[:], bc(early_rank[0:PT, None, :], [PT, GROUP, EXPERTS]), ALU.mult).then_inc(s["r_order"], 1)
                    wait(v, s, n, "r_order", "gate_exp")
                    v.tensor_reduce(top[:], rank[:], AX.X, ALU.max).then_inc(s["r_first"], 1)
                    wait(v, s, n, "r_first")
                    v.tensor_tensor(oh[p][:], rank[:], bc(top[:, :, None], [PT, GROUP, EXPERTS]), ALU.is_equal).then_inc(s["r_picked"], 1)
                    v.tensor_scalar(gate[p][:], gate[p][:], 1.0, None, ALU.add).then_inc(s["gate_one"], 1)
                    wait(v, s, n, "gate_one")
                    v.reciprocal(gate[p][:], gate[p][:]).then_inc(s["gate"], 1)
                    if not early(c, 1):
                        wait(v, s, c, "turned_n")
                    v.tensor_copy(y[:], h_n[:, c * GROUP:(c + 1) * GROUP, :]).then_inc(s["resid"], 1)
                    wait(v, s, n, "resid")
                    norm_vector(v, s, n, y[:], sq[:], st, D, 1e-5)

                def mask_rows(c, p):
                    wait(v, s, c + 1, "copied_n")
                    for e in range(EXPERTS):
                        if not (early(c, 1) and e == 0):
                            v.wait_ge(s["masked"], c * EXPERTS + e)
                        v.tensor_scalar(xa[:], xn[:], lg[:, e:e + 1], lb[:, e:e + 1], ALU.mult, ALU.add).then_inc(s["affine"], 1)
                        v.wait_ge(s["affine"], c * EXPERTS + (e + 1))
                        v.wait_ge(s["spread"], c * EXPERTS + (e + 1))
                        if e == 0 and not early(c, 2):
                            v.wait_ge(s["inner"], (c - 1) * 4)
                        v.tensor_tensor(xm[p][:, e, :], xa[:], spread[:, e % 2, 0:GT], ALU.mult).then_inc(s["masked"], 1)

                def body(c, p):
                    if c < 3:
                        route(c + 1, 1 - p)
                        mask_rows(c + 1, 1 - p)
                    for t in range(GROUP):
                        m = c * GROUP + (t + 1)
                        wait(v, s, m, "outer")
                        if m > 1:
                            wait(v, s, m - 1, "summed", "gated")
                        v.tensor_tensor(wy.rearrange("t (q e) d -> t q e d", q=2), inner[0:PT, 2 * (t % 2):2 * (t % 2) + 2, :].rearrange("t q (e d) -> t q e d", e=4),
                                        bc(oh[p][:, t, :].rearrange("t (q e) -> t q e", q=2)[:, :, :, None], [PT, 2, 4, D]), ALU.mult)\
                            .then_inc(s["weighed"], 1)
                        wait(v, s, m, "weighed")
                        v.tensor_reduce(fo[:], wy.rearrange("t e d -> t d e"), AX.X, ALU.add).then_inc(s["summed"], 1)
                        wait(v, s, m, "summed")
                        v.tensor_tensor(fo[:], fo[:], bias[0:PT, t * D:(t + 1) * D], ALU.add).then_inc(s["biased"], 1)
                        wait(v, s, m, "biased")
                        if t == 0 and not early(c, 1):
                            wait(v, s, c, "done")
                        v.scalar_tensor_tensor(res[:, t, :], fo[:], gate[p][:, t:t + 1], h_n[:, c * GROUP + t, :], ALU.mult, ALU.add)\
                            .then_inc(s["gated"], 1)
                    v.wait_ge(s["gated"], (c + 1) * GROUP)
                    here = slice(c * GROUP, (c + 1) * GROUP)
                    v.tensor_tensor(x[:, here, :], x[:, here, :], res[:], ALU.add).then_inc(s["done"], 1)

                route(0, 0)
                mask_rows(0, 0)
                walk(v, 4, body)

            @block.gpsimd
            def _(pool):
                walk(pool, 4, lambda c, p: norm_pool(pool, s, c + 1, st, g["half"][0:PT, 0:GROUP]))



STATES = 16


def l2_attention(nc, g, a):
    ident, x, h_t = g["ident"], g["x"], g["h_t"]
    names = ("loaded alog_exp a_ready dt_proj biased absed exped logged dt_ready du_ready y_start spread_w dA0 dA1 reset0 reset1 b_ready c_ready "
             "ub scan0 scan1 hc0 hc1 acc0 acc1 turned added")
    with stage(nc, "s2", names) as (s, sb, ps):
        wd = sb("w_dt", [D, D]); bd = sb("b_dt", [D, 1]); wbc = sb("w_bc", [D, 2, STATES]); an = sb("a", [D, STATES]); dd = sb("d", [D, 1])
        dt = sb("dt", [D, TOK]); ab = sb("abs", [D, TOK]); du = sb("du", [D, TOK]); y = sb("y", [D, TOK]); ub = sb("ub", [D, TOK])
        dA = [sb(f"dA{j}", [D, TOK]) for j in range(2)]; hc = [sb(f"hc{j}", [D, TOK]) for j in range(2)]
        wb = sb("wb", [D, 2, D])
        loads = ((wd[:], a["L2_dt"]), (bd[:], a["L2_bdt"]), (wbc[:], a["L2_bc"]), (an[:], a["L2_alog"]), (dd[:], a["L2_d"]))
        normalise(nc, g, "n6", [("layer", 1e-5)], loads=loads, loaded=s["loaded"])
        pb = ps("pb", [D, 4, 512]); pc = ps("pc", [D, 4, 512])
        four = lambda buf: buf.rearrange("d (a b) -> d a b", a=4)

        def in_turn(eng, states):
            states(0)
            with eng.Fori(1, STATES // 2) as i:
                states(i)

        def after(eng, sem, n):
            if not early(n, 1):
                eng.wait_ge(sem, n)

        with nc.Block() as block:
            @block.tensor
            def _(pe):
                pe.wait_ge(s["loaded"], 80)
                for b in range(4):
                    mm = pe.matmul(pb[:, b, 0:GT], wd[:], h_t[:, b * GT:(b + 1) * GT], start=True, stop=True)
                mm.then_inc(s["dt_proj"], 1)
                pe.wait_ge(s["biased"], 1)

                def states(i):
                    for j in range(2):
                        m = i * 2 + (j + 1)
                        wait(pe, s, m, "spread_w")
                        after(pe, s["ub"], i * 2 + j)
                        for b in range(4):
                            mm = pe.matmul(pb[:, b, 0:GT], wb[:, 0, :], h_t[:, b * GT:(b + 1) * GT], start=True, stop=True)
                        mm.then_inc(s["b_ready"], 1)
                        after(pe, s[f"hc{1 - j}"], i + j)
                        for b in range(4):
                            mm = pe.matmul(pc[:, b, 0:GT], wb[:, 1, :], h_t[:, b * GT:(b + 1) * GT], start=True, stop=True)
                        mm.then_inc(s["c_ready"], 1)
                in_turn(pe, states)
                pe.wait_ge(s["acc1"], STATES // 2)
                pe.wait_ge(s["hc1"], STATES // 2)
                for t in range(PAIRS):
                    mm = pe.transpose(pb[0:PT, t // 4, (t % 4) * D:(t % 4 + 1) * D], y[:, t * PT:(t + 1) * PT], ident[:])
                mm.then_inc(s["turned"], 1)

            @block.scalar
            def _(act):
                act.wait_ge(s["loaded"], 80)
                act.activation(an[:], an[:], ACT.Exp).then_inc(s["alog_exp"], 1)
                act.wait_ge(s["absed"], 1)
                act.activation(ab[:], ab[:], ACT.Exp, scale=-1.0).then_inc(s["exped"], 1)
                act.wait_ge(s["exped"], 1)
                act.activation(ab[:], ab[:], ACT.Ln, bias=1.0).then_inc(s["logged"], 1)
                act.wait_ge(s["dt_ready"], 1)
                act.wait_ge(s["a_ready"], 1)

                def states(i):
                    for j in range(2):
                        m = i * 2 + (j + 1)
                        n = i * 2 + j
                        after(act, s["c_ready"], i * 2 + j)
                        act.activation(wb[:], bc(wbc[:, :, bass.ds(n, 1)], [D, 2, D]), ACT.Copy).then_inc(s["spread_w"], 1)
                        after(act, s[f"scan{j}"], i)
                        act.activation(dA[j][:], dt[:], ACT.Exp, scale=an[:, bass.ds(n, 1)]).then_inc(s[f"dA{j}"], 1)
                in_turn(act, states)

            @block.vector
            def _(v):
                v.wait_ge(s["loaded"], 80)
                v.wait_ge(s["dt_proj"], 1)
                v.tensor_scalar(four(dt), pb[:, :, 0:GT], bd[:, 0:1], None, ALU.add).then_inc(s["biased"], 1)
                v.wait_ge(s["biased"], 1)
                v.scalar_tensor_tensor(ab[:], dt[:], -1.0, dt[:], ALU.mult, ALU.max).then_inc(s["absed"], 1)
                v.wait_ge(s["alog_exp"], 1)
                v.tensor_scalar(an[:], an[:], -1.0, None, ALU.mult).then_inc(s["a_ready"], 1)
                v.wait_ge(s["logged"], 1)
                v.scalar_tensor_tensor(dt[:], dt[:], 0.0, ab[:], ALU.max, ALU.add).then_inc(s["dt_ready"], 1)
                v.wait_ge(s["dt_ready"], 1)
                v.tensor_tensor(du[:], dt[:], h_t[:], ALU.mult).then_inc(s["du_ready"], 1)
                v.wait_ge(s["du_ready"], 1)

                def states(i):
                    for j in range(2):
                        m = i * 2 + (j + 1)
                        wait(v, s, m, "b_ready")
                        after(v, s[f"scan{1 - j}"], i + j)
                        v.tensor_tensor(four(ub), four(du), pb[:, :, 0:GT], ALU.mult).then_inc(s["ub"], 1)
                        v.wait_ge(s[f"reset{j}"], i + 1)
                        after(v, s[f"acc{j}"], i)
                        wait(v, s, m, "ub")
                        v.tensor_tensor_scan(hc[j][:], dA[j][:], ub[:], 0.0, ALU.mult, ALU.add).then_inc(s[f"scan{j}"], 1)
                        v.wait_ge(s[f"scan{j}"], i + 1)
                        wait(v, s, m, "c_ready")
                        v.tensor_tensor(four(hc[j]), four(hc[j]), pc[:, :, 0:GT], ALU.mult).then_inc(s[f"hc{j}"], 1)
                in_turn(v, states)
                v.wait_ge(s["turned"], 1)
                v.tensor_tensor(x.rearrange("t (a b) d -> t a (b d)", a=4), x.rearrange("t (a b) d -> t a (b d)", a=4), pb[0:PT, :, :], ALU.add)\
                    .then_inc(s["added"], 1)

            @block.gpsimd
            def _(pool):
                pool.wait_ge(s["loaded"], 80)
                pool.tensor_scalar(y[:], h_t[:], dd[:, 0:1], None, ALU.mult).then_inc(s["y_start"], 1)
                pool.wait_ge(s["y_start"], 1)

                def states(i):
                    for j in range(2):
                        pool.wait_ge(s[f"dA{j}"], i + 1)
                        apart(pool)
                        pool.memset(dA[j].rearrange("d (b t) -> d b t", t=SEQ)[:, :, 0:1], 0.0).then_inc(s[f"reset{j}"], 1)
                        after(pool, s[f"acc{1 - j}"], i + j)
                        pool.wait_ge(s[f"hc{j}"], i + 1)
                        pool.tensor_tensor(y[:], y[:], hc[j][:], ALU.add).then_inc(s[f"acc{j}"], 1)
                in_turn(pool, states)



def l2_cross(nc, g, a):
    ident, ones, x, h_t, csum = g["ident"], g["ones"], g["x"], g["h_t"], g["ctx_sum"]
    names = ("loaded cleared biassum cs cqw_ready scores rowmax negmax probs inverse turned copied pv c2q_normed c2q_turned c2q "
             "own own_row own_max own_shifted own_exp own_sum own_inv own_norm own_bc weighted q2c prod1 features out_ready out_sum done summed "
             "ctx0 ctx1 ctxt0 ctxt1")
    HALF = 64
    with stage(nc, "x2", names) as (s, sb, ps):
        cols = sb("cols", [D, 3]); bias = sb("bias", [D, 3]); bsum = sb("bsum", [D, 2]); wl = sb("wl", [D, 4, D]); bl = sb("bl", [PT, D])
        ct = [sb(f"ctx_t{p}", [D, 2, CTX]) for p in range(2)]; cn = [sb(f"ctx_n{p}", [TP, 2, TILES, D]) for p in range(2)]
        feat = [sb(f"feat{p}", [D, 4, 2, SEQ]) for p in range(2)]; cq = sb("cq", [D, 2, HALF]); hp = sb("hp", [D, 2, HALF]); pr = sb("pr", [D, CTX]); pt = sb("pt", [TP, TILES, D])
        mx = sb("mx", [D, 1]); nm = sb("nm", [D, 1]); l = sb("l", [D, 1]); il = sb("il", [D, 1]); c2n = sb("c2n", [D, D])
        own = sb("own", [D, 1]); row = sb("row", [1, 2, HALF]); r1 = sb("r1", [1, 3, 2]); wc = sb("wc", [D, 2, SEQ]); q2c = sb("q2c", [D, 2])
        acc = sb("acc", [PT, D])
        loads = ((cols[:], a["L2_x_cols"]), (bias[:], bc(a["L2_x_bias"], [D, 3])), (wl[:], a["L2_x_wl"]), (bl[:], bc(a["L2_x_bl"], [PT, D])))
        normalise(nc, g, "n7", [("layer", 1e-5)], loads=loads, loaded=s["loaded"])
        sc = ps("sc", [D, 3, 512]); turn = ps("turn", [D, 2, 512]); pv = ps("pv", [D, 512]); mi = ps("mi", [D, 512]); out = ps("out", [D, 512])
        flat = lambda buf: buf.rearrange("d j t -> d (j t)")

        def walk(eng, body):
            def two(q):
                for p in range(2):
                    body(q * 2 + p, p, q)
            two(0)
            with eng.Fori(1, PAIRS // 2 - 1) as q:
                two(q)
            two(PAIRS // 2 - 1)

        is_last = lambda i: isinstance(i, int) and i == PAIRS - 1
        at_start = lambda i, n: isinstance(i, int) and i < n

        with nc.Block() as block:
            @block.sync
            def _(sp):
                def body(i, p, q):
                    if not at_start(i, 2):
                        sp.wait_ge(s["scores"], i - 1)
                        apart(sp)
                        sp.wait_ge(s["summed"], (i - 1) * 2)
                    for j in range(2):
                        sp.dma_start(ct[p][:, j, :], a["ctx_t"][bass.ds(i * 2 + j, 1), :, :].rearrange("o d c -> (o d) c")).then_inc(s[f"ctxt{p}"], 16)
                    if not at_start(i, 2):
                        sp.wait_ge(s["pv"], i - 1)
                        apart(sp)
                    for j in range(2):
                        sp.dma_start(cn[p][:, j, :, :], a["ctx"][bass.ds(i * 2 + j, 1), :, :, :].rearrange("o p t d -> (o p) t d")).then_inc(s[f"ctx{p}"], 16)
                walk(sp, body)

            @block.tensor
            def _(pe):
                pe.wait_ge(s["loaded"], 64)

                def scores(i, p, q):
                    pe.wait_ge(s["cqw_ready"], i + 1)
                    pe.wait_ge(s[f"ctxt{p}"], (q + 1) * 32)
                    for b in range(3):
                        for j in range(2):
                            pe.matmul(sc[HALF * j:HALF * (j + 1), b, 0:BANKC], cq[:, j, :], ct[p][:, j, b * BANKC:(b + 1) * BANKC],
                                      start=True, stop=True, tile_position=(0, HALF * j))
                    pe.matmul(sc[:, 0, BANKC:BANKC + 1], flat(hp), cols[:, 1:2], start=True, stop=True).then_inc(s["scores"], 1)

                def turn_group(i, b):
                    apart(pe)
                    for t in range(4):
                        mm = pe.transpose(turn[0:TP, b % 2, t * D:(t + 1) * D], pr[:, (4 * b + t) * TP:(4 * b + t + 1) * TP], ident[:])
                    mm.then_inc(s["turned"], 1)

                def output(i, p):
                    pe.wait_ge(s["features"], i + 1)
                    if not at_start(i, 1):
                        pe.wait_ge(s["out_sum"], i)
                    for k in range(4):
                        mm = pe.matmul(out[0:PT, 0:D], feat[p][:, k], wl[:, k, :], start=(k == 0), stop=(k == 3))
                    mm.then_inc(s["out_ready"], 1)

                def body(i, p, q):
                    pe.wait_ge(s["probs"], i + 1)
                    turn_group(i, 0)
                    turn_group(i, 1)
                    if not at_start(i, 1):
                        output(i - 1, 1 - p)
                    pe.wait_ge(s["copied"], i * 3 + 1)
                    turn_group(i, 2)
                    pe.wait_ge(s["own"], i + 1)
                    if not at_start(i, 1):
                        pe.wait_ge(s["weighted"], i)
                    apart(pe)
                    pe.transpose(mi[0:1, 0:D], own[:], ident[:]).then_inc(s["own_row"], 1)
                    if not is_last(i):
                        scores(i + 1, 1 - p, q + p)
                    pe.wait_ge(s[f"ctx{p}"], (q + 1) * 32)
                    pe.wait_ge(s["copied"], i * 3 + 3)
                    if not at_start(i, 1):
                        pe.wait_ge(s["c2q"], i)
                    for t in range(TILES):
                        for j in range(2):
                            mm = pe.matmul(pv[HALF * j:HALF * (j + 1), 0:D], pt[:, t, HALF * j:HALF * (j + 1)], cn[p][:, j, t, :],
                                           start=(t == 0), stop=(t == TILES - 1), tile_position=(0, HALF * j))
                    mm.then_inc(s["pv"], 1)
                    pe.wait_ge(s["own_norm"], i + 1)
                    pe.matmul(mi[:, D:2 * D], ones[0:1, :], row.rearrange("o j t -> o (j t)"), start=True, stop=True).then_inc(s["own_bc"], 1)
                    pe.wait_ge(s["c2q_normed"], i + 1)
                    apart(pe)
                    pe.transpose(pv[:, D:2 * D], c2n[:], ident[:]).then_inc(s["c2q_turned"], 1)

                scores(0, 0, 0)
                walk(pe, body)
                output(PAIRS - 1, 1)

            @block.scalar
            def _(act):
                act.wait_ge(s["loaded"], 64)
                act.wait_ge(s["cleared"], 3)

                def stage_rows(i, p):
                    if not at_start(i, 2):
                        act.wait_ge(s["out_ready"], i - 1)
                    if not at_start(i, 1):
                        act.wait_ge(s["scores"], i)
                    here = h_t[:, bass.ds(i * PT, PT)].rearrange("d (j t) -> d j t", j=2)
                    act.activation(feat[p][:, 0], here, ACT.Copy).then_inc(s["cs"], 1)
                    act.activation(hp[:, :, 0:SEQ], here, ACT.Copy)
                    act.activation(cq[:, :, 0:SEQ], here, ACT.Identity, scale=cols[:, 0:1], bias=cols[:, 2:3]).then_inc(s["cqw_ready"], 1)

                def exps(i):
                    act.wait_ge(s["negmax"], i + 1)
                    act.wait_ge(s["own"], i + 1)
                    if not at_start(i, 1):
                        act.wait_ge(s["inverse"], i)
                    act.activation(pr.rearrange("q (a b) -> q a b", a=3), sc[:, :, 0:BANKC], ACT.Exp, bias=nm[:, 0:1], accum_out=l[:, 0:1])\
                        .then_inc(s["probs"], 1)

                def body(i, p, q):
                    def copy(b):
                        act.wait_ge(s["turned"], i * 3 + (b + 1))
                        act.activation(pt[:, 4 * b:4 * b + 4, :], turn[0:TP, b % 2, :].rearrange("p (t q) -> p t q", t=4), ACT.Copy)\
                            .then_inc(s["copied"], 1)
                    copy(0)
                    copy(1)
                    if not is_last(i):
                        stage_rows(i + 1, 1 - p)
                    copy(2)
                    act.wait_ge(s["own_shifted"], i + 1)
                    act.activation(row[:, :, 0:SEQ], row[:, :, 0:SEQ], ACT.Exp).then_inc(s["own_exp"], 1)
                    if not is_last(i):
                        exps(i + 1)

                stage_rows(0, 0)
                exps(0)
                walk(act, body)

            @block.vector
            def _(v):
                for buf in (cq, hp, row):
                    v.memset(buf[:], 0.0).then_inc(s["cleared"], 1)
                v.wait_ge(s["cleared"], 3)
                v.wait_ge(s["loaded"], 64)
                v.tensor_reduce(bsum[:, 0:1], bias[:], AX.X, ALU.add).then_inc(s["biassum"], 1)
                v.wait_ge(s["biassum"], 1)

                def maxima(i, p, q):
                    v.wait_ge(s["scores"], i + 1)
                    if not at_start(i, 1):
                        v.wait_ge(s["own_row"], i)
                        v.wait_ge(s["probs"], i)
                    v.tensor_reduce(mx[:], sc[:, :, 0:BANKC], AX.XY, ALU.max).then_inc(s["rowmax"], 1)
                    v.wait_ge(s["rowmax"], i + 1)
                    v.scalar_tensor_tensor(own[:], mx[:], bsum[:, 0:1], sc[:, 0, BANKC:BANKC + 1], ALU.add, ALU.add).then_inc(s["own"], 1)
                    v.tensor_scalar(nm[:], mx[:], -1.0, None, ALU.mult).then_inc(s["negmax"], 1)
                    v.wait_ge(s[f"ctxt{p}"], (q + 1) * 32)
                    for j in range(2):
                        v.tensor_reduce(csum[:, bass.ds(i * 2 + j, 1)], ct[p][:, j, :], AX.X, ALU.add).then_inc(s["summed"], 1)

                def output(i):
                    v.wait_ge(s["out_ready"], i + 1)
                    if not at_start(i, 1):
                        v.wait_ge(s["done"], i)
                    v.tensor_tensor(acc[:], out[0:PT, 0:D], bl[:], ALU.add).then_inc(s["out_sum"], 1)
                    v.wait_ge(s["out_sum"], i + 1)
                    v.tensor_tensor(x[:, i, :], acc[:], x[:, i, :], ALU.add).then_inc(s["done"], 1)

                def body(i, p, q):
                    n = i + 1
                    f = feat[p]
                    wait(v, s, n, "probs")
                    if not at_start(i, 1):
                        v.wait_ge(s["c2q_normed"], i)
                    v.reciprocal(il[:], l[:]).then_inc(s["inverse"], 1)
                    if not at_start(i, 1):
                        output(i - 1)
                    if not at_start(i, 1):
                        v.wait_ge(s["own_bc"], i)
                    wait(v, s, n, "own_row")
                    rows = mi[0:1, 0:D].rearrange("o (j t) -> o j t", j=2)[:, :, 0:SEQ]
                    v.tensor_reduce(r1[:, 0, :], rows, AX.X, ALU.max).then_inc(s["own_max"], 1)
                    wait(v, s, n, "own_max")
                    v.tensor_tensor(row[:, :, 0:SEQ], rows, bc(r1[:, 0, :, None], [1, 2, SEQ]), ALU.subtract).then_inc(s["own_shifted"], 1)
                    wait(v, s, n, "own_exp")
                    v.tensor_reduce(r1[:, 1, :], row[:, :, 0:SEQ], AX.X, ALU.add).then_inc(s["own_sum"], 1)
                    wait(v, s, n, "own_sum")
                    v.reciprocal(r1[:, 2, :], r1[:, 1, :]).then_inc(s["own_inv"], 1)
                    wait(v, s, n, "own_inv")
                    v.tensor_tensor(row[:, :, 0:SEQ], row[:, :, 0:SEQ], bc(r1[:, 2, :, None], [1, 2, SEQ]), ALU.mult).then_inc(s["own_norm"], 1)
                    if not is_last(i):
                        maxima(i + 1, 1 - p, q + p)
                    wait(v, s, n, "pv")
                    if not at_start(i, 1):
                        v.wait_ge(s["c2q_turned"], i)
                    v.tensor_scalar(c2n[:], pv[:, 0:D], il[:, 0:1], None, ALU.mult).then_inc(s["c2q_normed"], 1)
                    wait(v, s, n, "own_bc")
                    v.tensor_tensor(wc[:], f[:, 0], mi[:, D:2 * D].rearrange("d (j t) -> d j t", j=2)[:, :, 0:SEQ], ALU.mult).then_inc(s["weighted"], 1)
                    wait(v, s, n, "weighted")
                    v.tensor_reduce(q2c[:], wc[:], AX.X, ALU.add).then_inc(s["q2c"], 1)
                    wait(v, s, n, "q2c")
                    v.tensor_tensor(f[:, 3], f[:, 0], bc(q2c[:, :, None], [D, 2, SEQ]), ALU.mult)
                    wait(v, s, n, "c2q_turned")
                    v.tensor_copy(f[:, 1], pv[:, D:2 * D].rearrange("d (j t) -> d j t", j=2)[:, :, 0:SEQ]).then_inc(s["c2q"], 1)
                    wait(v, s, n, "c2q")
                    v.tensor_tensor(f[:, 2], f[:, 0], f[:, 1], ALU.mult).then_inc(s["features"], 1)

                maxima(0, 0, 0)
                walk(v, body)
                output(PAIRS - 1)



def l3_attention(nc, g, a):
    ident, x, h_t = g["ident"], g["x"], g["h_t"]
    names = ("loaded staged grouped copied0 copied1 scores masked rowmax shifted probs rowsum inverse weights sums o_ready out_ready out_sum done")
    R, BLOCKS, HALF = PT, 8, 64
    GROUPS = 10
    AHEAD = 6
    with stage(nc, "a3", names) as (s, sb, ps):
        w = sb("w", [D, 3 * 1024]); wo = sb("wo", [D, BLOCKS, D]); mk = sb("mask", [R, R]); bo = sb("bo", [R, D])
        hs = [sb(f"hs{p}", [D, R]) for p in range(2)]; qk = sb("qk", [D, 2 * BLOCKS, R]); vs = [sb(f"vs{p}", [R, 1024]) for p in range(2)]
        pr = sb("pr", [R, HEADS, R]); pt = sb("pt", [R, HEADS, R]); ot = sb("ot", [D, BLOCKS, R]); acc = sb("acc", [R, D])
        mx = sb("mx", [R, HEADS]); ls = sb("ls", [R, HEADS]); rl = sb("rl", [R, HEADS])
        loads = ((w[:], a["L3_wqkv"]), (wo[:], a["L3_wout"]), (mk[:], g["consts"]["batch_mask"]),
                 (bo[:], bc(a["L3_bout"], [R, D])))
        normalise(nc, g, "n9", [("layer", 1e-5), ("rms", 1e-6)], a["L3_scale"], loads=loads, loaded=s["loaded"])
        scores = ps("scores", [D, 4, 512]); ring = ps("ring", [D, 2, 512]); osum = ps("osum", [D, 512]); out = ps("out", [D, 512])
        last = PAIRS - 1
        is_last = lambda i: isinstance(i, int) and i == last

        def place(i, k):
            return i * GROUPS + (AHEAD + k)

        def ahead(i, b):
            return (0, b - AHEAD) if early(i, 1) else (i - 1, b)

        def turned(i, b):
            return (i, b if is_last(i) else AHEAD + b)

        def in_bank(i, k):
            bank = k % 2
            return bank, i * (GROUPS // 2) + ((AHEAD + k - bank) // 2 + 1)

        with nc.Block() as block:
            @block.tensor
            def _(pe):
                pe.wait_ge(s["loaded"], 64)

                def group(i, k, emit):
                    bank, n = in_bank(i, k)
                    if not (early(i, 1) and n == 1):
                        pe.wait_ge(s[f"copied{bank}"], n - 1)
                    apart(pe)
                    emit(ring[:, bank, :]).then_inc(s["grouped"], 1)

                def copied(i, k):
                    bank, n = in_bank(i, k)
                    pe.wait_ge(s[f"copied{bank}"], n)

                def project(i, p, b):
                    def blocks(bank):
                        for k in range(4):
                            mm = pe.matmul(bank[:, k * R:(k + 1) * R], w[:, (4 * b + k) * D:(4 * b + k + 1) * D], hs[p][:], start=True, stop=True)
                        return mm

                    def values(bank):
                        return pe.matmul(bank[0:R, :], hs[p][:], w[:, 2048 + (b - 4) * 512:2560 + (b - 4) * 512], start=True, stop=True)

                    if b == 0:
                        wait(pe, s, i + 1, "staged")
                    group(*ahead(i, b), blocks if b < 4 else values)

                def score(i, half):
                    if half == 0:
                        for b in (2, 3):
                            copied(*ahead(i, b))
                    for k in range(4):
                        for e in range(2):
                            rows = slice(HALF * e, HALF * (e + 1))
                            mm = pe.matmul(scores[0:R, 2 * half + e, k * R:(k + 1) * R], qk[rows, 4 * half + k, :], qk[rows, BLOCKS + 4 * half + k, :],
                                           start=True, stop=True)
                    mm.then_inc(s["scores"], 1)

                def turn_group(i, b):
                    def tiles(bank):
                        for k in range(4):
                            mm = pe.transpose(bank[0:R, k * R:(k + 1) * R], pr[:, 4 * b + k, :], ident[0:R, 0:R])
                        return mm
                    if b % 2 == 0:
                        pe.wait_ge(s["weights"], i * 2 + (b // 2 + 1))
                    group(*turned(i, b), tiles)

                def weigh(i, p, half):
                    for e in range(2):
                        copied(*turned(i, 2 * half + e))
                    if not early(i, 1) or half:
                        pe.wait_ge(s["o_ready"], i * 2 + half)
                    for k in range(4):
                        for e in range(2):
                            rows = slice(HALF * e, HALF * (e + 1))
                            head = 2 * (4 * half + k) + e
                            mm = pe.matmul(osum[rows, k * R:(k + 1) * R], vs[p][:, HALF * head:HALF * (head + 1)], pt[:, 4 * (2 * half + e) + k, :],
                                           start=True, stop=True, tile_position=(0, HALF * e))
                    mm.then_inc(s["sums"], 1)

                def output(i):
                    pe.wait_ge(s["o_ready"], i * 2 + 2)
                    if not early(i, 1):
                        wait(pe, s, i, "out_sum")
                    for b in range(BLOCKS):
                        mm = pe.matmul(out[0:R, 0:D], ot[:, b, :], wo[:, b, :], start=(b == 0), stop=(b == BLOCKS - 1))
                    mm.then_inc(s["out_ready"], 1)

                def body(i, p):
                    if not is_last(i):
                        for b in range(4):
                            project(i + 1, 1 - p, b)
                    if not early(i, 1):
                        output(i - 1)
                    if not is_last(i):
                        for b in (4, 5):
                            project(i + 1, 1 - p, b)
                    for half in range(2):
                        turn_group(i, 2 * half)
                        turn_group(i, 2 * half + 1)
                        if not is_last(i):
                            score(i + 1, half)
                        weigh(i, p, half)

                for b in range(AHEAD):
                    project(0, 0, b)
                for half in range(2):
                    score(0, half)
                walk(pe, PAIRS, body)
                output(last)

            @block.scalar
            def _(act):
                def stage_rows(i, p):
                    if not early(i, 2):
                        bank, n = in_bank(*ahead(i - 2, 5))
                        act.wait_ge(s["grouped"], place(*ahead(i - 2, 5)) + 1)
                    act.activation(hs[p][:], h_t[:, bass.ds(i * PT, PT)], ACT.Copy).then_inc(s["staged"], 1)

                def made(i, k):
                    act.wait_ge(s["grouped"], place(i, k) + 1)

                def exps(i, half):
                    act.wait_ge(s["shifted"], i * 2 + (half + 1))
                    act.activation(pr[:, 8 * half:8 * half + 8, :], pr[:, 8 * half:8 * half + 8, :], ACT.Exp).then_inc(s["probs"], 1)

                def copy_sums(i, half):
                    act.wait_ge(s["sums"], i * 2 + (half + 1))
                    if half == 0 and not early(i, 1):
                        act.wait_ge(s["out_ready"], i)
                    act.activation(ot[:, 4 * half:4 * half + 4, :].rearrange("d b t -> d (b t)"), osum[:, 0:4 * R], ACT.Copy).then_inc(s["o_ready"], 1)

                def rows_ahead(i, p, groups):
                    for b in groups:
                        made(*ahead(i, b))
                        if b < 4:
                            act.activation(qk[:, 4 * b:4 * b + 4, :].rearrange("d b t -> d (b t)"), ring[:, b % 2, 0:4 * R], ACT.Copy,
                                           scale=HALF ** -0.5 if b == 0 else 1.0).then_inc(s[f"copied{b % 2}"], 1)
                        else:
                            act.activation(vs[p][:, (b - 4) * 512:(b - 3) * 512], ring[0:R, b % 2, :], ACT.Copy).then_inc(s[f"copied{b % 2}"], 1)

                def body(i, p):
                    if not is_last(i):
                        rows_ahead(i + 1, 1 - p, (0,))
                    exps(i, 1)
                    if not is_last(i):
                        rows_ahead(i + 1, 1 - p, (2, 3, 4, 5))
                    for b in (0, 2, 3):
                        made(*turned(i, b))
                        act.activation(pt[:, 4 * b:4 * b + 4, :].rearrange("k a q -> k (a q)"), ring[0:R, b % 2, 0:4 * R], ACT.Copy)\
                            .then_inc(s[f"copied{b % 2}"], 1)
                        if b == 0:
                            if not isinstance(i, int) or i + 2 <= last:
                                stage_rows(i + 2, p)
                            copy_sums(i, 0)
                    if not is_last(i):
                        exps(i + 1, 0)
                    copy_sums(i, 1)

                stage_rows(0, 0)
                stage_rows(1, 1)
                rows_ahead(0, 0, (0, 2, 3, 4, 5))
                exps(0, 0)
                walk(act, PAIRS, body)

            @block.vector
            def _(v):
                v.wait_ge(s["loaded"], 64)

                def made(i, k):
                    v.wait_ge(s["grouped"], place(i, k) + 1)

                def queries_ahead(i):
                    made(*ahead(i, 1))
                    v.tensor_scalar(qk[:, 4:8, :].rearrange("d b t -> d (b t)"), ring[:, 1, 0:4 * R], HALF ** -0.5, None, ALU.mult).then_inc(s["copied1"], 1)

                def mask_scores(i, half):
                    heads = slice(8 * half, 8 * half + 8)
                    n = i * 2 + (half + 1)
                    v.wait_ge(s["scores"], n)
                    v.tensor_tensor(pr[:, heads, :].rearrange("q (a b) k -> q a b k", a=2),
                                    scores[0:R, 2 * half:2 * half + 2, 0:4 * R].rearrange("q a (b k) -> q a b k", b=4),
                                    bc(mk[:, None, None, :], [R, 2, 4, R]), ALU.add).then_inc(s["masked"], 1)
                    v.wait_ge(s["masked"], n)
                    if not early(i, 1):
                        v.wait_ge(s["shifted"], i * 2 + (half - 1))
                    v.tensor_reduce(mx[:, heads], pr[:, heads, :], AX.X, ALU.max).then_inc(s["rowmax"], 1)

                def shift_scores(i, half):
                    heads = slice(8 * half, 8 * half + 8)
                    v.wait_ge(s["rowmax"], i * 2 + (half + 1))
                    v.tensor_tensor(pr[:, heads, :], pr[:, heads, :], bc(mx[:, heads, None], [R, 8, R]), ALU.subtract).then_inc(s["shifted"], 1)

                def sum_rows(i, half):
                    heads = slice(8 * half, 8 * half + 8)
                    n = i * 2 + (half + 1)
                    v.wait_ge(s["probs"], n)
                    v.tensor_reduce(ls[:, heads], pr[:, heads, :], AX.X, ALU.add).then_inc(s["rowsum"], 1)
                    v.wait_ge(s["rowsum"], n)
                    if not early(i, 1):
                        v.wait_ge(s["weights"], n - 2)
                    v.reciprocal(rl[:, heads], ls[:, heads]).then_inc(s["inverse"], 1)

                def add_output(i):
                    wait(v, s, i + 1, "out_ready")
                    if not early(i, 1):
                        v.wait_ge(s["done"], i)
                    v.tensor_tensor(acc[:], out[0:R, 0:D], bo[:], ALU.add).then_inc(s["out_sum"], 1)
                    wait(v, s, i + 1, "out_sum")
                    v.tensor_tensor(x[:, i, :], acc[:], x[:, i, :], ALU.add).then_inc(s["done"], 1)

                def body(i, p):
                    if not is_last(i):
                        queries_ahead(i + 1)
                    sum_rows(i, 0)
                    shift_scores(i, 1)
                    if not early(i, 1):
                        add_output(i - 1)
                    sum_rows(i, 1)
                    made(*turned(i, 1))
                    v.tensor_copy(pt[:, 4:8, :].rearrange("k a q -> k (a q)"), ring[0:R, 1, 0:4 * R]).then_inc(s["copied1"], 1)
                    if not is_last(i):
                        mask_scores(i + 1, 0)
                        shift_scores(i + 1, 0)
                        mask_scores(i + 1, 1)

                queries_ahead(0)
                mask_scores(0, 0)
                shift_scores(0, 0)
                mask_scores(0, 1)
                walk(v, PAIRS, body)
                add_output(last)

            @block.gpsimd
            def _(pool):
                def weigh_rows(i, p):
                    for half in range(2):
                        heads = slice(8 * half, 8 * half + 8)
                        pool.wait_ge(s["inverse"], i * 2 + (half + 1))
                        pool.tensor_tensor(pr[:, heads, :], pr[:, heads, :], bc(rl[:, heads, None], [R, 8, R]), ALU.mult).then_inc(s["weights"], 1)
                walk(pool, PAIRS, weigh_rows)



def l3_cross(nc, g, a):
    x, h_t, csum = g["x"], g["h_t"], g["ctx_sum"]
    with stage(nc, "c3", "loaded spread part biased added") as (s, sb, ps):
        w = sb("w", [D, 2, D]); b = sb("b", [PT, D]); cs = sb("cs", [D, BATCH, SEQ]); y = sb("y", [PT, PAIRS, D])
        loads = ((w[:], a["L3_x_w"]), (b[:], bc(a["L3_x_b"], [PT, D])))
        normalise(nc, g, "n10", [("layer", 1e-5)], loads=loads, loaded=s["loaded"])
        acc = ps("acc", [D, 4, 512])
        with nc.Block() as block:
            @block.scalar
            def _(act):
                act.activation(cs[:], bc(csum[:, :, None], [D, BATCH, SEQ]), ACT.Copy, scale=1.0 / CTX).then_inc(s["spread"], 1)

            @block.tensor
            def _(pe):
                pe.wait_ge(s["loaded"], 32)
                pe.wait_ge(s["spread"], 1)
                for t in range(PAIRS):
                    dst = acc[0:PT, t // 4, (t % 4) * D:(t % 4 + 1) * D]
                    pe.matmul(dst, h_t[:, t * PT:(t + 1) * PT], w[:, 0, :], start=True, stop=False)
                    mm = pe.matmul(dst, cs[:, 2 * t:2 * t + 2, :], w[:, 1, :], start=False, stop=True)
                mm.then_inc(s["part"], 1)

            @block.vector
            def _(v):
                v.wait_ge(s["loaded"], 32)
                v.wait_ge(s["part"], 1)
                v.tensor_tensor(y.rearrange("t (a c) d -> t a c d", a=4), acc[0:PT, :, :].rearrange("t a (c d) -> t a c d", d=D),
                                bc(b[:, None, None, :], [PT, 4, 4, D]), ALU.add).then_inc(s["biased"], 1)
                v.wait_ge(s["biased"], 1)
                v.tensor_tensor(x[:], x[:], y[:], ALU.add).then_inc(s["added"], 1)


def l3_ffn(nc, g, a):
    x, h_t = g["x"], g["h_t"]
    with stage(nc, "f3", "loaded inner relu outer biased done") as (s, sb, ps):
        w1 = sb("w1", [D, 256]); b1 = sb("b1", [D, 2]); w2 = sb("w2", [D, 2, D]); b2 = sb("b2", [PT, D])
        re = sb("relu", [D, 2, 2, GT]); y = sb("y", [PT, 2, GROUP * D])
        loads = ((w1[:], a["L3_ffn_w1"]), (b1[:], a["L3_ffn_b1"]), (w2[:], a["L3_ffn_w2"]), (b2[:], bc(a["L3_ffn_b2"], [PT, D])))
        normalise(nc, g, "n11", [("layer", 1e-5)], loads=loads, loaded=s["loaded"])
        inner = ps("inner", [D, 2, 2, 512]); outer = ps("outer", [D, 2, 512])
        with nc.Block() as block:
            @block.tensor
            def _(pe):
                pe.wait_ge(s["loaded"], 64)

                def second(c):
                    pe.wait_ge(s["relu"], 2 * (c + 1))
                    if c >= 2:
                        pe.wait_ge(s["biased"], c - 1)
                    for t in range(GROUP):
                        for f in range(2):
                            mm = pe.matmul(outer[0:PT, c % 2, t * D:(t + 1) * D], re[:, c % 2, f, t * PT:(t + 1) * PT], w2[:, f, :],
                                           start=(f == 0), stop=(f == 1))
                    mm.then_inc(s["outer"], 1)

                for c in range(4):
                    if c >= 2:
                        pe.wait_ge(s["relu"], 2 * (c - 1))
                    for f in range(2):
                        pe.matmul(inner[:, c % 2, f, 0:GT], w1[:, f * D:(f + 1) * D], h_t[:, c * GT:(c + 1) * GT], start=True, stop=True)\
                            .then_inc(s["inner"], 1)
                    if c:
                        second(c - 1)
                second(3)

            @block.scalar
            def _(act):
                act.wait_ge(s["loaded"], 64)
                for c in range(4):
                    if c >= 2:
                        act.wait_ge(s["outer"], c - 1)
                    for f in range(2):
                        act.wait_ge(s["inner"], 2 * c + f + 1)
                        act.activation(re[:, c % 2, f, :], inner[:, c % 2, f, 0:GT], ACT.Relu, bias=b1[:, f:f + 1]).then_inc(s["relu"], 1)

            @block.vector
            def _(v):
                v.wait_ge(s["loaded"], 64)
                for c in range(4):
                    v.wait_ge(s["outer"], c + 1)
                    if c >= 2:
                        v.wait_ge(s["done"], c - 1)
                    v.tensor_tensor(y[:, c % 2, :].rearrange("t (a d) -> t a d", d=D), outer[0:PT, c % 2, :].rearrange("t (a d) -> t a d", d=D),
                                    bc(b2[:, None, :], [PT, GROUP, D]), ALU.add).then_inc(s["biased"], 1)
                    v.wait_ge(s["biased"], c + 1)
                    v.tensor_tensor(x[:, c * GROUP:(c + 1) * GROUP, :], x[:, c * GROUP:(c + 1) * GROUP, :],
                                    y[:, c % 2, :].rearrange("t (a d) -> t a d", d=D), ALU.add).then_inc(s["done"], 1)



def l2_ffn(nc, g, a):
    ident, x, h_n, h_t, C = g["ident"], g["x"], g["h_n"], g["h_t"], g["consts"]
    with ExitStack() as es:
        base = es.enter_context(nc.sbuf_tensor("m2_base", [PT, PAIRS, D], F32))
        normalise(nc, g, "n8a", [("layer", 1e-5)])
        with stage(nc, "m2keep", "kept") as (s, _, _):
            with nc.Block() as block:
                @block.vector
                def _(v):
                    v.tensor_copy(base[:], x[:]).then_inc(s["kept"], 1)
                    v.wait_ge(s["kept"], 1)
                    v.tensor_copy(x[:], h_n[:])
        narrow_attention(nc, g, "a2", D, SEQ // 4, SequenceTokens, C["sequence_mask"], 8 ** -0.5, a["L2_qkv"], a["L2_proj"],
                         ("n8b", [("layer", 1e-5)], a["L2_ln1_weight"], a["L2_ln1_bias"]), order=SequenceTokens.part)
        names = ("loaded staged shifted gates gate_sum gate_inv first_gone weighed weight inner gelu outer added done "
                 "r_logits g_max p_max p_best p_order p_first p_picked q_max q_best q_order q_first q_picked both normal")
        with stage(nc, "m2", names) as (s, sb, ps):
            wr = sb("router", [D, EXPERTS]); w1 = sb("w1", [D, EXPERTS, 256]); w2 = sb("w2", [D, EXPERTS, 2, D]); early_rank = sb("earlier", [D, EXPERTS])
            hs = [sb(f"hs{p}", [D, GT]) for p in range(2)]; ge = sb("gelu", [D, 2, 2, GT]); top = sb("top", [PT, GROUP])
            e3 = [PT, GROUP, EXPERTS]
            gt = [sb(f"gates{p}", e3) for p in range(2)]; rest = sb("rest", e3); rank = sb("rank", e3); p1 = sb("p1", e3); p2 = sb("p2", e3)
            y = sb("y", [PT, GROUP, D])
            loads = ((wr[:], a["L2_router"]), (w1[:], a["L2_moe_w1"]), (w2[:], a["L2_moe_w2"]), (early_rank[:], C["earlier"]))
            normalise(nc, g, "n8c", [("layer", 1e-5)], a["L2_ln2_weight"], a["L2_ln2_bias"], loads=loads, loaded=s["loaded"])
            small = ps("small", [D, 512]); inner = ps("inner", [D, 4, 512]); outer = ps("outer", [D, 2, 512])
            with nc.Block() as block:
                @block.tensor
                def _(pe):
                    pe.wait_ge(s["loaded"], 64)

                    def route(c, p):
                        wait(pe, s, c + 1, "staged")
                        if not early(c, 1):
                            wait(pe, s, c, "shifted")
                        for t in range(GROUP):
                            mm = pe.matmul(small[0:PT, t * EXPERTS:(t + 1) * EXPERTS], hs[p][:, t * PT:(t + 1) * PT], wr[:], start=True, stop=True)
                        mm.then_inc(s["r_logits"], 1)

                    def first(c, p, e):
                        n = c * EXPERTS + e
                        if n >= 2:
                            pe.wait_ge(s["gelu"], n - 1)
                        for f in range(2):
                            mm = pe.matmul(inner[:, 2 * (e % 2) + f, 0:GT], w1[:, e, f * D:(f + 1) * D], hs[p][:], start=True, stop=True)
                        mm.then_inc(s["inner"], 1)

                    def second(c, e):
                        n = c * EXPERTS + e
                        pe.wait_ge(s["gelu"], n + 1)
                        if n >= 2:
                            pe.wait_ge(s["added"], n - 1)
                        for t in range(GROUP):
                            for f in range(2):
                                mm = pe.matmul(outer[0:PT, e % 2, t * D:(t + 1) * D], ge[:, e % 2, f, t * PT:(t + 1) * PT], w2[:, e, f, :],
                                               start=(f == 0), stop=(f == 1))
                        mm.then_inc(s["outer"], 1)

                    def body(c, p):
                        if c < 3:
                            route(c + 1, 1 - p)
                        for e in range(EXPERTS - 1):
                            first(c, p, e + 1)
                            second(c, e)
                        if c < 3:
                            first(c + 1, 1 - p, 0)
                        second(c, EXPERTS - 1)

                    route(0, 0)
                    first(0, 0, 0)
                    walk(pe, 4, body)

                @block.scalar
                def _(act):
                    def stage_rows(c, p):
                        if not early(c, 2):
                            act.wait_ge(s["inner"], (c - 1) * EXPERTS)
                        act.activation(hs[p][:], h_t[:, c * GT:(c + 1) * GT], ACT.Copy).then_inc(s["staged"], 1)

                    def gate_exps(c, p):
                        wait(act, s, c + 1, "shifted")
                        act.activation(gt[p][:], gt[p][:], ACT.Exp).then_inc(s["gates"], 1)

                    def body(c, p):
                        for e in range(EXPERTS):
                            n = c * EXPERTS + e
                            act.wait_ge(s["inner"], n + 1)
                            if n >= 2:
                                act.wait_ge(s["outer"], n - 1)
                            act.activation(ge[:, e % 2, :, :], inner[:, 2 * (e % 2):2 * (e % 2) + 2, 0:GT], ACT.Gelu_apprx_tanh)\
                                .then_inc(s["gelu"], 1)
                            if e == 4 and c < 3:
                                gate_exps(c + 1, 1 - p)
                        if c < 2:
                            stage_rows(c + 2, p)

                    stage_rows(0, 0)
                    stage_rows(1, 1)
                    gate_exps(0, 0)
                    walk(act, 4, body)

                @block.vector
                def _(v):
                    v.wait_ge(s["loaded"], 64)

                    def route(c, p):
                        n = c + 1
                        gates = gt[p]
                        wait(v, s, n, "r_logits")
                        if not early(c, 1):
                            wait(v, s, c, "q_picked", "both", "weight")
                        logits = small[0:PT, 0:GROUP * EXPERTS].rearrange("t (a e) -> t a e", e=EXPERTS)
                        v.tensor_reduce(top[:], logits, AX.X, ALU.max).then_inc(s["g_max"], 1)
                        wait(v, s, n, "g_max")
                        if not early(c, 2):
                            v.wait_ge(s["added"], (c - 1) * EXPERTS)
                        v.tensor_tensor(gates[:], logits, bc(top[:, :, None], e3), ALU.subtract).then_inc(s["shifted"], 1)
                        wait(v, s, n, "gates")
                        v.tensor_reduce(top[:], gates[:], AX.X, ALU.add).then_inc(s["gate_sum"], 1)
                        wait(v, s, n, "gate_sum")
                        v.reciprocal(top[:], top[:]).then_inc(s["gate_inv"], 1)
                        wait(v, s, n, "gate_inv")
                        v.tensor_tensor(gates[:], gates[:], bc(top[:, :, None], e3), ALU.mult).then_inc(s["normal"], 1)
                        wait(v, s, n, "normal")
                        argmax_vector(v, s, n, "p", gates[:], top[:], rank[:], early_rank, p1[:])
                        wait(v, s, n, "p_picked")
                        v.scalar_tensor_tensor(rest[:], p1[:], -4.0, gates[:], ALU.mult, ALU.add).then_inc(s["first_gone"], 1)
                        wait(v, s, n, "first_gone")
                        argmax_vector(v, s, n, "q", rest[:], top[:], rank[:], early_rank, p2[:])
                        wait(v, s, n, "q_picked")
                        v.tensor_tensor(p1[:], p1[:], p2[:], ALU.add).then_inc(s["both"], 1)
                        wait(v, s, n, "both")
                        v.tensor_tensor(gates[:], gates[:], p1[:], ALU.mult).then_inc(s["weight"], 1)

                    def body(c, p):
                        wait(v, s, c + 1, "weight")
                        if not early(c, 1):
                            wait(v, s, c, "done")
                        for e in range(EXPERTS):
                            n = c * EXPERTS + e
                            v.wait_ge(s["outer"], n + 1)
                            if e:
                                v.wait_ge(s["added"], n)
                            for t in range(GROUP):
                                part = outer[0:PT, e % 2, t * D:(t + 1) * D]
                                if e == 0:
                                    last = v.tensor_scalar(y[:, t, :], part, gt[p][:, t, e:e + 1], None, ALU.mult)
                                else:
                                    last = v.scalar_tensor_tensor(y[:, t, :], part, gt[p][:, t, e:e + 1], y[:, t, :], ALU.mult, ALU.add)
                            last.then_inc(s["added"], 1)
                            if e == 3 and c < 3:
                                route(c + 1, 1 - p)
                        v.wait_ge(s["added"], (c + 1) * EXPERTS)
                        here = slice(c * GROUP, (c + 1) * GROUP)
                        v.tensor_tensor(y[:], y[:], base[:, here, :], ALU.add).then_inc(s["weighed"], 1)
                        wait(v, s, c + 1, "weighed")
                        v.tensor_tensor(x[:, here, :], x[:, here, :], y[:], ALU.add).then_inc(s["done"], 1)

                    route(0, 0)
                    walk(v, 4, body)



PARTS = [l0_attention, l0_cross, l0_ffn, l1_attention, l1_cross, l1_ffn, l2_attention, l2_cross, l2_ffn, l3_attention, l3_cross, l3_ffn]


def laid_out(v):
    col = lambda name: v[name].reshape(-1, 1)
    kb = lambda w: w.reshape(-1, 128, w.shape[-1]).transpose(1, 0, 2)
    r = {}
    r["x"] = v["x"].reshape(TOK, D)
    c = v["ctx_1024"].reshape(BATCH, TP, TILES, D)
    r["ctx"] = c
    r["ctx_t"] = c.transpose(0, 3, 2, 1).reshape(BATCH, D, CTX)
    r["ctx_mask"] = v["mask_Bx1x1xS2_ff0"].reshape(BATCH, TP, TILES).transpose(0, 2, 1).reshape(BATCH, 1, CTX)
    r["L0_attn_in_proj_weight"] = v["L0_attn_in_proj_weight"].T
    r["L0_attn_out_proj_weight"] = v["L0_attn_out_proj_weight"].T
    for k in ("L0_xattn_ln_m_w", "L0_xattn_ln_m_b", "L0_xattn_ln_l_w", "L0_xattn_ln_l_b"):
        r[k] = col(k)
    r["L0_xattn_wq_t"] = v["L0_xattn_Wq"].reshape(D, 8, 64).transpose(2, 1, 0)
    r["L0_xattn_wk_t"] = v["L0_xattn_Wkv"][:, :512].reshape(D, 8, 64).transpose(2, 1, 0)
    r["L0_xattn_wv"] = v["L0_xattn_Wkv"][:, 512:]
    r["L0_xattn_wout"] = kb(v["L0_xattn_Wout"])
    r["L0_ffn_router"] = v["L0_ffn_Wr"].T
    r["L0_ffn_w1"] = v["L0_ffn_W1"].transpose(1, 0, 2)
    r["L0_ffn_b1"] = v["L0_ffn_b1"]
    r["L0_ffn_wo"] = kb(v["L0_ffn_Wo"])
    r["L0_ffn_rows"] = np.stack([v["L0_ffn_bo"], v["L0_ffn_gamma"], v["L0_ffn_beta"]])
    for k in "xwkvrg":
        r[f"L1_maa_{k}"] = col(f"L1_attn_time_maa_{k}")
    r["L1_maa_w1"] = v["L1_attn_time_maa_w1"]
    r["L1_maa_w2"] = v["L1_attn_time_maa_w2"].transpose(1, 0, 2)
    r["L1_decay"] = col("L1_attn_time_decay")
    r["L1_decay_w1"] = v["L1_attn_time_decay_w1"]
    r["L1_decay_w2"] = v["L1_attn_time_decay_w2"]
    r["L1_bonus"] = v["L1_attn_time_faaaa"].reshape(D, 1)
    r["L1_w"] = np.stack([v[f"L1_attn_W{k}"] for k in "rkvgo"], 1)
    r["L1_ln_w"], r["L1_ln_b"] = col("L1_attn_ln_w"), col("L1_attn_ln_b")
    r["L1_xattn_wq"], r["L1_xattn_wkv"], r["L1_xattn_wp"] = v["L1_xattn_Wq"], v["L1_xattn_Wkv"], v["L1_xattn_Wp"]
    r["L1_xattn_bq"] = col("L1_xattn_bq")
    r["L1_xattn_bk"] = v["L1_xattn_bkv"][:D].reshape(D, 1)
    r["L1_xattn_bv"] = v["L1_xattn_bkv"][D:].reshape(D, 1)
    r["L1_xattn_bp"] = v["L1_xattn_bp"].reshape(1, D)
    r["L1_ffn_centroids"] = v["L1_ffn_centroids"].T
    r["L1_ffn_g"], r["L1_ffn_b"] = v["L1_ffn_ln_g"].T, v["L1_ffn_ln_b"].T
    r["L1_ffn_w1"] = v["L1_ffn_w1"].transpose(1, 0, 2)
    r["L1_ffn_b1"], r["L1_ffn_b2"] = v["L1_ffn_b1"], v["L1_ffn_b2"]
    r["L1_ffn_w2"] = v["L1_ffn_w2"].reshape(EXPERTS, 4, 128, D).transpose(2, 1, 0, 3)
    r["L2_dt"], r["L2_bdt"] = v["L2_attn_W_dt"].T, col("L2_attn_b_dt")
    r["L2_bc"] = np.stack([v["L2_attn_W_B"].T, v["L2_attn_W_C"].T], 1)
    r["L2_alog"], r["L2_d"] = v["L2_attn_A_log"], col("L2_attn_D")
    r["L2_x_cols"] = np.stack([v["L2_xattn_w_cq"], v["L2_xattn_w_c"], v["L2_xattn_w_q"]], 1)
    r["L2_x_bias"] = np.stack([v["L2_xattn_b_cq"], v["L2_xattn_b_c"], v["L2_xattn_b_q"]]).reshape(1, 3)
    r["L2_x_wl"] = kb(v["L2_xattn_W_l"].T)
    r["L2_x_bl"] = v["L2_xattn_b_l"].reshape(1, D)
    for k in ("ln1_weight", "ln1_bias", "ln2_weight", "ln2_bias"):
        r[f"L2_{k}"] = col(f"L2_ffn_{k}")
    w = v["L2_ffn_qkv_weight"]
    rep = lambda m: np.repeat(m.reshape(4, 8, D), 4, axis=0).reshape(D, D)
    r["L2_qkv"] = np.concatenate([w[:128], rep(w[128:160]), rep(w[160:192])]).T
    r["L2_proj"] = v["L2_ffn_proj_weight"].T
    r["L2_router"] = v["L2_ffn_router_weight"].T
    r["L2_moe_w1"] = v["L2_ffn_moe_w1"].transpose(1, 0, 2)
    r["L2_moe_w2"] = v["L2_ffn_moe_w2"].reshape(EXPERTS, 2, 128, D).transpose(2, 0, 1, 3)
    r["L3_scale"] = col("L3_attn_norm_scale")
    r["L3_wqkv"] = np.concatenate([v[f"L3_attn_w{k}"].reshape(D, 1024) for k in "qkv"], 1)
    r["L3_wout"] = kb(v["L3_attn_w_out"].reshape(1024, D))
    r["L3_bout"] = v["L3_attn_b_out"].reshape(1, D)
    r["L3_x_w"] = np.stack([v["L3_xattn_W"][:, :D].T, v["L3_xattn_W"][:, D:].T], 1)
    r["L3_x_b"] = v["L3_xattn_b"].reshape(1, D)
    r["L3_ffn_w1"] = v["L3_ffn_W1"][1]
    r["L3_ffn_b1"] = v["L3_ffn_b1"][1].reshape(2, 128).T
    r["L3_ffn_w2"] = kb(v["L3_ffn_W2"][1])
    r["L3_ffn_b2"] = v["L3_ffn_b2"][1].reshape(1, D)
    return r


def build(nc, a, out, consts):
    with ExitStack() as es:
        def sb(label, shape):
            return es.enter_context(nc.sbuf_tensor(label, shape, F32))

        g = {"x": sb("x_sb", [PT, PAIRS, D]), "h_n": sb("h_n", [PT, PAIRS, D]), "h_t": sb("h_t", [D, TOK]),
             "ident": sb("ident", [D, D]), "half": sb("half", [D, 16]),
             "ones": sb("ones", [D, D]), "ctx_sum": sb("ctx_sum", [D, BATCH]), "headmask": consts["headmask"],
             "consts": consts}
        with stage(nc, "start", "x_in const_in") as (s, _, _):
            with nc.Block() as block:
                @block.sync
                def _(sp):
                    sp.dma_start(g["x"][:], a["x"].rearrange("(n p) d -> p n d", p=PT)).then_inc(s["x_in"], 16)
                    sp.dma_start(g["ident"][:], consts["ident"]).then_inc(s["x_in"], 16)
                    sp.wait_ge(s["x_in"], 32)

                @block.vector
                def _(v):
                    v.memset(g["half"][:], -0.5)
                    v.memset(g["ones"][:], 1.0).then_inc(s["const_in"], 1)
                    v.wait_ge(s["const_in"], 1)
        for part in PARTS:
            part(nc, g, a)
        with stage(nc, "end", "stored") as (s, _, _):
            with nc.Block() as block:
                @block.sync
                def _(sp):
                    sp.dma_start(out.rearrange("(n p) d -> p n d", p=PT), g["x"][:]).then_inc(s["stored"], 16)
                    sp.wait_ge(s["stored"], 16)


def shape_constants():
    f = np.float32
    p = np.arange(PT)
    same = p[:, None] // SEQ == p[None, :] // SEQ
    q, t = np.arange(D)[:, None], np.arange(D)[None, :]
    src, dst = (p % SEQ)[:, None], (p % SEQ)[None, :]
    levels = [same & (src // (2 * m) == dst // (2 * m)) & (src // m < dst // m) for m in HALVES] + [same & (src == dst)]
    pick = np.zeros((EXPERTS, EXPERTS, D), f)
    for e in range(EXPERTS):
        pick[e, e] = 1
    return {
        "ident": np.eye(D, dtype=f),
        "headmask": (np.arange(D)[:, None] // 8 == np.arange(HEADS)[None, :]).astype(f),
        "headmask4": (np.arange(D)[:, None] % 32 // 8 == np.arange(4)[None, :]).astype(f),
        "causal_mask": np.where(same & (p[:, None] >= p[None, :]), 0, NEG).astype(f),
        "batch_mask": np.where(same, 0, NEG).astype(f),
        "sequence_mask": np.where((q // BATCH == t // BATCH) & (q >= t), 0, NEG).astype(f),
        "level_mask": np.stack(levels, 1).astype(f),
        "pick": pick,
        "earlier": np.tile(np.arange(EXPERTS, 0, -1).astype(f), (D, 1)),
    }


HALVES = (1, 2, 4, 8, 16, 32)


def kernel(**inputs):
    from concourse import bacc
    from concourse.bass_utils import run_bass_kernel_spmd

    nc = bacc.Bacc("TRN2", target_bir_lowering=False, num_devices=1)
    arrays = laid_out({k: np.asarray(v) for k, v in inputs.items()})
    consts = shape_constants()
    named = {**{f"in_{k}": v for k, v in arrays.items()}, **{f"c_{k}": v for k, v in consts.items()}}
    named = {k: np.ascontiguousarray(v) for k, v in named.items()}
    aps = {k: nc.dram_tensor(k, v.shape, F32, kind="ExternalInput").ap() for k, v in named.items()}
    out = nc.dram_tensor("out", (TOK, D), F32, kind="ExternalOutput").ap()
    build(nc, {k[3:]: ap for k, ap in aps.items() if k.startswith("in_")}, out,
          {k[2:]: ap for k, ap in aps.items() if k.startswith("c_")})
    got = run_bass_kernel_spmd(nc, [named], core_ids=[0])
    return got.results[0]["out"].reshape(BATCH, SEQ, D)
```
